# Optimizing a Trainium2 kernel written in Bass

```python
import numpy as np
import jax
import jax.numpy as jnp

def _softmax(x, axis=-1):
    return jax.nn.softmax(x, axis=axis)

def _gelu(x):
    return jax.nn.gelu(x, approximate=True)

def _silu(x):
    return jax.nn.silu(x)

def _sigmoid(x):
    return jax.nn.sigmoid(x)

def _layernorm(x, axis=-1, eps=1e-05):
    m = jnp.mean(x, axis=axis, keepdims=True)
    v = jnp.var(x, axis=axis, keepdims=True)
    return (x - m) / jnp.sqrt(v + eps)

def _scatter_add(tgt, idx, src, axis=0):
    return tgt.at[idx].add(src)

def _segment_sum(src, seg, n):
    return jax.ops.segment_sum(src, seg, n)
kernel_name = 'mk_vit_tower_d4_tok_img768_r4_21cdc2'

def setup_inputs(seed: int=0):
    np.random.seed(seed)
    _w = jnp.asarray

    def _rec_inputs():
        import jax
        import jax.numpy as jnp
        _rk = jax.random.key(seed)
        x = -1.80045e-05 + 0.999906 * jax.random.normal(jax.random.fold_in(_rk, 1), (64, 3, 96, 96), jnp.float32)
        return x
    x = _rec_inputs()

    def _L0_tok_setup():
        import jax, jax.numpy as jnp
        import numpy as np
        IMAGE_SIZE = 96
        PATCH = 16
        CHANNELS = 3
        TOKEN_DIM = 192
        NUM_PATCHES = (IMAGE_SIZE // PATCH) ** 2
        PATCH_DIM = CHANNELS * PATCH * PATCH
        N_TOKENS = NUM_PATCHES + 1

        def _fixed_pos_embedding(n_tokens, dim):
            i = np.arange(n_tokens, dtype=np.float32)[:, None]
            j = np.arange(dim, dtype=np.float32)[None, :]
            j_even = np.where(j % 2 == 0, j, j - 1)
            angle = i / np.power(10000.0, j_even / dim)
            tab = np.where(j % 2 == 0, np.sin(angle), np.cos(angle)).astype(np.float32)
            return jnp.asarray(tab)

        def _make_patches(image):
            B, C, H, Wd = image.shape
            p = PATCH
            hp, wp = (H // p, Wd // p)
            x = image.reshape(B, C, hp, p, wp, p)
            x = x.transpose(0, 1, 2, 4, 3, 5)
            return x.reshape(B, hp * wp, C * p * p)
        key = jax.random.key(seed)
        k_img, k_w, k_b, k_cls = jax.random.split(key, 4)
        image = jax.random.normal(k_img, (128, CHANNELS, IMAGE_SIZE, IMAGE_SIZE), dtype=jnp.float32)
        W = jax.random.normal(k_w, (TOKEN_DIM, PATCH_DIM), dtype=jnp.float32) / np.sqrt(PATCH_DIM)
        b = jax.random.normal(k_b, (TOKEN_DIM,), dtype=jnp.float32) * 0.01
        class_token = jax.random.normal(k_cls, (1, TOKEN_DIM), dtype=jnp.float32)
        pos_embedding = _fixed_pos_embedding(N_TOKENS, TOKEN_DIM)
        return {'image': image, 'W': W, 'b': b, 'class_token': class_token, 'pos_embedding': pos_embedding}
    _L0_tok_all = _L0_tok_setup()
    _L0_tok_in = {k: v for k, v in _L0_tok_all.items() if k in ('W', 'b', 'class_token', 'pos_embedding')}
    del _L0_tok_all

    def _L0_attn_setup():
        import jax, jax.numpy as jnp
        import numpy as np
        NUM_HEADS = 12
        OT_REG = 0.1
        SINKHORN_ITERS = 10
        DIAG_VAL = 1000.0

        def _sot(q):
            N = q.shape[-2]
            qn = q / (jnp.linalg.norm(q, axis=-1, keepdims=True) + 1e-08)
            C = 1.0 - jnp.einsum('bhnd,bhmd->bhnm', qn, qn)
            eye = jnp.eye(N, dtype=bool)
            C = jnp.where(eye, DIAG_VAL, C)
            log_K = -C / OT_REG
            log_marg = -jnp.log(jnp.float32(N))
            log_v = jnp.zeros(q.shape[:2] + (N,), dtype=q.dtype)
            for _ in range(SINKHORN_ITERS):
                log_u = log_marg - jax.nn.logsumexp(log_K + log_v[..., None, :], axis=-1)
                log_v = log_marg - jax.nn.logsumexp(log_K + log_u[..., :, None], axis=-2)
            log_T = log_u[..., :, None] + log_K + log_v[..., None, :]
            z = jnp.exp(log_T)
            z = z / jnp.max(z, axis=(-2, -1), keepdims=True)
            z = jnp.where(eye, 1.0, z)
            return z
        key = jax.random.key(seed)
        k1, k2, k3 = jax.random.split(key, 3)
        B, N, C = (64, 64, 192)
        x = jax.random.normal(k1, (B, N, C), dtype=jnp.float32)
        w_qkv = jax.random.normal(k2, (3 * C, C), dtype=jnp.float32) * C ** (-0.5)
        w_proj = jax.random.normal(k3, (C, C), dtype=jnp.float32) * C ** (-0.5)
        b_proj = jnp.zeros((C,), dtype=jnp.float32)
        return {'x': x, 'w_qkv': w_qkv, 'w_proj': w_proj, 'b_proj': b_proj}
    _L0_attn_all = _L0_attn_setup()
    _L0_attn_in = {k: v for k, v in _L0_attn_all.items() if k in ('w_qkv', 'w_proj', 'b_proj')}
    del _L0_attn_all

    def _L0_ffn_setup():
        import jax, jax.numpy as jnp
        import numpy as np
        B, S, D = (2, 256, 192)
        I = 96
        E = 8
        G = 4
        TOPK_GROUPS = 2
        K = 2
        ROUTE_SCALE = 1.0
        ALPHA, LIMIT = (1.702, 7.0)

        def swiglu(h):
            xg = jnp.minimum(h[..., ::2], LIMIT)
            xl = jnp.clip(h[..., 1::2], -LIMIT, LIMIT)
            return xg * jax.nn.sigmoid(ALPHA * xg) * (xl + 1.0)

        def gate(x, gate_w, gate_b):
            scores = jax.nn.softmax(jnp.einsum('td,ed->te', x, gate_w).astype(jnp.float32), axis=-1)
            original_scores = scores
            s = scores + gate_b
            T = x.shape[0]
            sg = s.reshape(T, G, E // G)
            group_scores = jnp.sum(jax.lax.top_k(sg, 2)[0], axis=-1)
            _, gidx = jax.lax.top_k(group_scores, TOPK_GROUPS)
            keep = jnp.any(jax.nn.one_hot(gidx, G, dtype=jnp.bool_), axis=1)
            sg = jnp.where(keep[:, :, None], sg, -jnp.inf)
            s = sg.reshape(T, E)
            _, idx = jax.lax.top_k(s, K)
            w = jnp.take_along_axis(original_scores, idx, axis=1) * ROUTE_SCALE
            return (w.astype(x.dtype), idx)

        def expert_ffn(x, W1, B1, W3, B3, W2, B2):
            h1 = jnp.einsum('td,edh->teh', x, W1) + B1
            h3 = jnp.einsum('td,edh->teh', x, W3) + B3
            g = swiglu(h1 * h3)
            return jnp.einsum('tei,eid->ted', g, W2) + B2

        def shared_ffn(x, Ws1, Bs1, Ws3, Bs3, Ws2, Bs2):
            h = (x @ Ws1 + Bs1) * (x @ Ws3 + Bs3)
            return swiglu(h) @ Ws2 + Bs2
        key = jax.random.key(seed)
        ks = jax.random.split(key, 16)
        sc = 0.02
        inp = {'x': jax.random.normal(ks[0], (B, S, D), jnp.float32), 'gate_w': jax.random.normal(ks[1], (E, D), jnp.float32) * sc, 'gate_b': jax.random.normal(ks[2], (E,), jnp.float32) * sc, 'W1': jax.random.normal(ks[3], (E, D, 2 * I), jnp.float32) * sc, 'B1': jax.random.normal(ks[4], (E, 2 * I), jnp.float32) * sc, 'W3': jax.random.normal(ks[5], (E, D, 2 * I), jnp.float32) * sc, 'B3': jax.random.normal(ks[6], (E, 2 * I), jnp.float32) * sc, 'W2': jax.random.normal(ks[7], (E, I, D), jnp.float32) * sc, 'B2': jax.random.normal(ks[8], (E, D), jnp.float32) * sc, 'Ws1': jax.random.normal(ks[9], (D, 2 * I), jnp.float32) * sc, 'Bs1': jax.random.normal(ks[10], (2 * I,), jnp.float32) * sc, 'Ws3': jax.random.normal(ks[11], (D, 2 * I), jnp.float32) * sc, 'Bs3': jax.random.normal(ks[12], (2 * I,), jnp.float32) * sc, 'Ws2': jax.random.normal(ks[13], (I, D), jnp.float32) * sc, 'Bs2': jax.random.normal(ks[14], (D,), jnp.float32) * sc}
        return inp
    _L0_ffn_all = _L0_ffn_setup()
    _L0_ffn_in = {k: v for k, v in _L0_ffn_all.items() if k in ('gate_w', 'gate_b', 'W1', 'B1', 'W3', 'B3', 'W2', 'B2', 'Ws1', 'Bs1', 'Ws3', 'Bs3', 'Ws2', 'Bs2')}
    del _L0_ffn_all

    def _L1_attn_setup():
        import jax, jax.numpy as jnp
        import numpy as np
        B, S, E, H, D = (2, 512, 192, 12, 64)
        EPS = 1e-05
        key = jax.random.key(seed)
        ks = jax.random.split(key, 6)
        bound = float(np.sqrt(6.0 / E))
        u = lambda k, shp: jax.random.uniform(k, shp, jnp.float32, -bound, bound)
        return {'x': jax.random.normal(ks[0], (B, S, E), jnp.float32), 'ln_w': jnp.ones((E,), jnp.float32), 'ln_b': jnp.zeros((E,), jnp.float32), 'wq': u(ks[1], (E, H * D)), 'bq': jnp.zeros((H * D,), jnp.float32), 'wk': u(ks[2], (E, H * D)), 'bk': jnp.zeros((H * D,), jnp.float32), 'wv': u(ks[3], (E, H * D)), 'bv': jnp.zeros((H * D,), jnp.float32), 'wo': u(ks[4], (H * D, E)), 'bo': jnp.zeros((E,), jnp.float32)}
    _L1_attn_all = _L1_attn_setup()
    _L1_attn_in = {k: v for k, v in _L1_attn_all.items() if k in ('ln_w', 'ln_b', 'wq', 'bq', 'wk', 'bk', 'wv', 'bv', 'wo', 'bo')}
    del _L1_attn_all

    def _L1_ffn_setup():
        import jax, jax.numpy as jnp
        import numpy as np
        import math
        N_HEAD = 12
        N_EXP = 8
        TOP_K = 2
        EVAL_CAPACITY = 1.0
        MIN_CAPACITY = 4
        EPS = 1e-05

        def layer_norm(x, w):
            mu = jnp.mean(x, axis=-1, keepdims=True)
            var = jnp.var(x, axis=-1, keepdims=True)
            return (x - mu) / jnp.sqrt(var + EPS) * w

        def attention(x, c_attn_w, c_proj_w):
            B, T, C = x.shape
            H, D = (N_HEAD, C // N_HEAD)
            qkv = x @ c_attn_w.T
            q, k, v = jnp.split(qkv, 3, axis=-1)
            q = q.reshape(B, T, H, D).transpose(0, 2, 1, 3)
            k = k.reshape(B, T, H, D).transpose(0, 2, 1, 3)
            v = v.reshape(B, T, H, D).transpose(0, 2, 1, 3)
            scores = jnp.einsum('bhqd,bhkd->bhqk', q, k) * (1.0 / math.sqrt(D))
            causal = jnp.tril(jnp.ones((T, T), dtype=bool))
            scores = jnp.where(causal, scores, -jnp.inf)
            att = jax.nn.softmax(scores, axis=-1)
            y = jnp.einsum('bhqk,bhkd->bhqd', att, v)
            y = y.transpose(0, 2, 1, 3).reshape(B, T, C)
            return y @ c_proj_w.T

        def get_capacity(num_tokens):
            cap = int(math.floor(TOP_K * EVAL_CAPACITY * num_tokens / N_EXP))
            cap += cap % 2
            return max(cap, MIN_CAPACITY)

        def moe(x_flat, w_g, c_fc, c_proj_e):
            n_tok, C = x_flat.shape
            logits = x_flat @ w_g.T
            top_vals, top_idx = jax.lax.top_k(logits, TOP_K)
            rows = jnp.arange(n_tok)[:, None]
            masked = jnp.full_like(logits, -jnp.inf).at[rows, top_idx].set(top_vals)
            probs = jax.nn.softmax(masked, axis=-1)
            cap = get_capacity(n_tok)
            flat_e = top_idx.reshape(-1)
            onehot = jax.nn.one_hot(flat_e, N_EXP, dtype=jnp.int32)
            pos = jnp.cumsum(onehot, axis=0) - onehot
            slot = jnp.take_along_axis(pos, flat_e[:, None], axis=1)[:, 0]
            valid = slot < cap
            tok = jnp.repeat(jnp.arange(n_tok), TOP_K)
            slot_c = jnp.where(valid, slot, cap)
            sec = jnp.zeros((n_tok, N_EXP, cap + 1), dtype=x_flat.dtype)
            sec = sec.at[tok, flat_e, slot_c].set(1.0)[:, :, :cap]
            w_tok = probs[tok, flat_e]
            cb = jnp.zeros((n_tok, N_EXP, cap + 1), dtype=x_flat.dtype)
            cb = cb.at[tok, flat_e, slot_c].set(w_tok)[:, :, :cap]
            dispatched = jnp.einsum('tec,td->ecd', sec, x_flat)
            h = jax.nn.gelu(jnp.einsum('ecd,edh->ech', dispatched, c_fc), approximate=False)
            out = jnp.einsum('ech,ehd->ecd', h, c_proj_e)
            return jnp.einsum('tec,ecd->td', cb, out)
        key = jax.random.key(seed)
        ks = jax.random.split(key, 7)
        B, T, C = (2, 512, 192)
        std = 0.02
        return {'x': jax.random.normal(ks[0], (B, T, C), dtype=jnp.float32), 'ln1_w': jnp.ones((C,), dtype=jnp.float32), 'ln2_w': jnp.ones((C,), dtype=jnp.float32), 'c_attn_w': jax.random.normal(ks[1], (3 * C, C), dtype=jnp.float32) * std, 'c_proj_w': jax.random.normal(ks[2], (C, C), dtype=jnp.float32) * std, 'w_g': jax.random.normal(ks[3], (N_EXP, C), dtype=jnp.float32) * std, 'c_fc': jax.random.normal(ks[4], (N_EXP, C, 4 * C), dtype=jnp.float32) * std, 'c_proj_e': jax.random.normal(ks[5], (N_EXP, 4 * C, C), dtype=jnp.float32) * std}
    _L1_ffn_all = _L1_ffn_setup()
    _L1_ffn_in = {k: v for k, v in _L1_ffn_all.items() if k in ('ln1_w', 'ln2_w', 'c_attn_w', 'c_proj_w', 'w_g', 'c_fc', 'c_proj_e')}
    del _L1_ffn_all

    def _L2_attn_setup():
        import jax, jax.numpy as jnp
        import numpy as np
        B, N, D, H = (8, 196, 192, 16)

        def _relative_pos(n_patch):
            img = int(round(n_patch ** 0.5))
            idx = jnp.arange(n_patch)
            cx = (idx % img).astype(jnp.float32)
            cy = (idx // img).astype(jnp.float32)
            dx = cx[None, :] - cx[:, None]
            dy = cy[None, :] - cy[:, None]
            return jnp.stack([dx, dy, dx * dx + dy * dy], axis=-1)
        key = jax.random.key(seed)
        ks = jax.random.split(key, 6)
        x = jax.random.normal(ks[0], (B, N, D), dtype=jnp.float32)
        w_qk = jax.random.normal(ks[1], (2 * D, D), dtype=jnp.float32) * 0.02
        w_v = jax.random.normal(ks[2], (D, D), dtype=jnp.float32) * 0.02
        w_proj = jax.random.normal(ks[3], (D, D), dtype=jnp.float32) * 0.02
        b_proj = jnp.zeros((D,), dtype=jnp.float32)
        w_pos = jax.random.normal(ks[4], (H, 3), dtype=jnp.float32) * 0.02
        b_pos = jnp.zeros((H,), dtype=jnp.float32)
        gating = jnp.ones((H,), dtype=jnp.float32)
        return {'x': x, 'w_qk': w_qk, 'w_v': w_v, 'w_proj': w_proj, 'b_proj': b_proj, 'w_pos': w_pos, 'b_pos': b_pos, 'gating': gating}
    _L2_attn_all = _L2_attn_setup()
    _L2_attn_in = {k: v for k, v in _L2_attn_all.items() if k in ('w_qk', 'w_v', 'w_proj', 'b_proj', 'w_pos', 'b_pos', 'gating')}
    del _L2_attn_all

    def _L2_ffn_setup():
        import jax, jax.numpy as jnp
        import numpy as np
        B, S, H = (2, 256, 192)
        E, K, I = (16, 4, 192)
        ALPHA, LIMIT, EPS = (1.702, 7.0, 1e-05)

        def _swiglu(h):
            x_glu, x_lin = jnp.split(h, 2, axis=-1)
            x_glu = jnp.minimum(x_glu, LIMIT)
            x_lin = jnp.clip(x_lin, -LIMIT, LIMIT)
            return x_glu * jax.nn.sigmoid(ALPHA * x_glu) * (x_lin + 1.0)
        key = jax.random.key(seed)
        ks = jax.random.split(key, 7)
        x = jax.random.normal(ks[0], (B, S, H), dtype=jnp.float32)
        scale = jnp.ones((H,), jnp.float32)
        gate_w = jax.random.normal(ks[1], (E, H), jnp.float32) * 0.02
        gate_b = jnp.zeros((E,), jnp.float32)
        w1 = jax.random.normal(ks[2], (E, H, 2 * I), jnp.float32) * 0.02
        b1 = jax.random.normal(ks[3], (E, 2 * I), jnp.float32) * 0.02
        w2 = jax.random.normal(ks[4], (E, I, H), jnp.float32) * 0.02
        b2 = jax.random.normal(ks[5], (E, H), jnp.float32) * 0.02
        return {'x': x, 'scale': scale, 'gate_w': gate_w, 'gate_b': gate_b, 'w1': w1, 'b1': b1, 'w2': w2, 'b2': b2}
    _L2_ffn_all = _L2_ffn_setup()
    _L2_ffn_in = {k: v for k, v in _L2_ffn_all.items() if k in ('scale', 'gate_w', 'gate_b', 'w1', 'b1', 'w2', 'b2')}
    del _L2_ffn_all

    def _L3_attn_setup():
        import jax, jax.numpy as jnp
        import numpy as np
        import math
        D_MODEL = 192
        N_HEADS = 12
        D_HEAD = D_MODEL // N_HEADS
        LATENT = 128
        HIDDEN = 512
        B, L = (1, 512)

        def _w(key, shape, scale=0.02):
            return jax.random.normal(key, shape, dtype=jnp.float32) * scale

        def rmsnorm(x, w, eps=1e-06):
            xf = x.astype(jnp.float32)
            rms = jax.lax.rsqrt(jnp.mean(xf * xf, axis=-1, keepdims=True) + eps)
            return w * (xf * rms).astype(x.dtype)

        def rope(x):
            Lx, Dh = (x.shape[1], x.shape[3])
            inv_freq = 1.0 / 10000.0 ** (jnp.arange(0, Dh, 2, dtype=jnp.float32) / Dh)
            t = jnp.arange(Lx, dtype=jnp.float32)
            freqs = jnp.outer(t, inv_freq)
            emb = jnp.concatenate([freqs, freqs], -1)
            cos = jnp.cos(emb)[None, :, None, :]
            sin = jnp.sin(emb)[None, :, None, :]
            x1, x2 = jnp.split(x, 2, axis=-1)
            x_rot = jnp.concatenate([-x2, x1], axis=-1)
            return x * cos + x_rot * sin
        key = jax.random.key(seed)
        ks = jax.random.split(key, 12)
        return {'x': jax.random.normal(ks[0], (B, L, D_MODEL), dtype=jnp.float32), 'ln_w': jnp.ones((D_MODEL,), jnp.float32), 'w_comp': _w(ks[1], (D_MODEL, LATENT)), 'w_qkv': _w(ks[2], (LATENT, 3 * D_MODEL)), 'w_reso': _w(ks[3], (LATENT, N_HEADS * 4)), 'qn_w': jnp.ones((D_HEAD,), jnp.float32), 'kn_w': jnp.ones((D_HEAD,), jnp.float32), 'w_outgate': _w(ks[4], (LATENT, D_MODEL)), 'head_decay': jnp.linspace(-3.0, 1.0, N_HEADS, dtype=jnp.float32), 'temperature': jnp.ones((1,), jnp.float32) * 0.5, 'w_proj': _w(ks[5], (D_MODEL, D_MODEL)), 'memn_w': jnp.ones((D_MODEL,), jnp.float32), 'ffn_ln_w': jnp.ones((D_MODEL,), jnp.float32), 'w1': _w(ks[6], (D_MODEL, HIDDEN)), 'w2': _w(ks[7], (D_MODEL, HIDDEN)), 'w3': _w(ks[8], (HIDDEN, D_MODEL))}
    _L3_attn_all = _L3_attn_setup()
    _L3_attn_in = {k: v for k, v in _L3_attn_all.items() if k in ('ln_w', 'w_comp', 'w_qkv', 'w_reso', 'qn_w', 'kn_w', 'w_outgate', 'head_decay', 'temperature', 'w_proj', 'memn_w', 'ffn_ln_w', 'w1', 'w2', 'w3')}
    del _L3_attn_all

    def _L3_ffn_setup():
        import jax, jax.numpy as jnp
        import numpy as np
        B, T, C = (2, 256, 192)
        H, NE, K = (768, 8, 2)
        key = jax.random.key(seed)
        k1, k2, k3, k4 = jax.random.split(key, 4)
        x = jax.random.normal(k1, (B, T, C), dtype=jnp.float32)
        w_fc = jax.random.normal(k2, (C, H * NE), dtype=jnp.float32) * 0.02
        w_proj = jax.random.normal(k3, (H * NE, C), dtype=jnp.float32) * (0.02 * (2 * 12) ** (-0.5))
        w_gate = jax.random.normal(k4, (C, NE), dtype=jnp.float32) * 0.02
        return {'x': x, 'w_fc': w_fc, 'w_proj': w_proj, 'w_gate': w_gate}
    _L3_ffn_all = _L3_ffn_setup()
    _L3_ffn_in = {k: v for k, v in _L3_ffn_all.items() if k in ('w_fc', 'w_proj', 'w_gate')}
    del _L3_ffn_all
    return {'x': x, 'L0_tok_W': _L0_tok_in['W'], 'L0_tok_b': _L0_tok_in['b'], 'L0_tok_class_token': _L0_tok_in['class_token'], 'L0_tok_pos_embedding': _L0_tok_in['pos_embedding'], 'L0_attn_w_qkv': _L0_attn_in['w_qkv'], 'L0_attn_w_proj': _L0_attn_in['w_proj'], 'L0_attn_b_proj': _L0_attn_in['b_proj'], 'L0_ffn_gate_w': _L0_ffn_in['gate_w'], 'L0_ffn_gate_b': _L0_ffn_in['gate_b'], 'L0_ffn_W1': _L0_ffn_in['W1'], 'L0_ffn_B1': _L0_ffn_in['B1'], 'L0_ffn_W3': _L0_ffn_in['W3'], 'L0_ffn_B3': _L0_ffn_in['B3'], 'L0_ffn_W2': _L0_ffn_in['W2'], 'L0_ffn_B2': _L0_ffn_in['B2'], 'L0_ffn_Ws1': _L0_ffn_in['Ws1'], 'L0_ffn_Bs1': _L0_ffn_in['Bs1'], 'L0_ffn_Ws3': _L0_ffn_in['Ws3'], 'L0_ffn_Bs3': _L0_ffn_in['Bs3'], 'L0_ffn_Ws2': _L0_ffn_in['Ws2'], 'L0_ffn_Bs2': _L0_ffn_in['Bs2'], 'L1_attn_ln_w': _L1_attn_in['ln_w'], 'L1_attn_ln_b': _L1_attn_in['ln_b'], 'L1_attn_wq': _L1_attn_in['wq'], 'L1_attn_bq': _L1_attn_in['bq'], 'L1_attn_wk': _L1_attn_in['wk'], 'L1_attn_bk': _L1_attn_in['bk'], 'L1_attn_wv': _L1_attn_in['wv'], 'L1_attn_bv': _L1_attn_in['bv'], 'L1_attn_wo': _L1_attn_in['wo'], 'L1_attn_bo': _L1_attn_in['bo'], 'L1_ffn_ln1_w': _L1_ffn_in['ln1_w'], 'L1_ffn_ln2_w': _L1_ffn_in['ln2_w'], 'L1_ffn_c_attn_w': _L1_ffn_in['c_attn_w'], 'L1_ffn_c_proj_w': _L1_ffn_in['c_proj_w'], 'L1_ffn_w_g': _L1_ffn_in['w_g'], 'L1_ffn_c_fc': _L1_ffn_in['c_fc'], 'L1_ffn_c_proj_e': _L1_ffn_in['c_proj_e'], 'L2_attn_w_qk': _L2_attn_in['w_qk'], 'L2_attn_w_v': _L2_attn_in['w_v'], 'L2_attn_w_proj': _L2_attn_in['w_proj'], 'L2_attn_b_proj': _L2_attn_in['b_proj'], 'L2_attn_w_pos': _L2_attn_in['w_pos'], 'L2_attn_b_pos': _L2_attn_in['b_pos'], 'L2_attn_gating': _L2_attn_in['gating'], 'L2_ffn_scale': _L2_ffn_in['scale'], 'L2_ffn_gate_w': _L2_ffn_in['gate_w'], 'L2_ffn_gate_b': _L2_ffn_in['gate_b'], 'L2_ffn_w1': _L2_ffn_in['w1'], 'L2_ffn_b1': _L2_ffn_in['b1'], 'L2_ffn_w2': _L2_ffn_in['w2'], 'L2_ffn_b2': _L2_ffn_in['b2'], 'L3_attn_ln_w': _L3_attn_in['ln_w'], 'L3_attn_w_comp': _L3_attn_in['w_comp'], 'L3_attn_w_qkv': _L3_attn_in['w_qkv'], 'L3_attn_w_reso': _L3_attn_in['w_reso'], 'L3_attn_qn_w': _L3_attn_in['qn_w'], 'L3_attn_kn_w': _L3_attn_in['kn_w'], 'L3_attn_w_outgate': _L3_attn_in['w_outgate'], 'L3_attn_head_decay': _L3_attn_in['head_decay'], 'L3_attn_temperature': _L3_attn_in['temperature'], 'L3_attn_w_proj': _L3_attn_in['w_proj'], 'L3_attn_memn_w': _L3_attn_in['memn_w'], 'L3_attn_ffn_ln_w': _L3_attn_in['ffn_ln_w'], 'L3_attn_w1': _L3_attn_in['w1'], 'L3_attn_w2': _L3_attn_in['w2'], 'L3_attn_w3': _L3_attn_in['w3'], 'L3_ffn_w_fc': _L3_ffn_in['w_fc'], 'L3_ffn_w_proj': _L3_ffn_in['w_proj'], 'L3_ffn_w_gate': _L3_ffn_in['w_gate']}

def reference(x, L0_tok_W, L0_tok_b, L0_tok_class_token, L0_tok_pos_embedding, L0_attn_w_qkv, L0_attn_w_proj, L0_attn_b_proj, L0_ffn_gate_w, L0_ffn_gate_b, L0_ffn_W1, L0_ffn_B1, L0_ffn_W3, L0_ffn_B3, L0_ffn_W2, L0_ffn_B2, L0_ffn_Ws1, L0_ffn_Bs1, L0_ffn_Ws3, L0_ffn_Bs3, L0_ffn_Ws2, L0_ffn_Bs2, L1_attn_ln_w, L1_attn_ln_b, L1_attn_wq, L1_attn_bq, L1_attn_wk, L1_attn_bk, L1_attn_wv, L1_attn_bv, L1_attn_wo, L1_attn_bo, L1_ffn_ln1_w, L1_ffn_ln2_w, L1_ffn_c_attn_w, L1_ffn_c_proj_w, L1_ffn_w_g, L1_ffn_c_fc, L1_ffn_c_proj_e, L2_attn_w_qk, L2_attn_w_v, L2_attn_w_proj, L2_attn_b_proj, L2_attn_w_pos, L2_attn_b_pos, L2_attn_gating, L2_ffn_scale, L2_ffn_gate_w, L2_ffn_gate_b, L2_ffn_w1, L2_ffn_b1, L2_ffn_w2, L2_ffn_b2, L3_attn_ln_w, L3_attn_w_comp, L3_attn_w_qkv, L3_attn_w_reso, L3_attn_qn_w, L3_attn_kn_w, L3_attn_w_outgate, L3_attn_head_decay, L3_attn_temperature, L3_attn_w_proj, L3_attn_memn_w, L3_attn_ffn_ln_w, L3_attn_w1, L3_attn_w2, L3_attn_w3, L3_ffn_w_fc, L3_ffn_w_proj, L3_ffn_w_gate):
    import jax
    import jax.numpy as jnp

    def _L0_tok_ref(image, W, b, class_token, pos_embedding):
        import jax, jax.numpy as jnp
        import numpy as np
        IMAGE_SIZE = 96
        PATCH = 16
        CHANNELS = 3
        TOKEN_DIM = 192
        NUM_PATCHES = (IMAGE_SIZE // PATCH) ** 2
        PATCH_DIM = CHANNELS * PATCH * PATCH
        N_TOKENS = NUM_PATCHES + 1

        def _fixed_pos_embedding(n_tokens, dim):
            i = np.arange(n_tokens, dtype=np.float32)[:, None]
            j = np.arange(dim, dtype=np.float32)[None, :]
            j_even = np.where(j % 2 == 0, j, j - 1)
            angle = i / np.power(10000.0, j_even / dim)
            tab = np.where(j % 2 == 0, np.sin(angle), np.cos(angle)).astype(np.float32)
            return jnp.asarray(tab)

        def _make_patches(image):
            B, C, H, Wd = image.shape
            p = PATCH
            hp, wp = (H // p, Wd // p)
            x = image.reshape(B, C, hp, p, wp, p)
            x = x.transpose(0, 1, 2, 4, 3, 5)
            return x.reshape(B, hp * wp, C * p * p)
        patches = _make_patches(image)
        tokens = jnp.einsum('bnd,td->bnt', patches, W) + b
        B = tokens.shape[0]
        cls = jnp.broadcast_to(class_token[None, :, :], (B, 1, TOKEN_DIM))
        tokens = jnp.concatenate([cls, tokens], axis=1)
        return tokens + pos_embedding[None, :, :]

    def _L0_attn_ref(x, w_qkv, w_proj, b_proj):
        import jax, jax.numpy as jnp
        import numpy as np
        NUM_HEADS = 12
        OT_REG = 0.1
        SINKHORN_ITERS = 10
        DIAG_VAL = 1000.0

        def _sot(q):
            N = q.shape[-2]
            qn = q / (jnp.linalg.norm(q, axis=-1, keepdims=True) + 1e-08)
            C = 1.0 - jnp.einsum('bhnd,bhmd->bhnm', qn, qn)
            eye = jnp.eye(N, dtype=bool)
            C = jnp.where(eye, DIAG_VAL, C)
            log_K = -C / OT_REG
            log_marg = -jnp.log(jnp.float32(N))
            log_v = jnp.zeros(q.shape[:2] + (N,), dtype=q.dtype)
            for _ in range(SINKHORN_ITERS):
                log_u = log_marg - jax.nn.logsumexp(log_K + log_v[..., None, :], axis=-1)
                log_v = log_marg - jax.nn.logsumexp(log_K + log_u[..., :, None], axis=-2)
            log_T = log_u[..., :, None] + log_K + log_v[..., None, :]
            z = jnp.exp(log_T)
            z = z / jnp.max(z, axis=(-2, -1), keepdims=True)
            z = jnp.where(eye, 1.0, z)
            return z
        B, N, C = x.shape
        H = NUM_HEADS
        hd = C // H
        scale = hd ** (-0.5)
        qkv = jnp.einsum('bnc,oc->bno', x, w_qkv)
        qkv = qkv.reshape(B, N, 3, H, hd).transpose(2, 0, 3, 1, 4)
        q, k, v = (qkv[0], qkv[1], qkv[2])
        attn = _sot(q)
        attn = jax.nn.softmax(attn * scale, axis=-1)
        out = jnp.einsum('bhnm,bhmd->bhnd', attn, v)
        out = out.transpose(0, 2, 1, 3).reshape(B, N, C)
        out = jnp.einsum('bnc,oc->bno', out, w_proj) + b_proj
        return out

    def _L0_ffn_ref(x, gate_w, gate_b, W1, B1, W3, B3, W2, B2, Ws1, Bs1, Ws3, Bs3, Ws2, Bs2):
        import jax, jax.numpy as jnp
        import numpy as np
        B, S, D = (2, 256, 192)
        I = 96
        E = 8
        G = 4
        TOPK_GROUPS = 2
        K = 2
        ROUTE_SCALE = 1.0
        ALPHA, LIMIT = (1.702, 7.0)

        def swiglu(h):
            xg = jnp.minimum(h[..., ::2], LIMIT)
            xl = jnp.clip(h[..., 1::2], -LIMIT, LIMIT)
            return xg * jax.nn.sigmoid(ALPHA * xg) * (xl + 1.0)

        def gate(x, gate_w, gate_b):
            scores = jax.nn.softmax(jnp.einsum('td,ed->te', x, gate_w).astype(jnp.float32), axis=-1)
            original_scores = scores
            s = scores + gate_b
            T = x.shape[0]
            sg = s.reshape(T, G, E // G)
            group_scores = jnp.sum(jax.lax.top_k(sg, 2)[0], axis=-1)
            _, gidx = jax.lax.top_k(group_scores, TOPK_GROUPS)
            keep = jnp.any(jax.nn.one_hot(gidx, G, dtype=jnp.bool_), axis=1)
            sg = jnp.where(keep[:, :, None], sg, -jnp.inf)
            s = sg.reshape(T, E)
            _, idx = jax.lax.top_k(s, K)
            w = jnp.take_along_axis(original_scores, idx, axis=1) * ROUTE_SCALE
            return (w.astype(x.dtype), idx)

        def expert_ffn(x, W1, B1, W3, B3, W2, B2):
            h1 = jnp.einsum('td,edh->teh', x, W1) + B1
            h3 = jnp.einsum('td,edh->teh', x, W3) + B3
            g = swiglu(h1 * h3)
            return jnp.einsum('tei,eid->ted', g, W2) + B2

        def shared_ffn(x, Ws1, Bs1, Ws3, Bs3, Ws2, Bs2):
            h = (x @ Ws1 + Bs1) * (x @ Ws3 + Bs3)
            return swiglu(h) @ Ws2 + Bs2
        inp_shape = x.shape
        xt = x.reshape(-1, D)
        w, idx = gate(xt, gate_w, gate_b)
        combine = jnp.einsum('tk,tke->te', w, jax.nn.one_hot(idx, E, dtype=w.dtype))
        per_expert = expert_ffn(xt, W1, B1, W3, B3, W2, B2)
        routed = jnp.einsum('ted,te->td', per_expert, combine)
        out = routed + shared_ffn(xt, Ws1, Bs1, Ws3, Bs3, Ws2, Bs2)
        return out.reshape(inp_shape)

    def _L1_attn_ref(x, ln_w, ln_b, wq, bq, wk, bk, wv, bv, wo, bo):
        import jax, jax.numpy as jnp
        import numpy as np
        B, S, E, H, D = (2, 512, 192, 12, 64)
        EPS = 1e-05
        b, s, _ = x.shape
        mu = x.mean(-1, keepdims=True)
        var = ((x - mu) ** 2).mean(-1, keepdims=True)
        xn = (x - mu) * jax.lax.rsqrt(var + EPS) * ln_w + ln_b
        q = (xn @ wq + bq).reshape(b, s, H, D)
        k = (xn @ wk + bk).reshape(b, s, H, D)
        v = (xn @ wv + bv).reshape(b, s, H, D)
        scale = 1.0 / np.sqrt(D).astype(np.float32)
        scores = jnp.einsum('bihd,bjhd->bhij', q, k) * scale
        mask = jnp.tril(jnp.ones((s, s), dtype=bool), k=-1)
        scores = jnp.where(mask, -jnp.inf, scores)
        a = jax.nn.softmax(scores, axis=-1)
        h = jnp.einsum('bhij,bjhd->bihd', a, v).reshape(b, s, H * D)
        return h @ wo + bo

    def _L1_ffn_ref(x, ln1_w, ln2_w, c_attn_w, c_proj_w, w_g, c_fc, c_proj_e):
        import jax, jax.numpy as jnp
        import numpy as np
        import math
        N_HEAD = 12
        N_EXP = 8
        TOP_K = 2
        EVAL_CAPACITY = 1.0
        MIN_CAPACITY = 4
        EPS = 1e-05

        def layer_norm(x, w):
            mu = jnp.mean(x, axis=-1, keepdims=True)
            var = jnp.var(x, axis=-1, keepdims=True)
            return (x - mu) / jnp.sqrt(var + EPS) * w

        def attention(x, c_attn_w, c_proj_w):
            B, T, C = x.shape
            H, D = (N_HEAD, C // N_HEAD)
            qkv = x @ c_attn_w.T
            q, k, v = jnp.split(qkv, 3, axis=-1)
            q = q.reshape(B, T, H, D).transpose(0, 2, 1, 3)
            k = k.reshape(B, T, H, D).transpose(0, 2, 1, 3)
            v = v.reshape(B, T, H, D).transpose(0, 2, 1, 3)
            scores = jnp.einsum('bhqd,bhkd->bhqk', q, k) * (1.0 / math.sqrt(D))
            causal = jnp.tril(jnp.ones((T, T), dtype=bool))
            scores = jnp.where(causal, scores, -jnp.inf)
            att = jax.nn.softmax(scores, axis=-1)
            y = jnp.einsum('bhqk,bhkd->bhqd', att, v)
            y = y.transpose(0, 2, 1, 3).reshape(B, T, C)
            return y @ c_proj_w.T

        def get_capacity(num_tokens):
            cap = int(math.floor(TOP_K * EVAL_CAPACITY * num_tokens / N_EXP))
            cap += cap % 2
            return max(cap, MIN_CAPACITY)

        def moe(x_flat, w_g, c_fc, c_proj_e):
            n_tok, C = x_flat.shape
            logits = x_flat @ w_g.T
            top_vals, top_idx = jax.lax.top_k(logits, TOP_K)
            rows = jnp.arange(n_tok)[:, None]
            masked = jnp.full_like(logits, -jnp.inf).at[rows, top_idx].set(top_vals)
            probs = jax.nn.softmax(masked, axis=-1)
            cap = get_capacity(n_tok)
            flat_e = top_idx.reshape(-1)
            onehot = jax.nn.one_hot(flat_e, N_EXP, dtype=jnp.int32)
            pos = jnp.cumsum(onehot, axis=0) - onehot
            slot = jnp.take_along_axis(pos, flat_e[:, None], axis=1)[:, 0]
            valid = slot < cap
            tok = jnp.repeat(jnp.arange(n_tok), TOP_K)
            slot_c = jnp.where(valid, slot, cap)
            sec = jnp.zeros((n_tok, N_EXP, cap + 1), dtype=x_flat.dtype)
            sec = sec.at[tok, flat_e, slot_c].set(1.0)[:, :, :cap]
            w_tok = probs[tok, flat_e]
            cb = jnp.zeros((n_tok, N_EXP, cap + 1), dtype=x_flat.dtype)
            cb = cb.at[tok, flat_e, slot_c].set(w_tok)[:, :, :cap]
            dispatched = jnp.einsum('tec,td->ecd', sec, x_flat)
            h = jax.nn.gelu(jnp.einsum('ecd,edh->ech', dispatched, c_fc), approximate=False)
            out = jnp.einsum('ech,ehd->ecd', h, c_proj_e)
            return jnp.einsum('tec,ecd->td', cb, out)
        x = x + attention(layer_norm(x, ln1_w), c_attn_w, c_proj_w)
        B, T, C = x.shape
        x_ln = layer_norm(x, ln2_w)
        moe_out = moe(x_ln.reshape(B * T, C), w_g, c_fc, c_proj_e)
        return x + moe_out.reshape(B, T, C)

    def _L2_attn_ref(x, w_qk, w_v, w_proj, b_proj, w_pos, b_pos, gating):
        import jax, jax.numpy as jnp
        import numpy as np
        B, N, D, H = (8, 196, 192, 16)

        def _relative_pos(n_patch):
            img = int(round(n_patch ** 0.5))
            idx = jnp.arange(n_patch)
            cx = (idx % img).astype(jnp.float32)
            cy = (idx // img).astype(jnp.float32)
            dx = cx[None, :] - cx[:, None]
            dy = cy[None, :] - cy[:, None]
            return jnp.stack([dx, dy, dx * dx + dy * dy], axis=-1)
        b, n, d = x.shape
        h = gating.shape[0]
        hd = d // h
        scale = hd ** (-0.5)
        rel = _relative_pos(n)
        pos_logits = jnp.einsum('nmc,hc->hnm', rel, w_pos) + b_pos[:, None, None]
        pos_score = jax.nn.softmax(pos_logits, axis=-1)
        qk = (x @ w_qk.T).reshape(b, n, 2, h, hd)
        q = jnp.transpose(qk[:, :, 0], (0, 2, 1, 3))
        k = jnp.transpose(qk[:, :, 1], (0, 2, 1, 3))
        attn_score = jax.nn.softmax(jnp.einsum('bhnd,bhmd->bhnm', q, k) * scale, axis=-1)
        g = jax.nn.sigmoid(gating)[None, :, None, None]
        attn = (1.0 - g) * attn_score + g * pos_score[None]
        attn = attn / jnp.sum(attn, axis=-1, keepdims=True)
        v = (x @ w_v.T).reshape(b, n, h, hd).transpose(0, 2, 1, 3)
        y = jnp.einsum('bhnm,bhmd->bhnd', attn, v)
        y = y.transpose(0, 2, 1, 3).reshape(b, n, d)
        return y @ w_proj.T + b_proj

    def _L2_ffn_ref(x, scale, gate_w, gate_b, w1, b1, w2, b2):
        import jax, jax.numpy as jnp
        import numpy as np
        B, S, H = (2, 256, 192)
        E, K, I = (16, 4, 192)
        ALPHA, LIMIT, EPS = (1.702, 7.0, 1e-05)

        def _swiglu(h):
            x_glu, x_lin = jnp.split(h, 2, axis=-1)
            x_glu = jnp.minimum(x_glu, LIMIT)
            x_lin = jnp.clip(x_lin, -LIMIT, LIMIT)
            return x_glu * jax.nn.sigmoid(ALPHA * x_glu) * (x_lin + 1.0)
        Bx, Sx, Hx = x.shape
        xf = x.astype(jnp.float32)
        t = xf * jax.lax.rsqrt(jnp.mean(xf * xf, axis=-1, keepdims=True) + EPS) * scale
        t = t.reshape(-1, Hx)
        T = t.shape[0]
        g = t @ gate_w.T + gate_b
        vals, idx = jax.lax.top_k(g, K)
        w = jax.nn.softmax(vals, axis=-1) / K
        full_w = jnp.zeros((T, E), jnp.float32).at[jnp.arange(T)[:, None], idx].set(w)
        h = jnp.einsum('th,ehf->tef', t, w1) + b1
        h = _swiglu(h)
        y = jnp.einsum('tei,eih->teh', h, w2) + b2
        out = jnp.einsum('teh,te->th', y, full_w) * K
        return x + out.astype(x.dtype).reshape(Bx, Sx, Hx)

    def _L3_attn_ref(x, ln_w, w_comp, w_qkv, w_reso, qn_w, kn_w, w_outgate, head_decay, temperature, w_proj, memn_w, ffn_ln_w, w1, w2, w3):
        import jax, jax.numpy as jnp
        import numpy as np
        import math
        D_MODEL = 192
        N_HEADS = 12
        D_HEAD = D_MODEL // N_HEADS
        LATENT = 128
        HIDDEN = 512
        B, L = (1, 512)

        def _w(key, shape, scale=0.02):
            return jax.random.normal(key, shape, dtype=jnp.float32) * scale

        def rmsnorm(x, w, eps=1e-06):
            xf = x.astype(jnp.float32)
            rms = jax.lax.rsqrt(jnp.mean(xf * xf, axis=-1, keepdims=True) + eps)
            return w * (xf * rms).astype(x.dtype)

        def rope(x):
            Lx, Dh = (x.shape[1], x.shape[3])
            inv_freq = 1.0 / 10000.0 ** (jnp.arange(0, Dh, 2, dtype=jnp.float32) / Dh)
            t = jnp.arange(Lx, dtype=jnp.float32)
            freqs = jnp.outer(t, inv_freq)
            emb = jnp.concatenate([freqs, freqs], -1)
            cos = jnp.cos(emb)[None, :, None, :]
            sin = jnp.sin(emb)[None, :, None, :]
            x1, x2 = jnp.split(x, 2, axis=-1)
            x_rot = jnp.concatenate([-x2, x1], axis=-1)
            return x * cos + x_rot * sin
        Bx, Lx, D = x.shape
        H, Dh = (N_HEADS, D_HEAD)
        x_norm = rmsnorm(x, ln_w)
        latent = jax.nn.silu(x_norm @ w_comp)
        qkv = latent @ w_qkv
        q, k, v = jnp.split(qkv, 3, axis=-1)
        q = q.reshape(Bx, Lx, H, Dh)
        k = k.reshape(Bx, Lx, H, Dh)
        v = v.reshape(Bx, Lx, H, Dh)
        q = rope(rmsnorm(q, qn_w))
        k = rope(rmsnorm(k, kn_w))
        q_f = jax.nn.elu(q.astype(jnp.float32)) + 1.0
        k_f = jax.nn.elu(k.astype(jnp.float32)) + 1.0
        v_f = v.astype(jnp.float32)
        params = (latent @ w_reso).reshape(Bx, Lx, H, 4)
        sem_amp = jax.nn.sigmoid(params[..., 0])
        sem_phase = jax.nn.sigmoid(params[..., 1]) * math.pi
        ctx_amp = jax.nn.sigmoid(params[..., 2])
        ctx_phase = jax.nn.sigmoid(params[..., 3]) * math.pi
        raw_decay = 0.3 + 0.65 * jax.nn.sigmoid(head_decay.reshape(1, 1, H))
        decay_rate = jnp.clip(raw_decay, 1e-05, 0.999)
        dt = 1.0 - decay_rate
        base_gate = jax.nn.sigmoid(sem_amp * ctx_amp * jnp.cos(sem_phase - ctx_phase) * temperature)
        gate = jnp.clip(base_gate * 1.2 - 0.1, 0.05, 0.95)
        kv_input = jnp.einsum('blhd,blhe->blhde', k_f, v_f) * gate[..., None, None]
        kv_input = kv_input * dt[..., None, None]
        z_input = k_f * dt[..., None]
        log_decay = jnp.log(decay_rate)[..., None]
        cum_log_decay = jnp.cumsum(jnp.broadcast_to(log_decay, (Bx, Lx, H, 1)), axis=1)
        df = jnp.exp(cum_log_decay)
        safe_df_z = df + 1e-08
        kv_states = jnp.cumsum(kv_input / safe_df_z[..., None], axis=1) * df[..., None]
        z_states = jnp.cumsum(z_input / safe_df_z, axis=1) * df
        out_num = jnp.einsum('blhd,blhde->blhe', q_f, kv_states)
        den = jnp.clip(jnp.sum(q_f * z_states, axis=-1, keepdims=True), 1e-05, None)
        out = (out_num / den).reshape(Bx, Lx, D)
        out = rmsnorm(out, memn_w)
        attn_out = out @ w_proj * jax.nn.silu(latent @ w_outgate)
        x = x + attn_out
        xn = rmsnorm(x, ffn_ln_w)
        ffn_out = jax.nn.silu(xn @ w1) * (xn @ w2) @ w3
        return x + ffn_out

    def _L3_ffn_ref(x, w_fc, w_proj, w_gate):
        import jax, jax.numpy as jnp
        import numpy as np
        B, T, C = (2, 256, 192)
        H, NE, K = (768, 8, 2)
        router_logits = jnp.einsum('btc,ce->bte', x, w_gate)
        router_probs = jax.nn.softmax(router_logits, axis=-1)
        top_p, top_i = jax.lax.top_k(router_probs, K)
        top_p = top_p / jnp.sum(top_p, axis=-1, keepdims=True)
        wf = w_fc.reshape(C, H, NE)
        h_all = jnp.einsum('btc,che->bthe', x, wf)
        h = jnp.take_along_axis(h_all, top_i[:, :, None, :], axis=-1)
        h = jax.nn.gelu(h, approximate=True)
        wp = w_proj.reshape(H, C, NE)
        o_all = jnp.einsum('bthk,hce->btcke', h, wp)
        o = jnp.take_along_axis(o_all, top_i[:, :, None, :, None], axis=-1)[..., 0]
        o = jnp.einsum('btck,btk->btc', o, top_p)
        return o
    h = _L0_tok_ref(x, L0_tok_W, L0_tok_b, L0_tok_class_token, L0_tok_pos_embedding)
    h = h + _L0_attn_ref(_layernorm(h, axis=-1), L0_attn_w_qkv, L0_attn_w_proj, L0_attn_b_proj)
    h = h + _L0_ffn_ref(_layernorm(h, axis=-1), L0_ffn_gate_w, L0_ffn_gate_b, L0_ffn_W1, L0_ffn_B1, L0_ffn_W3, L0_ffn_B3, L0_ffn_W2, L0_ffn_B2, L0_ffn_Ws1, L0_ffn_Bs1, L0_ffn_Ws3, L0_ffn_Bs3, L0_ffn_Ws2, L0_ffn_Bs2)
    h = h + _L1_attn_ref(_layernorm(h, axis=-1), L1_attn_ln_w, L1_attn_ln_b, L1_attn_wq, L1_attn_bq, L1_attn_wk, L1_attn_bk, L1_attn_wv, L1_attn_bv, L1_attn_wo, L1_attn_bo)
    h = h + _L1_ffn_ref(_layernorm(h, axis=-1), L1_ffn_ln1_w, L1_ffn_ln2_w, L1_ffn_c_attn_w, L1_ffn_c_proj_w, L1_ffn_w_g, L1_ffn_c_fc, L1_ffn_c_proj_e)
    h = h + _L2_attn_ref(_layernorm(h, axis=-1), L2_attn_w_qk, L2_attn_w_v, L2_attn_w_proj, L2_attn_b_proj, L2_attn_w_pos, L2_attn_b_pos, L2_attn_gating)
    h = h + _L2_ffn_ref(_layernorm(h, axis=-1), L2_ffn_scale, L2_ffn_gate_w, L2_ffn_gate_b, L2_ffn_w1, L2_ffn_b1, L2_ffn_w2, L2_ffn_b2)
    h = h + _L3_attn_ref(_layernorm(h, axis=-1), L3_attn_ln_w, L3_attn_w_comp, L3_attn_w_qkv, L3_attn_w_reso, L3_attn_qn_w, L3_attn_kn_w, L3_attn_w_outgate, L3_attn_head_decay, L3_attn_temperature, L3_attn_w_proj, L3_attn_memn_w, L3_attn_ffn_ln_w, L3_attn_w1, L3_attn_w2, L3_attn_w3)
    h = h + _L3_ffn_ref(_layernorm(h, axis=-1), L3_ffn_w_fc, L3_ffn_w_proj, L3_ffn_w_gate)
    return h

_drawn_inputs = setup_inputs


def setup_inputs(seed=0):
    import zlib

    import numpy as np

    out = dict(_drawn_inputs(seed))
    spreads = {'L0_attn_b_proj': (0.0, 0.1),
     'L1_attn_ln_w': (1.0, 0.2),
     'L1_attn_ln_b': (0.0, 0.1),
     'L1_attn_bq': (0.0, 0.1),
     'L1_attn_bk': (0.0, 2.0),
     'L1_attn_bv': (0.0, 0.1),
     'L1_attn_bo': (0.0, 0.303),
     'L1_ffn_ln1_w': (1.0, 0.6),
     'L1_ffn_ln2_w': (1.0, 0.6),
     'L2_attn_b_proj': (0.0, 0.383),
     'L2_attn_b_pos': (0.0, 2.0),
     'L2_attn_gating': (1.0, 0.6),
     'L2_ffn_scale': (1.0, 0.6),
     'L2_ffn_gate_b': (0.0, 0.8),
     'L3_attn_ln_w': (1.0, 0.6),
     'L3_attn_qn_w': (1.0, 0.6),
     'L3_attn_kn_w': (1.0, 0.6),
     'L3_attn_memn_w': (1.0, 0.6),
     'L3_attn_ffn_ln_w': (1.0, 0.6)}
    factors = {'L0_tok_b': 3.714,
     'L0_ffn_gate_w': 8.0,
     'L0_ffn_gate_b': 8.0,
     'L0_ffn_W1': 8.0,
     'L0_ffn_B1': 8.0,
     'L0_ffn_W3': 8.0,
     'L0_ffn_B3': 8.0,
     'L0_ffn_W2': 8.0,
     'L0_ffn_B2': 8.0,
     'L0_ffn_Ws1': 7.365,
     'L0_ffn_Bs1': 8.0,
     'L0_ffn_Ws3': 7.492,
     'L0_ffn_Bs3': 8.0,
     'L0_ffn_Ws2': 7.52,
     'L1_ffn_c_attn_w': 4.479,
     'L1_ffn_c_proj_w': 3.599,
     'L1_ffn_w_g': 6.339,
     'L1_ffn_c_fc': 5.581,
     'L1_ffn_c_proj_e': 5.676,
     'L2_attn_w_qk': 8.0,
     'L2_attn_w_v': 4.729,
     'L2_attn_w_proj': 4.669,
     'L2_attn_w_pos': 8.0,
     'L2_ffn_gate_w': 8.0,
     'L2_ffn_w1': 8.0,
     'L2_ffn_b1': 8.0,
     'L2_ffn_w2': 8.0,
     'L2_ffn_b2': 48.768,
     'L3_attn_w_comp': 8.0,
     'L3_attn_w_qkv': 8.0,
     'L3_attn_w_reso': 8.0,
     'L3_attn_w_outgate': 8.0,
     'L3_attn_head_decay': 8.0,
     'L3_attn_w_proj': 8.0,
     'L3_attn_w1': 8.0,
     'L3_attn_w2': 8.0,
     'L3_attn_w3': 8.0,
     'L3_ffn_w_fc': 23.76,
     'L3_ffn_w_proj': 8.0,
     'L3_ffn_w_gate': 22.522,
     'L0_ffn_Bs2': 2.908}
    for name, (base, spread) in spreads.items():
        noise = np.random.default_rng([zlib.crc32(name.encode()), seed]).standard_normal(out[name].shape)
        drawn = base * np.exp(spread * noise) if base else spread * noise
        out[name] = jnp.asarray(drawn.astype(out[name].dtype))
    for name, factor in factors.items():
        out[name] = (out[name] * factor).astype(out[name].dtype)
    return out
```

```python
from contextlib import ExitStack

import numpy as np
import concourse.bass as bass
from concourse import mybir

F32 = mybir.dt.float32
ALU = mybir.AluOpType
ACT = mybir.ActivationFunctionType
AX = mybir.AxisListType

C = 192
CK = 96
NTOK = 37
IMGS = 3
T = IMGS * NTOK
BATCH = 64
NT = 22
NP = NT * T
UB = 474
NB = 5
DIAG = NTOK + T
BIG = 1.0e30
PAD = -3.0e38
MARK = 3.0e38
ALPHA, LIMIT = 1.702, 7.0
CAP = 592


def steps(text):
    out, n = {}, 0
    for group in text.split():
        names = group.split("|")
        size = 0
        for name in names:
            name, _, many = name.partition(":")
            assert name not in out, name
            out[name] = n
            size += int(many) if many else 1
        n += size
    out["end"] = n
    return out


def ln_steps(g):
    return f"{g}_stats {g}_aggr {g}_log {g}_rstd {g}_norm "


def rms_steps(g):
    return f"{g}_sq {g}_log {g}_rstd {g}_norm "


def turn_steps(g):
    return f"{g}_tr {g}_cp "


SOFTMAX = "sm_scale sm_max sm_sub sm_exp sm_sum sm_inv "
SPREAD = "px0|px1 pt pc0|pc1 av "


def topk_steps(g):
    return f"{g}_top {g}_keys {g}_repl {g}_mask "



def over(ap, shape):
    return ap.broadcast_to(shape)



def norm_vector(dve, go, done, B, g, src, dst):
    for c in (0, 1):
        go(c, f"{g}_stats")
        dve.bn_stats(B[c]["stats"][:, :], src[c]).then_inc(done[c], 1)
    for c in (0, 1):
        go(c, f"{g}_aggr", B[c]["passed"])
        dve.bn_aggr(B[c]["mv"][:, :], B[c]["stats"][:, :]).then_inc(done[c], 1)
    for c in (0, 1):
        go(c, f"{g}_norm")
        dve.tensor_scalar(dst[c], src[c], B[c]["mv"][:, 0:1], B[c]["rstd"][:, 1:2],
                          ALU.subtract, ALU.mult).then_inc(done[c], 1)


def norm_scalar(act, go, done, B, g, eps):
    for c in (0, 1):
        go(c, f"{g}_log")
        act.activation(B[c]["rstd"][:, 0:1], B[c]["mv"][:, 1:2], ACT.Ln, bias=eps).then_inc(done[c], 1)
    for c in (0, 1):
        go(c, f"{g}_rstd")
        act.activation(B[c]["rstd"][:, 1:2], B[c]["rstd"][:, 0:1], ACT.Exp, scale=-0.5).then_inc(done[c], 1)


def rms_scalar(act, go, done, B, g, src, eps):
    for c in (0, 1):
        go(c, f"{g}_sq")
        act.activation(B[c]["junk"][:, :], src[c], ACT.Square, accum_out=B[c]["mv"][:, 0:1]).then_inc(done[c], 1)
    for c in (0, 1):
        go(c, f"{g}_log")
        act.activation(B[c]["rstd"][:, 0:1], B[c]["mv"][:, 0:1], ACT.Ln, bias=eps, scale=1.0 / C).then_inc(done[c], 1)
    for c in (0, 1):
        go(c, f"{g}_rstd")
        act.activation(B[c]["rstd"][:, 1:2], B[c]["rstd"][:, 0:1], ACT.Exp, scale=-0.5).then_inc(done[c], 1)


def rms_vector(dve, go, done, B, g, src, dst):
    for c in (0, 1):
        go(c, f"{g}_norm")
        dve.tensor_scalar(dst[c], src[c], B[c]["rstd"][:, 1:2], None, ALU.mult).then_inc(done[c], 1)


def turn_tensor(pe, go, done, g, src, ps, bank, ident):
    for c in (0, 1):
        go(c, f"{g}_tr")
        for o in range(2):
            mm = pe.transpose(ps[c][0:CK, bank, o * T:(o + 1) * T], src[c][:, o * CK:(o + 1) * CK],
                              ident[0:T, 0:T])
        mm.then_inc(done[c], 1)


def turn_scalar(act, go, done, g, ps, bank, dst, scale=None, bias=None):
    for c in (0, 1):
        go(c, f"{g}_cp")
        if scale is None:
            act.copy(dst[c][:, :, :].rearrange("p o t -> p (o t)"), ps[c][0:CK, bank, 0:2 * T]).then_inc(done[c], 1)
            continue
        for o in range(2):
            kw = {} if bias is None else {"bias": bias[:, o:o + 1]}
            ins = act.activation(dst[c][:, o, :], ps[c][0:CK, bank, o * T:(o + 1) * T], ACT.Identity,
                                 scale=scale[:, o:o + 1], **kw)
        ins.then_inc(done[c], 1)


def heads_expand(eng, go, done, B, step, o, HG, hmask):
    for c in (0, 1):
        go(c, step)
        for j in range(IMGS):
            k = B[c]["kT"][:, o, j * NTOK:(j + 1) * NTOK].unsqueeze(1)
            ins = eng.tensor_tensor(B[c]["kx"][:, o, j, 0:HG, :], over(k, [CK, HG, NTOK]),
                                    over(hmask[:, 0:HG].unsqueeze(2), [CK, HG, NTOK]), ALU.mult)
        ins.then_inc(done[c], 1)


def scores_tensor(pe, go, done, B, ps, HG):
    for c in (0, 1):
        go(c, "S")
        for o in range(2):
            for j in range(IMGS):
                mm = pe.matmul(ps[c][0:T, o, 0:HG * NTOK], B[c]["qx"][:, o, j * T:(j + 1) * T],
                               B[c]["kx"][:, o, j, 0:HG, :].rearrange("p h m -> p (h m)"),
                               start=(j == 0), stop=(j == IMGS - 1))
        mm.then_inc(done[c], 1)


def query_blocks(act, go, done, B, ps, step, bank):
    for c in (0, 1):
        go(c, step)
        for o in range(2):
            ins = act.copy(B[c]["qx"][:, o, :].rearrange("p (j x) -> p j x", x=DIAG)[:, :, 0:NTOK],
                           ps[c][0:CK, bank, o * T:(o + 1) * T].rearrange("p (j m) -> p j m", m=NTOK))
        ins.then_inc(done[c], 1)


def softmax_vector(dve, go, done, B, S, scale, bias, H):
    for c in (0, 1):
        go(c, "sm_scale")
        src, P = S[c], B[c]["P4"]
        for o in range(src.shape[1]):
            shape = [T, src.shape[2], NTOK]
            if bias is None:
                ins = dve.tensor_scalar(P[:, o], src[:, o], scale, None, ALU.mult)
            else:
                ins = dve.scalar_tensor_tensor(P[:, o], src[:, o], scale, over(bias[:, :].unsqueeze(1), shape),
                                               ALU.mult, ALU.add)
        ins.then_inc(done[c], 1)
    for c in (0, 1):
        go(c, "sm_max")
        dve.tensor_reduce(B[c]["hmax"][:, 0:H], B[c]["P"][:, 0:H, :], AX.X, ALU.max).then_inc(done[c], 1)
    for c in (0, 1):
        go(c, "sm_sub")
        dve.tensor_tensor(B[c]["P"][:, 0:H, :], B[c]["P"][:, 0:H, :],
                          over(B[c]["hmax"][:, 0:H].unsqueeze(2), [T, H, NTOK]), ALU.subtract).then_inc(done[c], 1)
    sums_vector(dve, go, done, B, H)


def sums_vector(dve, go, done, B, H):
    for c in (0, 1):
        go(c, "sm_sum")
        dve.tensor_reduce(B[c]["hsum"][:, 0:H], B[c]["P"][:, 0:H, :], AX.X, ALU.add).then_inc(done[c], 1)
    for c in (0, 1):
        go(c, "sm_inv")
        dve.reciprocal(B[c]["hinv"][:, 0:H], B[c]["hsum"][:, 0:H]).then_inc(done[c], 1)


def softmax_scalar(act, go, done, B, H):
    for c in (0, 1):
        go(c, "sm_exp")
        act.activation(B[c]["P"][:, 0:H, :], B[c]["P"][:, 0:H, :], ACT.Exp).then_inc(done[c], 1)


def blocks_expand(eng, go, done, B, step, h0, h1, bmask):
    for c in (0, 1):
        go(c, step)
        for h in range(h0, h1):
            ins = eng.tensor_tensor(B[c]["px"][:, h, :].rearrange("p (j m) -> p j m", m=NTOK),
                                    over(B[c]["P"][:, h, :].unsqueeze(1), [T, IMGS, NTOK]),
                                    bmask[:, :].rearrange("p (j m) -> p j m", m=NTOK), ALU.mult)
        ins.then_inc(done[c], 1)


def probs_turn_tensor(pe, go, done, B, ps, H, ident):
    for c in (0, 1):
        go(c, "pt")
        for h in range(H):
            mm = pe.transpose(ps[c][0:T, h // 4, (h % 4) * T:(h % 4 + 1) * T], B[c]["px"][:, h, :],
                              ident[0:T, 0:T])
        mm.then_inc(done[c], 1)


def probs_copy(copy, go, done, B, ps, step, b0, b1):
    for c in (0, 1):
        go(c, step)
        for b in range(b0, b1):
            ins = copy(B[c]["pT"][:, 4 * b:4 * b + 4, :].rearrange("p h n -> p (h n)"), ps[c][0:T, b, 0:4 * T])
        ins.then_inc(done[c], 1)


def values_tensor(pe, go, done, B, ps, H, D, V, per_bank, order=None):
    for c in (0, 1):
        go(c, "av")
        for h in range(H):
            b, r = h // per_bank, h % per_bank
            v = h if order is None else order[h]
            mm = pe.matmul(ps[c][0:T, b, r * D:(r + 1) * D], B[c]["pT"][:, h, :], V[c][:, v * D:(v + 1) * D],
                           start=True, stop=True)
        mm.then_inc(done[c], 1)


def topk_vector(dve, go, done, B, g, vals, keys, k, E, mask):
    for c in (0, 1):
        go(c, f"{g}_top", B[c]["passed"])
        dve.max(B[c]["max8"][:, :], B[c][vals][:, 0:E + 8]).then_inc(done[c], 1)
    for c in (0, 1):
        go(c, f"{g}_keys")
        dve.tensor_copy(B[c][keys][:, 0:k], B[c]["max8"][:, 0:k]).then_inc(done[c], 1)
    for c in (0, 1):
        go(c, f"{g}_repl", B[c]["passed"])
        dve.match_replace(B[c]["repl"][:, 0:E + 8], B[c][keys][:, :], B[c][vals][:, 0:E + 8], MARK).then_inc(done[c], 1)
    for c in (0, 1):
        go(c, f"{g}_mask")
        dve.tensor_scalar(mask[c], B[c]["repl"][:, 0:E], 0.5 * MARK, None, ALU.is_ge).then_inc(done[c], 1)



def vit_tower(nc, d, out):
    root = ExitStack()

    def sb(ctx, name, shape):
        return ctx.enter_context(nc.sbuf_tensor(name, shape, F32))

    def sem(name):
        return root.enter_context(nc.semaphore(name))

    with root:
        K = {}
        resident = load_list(root, sb, d, K, COMMON)
        K["tok_add"] = sb(root, "tok_add", [T, C])
        h_all = sb(root, "h_all", [T, NT, C])
        xT_all = sb(root, "xT_all", [CK, 2, NP])
        yT_all = sb(root, "yT_all", [CK, 2, NP])
        maskT = sb(root, "maskT", [8, NP])
        combT = sb(root, "combT", [16, NP])
        eps5 = sb(root, "eps5", [128, 1])
        eps6 = sb(root, "eps6", [128, 1])
        m10 = sb(root, "m10", [128, 1])
        ident = K["ident"]

        layer_weights = ExitStack()
        resident += load_list(layer_weights, sb, d, K, LAYER_WEIGHTS[0])
        resident_loaded = sem("resident_loaded")
        with nc.Block() as block:
            @block.sync
            def _(sp):
                start_loads(sp, resident, resident_loaded)
                sp.wait_ge(resident_loaded, 16 * len(resident))

            @block.vector
            def _(dve):
                dve.memset(eps5[:, :], 1e-5)
                dve.memset(eps6[:, :], 1e-6)
                dve.memset(m10[:, :], -10.0)
                dve.wait_ge(resident_loaded, 16 * len(resident))
                dve.tensor_tensor(K["tok_add"][:, :], K["tok_base"][:, :], K["tok_pos"][:, :], ALU.add)

        env = dict(nc=nc, d=d, out=out, K=K, h_all=h_all, xT_all=xT_all, yT_all=yT_all, combT=combT, maskT=maskT,
                   eps5=eps5, eps6=eps6, m10=m10, ident=ident, sem=sem, sb=sb)
        with layer_weights:
            layer0_tokens(**env)
        with ExitStack() as layer_weights:
            ahead = load_list(layer_weights, sb, d, K, LAYER_WEIGHTS[1])
            experts_swiglu(layer=0, E=9, ahead=ahead, **env)
            layer1_tokens(**env)
        capacity_limit(**env)
        with ExitStack() as layer_weights:
            ahead = load_list(layer_weights, sb, d, K, LAYER_WEIGHTS[2])
            experts_gelu(layer=1, func=ACT.Gelu, ahead=ahead, **env)
            layer2_tokens(**env)
        with ExitStack() as layer_weights:
            ahead = load_list(layer_weights, sb, d, K, LAYER_WEIGHTS[3])
            experts_swiglu(layer=2, E=16, ahead=ahead, **env)
            layer3_tokens(**env)
        experts_gelu(layer=3, func=ACT.Gelu_apprx_tanh, ahead=[], **env)
        last_tokens(**env)


def load_list(ctx, sb, d, K, names):
    for n in names:
        K[n] = sb(ctx, "c_" + n, list(d[n].shape))
    return [(K[n], d[n]) for n in names]


def start_loads(sp, loads, loaded):
    for tile, src in loads:
        idx = tuple(slice(None) for _ in src.shape)
        sp.dma_start(tile[idx], src[idx]).then_inc(loaded, 16)


def tile_buffers(ctx, nc, sb, layer, shapes):
    small = dict(stats=[T, 6], mv=[T, 2], rstd=[T, 2], hmax=[T, 16], hsum=[T, 16], hinv=[T, 16],
                 max8=[T, 8], repl=[T, 24], x=[T, C], hcur=[T, C], xT=[CK, 2, T])
    B = []
    for c in (0, 1):
        one = {n: sb(ctx, f"L{layer}t{c}_{n}", s) for n, s in {**small, **shapes}.items()}
        B.append(one)
    ps = [ctx.enter_context(nc.psum_tensor(f"L{layer}ps{c}", [128, 4, 512], F32)) for c in (0, 1)]
    return B, ps


def attention_shapes(H, D):
    HG = H // 2
    return dict(P=[T, H, NTOK], px=[T, H, T], pT=[T, H, T], kT=[CK, 2, T],
                qx=[CK, 2, IMGS * DIAG], V=[T, C], o=[T, C])


def halves(B, H):
    for b in B:
        b["kx"] = b["px"][0:CK, :, :].rearrange("p h n -> p (h n)").rearrange(
            "p (o j h m) -> p o j h m", o=2, j=IMGS, h=H // 2)
        b["oT"] = b["kT"]
        b["P4"] = b["P"][:, :, :].rearrange("p (o h) m -> p o h m", o=2)


def rhs2(w, o0, o1):
    return w[:, :, o0:o1]


def take_experts_back(eng, kind, go, done, B, ps, h_all, yT_all, ident, tile_of):
    if kind == "pool":
        for c in (0, 1):
            go(c, "y_cp")
            eng.tensor_copy(B[c]["xT"][:, :, :], yT_all[:, :, bass.ds(tile_of(c) * T, T)]).then_inc(done[c], 1)
    if kind == "tensor":
        for c in (0, 1):
            go(c, "y_tr")
            for o in range(2):
                mm = eng.transpose(ps[c][0:T, 0, o * CK:(o + 1) * CK], B[c]["xT"][:, o, :], ident[0:CK, 0:CK])
            mm.then_inc(done[c], 1)
    if kind == "vector":
        for c in (0, 1):
            go(c, "y_add")
            eng.tensor_tensor(B[c]["hcur"][:, :], ps[c][0:T, 0, 0:C],
                              h_all[:, bass.ds(tile_of(c), 1), :].rearrange("p a c -> p (a c)"),
                              ALU.add).then_inc(done[c], 1)


def width_product(pe, go, done, step, ps, bank, lhsT, rhs, N):
    for c in (0, 1):
        go(c, step)
        for k in range(2):
            mm = pe.matmul(ps[c][0:T, bank, 0:N], lhsT[c][:, k, :], rhs[:, k, 0:N], start=(k == 0), stop=(k == 1))
        mm.then_inc(done[c], 1)


def store_tile(pool, go, done, B, h_all, xT_all, tile_of, src):
    for c in (0, 1):
        go(c, "h_st")
        pool.tensor_copy(h_all[:, bass.ds(tile_of(c), 1), :].rearrange("p a c -> p (a c)"),
                         B[c][src][:, :]).then_inc(done[c], 1)


def store_xT(pool, go, done, B, xT_all, tile_of):
    for c in (0, 1):
        go(c, "x_st")
        pool.tensor_copy(xT_all[:, :, bass.ds(tile_of(c) * T, T)], B[c]["xT"][:, :, :]).then_inc(done[c], 1)


def weights_out(eng, kind, go, done, B, ps, combT, ident, tile_of, E):
    for c in (0, 1):
        if kind == "tensor":
            go(c, "c_tr")
            eng.transpose(ps[c][0:E, 2, 0:T], B[c]["comb"][:, 0:E], ident[0:T, 0:T]).then_inc(done[c], 1)
        else:
            go(c, "c_st")
            eng.copy(combT[0:E, bass.ds(tile_of(c) * T, T)], ps[c][0:E, 2, 0:T]).then_inc(done[c], 1)


SINK = 7
ITERS = 10


def layer0_tokens(nc, d, K, h_all, xT_all, yT_all, combT, eps5, m10, ident, sem, sb, **_):
    H, D, HG, E = 12, 16, 6, 8
    S = steps("embed hcur " + ln_steps("n0") + turn_steps("f0") + "qv q_cp v_cp q_sq q_ss q_floor q_log q_nrm q_add "
              "q_rc q_n q_tr q_dg k_cp kx0|kx1 S K_exp|v_one K_off it:%d " % (SINK * ITERS) +
              "T1 T2 rm rm_tr im ix ix_mm ir T3 T4 sm_exp sm_sum sm_inv " + SPREAD + "o " + turn_steps("fo") +
              "proj h1 h2 h_st " + ln_steps("n1") + turn_steps("f1") + "x_st gt g_cp g_mx g_sub g_exp g_sum g_rc "
              "g_p g_s g_gs " + topk_steps("gg") + "g_pen g_sm " + topk_steps("ge") + "g_w c_tr c_st")
    N = S["end"]
    done = [sem(f"l0_tile{c}_steps") for c in (0, 1)]
    patch_loaded = [sem(f"l0_patch_loaded{c}") for c in (0, 1)]
    zeroed, passed = sem("l0_zeroed"), sem("l0_passed")
    with ExitStack() as ctx:
        shapes = attention_shapes(H, D)
        shapes.update(patch=[128, 6, T], q=[T, H, D], vb=[T, H, NTOK], kv=[T, H, NTOK], small=[T, 8, 12],
                      MX=[12, IMGS, NTOK], MI=[12, 4], rmT=[12, T], lg=[T, 8], gs=[T, 12], gm=[T, 4], sv=[T, 16],
                      keys2=[T, 8], keys8=[T, 8], mask=[T, 8], comb=[T, 16], p=[T, 8], s=[T, 8])
        B, ps = tile_buffers(ctx, nc, sb, 0, shapes)
        halves(B, H)
        for b in B:
            b["passed"] = passed
        X = [b["x"][:, :] for b in B]
        HC = [b["hcur"][:, :] for b in B]
        xT = [b["xT"] for b in B]
        oT = [b["oT"] for b in B]
        flat = [b["q"][:, :, :].rearrange("p h d -> p (h d)") for b in B]
        with nc.Block() as block:
            @block.sync
            def _(sp):
                for c in (0, 1):
                    sp.dma_start(B[c]["patch"][:, :, :].rearrange("p k t -> p (k t)"),
                                 d["patches"][c, :, :]).then_inc(patch_loaded[c], 16)
                with sp.Fori(1, NT // 2) as i:
                    for c in (0, 1):
                        sp.wait_ge(done[c], i * N - (N - S["embed"] - 2))
                        sp.dma_start(B[c]["patch"][:, :, :].rearrange("p k t -> p (k t)"),
                                     d["patches"][bass.ds(2 * i + c, 1), :, :].rearrange("a p x -> (a p) x")
                                     ).then_inc(patch_loaded[c], 16)

            @block.vector
            def _(dve):
                for c in (0, 1):
                    dve.memset(B[c]["qx"][:, :, :], 0.0)
                    dve.memset(B[c]["gs"][:, 4:12], PAD)
                    dve.memset(B[c]["sv"][:, 8:16], PAD)
                    dve.memset(B[c]["keys2"][:, :], PAD)
                    dve.memset(B[c]["keys8"][:, :], PAD)
                    ins = dve.memset(B[c]["comb"][:, 8:16], 1.0)
                ins.then_inc(zeroed, 1)
                dve.wait_ge(zeroed, 1)
                for c in (0, 1):
                    dve.sem_inc(done[c], 1)
                with dve.Fori(0, NT // 2) as i:
                    def go(c, step, passed=None):
                        dve.wait_ge(done[c], i * N + (S[step] + 1))
                        if passed is not None:
                            dve.sem_inc(passed, 1)

                    for c in (0, 1):
                        go(c, "hcur")
                        dve.tensor_tensor(HC[c], ps[c][0:T, 0, 0:C], K["tok_add"][:, :], ALU.add).then_inc(done[c], 1)
                    norm_vector(dve, go, done, B, "n0", HC, X)
                    for c in (0, 1):
                        go(c, "q_sq")
                        dve.tensor_tensor(B[c]["kv"][:, :, 0:D], B[c]["q"][:, :, :], B[c]["q"][:, :, :],
                                          ALU.mult).then_inc(done[c], 1)
                    for c in (0, 1):
                        go(c, "q_ss")
                        dve.tensor_reduce(B[c]["small"][:, 0, :], B[c]["kv"][:, :, 0:D], AX.X, ALU.add).then_inc(done[c], 1)
                    for c in (0, 1):
                        go(c, "q_floor")
                        dve.tensor_scalar(B[c]["small"][:, 1, :], B[c]["small"][:, 0, :], 1e-19, None, ALU.max
                                          ).then_inc(done[c], 1)
                    for c in (0, 1):
                        go(c, "q_add")
                        dve.tensor_scalar(B[c]["small"][:, 3, :], B[c]["small"][:, 2, :], 1e-8, None, ALU.add
                                          ).then_inc(done[c], 1)
                    for c in (0, 1):
                        go(c, "q_rc")
                        dve.reciprocal(B[c]["small"][:, 4, :], B[c]["small"][:, 3, :]).then_inc(done[c], 1)
                    for c in (0, 1):
                        go(c, "q_n")
                        dve.tensor_tensor(B[c]["q"][:, :, :], B[c]["q"][:, :, :],
                                          over(B[c]["small"][:, 4, :].unsqueeze(2), [T, H, D]), ALU.mult
                                          ).then_inc(done[c], 1)
                    for c in (0, 1):
                        go(c, "k_cp")
                        dve.tensor_copy(B[c]["kT"][:, :, :].rearrange("p o t -> p (o t)"), ps[c][0:CK, 0, 0:2 * T]
                                        ).then_inc(done[c], 1)
                    heads_expand(dve, go, done, B, "kx0", 0, HG, K["hmask16"])
                    for c in (0, 1):
                        go(c, "v_one")
                        dve.memset(B[c]["vb"][:, :, :], 1.0).then_inc(done[c], 1)
                    for c in (0, 1):
                        go(c, "K_off")
                        dve.tensor_tensor(B[c]["P"][:, :, :], B[c]["P"][:, :, :],
                                          over(K["off_diag"][:, :].unsqueeze(1), [T, H, NTOK]), ALU.mult
                                          ).then_inc(done[c], 1)
                    with dve.Fori(0, ITERS) as r:
                        def at(c, k):
                            dve.wait_ge(done[c], i * N + r * SINK + (S["it"] + 1 + k))
                        for c in (0, 1):
                            at(c, 0)
                            dve.tensor_tensor(B[c]["kv"][:, :, :], B[c]["P"][:, :, :], B[c]["vb"][:, :, :], ALU.mult
                                              ).then_inc(done[c], 1)
                        for c in (0, 1):
                            at(c, 1)
                            dve.tensor_reduce(B[c]["small"][:, 5, :], B[c]["kv"][:, :, :], AX.X, ALU.add
                                              ).then_inc(done[c], 1)
                        for c in (0, 1):
                            at(c, 2)
                            dve.reciprocal(B[c]["small"][:, 6, :], B[c]["small"][:, 5, :]).then_inc(done[c], 1)
                    for c in (0, 1):
                        go(c, "T1")
                        dve.tensor_tensor(B[c]["kv"][:, :, :], B[c]["P"][:, :, :], B[c]["vb"][:, :, :], ALU.mult
                                          ).then_inc(done[c], 1)
                    for c in (0, 1):
                        go(c, "T2")
                        dve.tensor_tensor(B[c]["kv"][:, :, :], B[c]["kv"][:, :, :],
                                          over(B[c]["small"][:, 6, :].unsqueeze(2), [T, H, NTOK]), ALU.mult
                                          ).then_inc(done[c], 1)
                    for c in (0, 1):
                        go(c, "rm")
                        dve.tensor_reduce(B[c]["small"][:, 0, :], B[c]["kv"][:, :, :], AX.X, ALU.max).then_inc(done[c], 1)
                    for c in (0, 1):
                        go(c, "im")
                        dve.tensor_reduce(B[c]["MI"][:, 0:IMGS],
                                          ps[c][0:H, 0, 0:T].rearrange("p (j n) -> p j n", n=NTOK), AX.X, ALU.max
                                          ).then_inc(done[c], 1)
                    for c in (0, 1):
                        go(c, "ix")
                        dve.tensor_copy(B[c]["MX"][:, :, :], over(B[c]["MI"][:, 0:IMGS].unsqueeze(2),
                                                                  [H, IMGS, NTOK])).then_inc(done[c], 1)
                    for c in (0, 1):
                        go(c, "ir")
                        dve.reciprocal(B[c]["small"][:, 1, :], ps[c][0:T, 1, 0:H]).then_inc(done[c], 1)
                    for c in (0, 1):
                        go(c, "T3")
                        dve.tensor_tensor(B[c]["kv"][:, :, :], B[c]["kv"][:, :, :],
                                          over(B[c]["small"][:, 1, :].unsqueeze(2), [T, H, NTOK]), ALU.mult
                                          ).then_inc(done[c], 1)
                    for c in (0, 1):
                        go(c, "T4")
                        dve.tensor_tensor(B[c]["P"][:, :, :], B[c]["kv"][:, :, :],
                                          over(K["on_diag"][:, :].unsqueeze(1), [T, H, NTOK]), ALU.add
                                          ).then_inc(done[c], 1)
                    sums_vector(dve, go, done, B, H)
                    blocks_expand(dve, go, done, B, "px0", 0, 8, K["bmask"])
                    probs_copy(dve.tensor_copy, go, done, B, ps, "pc1", 2, 3)
                    for c in (0, 1):
                        go(c, "o")
                        dve.tensor_tensor(B[c]["o"][:, :].rearrange("p (h d) -> p h d", d=D),
                                          ps[c][0:T, 0, 0:C].rearrange("p (h d) -> p h d", d=D),
                                          over(B[c]["hinv"][:, 0:H].unsqueeze(2), [T, H, D]), ALU.mult
                                          ).then_inc(done[c], 1)
                    for c in (0, 1):
                        go(c, "h1")
                        dve.tensor_tensor(HC[c], HC[c], ps[c][0:T, 1, 0:C], ALU.add).then_inc(done[c], 1)
                    for c in (0, 1):
                        go(c, "h2")
                        dve.tensor_tensor(HC[c], HC[c], K["l0_bproj"][:, :], ALU.add).then_inc(done[c], 1)
                    norm_vector(dve, go, done, B, "n1", HC, X)
                    for c in (0, 1):
                        go(c, "g_cp")
                        dve.tensor_copy(B[c]["lg"][:, :], ps[c][0:T, 1, 0:E]).then_inc(done[c], 1)
                    for c in (0, 1):
                        go(c, "g_mx")
                        dve.tensor_reduce(B[c]["mv"][:, 0:1], B[c]["lg"][:, :], AX.X, ALU.max).then_inc(done[c], 1)
                    for c in (0, 1):
                        go(c, "g_sub")
                        dve.tensor_scalar(B[c]["lg"][:, :], B[c]["lg"][:, :], B[c]["mv"][:, 0:1], None, ALU.subtract
                                          ).then_inc(done[c], 1)
                    for c in (0, 1):
                        go(c, "g_sum")
                        dve.tensor_reduce(B[c]["mv"][:, 0:1], B[c]["lg"][:, :], AX.X, ALU.add).then_inc(done[c], 1)
                    for c in (0, 1):
                        go(c, "g_rc")
                        dve.reciprocal(B[c]["mv"][:, 1:2], B[c]["mv"][:, 0:1]).then_inc(done[c], 1)
                    for c in (0, 1):
                        go(c, "g_p")
                        dve.tensor_scalar(B[c]["p"][:, :], B[c]["lg"][:, :], B[c]["mv"][:, 1:2], None, ALU.mult
                                          ).then_inc(done[c], 1)
                    for c in (0, 1):
                        go(c, "g_s")
                        dve.tensor_tensor(B[c]["s"][:, :], B[c]["p"][:, :], K["l0_gate_b"][:, :], ALU.add
                                          ).then_inc(done[c], 1)
                    for c in (0, 1):
                        go(c, "g_gs")
                        pair = B[c]["s"][:, :].rearrange("p (g e) -> p g e", e=2)
                        dve.tensor_tensor(B[c]["gs"][:, 0:4], pair[:, :, 0], pair[:, :, 1], ALU.add).then_inc(done[c], 1)
                    topk_vector(dve, go, done, B, "gg", "gs", "keys2", 2, 4, [b["gm"][:, :] for b in B])
                    for c in (0, 1):
                        go(c, "g_pen")
                        dve.tensor_scalar(B[c]["gm"][:, :], B[c]["gm"][:, :], BIG, -BIG, ALU.mult, ALU.add
                                          ).then_inc(done[c], 1)
                    for c in (0, 1):
                        go(c, "g_sm")
                        dve.tensor_tensor(B[c]["sv"][:, 0:8].rearrange("p (g e) -> p g e", e=2),
                                          B[c]["s"][:, :].rearrange("p (g e) -> p g e", e=2),
                                          over(B[c]["gm"][:, :].unsqueeze(2), [T, 4, 2]), ALU.add).then_inc(done[c], 1)
                    topk_vector(dve, go, done, B, "ge", "sv", "keys8", 2, 8, [b["mask"][:, :] for b in B])
                    for c in (0, 1):
                        go(c, "g_w")
                        dve.tensor_tensor(B[c]["comb"][:, 0:8], B[c]["p"][:, :], B[c]["mask"][:, :], ALU.mult
                                          ).then_inc(done[c], 1)

            @block.scalar
            def _(act):
                with act.Fori(0, NT // 2) as i:
                    def go(c, step):
                        act.wait_ge(done[c], i * N + (S[step] + 1))

                    def tile_of(c):
                        return 2 * i + c
                    norm_scalar(act, go, done, B, "n0", eps5[0:T, :])
                    turn_scalar(act, go, done, "f0", ps, 1, xT)
                    for c in (0, 1):
                        go(c, "q_cp")
                        act.copy(flat[c], ps[c][0:T, 2, 0:C]).then_inc(done[c], 1)
                        go(c, "v_cp")
                        act.copy(B[c]["V"][:, :], ps[c][0:T, 2, C:2 * C]).then_inc(done[c], 1)
                    for c in (0, 1):
                        go(c, "q_log")
                        act.activation(B[c]["small"][:, 2, :], B[c]["small"][:, 1, :], ACT.Ln).then_inc(done[c], 1)
                    for c in (0, 1):
                        go(c, "q_nrm")
                        act.activation(B[c]["small"][:, 2, :], B[c]["small"][:, 2, :], ACT.Exp, scale=0.5
                                       ).then_inc(done[c], 1)
                    query_blocks(act, go, done, B, ps, "q_dg", 0)
                    for c in (0, 1):
                        go(c, "K_exp")
                        for o in range(2):
                            ins = act.activation(B[c]["P4"][:, o].rearrange("p h m -> p (h m)"),
                                                 ps[c][0:T, o, 0:HG * NTOK], ACT.Exp,
                                                 bias=m10[0:T, :], scale=10.0)
                        ins.then_inc(done[c], 1)
                    with act.Fori(0, ITERS) as r:
                        def at(c, k):
                            act.wait_ge(done[c], i * N + r * SINK + (S["it"] + 1 + k))
                        for c in (0, 1):
                            at(c, 5)
                            act.activation(B[c]["vb"][:, :, :].rearrange("p h m -> p (h m)"),
                                           ps[c][0:T, 3, 0:H * NTOK], ACT.Ln).then_inc(done[c], 1)
                        for c in (0, 1):
                            at(c, 6)
                            act.activation(B[c]["vb"][:, :, :], B[c]["vb"][:, :, :], ACT.Exp, scale=-1.0
                                           ).then_inc(done[c], 1)
                    for c in (0, 1):
                        go(c, "sm_exp")
                        act.activation(B[c]["P"][:, :, :], B[c]["P"][:, :, :], ACT.Exp,
                                       bias=K["quarter"][0:T, :], scale=D ** -0.5).then_inc(done[c], 1)
                    probs_copy(act.copy, go, done, B, ps, "pc0", 0, 2)
                    turn_scalar(act, go, done, "fo", ps, 2, oT)
                    norm_scalar(act, go, done, B, "n1", eps5[0:T, :])
                    turn_scalar(act, go, done, "f1", ps, 0, xT)
                    for c in (0, 1):
                        go(c, "g_exp")
                        act.activation(B[c]["lg"][:, :], B[c]["lg"][:, :], ACT.Exp).then_inc(done[c], 1)
                    weights_out(act, "scalar", go, done, B, ps, combT, ident, tile_of, E + 1)

            @block.gpsimd
            def _(pool):
                with pool.Fori(0, NT // 2) as i:
                    def go(c, step):
                        pool.wait_ge(done[c], i * N + (S[step] + 1))

                    def tile_of(c):
                        return 2 * i + c
                    heads_expand(pool, go, done, B, "kx1", 1, HG, K["hmask16"])
                    with pool.Fori(0, ITERS) as r:
                        for c in (0, 1):
                            pool.wait_ge(done[c], i * N + r * SINK + (S["it"] + 1 + 3))
                            pool.tensor_tensor(B[c]["kv"][:, :, :], B[c]["P"][:, :, :],
                                               over(B[c]["small"][:, 6, :].unsqueeze(2), [T, H, NTOK]), ALU.mult
                                               ).then_inc(done[c], 1)
                    blocks_expand(pool, go, done, B, "px1", 8, H, K["bmask"])
                    store_tile(pool, go, done, B, h_all, xT_all, tile_of, "hcur")
                    store_xT(pool, go, done, B, xT_all, tile_of)

            @block.tensor
            def _(pe):
                with pe.Fori(0, NT // 2) as i:
                    def go(c, step):
                        pe.wait_ge(done[c], i * N + (S[step] + 1))

                    def tile_of(c):
                        return 2 * i + c
                    for c in (0, 1):
                        pe.wait_ge(patch_loaded[c], 16 * i + 16)
                        go(c, "embed")
                        for k in range(6):
                            mm = pe.matmul(ps[c][0:T, 0, 0:C], B[c]["patch"][:, k, :], K["tok_w"][:, k, :],
                                           start=(k == 0), stop=(k == 5))
                        mm.then_inc(done[c], 1)
                    turn_tensor(pe, go, done, "f0", X, ps, 1, ident)
                    width_product(pe, go, done, "qv", ps, 2, xT, K["l0_wqv"], 2 * C)
                    turn_tensor_named(pe, go, done, "q_tr", flat, ps, 0, ident)
                    scores_tensor(pe, go, done, B, ps, HG)
                    with pe.Fori(0, ITERS) as r:
                        for c in (0, 1):
                            pe.wait_ge(done[c], i * N + r * SINK + (S["it"] + 1 + 4))
                            pe.matmul(ps[c][0:T, 3, 0:H * NTOK], K["bmask"][:, :],
                                      B[c]["kv"][:, :, :].rearrange("p h m -> p (h m)"), start=True, stop=True
                                      ).then_inc(done[c], 1)
                    for c in (0, 1):
                        go(c, "rm_tr")
                        pe.transpose(ps[c][0:H, 0, 0:T], B[c]["small"][:, 0, :], ident[0:T, 0:T]).then_inc(done[c], 1)
                    for c in (0, 1):
                        go(c, "ix_mm")
                        pe.matmul(ps[c][0:T, 1, 0:H], B[c]["MX"][:, :, :].rearrange("p j n -> p (j n)"),
                                  ident[0:H, 0:H], start=True, stop=True).then_inc(done[c], 1)
                    probs_turn_tensor(pe, go, done, B, ps, H, ident)
                    values_tensor(pe, go, done, B, ps, H, D, [b["V"] for b in B], H)
                    turn_tensor(pe, go, done, "fo", [b["o"][:, :] for b in B], ps, 2, ident)
                    width_product(pe, go, done, "proj", ps, 1, oT, K["l0_wproj"], C)
                    turn_tensor(pe, go, done, "f1", X, ps, 0, ident)
                    width_product(pe, go, done, "gt", ps, 1, xT, K["l0_gate_w"], E)
                    weights_out(pe, "tensor", go, done, B, ps, combT, ident, tile_of, E + 1)


def turn_tensor_named(pe, go, done, step, src, ps, bank, ident):
    for c in (0, 1):
        go(c, step)
        for o in range(2):
            mm = pe.transpose(ps[c][0:CK, bank, o * T:(o + 1) * T], src[c][:, o * CK:(o + 1) * CK],
                              ident[0:T, 0:T])
        mm.then_inc(done[c], 1)


def experts_gelu(layer, func, ahead, nc, d, K, xT_all, yT_all, combT, sem, sb, ident, **_):
    E, M = 8, 6
    w1_d, w2_d = d[f"l{layer}_w1"], d[f"l{layer}_w2"]
    nm = f"l{layer}e_"
    weights_loaded = [sem(nm + f"weights_loaded{s}") for s in (0, 1)]
    select_ready = sem(nm + "select_ready")
    passed = sem(nm + "passed")
    ahead_loaded = sem(nm + "ahead_loaded")
    cleared = sem(nm + "cleared")
    spread_done = sem(nm + "spread_done")
    spread_copied = sem(nm + "spread_copied")
    hidden_done = sem(nm + "hidden_done")
    hidden_read = sem(nm + "hidden_read")
    out_done = sem(nm + "out_done")
    out_read = sem(nm + "out_read")
    summed = sem(nm + "summed")
    with ExitStack() as ctx:
        w1 = [sb(ctx, nm + f"w1_{s}", [CK, 2, 128 * M]) for s in (0, 1)]
        w2 = [sb(ctx, nm + f"w2_{s}", [128, M, C]) for s in (0, 1)]
        select = [sb(ctx, nm + f"select{s}", [E, CK]) for s in (0, 1)]
        act_out = sb(ctx, nm + "act_out", [128, M, UB])
        spread = sb(ctx, nm + "spread", [CK, UB])
        part = sb(ctx, nm + "part", [CK, 2, UB])
        psH = ctx.enter_context(nc.psum_tensor(nm + "psH", [128, 3, 512], F32))
        psY = ctx.enter_context(nc.psum_tensor(nm + "psY", [128, 2, 512], F32))
        psS = ctx.enter_context(nc.psum_tensor(nm + "psS", [128, 512], F32))
        with nc.Block() as block:
            def fetch(sp, s, e):
                sp.dma_start(w1[s][:, :, :].rearrange("p k m -> p (k m)"),
                             w1_d[e, :, :].rearrange("a p x -> (a p) x")).then_inc(weights_loaded[s], 16)
                sp.dma_start(w2[s][:, :, :].rearrange("p k m -> p (k m)"),
                             w2_d[e, :, :].rearrange("a p x -> (a p) x")).then_inc(weights_loaded[s], 16)

            def choose(pool, s, e):
                pool.tensor_copy(select[s][:, :], over(ident[0:E, e], [E, CK])).then_inc(select_ready, 1)

            @block.sync
            def _(sp):
                for s in (0, 1):
                    fetch(sp, s, slice(s, s + 1))
                start_loads(sp, ahead, ahead_loaded)
                with sp.Fori(1, E // 2) as q:
                    for s in (0, 1):
                        sp.wait_ge(out_done, 2 * NB * q + (NB * s - NB + 1))
                        fetch(sp, s, bass.ds(2 * q + s, 1))
                if ahead:
                    sp.wait_ge(ahead_loaded, 16 * len(ahead))

            @block.gpsimd
            def _(pool):
                pool.memset(yT_all[:, :, :], 0.0).then_inc(cleared, 1)
                for s in (0, 1):
                    choose(pool, s, slice(s, s + 1))
                with pool.Fori(1, E // 2) as q:
                    for s in (0, 1):
                        pool.wait_ge(out_done, 2 * NB * q + (NB * s - NB + 1))
                        choose(pool, s, bass.ds(2 * q + s, 1))

            @block.tensor
            def _(pe):
                pe.sem_inc(out_done, 1)
                with pe.Fori(0, E // 2) as q:
                    for s in (0, 1):
                        pe.wait_ge(select_ready, 2 * q + (s + 1))
                        pe.wait_ge(weights_loaded[s], 32 * q + 32)
                        pe.sem_inc(passed, 1)
                        with pe.Fori(0, NB) as b:
                            n = 2 * NB * q + b + s * NB
                            cols = bass.ds(b * UB, UB)
                            pe.wait_ge(spread_copied, n + 1)
                            pe.matmul(psS[0:CK, 0:UB], select[s][:, :], combT[0:E, cols], start=True, stop=True
                                      ).then_inc(spread_done, 1)
                            for m in range(M):
                                pe.wait_ge(hidden_read, M * n + (m + 1))
                                for k in range(2):
                                    mm = pe.matmul(psH[:, m % 3, 0:UB], w1[s][:, k, m * 128:(m + 1) * 128],
                                                   xT_all[:, k, cols], start=(k == 0), stop=(k == 1))
                                mm.then_inc(hidden_done, 1)
                            pe.wait_ge(out_read, n + 1)
                            for m in range(M):
                                pe.wait_ge(hidden_read, M * n + (m + 4))
                                for o in range(2):
                                    mm = pe.matmul(psY[0:CK, o, 0:UB], w2[s][:, m, o * CK:(o + 1) * CK],
                                                   act_out[:, m, :], start=(m == 0), stop=(m == M - 1))
                            mm.then_inc(out_done, 1)

            @block.scalar
            def _(act):
                act.sem_inc(hidden_read, 3)
                act.sem_inc(spread_copied, 1)
                with act.Fori(0, E) as e:
                    with act.Fori(0, NB) as b:
                        n = NB * e + b
                        act.wait_ge(spread_done, n + 1)
                        act.wait_ge(out_read, n + 1)
                        act.copy(spread[:, :], psS[0:CK, 0:UB]).then_inc(spread_copied, 1)
                        act.wait_ge(out_done, n + 1)
                        for m in range(M):
                            act.wait_ge(hidden_done, M * n + (m + 1))
                            act.activation(act_out[:, m, :], psH[:, m % 3, 0:UB], func).then_inc(hidden_read, 1)

            @block.vector
            def _(dve):
                dve.sem_inc(out_read, 1)
                dve.sem_inc(summed, 1)
                dve.wait_ge(cleared, 1)
                with dve.Fori(0, E) as e:
                    with dve.Fori(0, NB) as b:
                        n = NB * e + b
                        y = yT_all[:, :, bass.ds(b * UB, UB)]
                        dve.wait_ge(out_done, n + 2)
                        dve.wait_ge(spread_copied, n + 2)
                        dve.wait_ge(summed, n + 1)
                        dve.tensor_tensor(part[:, :, :], psY[0:CK, :, 0:UB],
                                          over(spread[:, :].unsqueeze(1), [CK, 2, UB]), ALU.mult).then_inc(out_read, 1)
                        dve.wait_ge(out_read, n + 2)
                        dve.tensor_tensor(y, y, part[:, :, :], ALU.add).then_inc(summed, 1)
                dve.wait_ge(summed, E * NB + 1)


def experts_swiglu(layer, E, ahead, nc, d, K, xT_all, yT_all, combT, sem, sb, ident, **_):
    gated = layer == 0
    A = 1 if gated else 2
    HB = 4
    w1_d, w2_d, b_d = d[f"l{layer}_w1"], d[f"l{layer}_w2"], d[f"l{layer}_b"]
    nm = f"l{layer}e_"
    weights_loaded = [sem(nm + f"weights_loaded{s}") for s in (0, 1)]
    select_ready = sem(nm + "select_ready")
    passed = sem(nm + "passed")
    ahead_loaded = sem(nm + "ahead_loaded")
    cleared = sem(nm + "cleared")
    spread_done = sem(nm + "spread_done")
    spread_copied = sem(nm + "spread_copied")
    hidden_done = sem(nm + "hidden_done")
    third_ready = sem(nm + "third_ready")
    prod_ready = sem(nm + "prod_ready")
    hidden_read = sem(nm + "hidden_read")
    silu_ready = sem(nm + "silu_ready")
    lin_ready = sem(nm + "lin_ready")
    glu_ready = sem(nm + "glu_ready")
    out_done = sem(nm + "out_done")
    out_read = sem(nm + "out_read")
    summed = sem(nm + "summed")
    W1N = 384
    NBIAS = 6
    with ExitStack() as ctx:
        w1 = [sb(ctx, nm + f"w1_{s}", [CK, 2, W1N]) for s in (0, 1)]
        w2 = [sb(ctx, nm + f"w2_{s}", [CK, A, C]) for s in (0, 1)]
        bias = sb(ctx, nm + "bias", [CK, E, NBIAS])
        bcur = [sb(ctx, nm + f"bcur{k}", [CK, NBIAS]) for k in range(2)]
        select = [sb(ctx, nm + f"select{s}", [E, CK]) for s in (0, 1)]
        gate = sb(ctx, nm + "gate", [CK, UB])
        lin = sb(ctx, nm + "lin", [CK, UB])
        third = sb(ctx, nm + "third", [CK, 2, UB])
        prod = sb(ctx, nm + "prod", [CK, 2, UB])
        silu = sb(ctx, nm + "silu", [CK, UB])
        glu = sb(ctx, nm + "glu", [CK, A, UB])
        spread = sb(ctx, nm + "spread", [CK, UB])
        part = sb(ctx, nm + "part", [CK, 2, UB])
        psH = ctx.enter_context(nc.psum_tensor(nm + "psH", [128, HB, 512], F32))
        psY = ctx.enter_context(nc.psum_tensor(nm + "psY", [128, 2, 512], F32))
        psS = ctx.enter_context(nc.psum_tensor(nm + "psS", [128, 512], F32))
        bias_loaded = sem(nm + "bias_loaded")
        bias_cur = [sem(nm + f"bias_cur{k}") for k in range(2)]
        pairs, tail = E // 2, E % 2
        with nc.Block() as block:
            def fetch(sp, s, e):
                sp.dma_start(w1[s][:, :, :].rearrange("p k m -> p (k m)"),
                             w1_d[e, :, :].rearrange("a p x -> (a p) x")).then_inc(weights_loaded[s], 16)
                sp.dma_start(w2[s][:, :, :].rearrange("p k m -> p (k m)"),
                             w2_d[e, :, :].rearrange("a p x -> (a p) x")).then_inc(weights_loaded[s], 16)

            def choose(pool, s, e):
                pool.tensor_copy(select[s][:, :], over(ident[0:E, e], [E, CK])).then_inc(select_ready, 1)

            @block.sync
            def _(sp):
                sp.dma_start(bias[:, :, :], b_d[:, :, :]).then_inc(bias_loaded, 16)
                for s in (0, 1):
                    fetch(sp, s, slice(s, s + 1))
                start_loads(sp, ahead, ahead_loaded)
                with sp.Fori(1, pairs) as q:
                    for s in (0, 1):
                        sp.wait_ge(out_done, 2 * NB * q + (NB * s - NB + 1))
                        fetch(sp, s, bass.ds(2 * q + s, 1))
                if ahead:
                    sp.wait_ge(ahead_loaded, 16 * len(ahead))
                if tail:
                    sp.wait_ge(out_done, NB * (E - 2) + 1)
                    fetch(sp, 0, slice(E - 1, E))

            @block.gpsimd
            def _(pool):
                pool.memset(yT_all[:, :, :], 0.0).then_inc(cleared, 1)
                for s in (0, 1):
                    choose(pool, s, slice(s, s + 1))
                with pool.Fori(1, pairs) as q:
                    for s in (0, 1):
                        pool.wait_ge(out_done, 2 * NB * q + (NB * s - NB + 1))
                        choose(pool, s, bass.ds(2 * q + s, 1))
                if tail:
                    pool.wait_ge(out_done, NB * (E - 2) + 1)
                    choose(pool, 0, slice(E - 1, E))

            def expert_products(pe, q, s):
                pe.wait_ge(select_ready, 2 * q + (s + 1))
                pe.wait_ge(weights_loaded[s], 32 * q + 32)
                pe.sem_inc(passed, 1)
                with pe.Fori(0, NB) as b:
                    n = b + (2 * NB * q + s * NB)
                    cols = bass.ds(b * UB, UB)
                    pe.wait_ge(spread_copied, n + 1)
                    pe.matmul(psS[0:CK, 0:UB], select[s][:, :], combT[0:E, cols], start=True, stop=True
                              ).then_inc(spread_done, 1)
                    for a in range(A):
                        pe.wait_ge(hidden_read, A * n + (a + 1))
                        for col in ((0, 1, 2, 3) if gated else (a, A + a)):
                            for k in range(2):
                                mm = pe.matmul(psH[0:CK, col, 0:UB], w1[s][:, k, col * CK:(col + 1) * CK],
                                               xT_all[:, k, cols], start=(k == 0), stop=(k == 1))
                        mm.then_inc(hidden_done, 1)
                    pe.wait_ge(out_read, n + 1)
                    for a in range(A):
                        pe.wait_ge(glu_ready, A * n + (a + 2))
                        for o in range(2):
                            mm = pe.matmul(psY[0:CK, o, 0:UB], w2[s][:, a, o * CK:(o + 1) * CK], glu[:, a, :],
                                           start=(a == 0), stop=(a == A - 1))
                    mm.then_inc(out_done, 1)

            @block.tensor
            def _(pe):
                pe.sem_inc(out_done, 1)
                with pe.Fori(0, pairs) as q:
                    for s in (0, 1):
                        expert_products(pe, q, s)
                if tail:
                    expert_products(pe, pairs, 0)

            @block.scalar
            def _(act):
                act.sem_inc(spread_copied, 1)
                if gated:
                    act.sem_inc(third_ready, 1)
                act.wait_ge(bias_loaded, 16)
                with act.Fori(0, E) as e:
                    if gated:
                        act.wait_ge(third_ready, NB * e + 1)
                        act.copy(bcur[1][:, :], bias[:, bass.ds(e, 1), :].rearrange("p a x -> p (a x)")
                                 ).then_inc(bias_cur[1], 1)
                        act.wait_ge(bias_cur[1], e + 1)
                    with act.Fori(0, NB) as b:
                        n = NB * e + b
                        act.wait_ge(spread_done, n + 1)
                        act.wait_ge(out_read, n + 1)
                        act.copy(spread[:, :], psS[0:CK, 0:UB]).then_inc(spread_copied, 1)
                        if gated:
                            act.wait_ge(hidden_done, n + 1)
                            act.wait_ge(prod_ready, n + 1)
                            for col in range(2):
                                ins = act.activation(third[:, col, :], psH[0:CK, 2 + col, 0:UB], ACT.Identity,
                                                     bias=bcur[1][:, 2 + col:3 + col])
                            ins.then_inc(third_ready, 1)
                        for a in range(A):
                            act.wait_ge(hidden_read, A * n + (a + 1 + A))
                            act.wait_ge(glu_ready, A * n + (a + 1))
                            act.activation(silu[:, :], gate[:, :], ACT.Silu, scale=ALPHA).then_inc(silu_ready, 1)

            @block.vector
            def _(dve):
                dve.sem_inc(hidden_read, A)
                for started in (out_read, summed, prod_ready, glu_ready):
                    dve.sem_inc(started, 1)
                dve.wait_ge(cleared, 1)
                dve.wait_ge(bias_loaded, 16)
                with dve.Fori(0, E) as e:
                    dve.wait_ge(summed, NB * e + 1)
                    dve.tensor_copy(bcur[0][:, :], bias[:, bass.ds(e, 1), :].rearrange("p a x -> p (a x)")
                                    ).then_inc(bias_cur[0], 1)
                    dve.wait_ge(bias_cur[0], e + 1)
                    dve.sem_inc(passed, 1)
                    with dve.Fori(0, NB) as b:
                        n = NB * e + b
                        y = yT_all[:, :, bass.ds(b * UB, UB)]
                        for a in range(A):
                            dve.wait_ge(hidden_done, A * n + (a + 1))
                            dve.wait_ge(glu_ready, A * n + (a + 1))
                            if gated:
                                dve.wait_ge(third_ready, n + 2)
                                for col in range(2):
                                    ins = dve.scalar_tensor_tensor(prod[:, col, :], psH[0:CK, col, 0:UB],
                                                                   bcur[0][:, col:col + 1], third[:, col, :],
                                                                   ALU.add, ALU.mult)
                                ins.then_inc(prod_ready, 1)
                                dve.wait_ge(prod_ready, n + 2)
                                dve.tensor_scalar(lin[:, :], prod[:, 1, :], LIMIT, None, ALU.min)
                                dve.tensor_scalar(gate[:, :], prod[:, 0, :], LIMIT, None, ALU.min
                                                  ).then_inc(hidden_read, 1)
                            else:
                                dve.tensor_scalar(lin[:, :], psH[0:CK, A + a, 0:UB], bcur[0][:, A + a:A + a + 1],
                                                  LIMIT, ALU.add, ALU.min)
                                dve.tensor_scalar(gate[:, :], psH[0:CK, a, 0:UB], bcur[0][:, a:a + 1],
                                                  LIMIT, ALU.add, ALU.min).then_inc(hidden_read, 1)
                            dve.wait_ge(hidden_read, A * n + (a + 1 + A))
                            dve.tensor_scalar(lin[:, :], lin[:, :], -LIMIT, 1.0, ALU.max, ALU.add
                                              ).then_inc(lin_ready, 1)
                            dve.wait_ge(lin_ready, A * n + (a + 1))
                            dve.wait_ge(silu_ready, A * n + (a + 1))
                            if a == 0:
                                dve.wait_ge(out_done, n + 1)
                            dve.scalar_tensor_tensor(glu[:, a, :], silu[:, :], 1.0 / ALPHA, lin[:, :],
                                                     ALU.mult, ALU.mult).then_inc(glu_ready, 1)
                        dve.wait_ge(out_done, n + 2)
                        dve.wait_ge(spread_copied, n + 2)
                        dve.wait_ge(summed, n + 1)
                        for o in range(2):
                            ins = dve.scalar_tensor_tensor(part[:, o, :], psY[0:CK, o, 0:UB],
                                                           bcur[0][:, 4 + o:5 + o], spread[:, :], ALU.add, ALU.mult)
                        ins.then_inc(out_read, 1)
                        dve.wait_ge(out_read, n + 2)
                        dve.tensor_tensor(y, y, part[:, :, :], ALU.add).then_inc(summed, 1)
                dve.wait_ge(summed, E * NB + 1)


def capacity_limit(nc, xT_all, yT_all, combT, maskT, sem, sb, **_):
    scanned, kept, cleared = sem("cap_scanned"), sem("cap_kept"), sem("cap_cleared")
    with ExitStack() as ctx:
        count = sb(ctx, "cap_count", [8, NP])
        ones = sb(ctx, "cap_ones", [8, NP])
        with nc.Block() as block:
            @block.vector
            def _(dve):
                dve.memset(ones[:, :], 1.0).then_inc(scanned, 1)
                dve.wait_ge(scanned, 1)
                dve.tensor_tensor_scan(count[:, :], ones[:, :], maskT[:, :], 0.0, ALU.mult, ALU.add
                                       ).then_inc(scanned, 1)
                dve.wait_ge(scanned, 2)
                dve.scalar_tensor_tensor(combT[0:8, :], count[:, :], CAP + 0.5, combT[0:8, :], ALU.is_lt, ALU.mult
                                         ).then_inc(kept, 1)
                dve.wait_ge(kept, 1)


def attend_vector(dve, go, done, B, ps, S_view, scale, bias, H, D, hmask, K, V):
    softmax_vector(dve, go, done, B, S_view, scale, bias, H)
    blocks_expand(dve, go, done, B, "px0", 0, H * 2 // 3, K["bmask"])
    probs_copy(dve.tensor_copy, go, done, B, ps, "pc1", 2, H // 4)


def per_head(ap, D):
    return ap.rearrange("p (h d) -> p h d", d=D)


def normed_output(dve, go, done, B, ps, H, D):
    for c in (0, 1):
        go(c, "o")
        dve.tensor_tensor(per_head(B[c]["o"][:, :], D), per_head(ps[c][0:T, 0, 0:C], D),
                          over(B[c]["hinv"][:, 0:H].unsqueeze(2), [T, H, D]), ALU.mult).then_inc(done[c], 1)


def add2(dve, go, done, step, out_, a, b):
    for c in (0, 1):
        go(c, step)
        dve.tensor_tensor(out_[c], a[c], b[c], ALU.add).then_inc(done[c], 1)


def router_vector(dve, go, done, B, ps, E, k, gate_b):
    for c in (0, 1):
        go(c, "g_cp")
        if gate_b is None:
            dve.tensor_copy(B[c]["sv"][:, 0:E], ps[c][0:T, 1, 0:E]).then_inc(done[c], 1)
        else:
            dve.tensor_tensor(B[c]["sv"][:, 0:E], ps[c][0:T, 1, 0:E], gate_b[:, :], ALU.add).then_inc(done[c], 1)
    topk_vector(dve, go, done, B, "ge", "sv", "keys", k, E, [b["mask"][:, 0:E] for b in B])
    for c in (0, 1):
        go(c, "g_sub")
        dve.tensor_scalar(B[c]["lg"][:, 0:E], B[c]["sv"][:, 0:E], B[c]["max8"][:, 0:1], None, ALU.subtract
                          ).then_inc(done[c], 1)
    for c in (0, 1):
        go(c, "g_w")
        dve.tensor_tensor(B[c]["lg"][:, 0:E], B[c]["lg"][:, 0:E], B[c]["mask"][:, 0:E], ALU.mult).then_inc(done[c], 1)
    for c in (0, 1):
        go(c, "g_sum")
        dve.tensor_reduce(B[c]["mv"][:, 0:1], B[c]["lg"][:, 0:E], AX.X, ALU.add).then_inc(done[c], 1)
    for c in (0, 1):
        go(c, "g_rc")
        dve.reciprocal(B[c]["mv"][:, 1:2], B[c]["mv"][:, 0:1]).then_inc(done[c], 1)
    for c in (0, 1):
        go(c, "g_n")
        dve.tensor_scalar(B[c]["comb"][:, 0:E], B[c]["lg"][:, 0:E], B[c]["mv"][:, 1:2], None, ALU.mult
                          ).then_inc(done[c], 1)


def router_scalar(act, go, done, B, E):
    for c in (0, 1):
        go(c, "g_exp")
        act.activation(B[c]["lg"][:, 0:E], B[c]["lg"][:, 0:E], ACT.Exp).then_inc(done[c], 1)


ROUTER = "g_cp " + topk_steps("ge") + "g_sub g_exp g_w g_sum g_rc g_n c_tr "
ROUTER_SHAPES = dict(sv=[T, 24], keys=[T, 8], mask=[T, 16], lg=[T, 16], comb=[T, 16])


def layer1_tokens(nc, d, K, h_all, xT_all, yT_all, combT, maskT, eps5, ident, sem, sb, **_):
    H, E, HP, DA = 12, 8, 6, 64
    D, HG = 16, 6
    MAIN = "sm_scale sm_max sm_sub sm_exp sm_sum sm_inv " + SPREAD
    first = MAIN.replace("sm_", "a.sm_").replace("px", "a.px").replace("pt", "a.pt").replace("pc", "a.pc").replace(
        "av", "a.av")
    S = steps("y_cp y_tr y_add " + ln_steps("n0") + ln_steps("n1") + turn_steps("f0") +
              "wide_qk wq_cp|wk_cp wide_v wv_cp a.S " + first + "a.o a.o_tr a.o_cp wide_out h1 h2 " +
              ln_steps("n2") + ln_steps("n3") + turn_steps("f3") + "qkT v q_dg|k_cp v_cp kx0|kx1 S " + MAIN + "o " +
              turn_steps("fo") + "proj x2 h3 h_st " + ln_steps("n4") + turn_steps("f4") + "x_st gt " + ROUTER +
              "c_st m_tr m_st")
    N = S["end"]
    done = [sem(f"l1_tile{c}_steps") for c in (0, 1)]
    zeroed, passed = sem("l1_zeroed"), sem("l1_passed")
    with ExitStack() as ctx:
        shapes = attention_shapes(H, D)
        shapes.update(ROUTER_SHAPES)
        shapes.update(wqx=[128, HP, IMGS * DIAG], wkT=[128, HP, T], wV=[T, H * DA], wo=[T, H * DA],
                      )
        del shapes["o"], shapes["V"]
        B, ps = tile_buffers(ctx, nc, sb, 1, shapes)
        halves(B, H)
        for b in B:
            b["passed"] = passed
        for b in B:
            b["o"], b["V"], b["woT"] = b["wo"], b["wV"], b["wkT"]
        X = [b["x"][:, :] for b in B]
        HC = [b["hcur"][:, :] for b in B]
        xT = [b["xT"] for b in B]
        oT = [b["oT"] for b in B]
        O = [b["wo"][:, 0:C] for b in B]
        order = [2 * f + r for r in (0, 1) for f in range(HP)]
        wide_scores = [p[0:T, 2:4, 0:HP * NTOK].rearrange("p o (h m) -> p o h m", m=NTOK) for p in ps]
        scores = [p[0:T, 0:2, 0:HG * NTOK].rearrange("p o (h m) -> p o h m", m=NTOK) for p in ps]
        with nc.Block() as block:
            @block.vector
            def _(dve):
                for c in (0, 1):
                    dve.memset(B[c]["qx"][:, :, :], 0.0)
                    dve.memset(B[c]["wqx"][:, :, :], 0.0)
                    dve.memset(B[c]["sv"][:, :], PAD)
                    ins = dve.memset(B[c]["keys"][:, :], PAD)
                ins.then_inc(zeroed, 1)
                dve.wait_ge(zeroed, 1)
                for c in (0, 1):
                    dve.sem_inc(done[c], 1)
                with dve.Fori(0, NT // 2) as i:
                    def go(c, step, passed=None):
                        dve.wait_ge(done[c], i * N + (S[step] + 1))
                        if passed is not None:
                            dve.sem_inc(passed, 1)

                    def ga(c, step, passed=None):
                        go(c, "a." + step, passed)

                    def tile_of(c):
                        return 2 * i + c
                    take_experts_back(dve, "vector", go, done, B, ps, h_all, yT_all, ident, tile_of)
                    norm_vector(dve, go, done, B, "n0", HC, X)
                    norm_vector(dve, go, done, B, "n1", X, X)
                    for c in (0, 1):
                        go(c, "wk_cp")
                        for f in range(HP):
                            ins = dve.tensor_scalar(B[c]["wkT"][:, f, :], ps[c][:, 2 + f // 4, (f % 4) * T:(f % 4 + 1) * T],
                                                    K["l1_bk"][:, f:f + 1], None, ALU.add)
                        ins.then_inc(done[c], 1)
                    for c in (0, 1):
                        go(c, "wv_cp")
                        for b in range(2):
                            ins = dve.tensor_tensor(B[c]["wV"][:, b * 384:(b + 1) * 384], ps[c][0:T, b, 0:384],
                                                    K["l1_bv"][:, b * 384:(b + 1) * 384], ALU.add)
                        ins.then_inc(done[c], 1)
                    softmax_vector(dve, ga, done, B, wide_scores, DA ** -0.5, K["anti_causal"], H)
                    blocks_expand(dve, ga, done, B, "px0", 0, 8, K["bmask"])
                    probs_copy(dve.tensor_copy, ga, done, B, ps, "pc1", 2, 3)
                    for c in (0, 1):
                        ga(c, "o")
                        for b, h0, h1 in ((0, 0, 8), (1, 8, 12)):
                            ins = dve.tensor_tensor(per_head(B[c]["wo"][:, h0 * DA:h1 * DA], DA),
                                                    per_head(ps[c][0:T, b, 0:(h1 - h0) * DA], DA),
                                                    over(B[c]["hinv"][:, h0:h1].unsqueeze(2), [T, h1 - h0, DA]),
                                                    ALU.mult)
                        ins.then_inc(done[c], 1)
                    add2(dve, go, done, "h1", HC, HC, [p[0:T, 0, 0:C] for p in ps])
                    add2(dve, go, done, "h2", HC, HC, [K["l1_bo"][:, :]] * 2)
                    norm_vector(dve, go, done, B, "n2", HC, X)
                    norm_vector(dve, go, done, B, "n3", X, O)
                    for c in (0, 1):
                        go(c, "k_cp")
                        dve.tensor_copy(B[c]["kT"][:, :, :].rearrange("p o t -> p (o t)"), ps[c][0:CK, 1, 0:2 * T]
                                        ).then_inc(done[c], 1)
                    heads_expand(dve, go, done, B, "kx0", 0, HG, K["hmask16"])
                    softmax_vector(dve, go, done, B, scores, D ** -0.5, K["causal"], H)
                    blocks_expand(dve, go, done, B, "px0", 0, 8, K["bmask"])
                    probs_copy(dve.tensor_copy, go, done, B, ps, "pc1", 2, 3)
                    for c in (0, 1):
                        go(c, "o")
                        dve.tensor_tensor(per_head(O[c], D), per_head(ps[c][0:T, 0, 0:C], D),
                                          over(B[c]["hinv"][:, 0:H].unsqueeze(2), [T, H, D]), ALU.mult
                                          ).then_inc(done[c], 1)
                    add2(dve, go, done, "x2", X, X, [p[0:T, 1, 0:C] for p in ps])
                    add2(dve, go, done, "h3", HC, HC, X)
                    norm_vector(dve, go, done, B, "n4", X, X)
                    router_vector(dve, go, done, B, ps, E, 2, None)

            @block.scalar
            def _(act):
                act.wait_ge(zeroed, 1)
                with act.Fori(0, NT // 2) as i:
                    def go(c, step):
                        act.wait_ge(done[c], i * N + (S[step] + 1))

                    def ga(c, step):
                        go(c, "a." + step)

                    def tile_of(c):
                        return 2 * i + c
                    norm_scalar(act, go, done, B, "n0", eps5[0:T, :])
                    norm_scalar(act, go, done, B, "n1", eps5[0:T, :])
                    turn_scalar(act, go, done, "f0", ps, 0, xT, K["l1_ln_w"], K["l1_ln_b"])
                    for c in (0, 1):
                        go(c, "wq_cp")
                        for f in range(HP):
                            ins = act.activation(
                                B[c]["wqx"][:, f, :].rearrange("p (j x) -> p j x", x=DIAG)[:, :, 0:NTOK],
                                ps[c][:, f // 4, (f % 4) * T:(f % 4 + 1) * T].rearrange("p (j m) -> p j m", m=NTOK),
                                ACT.Identity, bias=K["l1_bq"][:, f:f + 1])
                        ins.then_inc(done[c], 1)
                    softmax_scalar(act, ga, done, B, H)
                    probs_copy(act.copy, ga, done, B, ps, "pc0", 0, 2)
                    for c in (0, 1):
                        ga(c, "o_cp")
                        act.copy(B[c]["woT"][:, 0:4, :].rearrange("p f t -> p (f t)"), ps[c][:, 2, 0:4 * T])
                        act.copy(B[c]["woT"][:, 4:6, :].rearrange("p f t -> p (f t)"), ps[c][:, 3, 0:2 * T]
                                 ).then_inc(done[c], 1)
                    norm_scalar(act, go, done, B, "n2", eps5[0:T, :])
                    norm_scalar(act, go, done, B, "n3", eps5[0:T, :])
                    turn_scalar(act, go, done, "f3", ps, 0, xT, K["l1_ln1_w"])
                    query_blocks(act, go, done, B, ps, "q_dg", 0)
                    for c in (0, 1):
                        go(c, "v_cp")
                        act.copy(B[c]["wV"][:, 0:C], ps[c][0:T, 2, 0:C]).then_inc(done[c], 1)
                    softmax_scalar(act, go, done, B, H)
                    probs_copy(act.copy, go, done, B, ps, "pc0", 0, 2)
                    turn_scalar(act, go, done, "fo", ps, 2, oT)
                    norm_scalar(act, go, done, B, "n4", eps5[0:T, :])
                    turn_scalar(act, go, done, "f4", ps, 0, xT, K["l1_ln2_w"])
                    router_scalar(act, go, done, B, E)
                    weights_out(act, "scalar", go, done, B, ps, combT, ident, tile_of, E)
                    for c in (0, 1):
                        go(c, "m_st")
                        act.copy(maskT[:, bass.ds(tile_of(c) * T, T)], ps[c][0:E, 3, 0:T]).then_inc(done[c], 1)

            @block.gpsimd
            def _(pool):
                with pool.Fori(0, NT // 2) as i:
                    def go(c, step):
                        pool.wait_ge(done[c], i * N + (S[step] + 1))

                    def ga(c, step):
                        go(c, "a." + step)

                    def tile_of(c):
                        return 2 * i + c
                    take_experts_back(pool, "pool", go, done, B, ps, h_all, yT_all, ident, tile_of)
                    blocks_expand(pool, ga, done, B, "px1", 8, H, K["bmask"])
                    heads_expand(pool, go, done, B, "kx1", 1, HG, K["hmask16"])
                    blocks_expand(pool, go, done, B, "px1", 8, H, K["bmask"])
                    store_tile(pool, go, done, B, h_all, xT_all, tile_of, "hcur")
                    store_xT(pool, go, done, B, xT_all, tile_of)

            @block.tensor
            def _(pe):
                with pe.Fori(0, NT // 2) as i:
                    def go(c, step):
                        pe.wait_ge(done[c], i * N + (S[step] + 1))

                    def ga(c, step):
                        go(c, "a." + step)

                    def tile_of(c):
                        return 2 * i + c
                    take_experts_back(pe, "tensor", go, done, B, ps, h_all, yT_all, ident, tile_of)
                    turn_tensor(pe, go, done, "f0", X, ps, 0, ident)
                    for c in (0, 1):
                        go(c, "wide_qk")
                        for w, b0 in ((K["l1_wq"], 0), (K["l1_wk"], 2)):
                            for f in range(HP):
                                for k in range(2):
                                    mm = pe.matmul(ps[c][:, b0 + f // 4, (f % 4) * T:(f % 4 + 1) * T],
                                                   w[:, k, f * 128:(f + 1) * 128], xT[c][:, k, :],
                                                   start=(k == 0), stop=(k == 1))
                        mm.then_inc(done[c], 1)
                    for c in (0, 1):
                        go(c, "wide_v")
                        for b in range(2):
                            for k in range(2):
                                mm = pe.matmul(ps[c][0:T, b, 0:384], xT[c][:, k, :],
                                               K["l1_wv"][:, k, b * 384:(b + 1) * 384], start=(k == 0), stop=(k == 1))
                        mm.then_inc(done[c], 1)
                    for c in (0, 1):
                        ga(c, "S")
                        for h in range(H):
                            r = slice((h % 2) * DA, (h % 2 + 1) * DA)
                            for j in range(IMGS):
                                mm = pe.matmul(ps[c][0:T, 2 + h % 2, (h // 2) * NTOK:(h // 2 + 1) * NTOK],
                                               B[c]["wqx"][r, h // 2, j * T:(j + 1) * T],
                                               B[c]["wkT"][r, h // 2, j * NTOK:(j + 1) * NTOK],
                                               start=(j == 0), stop=(j == IMGS - 1))
                        mm.then_inc(done[c], 1)
                    probs_turn_tensor(pe, ga, done, B, ps, H, ident)
                    values_tensor(pe, ga, done, B, ps, H, DA, [b["wV"] for b in B], 8, order)
                    for c in (0, 1):
                        ga(c, "o_tr")
                        for f in range(HP):
                            mm = pe.transpose(ps[c][:, 2 + f // 4, (f % 4) * T:(f % 4 + 1) * T],
                                              B[c]["wo"][:, f * 128:(f + 1) * 128], ident[0:T, 0:T])
                        mm.then_inc(done[c], 1)
                    for c in (0, 1):
                        go(c, "wide_out")
                        for f in range(HP):
                            mm = pe.matmul(ps[c][0:T, 0, 0:C], B[c]["woT"][:, f, :], K["l1_wo"][:, f, :],
                                           start=(f == 0), stop=(f == HP - 1))
                        mm.then_inc(done[c], 1)
                    turn_tensor(pe, go, done, "f3", O, ps, 0, ident)
                    qk_tensor(pe, go, done, ps, xT, K["l1_wqk"])
                    width_product(pe, go, done, "v", ps, 2, xT, K["l1_wv2"], C)
                    scores_tensor(pe, go, done, B, ps, HG)
                    probs_turn_tensor(pe, go, done, B, ps, H, ident)
                    values_tensor(pe, go, done, B, ps, H, D, [b["wV"] for b in B], H)
                    turn_tensor(pe, go, done, "fo", O, ps, 2, ident)
                    width_product(pe, go, done, "proj", ps, 1, oT, K["l1_wproj"], C)
                    turn_tensor(pe, go, done, "f4", X, ps, 0, ident)
                    width_product(pe, go, done, "gt", ps, 1, xT, K["l1_gate_w"], E)
                    weights_out(pe, "tensor", go, done, B, ps, combT, ident, tile_of, E)
                    for c in (0, 1):
                        go(c, "m_tr")
                        pe.transpose(ps[c][0:E, 3, 0:T], B[c]["mask"][:, 0:E], ident[0:T, 0:T]).then_inc(done[c], 1)


def qk_tensor(pe, go, done, ps, xT, w):
    for c in (0, 1):
        go(c, "qkT")
        for o in range(4):
            for k in range(2):
                mm = pe.matmul(ps[c][0:CK, o // 2, (o % 2) * T:(o % 2 + 1) * T], w[:, k, o * CK:(o + 1) * CK],
                               xT[c][:, k, :], start=(k == 0), stop=(k == 1))
        mm.then_inc(done[c], 1)


def layer2_tokens(nc, d, K, h_all, xT_all, yT_all, combT, eps5, ident, sem, sb, **_):
    H, D, HG, E = 16, 12, 8, 16
    S = steps("y_cp y_tr y_add " + ln_steps("n0") + turn_steps("f0") + "qkT v q_dg|k_cp v_cp kx0|kx1 S " + SOFTMAX +
              "mix_f mix_a mix_b m_sum m_inv " + SPREAD + "o " + turn_steps("fo") + "proj h1 h2 " + ln_steps("n1") +
              "h3 h_st " + rms_steps("r1") + turn_steps("f1") + "x_st gt " + ROUTER + "c_st")
    N = S["end"]
    done = [sem(f"l2_tile{c}_steps") for c in (0, 1)]
    zeroed, setup, passed = sem("l2_zeroed"), sem("l2_setup"), sem("l2_passed")
    with ExitStack() as ctx:
        shapes = attention_shapes(H, D)
        shapes.update(ROUTER_SHAPES)
        shapes.update(junk=[T, C])
        B, ps = tile_buffers(ctx, nc, sb, 2, shapes)
        halves(B, H)
        for b in B:
            b["passed"] = passed
        pos = sb(ctx, "l2_pos", [T, H, NTOK])
        tmp = sb(ctx, "l2_tmp", [T, H, NTOK])
        hs = sb(ctx, "l2_hs", [T, 4, H])
        X = [b["x"][:, :] for b in B]
        HC = [b["hcur"][:, :] for b in B]
        xT = [b["xT"] for b in B]
        oT = [b["oT"] for b in B]
        scores = [p[0:T, 0:2, 0:HG * NTOK].rearrange("p o (h m) -> p o h m", m=NTOK) for p in ps]
        shape = [T, H, NTOK]
        with nc.Block() as block:
            @block.vector
            def _(dve):
                for c in (0, 1):
                    dve.memset(B[c]["qx"][:, :, :], 0.0)
                    dve.memset(B[c]["sv"][:, :], PAD)
                    ins = dve.memset(B[c]["keys"][:, :], PAD)
                ins.then_inc(zeroed, 1)
                dve.wait_ge(zeroed, 1)
                dve.tensor_tensor(pos[:, :, :], over(K["rel"][:, 0, :].unsqueeze(1), shape),
                                  over(K["l2_wpos"][:, 0, :].unsqueeze(2), shape), ALU.mult).then_inc(setup, 1)
                n = 1
                for q in (1, 2):
                    dve.wait_ge(setup, n)
                    dve.tensor_tensor(tmp[:, :, :], over(K["rel"][:, q, :].unsqueeze(1), shape),
                                      over(K["l2_wpos"][:, q, :].unsqueeze(2), shape), ALU.mult).then_inc(setup, 1)
                    dve.wait_ge(setup, n + 1)
                    dve.tensor_tensor(pos[:, :, :], pos[:, :, :], tmp[:, :, :], ALU.add).then_inc(setup, 1)
                    n += 2
                dve.wait_ge(setup, 5)
                dve.tensor_tensor(pos[:, :, :], pos[:, :, :], over(K["l2_bpos"][:, :].unsqueeze(2), shape), ALU.add
                                  ).then_inc(setup, 1)
                dve.wait_ge(setup, 6)
                dve.tensor_reduce(hs[:, 0, :], pos[:, :, :], AX.X, ALU.max).then_inc(setup, 1)
                dve.wait_ge(setup, 7)
                dve.tensor_tensor(pos[:, :, :], pos[:, :, :], over(hs[:, 0, :].unsqueeze(2), shape), ALU.subtract
                                  ).then_inc(setup, 1)
                dve.wait_ge(setup, 10)
                dve.tensor_reduce(hs[:, 1, :], pos[:, :, :], AX.X, ALU.add).then_inc(setup, 1)
                dve.wait_ge(setup, 11)
                dve.tensor_scalar(hs[:, 2, :], hs[:, 2, :], 1.0, None, ALU.add).then_inc(setup, 1)
                dve.wait_ge(setup, 12)
                dve.tensor_tensor(hs[:, 1, :], hs[:, 1, :], hs[:, 2, :], ALU.mult).then_inc(setup, 1)
                dve.wait_ge(setup, 13)
                dve.reciprocal(hs[:, 1, :], hs[:, 1, :]).then_inc(setup, 1)
                dve.wait_ge(setup, 14)
                dve.reciprocal(hs[:, 2, :], hs[:, 2, :]).then_inc(setup, 1)
                dve.wait_ge(setup, 15)
                dve.tensor_scalar(hs[:, 3, :], hs[:, 2, :], -1.0, 1.0, ALU.mult, ALU.add).then_inc(setup, 1)
                dve.wait_ge(setup, 16)
                dve.tensor_tensor(pos[:, :, :], pos[:, :, :], over(hs[:, 1, :].unsqueeze(2), shape), ALU.mult
                                  ).then_inc(setup, 1)
                dve.wait_ge(setup, 17)
                for c in (0, 1):
                    dve.sem_inc(done[c], 1)
                with dve.Fori(0, NT // 2) as i:
                    def go(c, step, passed=None):
                        dve.wait_ge(done[c], i * N + (S[step] + 1))
                        if passed is not None:
                            dve.sem_inc(passed, 1)

                    def tile_of(c):
                        return 2 * i + c
                    take_experts_back(dve, "vector", go, done, B, ps, h_all, yT_all, ident, tile_of)
                    norm_vector(dve, go, done, B, "n0", HC, X)
                    for c in (0, 1):
                        go(c, "k_cp")
                        dve.tensor_copy(B[c]["kT"][:, :, :].rearrange("p o t -> p (o t)"), ps[c][0:CK, 1, 0:2 * T]
                                        ).then_inc(done[c], 1)
                    heads_expand(dve, go, done, B, "kx0", 0, HG, K["hmask12"])
                    softmax_vector(dve, go, done, B, scores, D ** -0.5, None, H)
                    for c in (0, 1):
                        go(c, "mix_f")
                        dve.tensor_tensor(B[c]["hmax"][:, 0:H], B[c]["hinv"][:, 0:H], hs[:, 3, :], ALU.mult
                                          ).then_inc(done[c], 1)
                    for c in (0, 1):
                        go(c, "mix_a")
                        dve.tensor_tensor(B[c]["P"][:, :, :], B[c]["P"][:, :, :],
                                          over(B[c]["hmax"][:, 0:H].unsqueeze(2), shape), ALU.mult).then_inc(done[c], 1)
                    for c in (0, 1):
                        go(c, "mix_b")
                        dve.tensor_tensor(B[c]["P"][:, :, :], B[c]["P"][:, :, :], pos[:, :, :], ALU.add
                                          ).then_inc(done[c], 1)
                    for c in (0, 1):
                        go(c, "m_sum")
                        dve.tensor_reduce(B[c]["hsum"][:, 0:H], B[c]["P"][:, 0:H, :], AX.X, ALU.add
                                          ).then_inc(done[c], 1)
                    for c in (0, 1):
                        go(c, "m_inv")
                        dve.reciprocal(B[c]["hinv"][:, 0:H], B[c]["hsum"][:, 0:H]).then_inc(done[c], 1)
                    blocks_expand(dve, go, done, B, "px0", 0, 11, K["bmask"])
                    probs_copy(dve.tensor_copy, go, done, B, ps, "pc1", 2, 4)
                    normed_output(dve, go, done, B, ps, H, D)
                    add2(dve, go, done, "h1", HC, HC, [p[0:T, 1, 0:C] for p in ps])
                    add2(dve, go, done, "h2", HC, HC, [K["l2_bproj"][:, :]] * 2)
                    norm_vector(dve, go, done, B, "n1", HC, X)
                    add2(dve, go, done, "h3", HC, HC, X)
                    rms_vector(dve, go, done, B, "r1", X, X)
                    router_vector(dve, go, done, B, ps, E, 4, K["l2_gate_b"])

            @block.scalar
            def _(act):
                act.wait_ge(setup, 8)
                act.activation(pos[:, :, :], pos[:, :, :], ACT.Exp).then_inc(setup, 1)
                act.activation(hs[:, 2, :], K["l2_gating"][:, :], ACT.Exp, scale=-1.0).then_inc(setup, 1)
                with act.Fori(0, NT // 2) as i:
                    def go(c, step):
                        act.wait_ge(done[c], i * N + (S[step] + 1))

                    def tile_of(c):
                        return 2 * i + c
                    norm_scalar(act, go, done, B, "n0", eps5[0:T, :])
                    turn_scalar(act, go, done, "f0", ps, 0, xT)
                    query_blocks(act, go, done, B, ps, "q_dg", 0)
                    for c in (0, 1):
                        go(c, "v_cp")
                        act.copy(B[c]["V"][:, :], ps[c][0:T, 2, 0:C]).then_inc(done[c], 1)
                    softmax_scalar(act, go, done, B, H)
                    probs_copy(act.copy, go, done, B, ps, "pc0", 0, 2)
                    turn_scalar(act, go, done, "fo", ps, 2, oT)
                    norm_scalar(act, go, done, B, "n1", eps5[0:T, :])
                    rms_scalar(act, go, done, B, "r1", X, eps5[0:T, :])
                    turn_scalar(act, go, done, "f1", ps, 0, xT, K["l2_scale"])
                    router_scalar(act, go, done, B, E)
                    weights_out(act, "scalar", go, done, B, ps, combT, ident, tile_of, E)

            @block.gpsimd
            def _(pool):
                with pool.Fori(0, NT // 2) as i:
                    def go(c, step):
                        pool.wait_ge(done[c], i * N + (S[step] + 1))

                    def tile_of(c):
                        return 2 * i + c
                    take_experts_back(pool, "pool", go, done, B, ps, h_all, yT_all, ident, tile_of)
                    heads_expand(pool, go, done, B, "kx1", 1, HG, K["hmask12"])
                    blocks_expand(pool, go, done, B, "px1", 11, H, K["bmask"])
                    store_tile(pool, go, done, B, h_all, xT_all, tile_of, "hcur")
                    store_xT(pool, go, done, B, xT_all, tile_of)

            @block.tensor
            def _(pe):
                with pe.Fori(0, NT // 2) as i:
                    def go(c, step):
                        pe.wait_ge(done[c], i * N + (S[step] + 1))

                    def tile_of(c):
                        return 2 * i + c
                    take_experts_back(pe, "tensor", go, done, B, ps, h_all, yT_all, ident, tile_of)
                    turn_tensor(pe, go, done, "f0", X, ps, 0, ident)
                    qk_tensor(pe, go, done, ps, xT, K["l2_wqk"])
                    width_product(pe, go, done, "v", ps, 2, xT, K["l2_wv"], C)
                    scores_tensor(pe, go, done, B, ps, HG)
                    probs_turn_tensor(pe, go, done, B, ps, H, ident)
                    values_tensor(pe, go, done, B, ps, H, D, [b["V"] for b in B], H)
                    turn_tensor(pe, go, done, "fo", [b["o"][:, :] for b in B], ps, 2, ident)
                    width_product(pe, go, done, "proj", ps, 1, oT, K["l2_wproj"], C)
                    turn_tensor(pe, go, done, "f1", X, ps, 0, ident)
                    width_product(pe, go, done, "gt", ps, 1, xT, K["l2_gate_w"], E)
                    weights_out(pe, "tensor", go, done, B, ps, combT, ident, tile_of, E)


def layer3_tokens(nc, d, K, h_all, xT_all, yT_all, combT, eps5, eps6, ident, sem, sb, **_):
    H, D, HG, E, DV = 12, 16, 6, 8, 17
    HID = 4
    S = steps("y_cp y_tr y_add " + ln_steps("n0") + rms_steps("r1") + turn_steps("f1") +
              "lat lat_act big big_cp qk_sq qk_ss qk_log qk_rs qk_n qk_w r_cos|r_sin r_add e_min e_exp e_max "
              "q_tr q_dg|k_cp p_sig p_amp p_ph p_abs p_cos p_mul p_tmp p_sig2 p_lin p_clip p_dec v_x "
              "kx0|kx1 S P_m " + SPREAD + "d_s d_m d_r d_f o " + rms_steps("r2") + turn_steps("fo") +
              "proj og ao x2 h3 " + rms_steps("r3") + turn_steps("f3") + "ff1 ff_s ff_m ff2 h4 h_st " +
              ln_steps("n4") + turn_steps("f4") + "x_st gt " + ROUTER + "c_st")
    N = S["end"]
    done = [sem(f"l3_tile{c}_steps") for c in (0, 1)]
    zeroed, setup, passed = sem("l3_zeroed"), sem("l3_setup"), sem("l3_passed")
    with ExitStack() as ctx:
        shapes = attention_shapes(H, D)
        shapes.update(ROUTER_SHAPES)
        shapes.update(junk=[T, C], latT=[128, T], big=[T, 816], rA=[T, 2 * H, D], rB=[T, 2 * H, D], sg=[T, H, 4],
                      pm=[T, 4, H], Vx=[T, H, DV], qs=[T, 3, 2 * H], ff=[128, HID, T], og=[T, C])
        B, ps = tile_buffers(ctx, nc, sb, 3, shapes)
        halves(B, H)
        for b in B:
            b["passed"] = passed
        hs = sb(ctx, "l3_hs", [T, 6, H])
        X = [b["x"][:, :] for b in B]
        O = [b["o"][:, :] for b in B]
        HC = [b["hcur"][:, :] for b in B]
        xT = [b["xT"] for b in B]
        oT = [b["oT"] for b in B]
        qk = [b["big"][:, 0:2 * C].rearrange("p (h d) -> p h d", d=D) for b in B]
        shape24 = [T, 2 * H, D]
        half_pi = K["half_pi"]
        with nc.Block() as block:
            @block.vector
            def _(dve):
                for c in (0, 1):
                    dve.memset(B[c]["qx"][:, :, :], 0.0)
                    dve.memset(B[c]["sv"][:, :], PAD)
                    ins = dve.memset(B[c]["keys"][:, :], PAD)
                ins.then_inc(zeroed, 1)
                dve.wait_ge(zeroed, 1)
                dve.wait_ge(setup, 1)
                dve.tensor_scalar(hs[:, 1, :], hs[:, 0, :], 1.0, None, ALU.add).then_inc(setup, 1)
                dve.wait_ge(setup, 2)
                dve.reciprocal(hs[:, 0, :], hs[:, 1, :]).then_inc(setup, 1)
                dve.wait_ge(setup, 3)
                dve.tensor_scalar(hs[:, 1, :], hs[:, 0, :], 0.65, 0.3, ALU.mult, ALU.add).then_inc(setup, 1)
                dve.wait_ge(setup, 4)
                dve.tensor_scalar(hs[:, 0, :], hs[:, 1, :], 1e-5, 0.999, ALU.max, ALU.min).then_inc(setup, 1)
                dve.wait_ge(setup, 7)
                dve.tensor_scalar(hs[:, 3, :], hs[:, 0, :], -1.0, 1.0, ALU.mult, ALU.add).then_inc(setup, 1)
                dve.tensor_scalar(hs[:, 4, :], hs[:, 2, :], 1e-8, None, ALU.add).then_inc(setup, 1)
                dve.wait_ge(setup, 9)
                dve.reciprocal(hs[:, 5, :], hs[:, 4, :]).then_inc(setup, 1)
                dve.wait_ge(setup, 10)
                dve.tensor_tensor(hs[:, 4, :], hs[:, 5, :], hs[:, 3, :], ALU.mult).then_inc(setup, 1)
                dve.wait_ge(setup, 11)
                for c in (0, 1):
                    ins = dve.tensor_copy(B[c]["Vx"][:, :, D:D + 1], hs[:, 4, :].unsqueeze(2))
                ins.then_inc(setup, 1)
                dve.wait_ge(setup, 12)
                for c in (0, 1):
                    dve.sem_inc(done[c], 1)
                with dve.Fori(0, NT // 2) as i:
                    def go(c, step, passed=None):
                        dve.wait_ge(done[c], i * N + (S[step] + 1))
                        if passed is not None:
                            dve.sem_inc(passed, 1)

                    def tile_of(c):
                        return 2 * i + c
                    take_experts_back(dve, "vector", go, done, B, ps, h_all, yT_all, ident, tile_of)
                    norm_vector(dve, go, done, B, "n0", HC, X)
                    rms_vector(dve, go, done, B, "r1", X, O)
                    for c in (0, 1):
                        go(c, "qk_sq")
                        dve.tensor_tensor(B[c]["rA"][:, :, :], qk[c], qk[c], ALU.mult).then_inc(done[c], 1)
                    for c in (0, 1):
                        go(c, "qk_ss")
                        dve.tensor_reduce(B[c]["qs"][:, 0, :], B[c]["rA"][:, :, :], AX.X, ALU.add).then_inc(done[c], 1)
                    for c in (0, 1):
                        go(c, "qk_n")
                        dve.tensor_tensor(qk[c], qk[c], over(B[c]["qs"][:, 2, :].unsqueeze(2), shape24), ALU.mult
                                          ).then_inc(done[c], 1)
                    for c in (0, 1):
                        go(c, "qk_w")
                        for w in range(2):
                            v = qk[c][:, w * H:(w + 1) * H, :]
                            ins = dve.tensor_tensor(v, v, over(K["l3_qkn"][:, w, :].unsqueeze(1), [T, H, D]), ALU.mult)
                        ins.then_inc(done[c], 1)
                    for c in (0, 1):
                        go(c, "r_cos")
                        dve.tensor_tensor(B[c]["rA"][:, :, :], qk[c], over(K["rope_cos"][:, :].unsqueeze(1), shape24),
                                          ALU.mult).then_inc(done[c], 1)
                    for c in (0, 1):
                        go(c, "r_add")
                        dve.tensor_tensor(qk[c], B[c]["rA"][:, :, :], B[c]["rB"][:, :, :], ALU.add
                                          ).then_inc(done[c], 1)
                    for c in (0, 1):
                        go(c, "e_min")
                        dve.tensor_scalar(B[c]["rA"][:, :, :], qk[c], 0.0, None, ALU.min).then_inc(done[c], 1)
                    for c in (0, 1):
                        go(c, "e_max")
                        dve.scalar_tensor_tensor(qk[c], qk[c], 0.0, B[c]["rA"][:, :, :], ALU.max, ALU.add
                                                 ).then_inc(done[c], 1)
                    for c in (0, 1):
                        go(c, "k_cp")
                        dve.tensor_copy(B[c]["kT"][:, :, :].rearrange("p o t -> p (o t)"), ps[c][0:CK, 1, 0:2 * T]
                                        ).then_inc(done[c], 1)
                    for c in (0, 1):
                        go(c, "p_amp")
                        dve.tensor_tensor(B[c]["pm"][:, 0, :], B[c]["sg"][:, :, 0], B[c]["sg"][:, :, 2], ALU.mult
                                          ).then_inc(done[c], 1)
                    for c in (0, 1):
                        go(c, "p_ph")
                        dve.tensor_tensor(B[c]["pm"][:, 1, :], B[c]["sg"][:, :, 1], B[c]["sg"][:, :, 3], ALU.subtract
                                          ).then_inc(done[c], 1)
                    for c in (0, 1):
                        go(c, "p_abs")
                        dve.scalar_tensor_tensor(B[c]["pm"][:, 2, :], B[c]["pm"][:, 1, :], -1.0, B[c]["pm"][:, 1, :],
                                                 ALU.mult, ALU.max).then_inc(done[c], 1)
                    for c in (0, 1):
                        go(c, "p_mul")
                        dve.tensor_tensor(B[c]["pm"][:, 0, :], B[c]["pm"][:, 0, :], B[c]["pm"][:, 1, :], ALU.mult
                                          ).then_inc(done[c], 1)
                    for c in (0, 1):
                        go(c, "p_tmp")
                        dve.tensor_scalar(B[c]["pm"][:, 1, :], B[c]["pm"][:, 0, :], K["l3_temp"][:, 0:1], None,
                                          ALU.mult).then_inc(done[c], 1)
                    for c in (0, 1):
                        go(c, "p_lin")
                        dve.tensor_scalar(B[c]["pm"][:, 1, :], B[c]["pm"][:, 2, :], 1.2, -0.1, ALU.mult, ALU.add
                                          ).then_inc(done[c], 1)
                    for c in (0, 1):
                        go(c, "p_clip")
                        dve.tensor_scalar(B[c]["pm"][:, 2, :], B[c]["pm"][:, 1, :], 0.05, 0.95, ALU.max, ALU.min
                                          ).then_inc(done[c], 1)
                    for c in (0, 1):
                        go(c, "p_dec")
                        dve.tensor_tensor(B[c]["pm"][:, 3, :], B[c]["pm"][:, 2, :], hs[:, 4, :], ALU.mult
                                          ).then_inc(done[c], 1)
                    for c in (0, 1):
                        go(c, "v_x")
                        dve.tensor_tensor(B[c]["Vx"][:, :, 0:D], per_head(B[c]["big"][:, 2 * C:3 * C], D),
                                          over(B[c]["pm"][:, 3, :].unsqueeze(2), [T, H, D]), ALU.mult
                                          ).then_inc(done[c], 1)
                    heads_expand(dve, go, done, B, "kx0", 0, HG, K["hmask16"])
                    for c in (0, 1):
                        go(c, "P_m")
                        for o in range(2):
                            ins = dve.tensor_tensor(B[c]["P4"][:, o],
                                                    ps[c][0:T, o, 0:HG * NTOK].rearrange("p (h m) -> p h m", m=NTOK),
                                                    over(K["causal01"][:, :].unsqueeze(1), [T, HG, NTOK]), ALU.mult)
                        ins.then_inc(done[c], 1)
                    blocks_expand(dve, go, done, B, "px0", 0, 8, K["bmask"])
                    probs_copy(dve.tensor_copy, go, done, B, ps, "pc1", 2, 3)
                    AV = [p[0:T, 0, 0:H * DV].rearrange("p (h d) -> p h d", d=DV) for p in ps]
                    for c in (0, 1):
                        go(c, "d_s")
                        dve.tensor_tensor(B[c]["hsum"][:, 0:H], AV[c][:, :, D], hs[:, 2, :], ALU.mult
                                          ).then_inc(done[c], 1)
                    for c in (0, 1):
                        go(c, "d_m")
                        dve.tensor_scalar(B[c]["hmax"][:, 0:H], B[c]["hsum"][:, 0:H], 1e-5, None, ALU.max
                                          ).then_inc(done[c], 1)
                    for c in (0, 1):
                        go(c, "d_r")
                        dve.reciprocal(B[c]["hinv"][:, 0:H], B[c]["hmax"][:, 0:H]).then_inc(done[c], 1)
                    for c in (0, 1):
                        go(c, "d_f")
                        dve.tensor_tensor(B[c]["hsum"][:, 0:H], B[c]["hinv"][:, 0:H], hs[:, 2, :], ALU.mult
                                          ).then_inc(done[c], 1)
                    for c in (0, 1):
                        go(c, "o")
                        dve.tensor_tensor(per_head(O[c], D), AV[c][:, :, 0:D],
                                          over(B[c]["hsum"][:, 0:H].unsqueeze(2), [T, H, D]), ALU.mult
                                          ).then_inc(done[c], 1)
                    rms_vector(dve, go, done, B, "r2", O, O)
                    for c in (0, 1):
                        go(c, "ao")
                        dve.tensor_tensor(O[c], ps[c][0:T, 1, 0:C], B[c]["og"][:, :], ALU.mult).then_inc(done[c], 1)
                    add2(dve, go, done, "x2", X, X, O)
                    add2(dve, go, done, "h3", HC, HC, X)
                    rms_vector(dve, go, done, B, "r3", X, O)
                    for c in (0, 1):
                        go(c, "ff_m")
                        ff = B[c]["ff"][:, :, :].rearrange("p f t -> p (f t)")
                        dve.tensor_tensor(ff, ff, ps[c][:, 1, 0:HID * T], ALU.mult).then_inc(done[c], 1)
                    add2(dve, go, done, "h4", HC, HC, [p[0:T, 2, 0:C] for p in ps])
                    norm_vector(dve, go, done, B, "n4", HC, X)
                    router_vector(dve, go, done, B, ps, E, 2, None)

            @block.scalar
            def _(act):
                act.activation(hs[:, 0, :], K["l3_hd"][:, :], ACT.Exp, scale=-1.0).then_inc(setup, 1)
                act.wait_ge(setup, 5)
                act.activation(hs[:, 1, :], hs[:, 0, :], ACT.Ln).then_inc(setup, 1)
                act.wait_ge(setup, 6)
                act.activation(hs[:, 2, :], hs[:, 1, :], ACT.Exp, scale=K["pos1"][:, 0:1]).then_inc(setup, 1)
                with act.Fori(0, NT // 2) as i:
                    def go(c, step):
                        act.wait_ge(done[c], i * N + (S[step] + 1))

                    def tile_of(c):
                        return 2 * i + c
                    norm_scalar(act, go, done, B, "n0", eps5[0:T, :])
                    rms_scalar(act, go, done, B, "r1", X, eps6[0:T, :])
                    turn_scalar(act, go, done, "f1", ps, 0, xT, K["l3_ln_w"])
                    for c in (0, 1):
                        go(c, "lat_act")
                        act.activation(B[c]["latT"][:, :], ps[c][:, 1, 0:T], ACT.Silu).then_inc(done[c], 1)
                    for c in (0, 1):
                        go(c, "big_cp")
                        for b in range(2):
                            ins = act.copy(B[c]["big"][:, b * 408:(b + 1) * 408], ps[c][0:T, 2 + b, 0:408])
                        ins.then_inc(done[c], 1)
                    for c in (0, 1):
                        go(c, "qk_log")
                        act.activation(B[c]["qs"][:, 1, :], B[c]["qs"][:, 0, :], ACT.Ln, bias=eps6[0:T, :],
                                       scale=1.0 / D).then_inc(done[c], 1)
                    for c in (0, 1):
                        go(c, "qk_rs")
                        act.activation(B[c]["qs"][:, 2, :], B[c]["qs"][:, 1, :], ACT.Exp, scale=-0.5
                                       ).then_inc(done[c], 1)
                    for c in (0, 1):
                        go(c, "e_exp")
                        act.activation(B[c]["rA"][:, :, :], B[c]["rA"][:, :, :], ACT.Exp).then_inc(done[c], 1)
                    query_blocks(act, go, done, B, ps, "q_dg", 0)
                    for c in (0, 1):
                        go(c, "p_sig")
                        act.activation(B[c]["sg"][:, :, :].rearrange("p h f -> p (h f)"), B[c]["big"][:, 576:624],
                                       ACT.Sigmoid).then_inc(done[c], 1)
                    for c in (0, 1):
                        go(c, "p_cos")
                        act.activation(B[c]["pm"][:, 1, :], B[c]["pm"][:, 2, :], ACT.Sin, bias=half_pi[0:T, :],
                                       scale=-float(np.pi)).then_inc(done[c], 1)
                    for c in (0, 1):
                        go(c, "p_sig2")
                        act.activation(B[c]["pm"][:, 2, :], B[c]["pm"][:, 1, :], ACT.Sigmoid).then_inc(done[c], 1)
                    probs_copy(act.copy, go, done, B, ps, "pc0", 0, 2)
                    rms_scalar(act, go, done, B, "r2", O, eps6[0:T, :])
                    turn_scalar(act, go, done, "fo", ps, 2, oT, K["l3_memn_w"])
                    for c in (0, 1):
                        go(c, "og")
                        act.activation(B[c]["og"][:, :], B[c]["big"][:, 624:816], ACT.Silu).then_inc(done[c], 1)
                    rms_scalar(act, go, done, B, "r3", X, eps6[0:T, :])
                    turn_scalar(act, go, done, "f3", ps, 0, xT, K["l3_ffn_ln_w"])
                    for c in (0, 1):
                        go(c, "ff_s")
                        act.activation(B[c]["ff"][:, :, :].rearrange("p f t -> p (f t)"), ps[c][:, 0, 0:HID * T],
                                       ACT.Silu).then_inc(done[c], 1)
                    norm_scalar(act, go, done, B, "n4", eps5[0:T, :])
                    turn_scalar(act, go, done, "f4", ps, 0, xT)
                    router_scalar(act, go, done, B, E)
                    weights_out(act, "scalar", go, done, B, ps, combT, ident, tile_of, E)

            @block.gpsimd
            def _(pool):
                with pool.Fori(0, NT // 2) as i:
                    def go(c, step):
                        pool.wait_ge(done[c], i * N + (S[step] + 1))

                    def tile_of(c):
                        return 2 * i + c
                    take_experts_back(pool, "pool", go, done, B, ps, h_all, yT_all, ident, tile_of)
                    for c in (0, 1):
                        go(c, "r_sin")
                        hd = D // 2
                        for a, z in ((0, hd), (hd, 0)):
                            ins = pool.tensor_tensor(B[c]["rB"][:, :, a:a + hd], qk[c][:, :, z:z + hd],
                                                     over(K["rope_sin"][:, a:a + hd].unsqueeze(1), [T, 2 * H, hd]),
                                                     ALU.mult)
                        ins.then_inc(done[c], 1)
                    heads_expand(pool, go, done, B, "kx1", 1, HG, K["hmask16"])
                    blocks_expand(pool, go, done, B, "px1", 8, H, K["bmask"])
                    store_tile(pool, go, done, B, h_all, xT_all, tile_of, "hcur")
                    store_xT(pool, go, done, B, xT_all, tile_of)

            @block.tensor
            def _(pe):
                pe.wait_ge(setup, 12)
                with pe.Fori(0, NT // 2) as i:
                    def go(c, step):
                        pe.wait_ge(done[c], i * N + (S[step] + 1))

                    def tile_of(c):
                        return 2 * i + c
                    take_experts_back(pe, "tensor", go, done, B, ps, h_all, yT_all, ident, tile_of)
                    turn_tensor(pe, go, done, "f1", O, ps, 0, ident)
                    for c in (0, 1):
                        go(c, "lat")
                        for k in range(2):
                            mm = pe.matmul(ps[c][:, 1, 0:T], K["l3_wcomp"][:, k, :], xT[c][:, k, :],
                                           start=(k == 0), stop=(k == 1))
                        mm.then_inc(done[c], 1)
                    for c in (0, 1):
                        go(c, "big")
                        for b in range(2):
                            mm = pe.matmul(ps[c][0:T, 2 + b, 0:408], B[c]["latT"][:, :],
                                           K["l3_wcat"][:, b * 408:(b + 1) * 408], start=True, stop=True)
                        mm.then_inc(done[c], 1)
                    for c in (0, 1):
                        go(c, "q_tr")
                        for w in range(2):
                            for o in range(2):
                                mm = pe.transpose(ps[c][0:CK, w, o * T:(o + 1) * T],
                                                  B[c]["big"][:, w * C + o * CK:w * C + (o + 1) * CK], ident[0:T, 0:T])
                        mm.then_inc(done[c], 1)
                    scores_tensor(pe, go, done, B, ps, HG)
                    probs_turn_tensor(pe, go, done, B, ps, H, ident)
                    values_tensor(pe, go, done, B, ps, H, DV,
                                  [b["Vx"][:, :, :].rearrange("p h d -> p (h d)") for b in B], H)
                    turn_tensor(pe, go, done, "fo", O, ps, 2, ident)
                    width_product(pe, go, done, "proj", ps, 1, oT, K["l3_wproj"], C)
                    turn_tensor(pe, go, done, "f3", O, ps, 0, ident)
                    for c in (0, 1):
                        go(c, "ff1")
                        for b in range(2):
                            for f in range(HID):
                                for k in range(2):
                                    mm = pe.matmul(ps[c][:, b, f * T:(f + 1) * T],
                                                   K["l3_w12"][:, k, (b * HID + f) * 128:(b * HID + f + 1) * 128],
                                                   xT[c][:, k, :], start=(k == 0), stop=(k == 1))
                        mm.then_inc(done[c], 1)
                    for c in (0, 1):
                        go(c, "ff2")
                        for f in range(HID):
                            mm = pe.matmul(ps[c][0:T, 2, 0:C], B[c]["ff"][:, f, :], K["l3_w3"][:, f, :],
                                           start=(f == 0), stop=(f == HID - 1))
                        mm.then_inc(done[c], 1)
                    turn_tensor(pe, go, done, "f4", X, ps, 0, ident)
                    width_product(pe, go, done, "gt", ps, 1, xT, K["l3_gate_w"], E)
                    weights_out(pe, "tensor", go, done, B, ps, combT, ident, tile_of, E)


def last_tokens(nc, out, h_all, yT_all, ident, sem, sb, **_):
    S = steps("y_cp y_tr y_add")
    N = S["end"]
    done = [sem(f"out_tile{c}_steps") for c in (0, 1)]
    stored = [sem(f"out_stored{c}") for c in (0, 1)]
    with ExitStack() as ctx:
        B, ps = tile_buffers(ctx, nc, sb, 4, {})
        with nc.Block() as block:
            @block.gpsimd
            def _(pool):
                with pool.Fori(0, NT // 2) as i:
                    take_experts_back(pool, "pool", lambda c, s: pool.wait_ge(done[c], i * N + (S[s] + 1)), done, B, ps,
                                      h_all, yT_all, ident, lambda c: 2 * i + c)

            @block.tensor
            def _(pe):
                with pe.Fori(0, NT // 2) as i:
                    take_experts_back(pe, "tensor", lambda c, s: pe.wait_ge(done[c], i * N + (S[s] + 1)), done, B, ps,
                                      h_all, yT_all, ident, lambda c: 2 * i + c)

            @block.vector
            def _(dve):
                for c in (0, 1):
                    dve.sem_inc(done[c], 1)
                with dve.Fori(0, NT // 2) as i:
                    for c in (0, 1):
                        dve.wait_ge(stored[c], 16 * i + 1)
                    take_experts_back(dve, "vector", lambda c, s: dve.wait_ge(done[c], i * N + (S[s] + 1)), done, B, ps,
                                      h_all, yT_all, ident, lambda c: 2 * i + c)

            @block.sync
            def _(sp):
                for c in (0, 1):
                    sp.sem_inc(stored[c], 1)
                with sp.Fori(0, NT // 2) as i:
                    for c in (0, 1):
                        sp.wait_ge(done[c], i * N + (N + 1))
                        sp.dma_start(out[bass.ds(2 * i + c, 1), :, :].rearrange("a t c -> (a t) c"),
                                     B[c]["hcur"][:, :]).then_inc(stored[c], 16)
                for c in (0, 1):
                    sp.wait_ge(stored[c], 16 * (NT // 2) + 1)



COMMON = ["ident", "bmask", "hmask16", "hmask12", "off_diag", "on_diag", "causal", "anti_causal", "causal01",
          "quarter", "half_pi", "pos1"]
LAYER_WEIGHTS = [
    ["tok_w", "tok_base", "tok_pos", "l0_wqv", "l0_wproj", "l0_bproj", "l0_gate_w", "l0_gate_b"],
    ["l1_wq", "l1_wk", "l1_wv", "l1_bq", "l1_bk", "l1_bv", "l1_wo", "l1_bo", "l1_ln_w", "l1_ln_b", "l1_ln1_w",
     "l1_ln2_w", "l1_wqk", "l1_wv2", "l1_wproj", "l1_gate_w"],
    ["rel", "l2_wqk", "l2_wv", "l2_wproj", "l2_bproj", "l2_wpos", "l2_bpos", "l2_gating", "l2_scale", "l2_gate_w",
     "l2_gate_b"],
    ["rope_cos", "rope_sin", "l3_ln_w", "l3_wcomp", "l3_wcat", "l3_qkn", "l3_hd", "l3_temp", "l3_wproj",
     "l3_memn_w", "l3_ffn_ln_w", "l3_w12", "l3_w3", "l3_gate_w"]]


def shape_constants():
    f = np.float32
    n = np.arange(T) % NTOK
    img = np.arange(T) // NTOK
    m = np.arange(NTOK)
    side = int(round(NTOK ** 0.5))
    dx = (m % side)[None, :] - (n % side)[:, None]
    dy = (m // side)[None, :] - (n // side)[:, None]
    half = np.arange(0, 16, 2, dtype=f) / f(16)
    freq = np.outer(np.arange(NTOK, dtype=f), f(1.0) / (f(10000.0) ** half)).astype(f)
    cos = np.concatenate([np.cos(freq), np.cos(freq)], 1)[n]
    sin = np.concatenate([-np.sin(freq), np.sin(freq)], 1)[n]
    row = np.arange(CK)
    return {
        "ident": np.eye(128, dtype=f),
        "bmask": (img[:, None] == img[None, :]).astype(f),
        "hmask16": (row[:, None] // 16 == np.arange(6)[None, :]).astype(f),
        "hmask12": (row[:, None] // 12 == np.arange(8)[None, :]).astype(f),
        "on_diag": (n[:, None] == m[None, :]).astype(f),
        "off_diag": (n[:, None] != m[None, :]).astype(f),
        "causal": np.where(m[None, :] <= n[:, None], 0.0, -BIG).astype(f),
        "anti_causal": np.where(m[None, :] >= n[:, None], 0.0, -BIG).astype(f),
        "causal01": (m[None, :] <= n[:, None]).astype(f),
        "quarter": np.full((128, 1), -0.25, f),
        "half_pi": np.full((128, 1), np.pi / 2, f),
        "pos1": (n + 1).astype(f)[:, None],
        "rel": np.stack([dx, dy, dx * dx + dy * dy], 1).astype(f),
        "rope_cos": cos.astype(f),
        "rope_sin": sin.astype(f),
    }


def lay_out(a):
    def kxm(w, rows):
        return w.reshape(w.shape[0] // rows, rows, w.shape[1]).transpose(1, 0, 2)

    def rows(v):
        return np.broadcast_to(v[None, :], (T, v.shape[0]))

    def col(v, r):
        return v.reshape(-1, r).T

    def tiles(v, r):
        e, k, m = v.shape
        return v.reshape(e, k // r, r, m).transpose(0, 2, 1, 3).reshape(e, r, k // r * m)

    o = shape_constants()
    x = a["x"].reshape(BATCH, 3, 6, 16, 6, 16).transpose(0, 1, 2, 4, 3, 5).reshape(BATCH, 36, 768)
    full = np.zeros((NT * IMGS, NTOK, 768), x.dtype)
    full[:BATCH, 1:] = x
    o["patches"] = full.reshape(NT, T, 6, 128).transpose(0, 3, 2, 1).reshape(NT, 128, 6 * T)
    o["tok_w"] = kxm(a["L0_tok_W"].T, 128)
    o["tok_base"] = np.tile(np.concatenate([a["L0_tok_class_token"], np.broadcast_to(a["L0_tok_b"], (36, C))]),
                            (IMGS, 1))
    o["tok_pos"] = np.tile(a["L0_tok_pos_embedding"], (IMGS, 1))
    q = a["L0_attn_w_qkv"]
    o["l0_wqv"] = kxm(np.concatenate([q[0:C], q[2 * C:3 * C]]).T, CK)
    o["l0_wproj"] = kxm(a["L0_attn_w_proj"].T, CK)
    o["l0_bproj"] = rows(a["L0_attn_b_proj"])
    o["l0_gate_w"] = kxm(a["L0_ffn_gate_w"].T, CK)
    o["l0_gate_b"] = rows(a["L0_ffn_gate_b"])
    apart = np.concatenate([np.arange(0, C, 2), np.arange(1, C, 2)])
    w1 = np.concatenate([a["L0_ffn_W1"], a["L0_ffn_Ws1"][None]])[:, :, apart]
    w3 = np.concatenate([a["L0_ffn_W3"], a["L0_ffn_Ws3"][None]])[:, :, apart]
    o["l0_w1"] = tiles(np.concatenate([w1, w3], 2), CK)
    o["l0_w2"] = tiles(np.concatenate([a["L0_ffn_W2"], a["L0_ffn_Ws2"][None]]), CK)
    b = np.concatenate([np.concatenate([a["L0_ffn_B1"], a["L0_ffn_Bs1"][None]])[:, apart],
                        np.concatenate([a["L0_ffn_B3"], a["L0_ffn_Bs3"][None]])[:, apart],
                        np.concatenate([a["L0_ffn_B2"], a["L0_ffn_Bs2"][None]])], 1)
    o["l0_b"] = b.reshape(9, 6, CK).transpose(2, 0, 1)
    for n in "qkv":
        o["l1_w" + n] = kxm(a["L1_attn_w" + n], CK)
    o["l1_bq"] = col(a["L1_attn_bq"], 128)
    o["l1_bk"] = col(a["L1_attn_bk"], 128)
    o["l1_bv"] = rows(a["L1_attn_bv"])
    order = np.concatenate([np.arange(0, 12, 2), np.arange(1, 12, 2)])
    o["l1_wo"] = kxm(a["L1_attn_wo"].reshape(12, 64, C)[order].reshape(768, C), 128)
    o["l1_bo"] = rows(a["L1_attn_bo"])
    o["l1_ln_w"] = col(a["L1_attn_ln_w"], CK)
    o["l1_ln_b"] = col(a["L1_attn_ln_b"], CK)
    o["l1_ln1_w"] = col(a["L1_ffn_ln1_w"], CK)
    o["l1_ln2_w"] = col(a["L1_ffn_ln2_w"], CK)
    w = a["L1_ffn_c_attn_w"].T
    o["l1_wqk"] = kxm(w[:, 0:2 * C], CK)
    o["l1_wv2"] = kxm(w[:, 2 * C:3 * C], CK)
    o["l1_wproj"] = kxm(a["L1_ffn_c_proj_w"].T, CK)
    o["l1_gate_w"] = kxm(a["L1_ffn_w_g"].T, CK)
    o["l1_w1"] = tiles(a["L1_ffn_c_fc"], CK)
    o["l1_w2"] = tiles(a["L1_ffn_c_proj_e"], 128)
    o["l2_wqk"] = kxm(a["L2_attn_w_qk"].T, CK)
    o["l2_wv"] = kxm(a["L2_attn_w_v"].T, CK)
    o["l2_wproj"] = kxm(a["L2_attn_w_proj"].T, CK)
    o["l2_bproj"] = rows(a["L2_attn_b_proj"])
    o["l2_wpos"] = np.broadcast_to(a["L2_attn_w_pos"].T[None], (T, 3, 16))
    o["l2_bpos"] = rows(a["L2_attn_b_pos"])
    o["l2_gating"] = rows(a["L2_attn_gating"])
    o["l2_scale"] = col(a["L2_ffn_scale"], CK)
    o["l2_gate_w"] = kxm(a["L2_ffn_gate_w"].T, CK)
    o["l2_gate_b"] = rows(a["L2_ffn_gate_b"])
    o["l2_w1"] = tiles(a["L2_ffn_w1"], CK)
    o["l2_w2"] = tiles(a["L2_ffn_w2"], CK)
    o["l2_b"] = np.concatenate([a["L2_ffn_b1"], a["L2_ffn_b2"]], 1).reshape(16, 6, CK).transpose(2, 0, 1)
    o["l3_ln_w"] = col(a["L3_attn_ln_w"], CK)
    o["l3_wcomp"] = kxm(a["L3_attn_w_comp"], CK)
    o["l3_wcat"] = np.concatenate([a["L3_attn_w_qkv"], a["L3_attn_w_reso"], a["L3_attn_w_outgate"]], 1)
    o["l3_qkn"] = np.broadcast_to(np.stack([a["L3_attn_qn_w"], a["L3_attn_kn_w"]])[None], (T, 2, 16))
    o["l3_hd"] = rows(a["L3_attn_head_decay"])
    o["l3_temp"] = rows(a["L3_attn_temperature"])
    o["l3_wproj"] = kxm(a["L3_attn_w_proj"], CK)
    o["l3_memn_w"] = col(a["L3_attn_memn_w"], CK)
    o["l3_ffn_ln_w"] = col(a["L3_attn_ffn_ln_w"], CK)
    o["l3_w12"] = kxm(np.concatenate([a["L3_attn_w1"], a["L3_attn_w2"]], 1), CK)
    o["l3_w3"] = kxm(a["L3_attn_w3"], 128)
    o["l3_gate_w"] = kxm(a["L3_ffn_w_gate"], CK)
    o["l3_w1"] = tiles(a["L3_ffn_w_fc"].reshape(C, 768, 8).transpose(2, 0, 1), CK)
    o["l3_w2"] = tiles(a["L3_ffn_w_proj"].reshape(768, C, 8).transpose(2, 0, 1), 128)
    return {n: np.ascontiguousarray(v) for n, v in o.items()}


def kernel(**inputs):
    import concourse.bacc as _bacc
    from concourse.bass_utils import run_bass_kernel_spmd as _run

    arrays = {f"in_{n}": v for n, v in lay_out({n: np.asarray(v) for n, v in inputs.items()}).items()}
    nc = _bacc.Bacc("TRN2", target_bir_lowering=False, num_devices=1)
    d = {n[3:]: nc.dram_tensor(n, v.shape, mybir.dt.from_np(v.dtype), kind="ExternalInput").ap()
         for n, v in arrays.items()}
    out = nc.dram_tensor("out", (NT, T, C), F32, kind="ExternalOutput").ap()
    vit_tower(nc, d, out)
    r = _run(nc, [arrays], core_ids=[0])
    got = r.results[0]["out"].reshape(NT * IMGS, NTOK, C)
    return np.ascontiguousarray(got[:BATCH])
```

```python
from contextlib import ExitStack

import numpy as np
import concourse.bass as bass
from concourse import mybir

F32 = mybir.dt.float32
F32R = mybir.dt.float32r
ALU = mybir.AluOpType
ACT = mybir.ActivationFunctionType
AX = mybir.AxisListType

C = 192
CK = 96
NTOK = 37
IMGS = 3
T = IMGS * NTOK
BATCH = 64
NT = 22
NP = NT * T
WAYS = 4
UB = 474
NB = 5
DIAG = NTOK + T
BIG = 1.0e30
PAD = -3.0e38
MARK = 3.0e38
ALPHA, LIMIT = 1.702, 7.0
CAP = 592


def steps(text):
    out, n = {}, 0
    for group in text.split():
        names = group.split("|")
        size = 0
        for name in names:
            name, _, many = name.partition(":")
            assert name not in out, name
            out[name] = n
            size += int(many) if many else 1
        n += size
    out["end"] = n
    return out


def ln_steps(g):
    return f"{g}_stats {g}_aggr {g}_log {g}_rstd {g}_norm "


def rms_steps(g):
    return f"{g}_sq {g}_log {g}_rstd {g}_norm "


def turn_steps(g):
    return f"{g}_tr {g}_cp "


SOFTMAX = "sm_scale sm_max sm_sub sm_exp sm_sum sm_inv "
SPREAD = "px0|px1 pt pc0|pc1 pt2 pc2 av "
SPREAD16 = "px0|px1 pt pc0|pc1 pt2 pc2|pc3 av "


def topk_steps(g):
    return f"{g}_top {g}_keys {g}_repl {g}_mask "



def over(ap, shape):
    return ap.broadcast_to(shape)



def norm_vector(dve, go, done, B, g, src, dst):
    for c in range(len(done)):
        go(c, f"{g}_stats")
        dve.bn_stats(B[c]["stats"][:, :], src[c]).then_inc(done[c], 1)
    for c in range(len(done)):
        go(c, f"{g}_aggr", B[c]["passed"])
        dve.bn_aggr(B[c]["mv"][:, :], B[c]["stats"][:, :]).then_inc(done[c], 1)
    for c in range(len(done)):
        go(c, f"{g}_norm")
        dve.tensor_scalar(dst[c], src[c], B[c]["mv"][:, 0:1], B[c]["rstd"][:, 1:2],
                          ALU.subtract, ALU.mult).then_inc(done[c], 1)


def norm_scalar(act, go, done, B, g, eps):
    for c in range(len(done)):
        go(c, f"{g}_log")
        act.activation(B[c]["rstd"][:, 0:1], B[c]["mv"][:, 1:2], ACT.Ln, bias=eps).then_inc(done[c], 1)
    for c in range(len(done)):
        go(c, f"{g}_rstd")
        act.activation(B[c]["rstd"][:, 1:2], B[c]["rstd"][:, 0:1], ACT.Exp, scale=-0.5).then_inc(done[c], 1)


def rms_scalar(act, go, done, B, g, src, eps):
    for c in range(len(done)):
        go(c, f"{g}_sq")
        act.activation(B[c]["junk"], src[c], ACT.Square, accum_out=B[c]["mv"][:, 0:1]).then_inc(done[c], 1)
    for c in range(len(done)):
        go(c, f"{g}_log")
        act.activation(B[c]["rstd"][:, 0:1], B[c]["mv"][:, 0:1], ACT.Ln, bias=eps, scale=1.0 / C).then_inc(done[c], 1)
    for c in range(len(done)):
        go(c, f"{g}_rstd")
        act.activation(B[c]["rstd"][:, 1:2], B[c]["rstd"][:, 0:1], ACT.Exp, scale=-0.5).then_inc(done[c], 1)


def rms_vector(dve, go, done, B, g, src, dst):
    for c in range(len(done)):
        go(c, f"{g}_norm")
        dve.tensor_scalar(dst[c], src[c], B[c]["rstd"][:, 1:2], None, ALU.mult).then_inc(done[c], 1)


def turn_tensor(pe, go, done, g, src, ps, bank, ident):
    for c in range(len(done)):
        go(c, f"{g}_tr")
        for o in range(2):
            mm = pe.transpose(ps[c][0:CK, bank, o * T:(o + 1) * T], src[c][:, o * CK:(o + 1) * CK],
                              ident[0:T, 0:T])
        mm.then_inc(done[c], 1)


def turn_scalar(act, go, done, g, ps, bank, dst, scale=None, bias=None):
    for c in range(len(done)):
        go(c, f"{g}_cp")
        if scale is None:
            act.copy(dst[c][:, :, :].rearrange("p o t -> p (o t)"), ps[c][0:CK, bank, 0:2 * T]).then_inc(done[c], 1)
            continue
        for o in range(2):
            kw = {} if bias is None else {"bias": bias[:, o:o + 1]}
            ins = act.activation(dst[c][:, o, :], ps[c][0:CK, bank, o * T:(o + 1) * T], ACT.Identity,
                                 scale=scale[:, o:o + 1], **kw)
        ins.then_inc(done[c], 1)


def heads_expand(eng, go, done, B, step, o, HG, hmask):
    for c in range(len(done)):
        go(c, step)
        for j in range(IMGS):
            k = B[c]["kT"][:, o, j * NTOK:(j + 1) * NTOK].unsqueeze(1)
            ins = eng.tensor_tensor(B[c]["kx"][:, o, j, 0:HG, :], over(k, [CK, HG, NTOK]),
                                    over(hmask[:, 0:HG].unsqueeze(2), [CK, HG, NTOK]), ALU.mult)
        ins.then_inc(done[c], 1)


def score_place(ps, o, HG):
    if 2 * HG * NTOK <= 512:
        return ps[0:T, 0, o * HG * NTOK:(o + 1) * HG * NTOK]
    return ps[0:T, o, 0:HG * NTOK]


def scores_tensor(pe, go, done, B, ps, HG):
    for c in range(len(done)):
        go(c, "S")
        for o in range(2):
            for j in range(IMGS):
                mm = pe.matmul(score_place(ps[c], o, HG), B[c]["qx"][:, o, j * T:(j + 1) * T],
                               B[c]["kx"][:, o, j, 0:HG, :].rearrange("p h m -> p (h m)"),
                               start=(j == 0), stop=(j == IMGS - 1))
        mm.then_inc(done[c], 1)


def query_blocks(act, go, done, B, ps, step, bank):
    for c in range(len(done)):
        go(c, step)
        for o in range(2):
            ins = act.copy(B[c]["qx"][:, o, :].rearrange("p (j x) -> p j x", x=DIAG)[:, :, 0:NTOK],
                           ps[c][0:CK, bank, o * T:(o + 1) * T].rearrange("p (j m) -> p j m", m=NTOK))
        ins.then_inc(done[c], 1)


def softmax_vector(dve, go, done, B, S, scale, bias, H):
    for c in range(len(done)):
        go(c, "sm_scale")
        h = 0
        for src in S[c]:
            dst = B[c]["P"][:, h:h + src.shape[1], :]
            if bias is None:
                ins = dve.tensor_scalar(dst, src, scale, None, ALU.mult)
            else:
                ins = dve.scalar_tensor_tensor(dst, src, scale, over(bias[:, :].unsqueeze(1), list(src.shape)),
                                               ALU.mult, ALU.add)
            h += src.shape[1]
        ins.then_inc(done[c], 1)
    for c in range(len(done)):
        go(c, "sm_max")
        dve.tensor_reduce(B[c]["hmax"][:, 0:H], B[c]["P"][:, 0:H, :], AX.X, ALU.max).then_inc(done[c], 1)
    for c in range(len(done)):
        go(c, "sm_sub")
        dve.tensor_tensor(B[c]["P"][:, 0:H, :], B[c]["P"][:, 0:H, :],
                          over(B[c]["hmax"][:, 0:H].unsqueeze(2), [T, H, NTOK]), ALU.subtract).then_inc(done[c], 1)
    sums_vector(dve, go, done, B, H)


def sums_vector(dve, go, done, B, H):
    for c in range(len(done)):
        go(c, "sm_sum")
        dve.tensor_reduce(B[c]["hsum"][:, 0:H], B[c]["P"][:, 0:H, :], AX.X, ALU.add).then_inc(done[c], 1)
    for c in range(len(done)):
        go(c, "sm_inv")
        dve.reciprocal(B[c]["hinv"][:, 0:H], B[c]["hsum"][:, 0:H]).then_inc(done[c], 1)


def softmax_scalar(act, go, done, B, H):
    for c in range(len(done)):
        go(c, "sm_exp")
        act.activation(B[c]["P"][:, 0:H, :], B[c]["P"][:, 0:H, :], ACT.Exp).then_inc(done[c], 1)


def blocks_expand(eng, go, done, B, step, h0, h1, bmask):
    for c in range(len(done)):
        go(c, step)
        for h in range(h0, h1):
            ins = eng.tensor_tensor(B[c]["px"][:, h, :].rearrange("p (j m) -> p j m", m=NTOK),
                                    over(B[c]["P"][:, h, :].unsqueeze(1), [T, IMGS, NTOK]),
                                    bmask[:, :].rearrange("p (j m) -> p j m", m=NTOK), ALU.mult)
        ins.then_inc(done[c], 1)


def probs_turn_tensor(pe, go, done, B, ps, step, h0, h1, ident):
    for c in range(len(done)):
        go(c, step)
        for h in range(h0, h1):
            r = h - h0
            mm = pe.transpose(ps[c][0:T, r // 4, (r % 4) * T:(r % 4 + 1) * T], B[c]["px"][:, h, :],
                              ident[0:T, 0:T])
        mm.then_inc(done[c], 1)


def probs_copy(copy, go, done, B, ps, step, b, h0):
    for c in range(len(done)):
        go(c, step)
        copy(B[c]["pT"][0:T, h0:h0 + 4, :].rearrange("p h n -> p (h n)"), ps[c][0:T, b, 0:4 * T]).then_inc(done[c], 1)


def values_stage(pe, go, done, B, ps, H, D, V, per_bank, ident, order=None):
    probs_turn_tensor(pe, go, done, B, ps, "pt", 0, 8, ident)
    probs_turn_tensor(pe, go, done, B, ps, "pt2", 8, H, ident)
    values_tensor(pe, go, done, B, ps, H, D, V, per_bank, order)


def values_tensor(pe, go, done, B, ps, H, D, V, per_bank, order=None):
    for c in range(len(done)):
        go(c, "av")
        for h in range(H):
            b, r = h // per_bank, h % per_bank
            v = h if order is None else order[h]
            mm = pe.matmul(ps[c][0:T, b, r * D:(r + 1) * D], B[c]["pT"][0:T, h, :], V[c][:, v * D:(v + 1) * D],
                           start=True, stop=True)
        mm.then_inc(done[c], 1)


def topk_vector(dve, go, done, B, g, vals, keys, k, E, mask):
    for c in range(len(done)):
        go(c, f"{g}_top", B[c]["passed"])
        dve.max(B[c]["max8"][:, :], B[c][vals][:, 0:E + 8]).then_inc(done[c], 1)
    for c in range(len(done)):
        go(c, f"{g}_keys")
        dve.tensor_copy(B[c][keys][:, 0:k], B[c]["max8"][:, 0:k]).then_inc(done[c], 1)
    for c in range(len(done)):
        go(c, f"{g}_repl", B[c]["passed"])
        dve.match_replace(B[c]["repl"][:, 0:E + 8], B[c][keys][:, :], B[c][vals][:, 0:E + 8], MARK).then_inc(done[c], 1)
    for c in range(len(done)):
        go(c, f"{g}_mask")
        dve.tensor_scalar(mask[c], B[c]["repl"][:, 0:E], 0.5 * MARK, None, ALU.is_ge).then_inc(done[c], 1)



def vit_tower(nc, d, out):
    root = ExitStack()

    def sb(ctx, name, shape):
        return ctx.enter_context(nc.sbuf_tensor(name, shape, F32))

    def sem(name):
        return root.enter_context(nc.semaphore(name))

    with root:
        K = {}
        resident = load_list(root, sb, d, K, COMMON)
        K["tok_add"] = sb(root, "tok_add", [T, C])
        h_all = sb(root, "h_all", [T, NT, C])
        xT_all = sb(root, "xT_all", [CK, 2, NP])
        yT_all = sb(root, "yT_all", [CK, 2, NP])
        combT = sb(root, "combT", [40, NP])
        maskT = combT[32:40, :]
        eps5 = sb(root, "eps5", [128, 1])
        eps6 = sb(root, "eps6", [128, 1])
        m10 = sb(root, "m10", [128, 1])
        ident = K["ident"]

        layer_weights = ExitStack()
        resident += load_list(layer_weights, sb, d, K, LAYER_WEIGHTS[0])
        resident_loaded = sem("resident_loaded")
        with nc.Block() as block:
            @block.sync
            def _(sp):
                start_loads(sp, resident, resident_loaded)
                sp.wait_ge(resident_loaded, 16 * len(resident))

            @block.vector
            def _(dve):
                dve.memset(eps5[:, :], 1e-5)
                dve.memset(eps6[:, :], 1e-6)
                dve.memset(m10[:, :], -10.0)
                dve.wait_ge(resident_loaded, 16 * len(resident))
                dve.tensor_tensor(K["tok_add"][:, :], K["tok_base"][:, :], K["tok_pos"][:, :], ALU.add)

        env = dict(nc=nc, d=d, out=out, K=K, h_all=h_all, xT_all=xT_all, yT_all=yT_all, combT=combT, maskT=maskT,
                   eps5=eps5, eps6=eps6, m10=m10, ident=ident, sem=sem, sb=sb)
        with layer_weights:
            layer0_tokens(**env)
        with ExitStack() as layer_weights:
            ahead = load_list(layer_weights, sb, d, K, LAYER_WEIGHTS[1])
            experts_swiglu(layer=0, E=9, ahead=ahead, **env)
            layer1_tokens(**env)
        capacity_limit(**env)
        with ExitStack() as layer_weights:
            ahead = load_list(layer_weights, sb, d, K, LAYER_WEIGHTS[2])
            experts_gelu(layer=1, func=ACT.Gelu, ahead=ahead, **env)
            layer2_tokens(**env)
        with ExitStack() as layer_weights:
            ahead = load_list(layer_weights, sb, d, K, LAYER_WEIGHTS[3])
            experts_swiglu(layer=2, E=16, ahead=ahead, **env)
            layer3_tokens(**env)
        experts_gelu(layer=3, func=ACT.Gelu_apprx_tanh, ahead=[], **env)
        last_tokens(**env)


def load_list(ctx, sb, d, K, names):
    for n in names:
        K[n] = sb(ctx, "c_" + n, list(d[n].shape))
    return [(K[n], d[n]) for n in names]


def start_loads(sp, loads, loaded):
    for tile, src in loads:
        idx = tuple(slice(None) for _ in src.shape)
        sp.dma_start(tile[idx], src[idx]).then_inc(loaded, 16)


def tile_buffers(ctx, nc, sb, layer, shapes):
    small = dict(stats=[T, 6], mv=[T, 2], rstd=[T, 2], hmax=[T, 16], hsum=[T, 16], hinv=[T, 16],
                 max8=[T, 8], repl=[T, 24], x=[T, C], hcur=[T, C], xT=[CK, 2, T])
    B = []
    for c in range(WAYS):
        one = {n: sb(ctx, f"L{layer}t{c}_{n}", s) for n, s in {**small, **shapes}.items()}
        B.append(one)
    ps = [ctx.enter_context(nc.psum_tensor(f"L{layer}ps{c}", [128, 2, 512], F32)) for c in range(WAYS)]
    return B, ps


def attention_shapes(H, D):
    HG = H // 2
    return dict(P=[T, H, NTOK], px=[T, H, T], pT=[128, H, T], kT=[CK, 2, T],
                qx=[CK, 2, IMGS * DIAG], V=[T, C])


def share(B, H):
    for b in B:
        b["kx"] = b["px"][0:CK, :, :].rearrange("p h n -> p (h n)").rearrange(
            "p (o j h m) -> p o j h m", o=2, j=IMGS, h=H // 2)
        b["oT"] = b["kT"]
        b["o"] = b["V"]


def take_experts_back(eng, kind, go, done, B, ps, h_all, yT_all, ident, tile_of):
    if kind == "pool":
        for c in range(len(done)):
            go(c, "y_cp")
            eng.tensor_copy(B[c]["xT"][:, :, :], yT_all[:, :, bass.ds(tile_of(c) * T, T)]).then_inc(done[c], 1)
    if kind == "tensor":
        for c in range(len(done)):
            go(c, "y_tr")
            for o in range(2):
                mm = eng.transpose(ps[c][0:T, 0, o * CK:(o + 1) * CK], B[c]["xT"][:, o, :], ident[0:CK, 0:CK])
            mm.then_inc(done[c], 1)
    if kind == "vector":
        for c in range(len(done)):
            go(c, "y_add")
            eng.tensor_tensor(B[c]["hcur"][:, :], ps[c][0:T, 0, 0:C],
                              h_all[:, bass.ds(tile_of(c), 1), :].rearrange("p a c -> p (a c)"),
                              ALU.add).then_inc(done[c], 1)


def width_product(pe, go, done, step, ps, bank, lhsT, rhs, N, at=0):
    for c in range(len(done)):
        go(c, step)
        for k in range(2):
            mm = pe.matmul(ps[c][0:T, bank, at:at + N], lhsT[c][:, k, :], rhs[:, k, 0:N], start=(k == 0), stop=(k == 1))
        mm.then_inc(done[c], 1)


def store_tile(pool, go, done, B, h_all, xT_all, tile_of, src):
    for c in range(len(done)):
        go(c, "h_st")
        pool.tensor_copy(h_all[:, bass.ds(tile_of(c), 1), :].rearrange("p a c -> p (a c)"),
                         B[c][src][:, :]).then_inc(done[c], 1)


def store_xT(pool, go, done, B, xT_all, tile_of):
    for c in range(len(done)):
        go(c, "x_st")
        pool.tensor_copy(xT_all[:, :, bass.ds(tile_of(c) * T, T)], B[c]["xT"][:, :, :]).then_inc(done[c], 1)


def weights_out(eng, kind, go, done, B, ps, combT, ident, tile_of, E):
    for c in range(len(done)):
        if kind == "tensor":
            go(c, "c_tr")
            eng.transpose(ps[c][0:E, 0, 0:T], B[c]["comb"][:, 0:E], ident[0:T, 0:T]).then_inc(done[c], 1)
        else:
            go(c, "c_st")
            eng.copy(combT[0:E, bass.ds(tile_of(c) * T, T)], ps[c][0:E, 0, 0:T]).then_inc(done[c], 1)


EXP_LN = "natural_log_exp_and_others"
SINK = 7
ITERS = 10


def layer0_tokens(nc, d, K, h_all, xT_all, yT_all, combT, eps5, m10, ident, sem, sb, **_):
    H, D, HG, E = 12, 16, 6, 8
    S = steps("embed hcur " + ln_steps("n0") + turn_steps("f0") + "qv q_cp v_cp q_sq q_ss q_floor q_log q_nrm q_add "
              "q_rc q_n q_tr q_dg k_cp kx0|kx1 S K_exp|v_one K_off it:%d " % (SINK * ITERS) +
              "T1 T2 rm rm_tr im ix ix_mm ir T3 T4 sm_exp sm_sum sm_inv " + SPREAD + "o " + turn_steps("fo") +
              "proj h1 h2 h_st " + ln_steps("n1") + turn_steps("f1") + "x_st gt g_cp g_mx g_sub g_exp g_sum g_rc "
              "g_p g_s g_gs " + topk_steps("gg") + "g_pen g_sm " + topk_steps("ge") + "g_w c_tr c_st")
    N = S["end"]
    done = [sem(f"l0_tile{c}_steps") for c in range(WAYS)]
    patch_loaded = [sem(f"l0_patch_loaded{c}") for c in range(WAYS)]
    zeroed, passed = sem("l0_zeroed"), sem("l0_passed")
    with ExitStack() as ctx:
        shapes = attention_shapes(H, D)
        shapes.update(patch=[128, 6, T], q=[T, H, D], vb=[T, H, NTOK], kv=[T, H, NTOK], small=[T, 8, 12],
                      MX=[12, IMGS, NTOK], MI=[12, 4], rmT=[12, T], lg=[T, 8], gs=[T, 12], gm=[T, 4], sv=[T, 16],
                      keys2=[T, 8], keys8=[T, 8], mask=[T, 8], comb=[T, 16], p=[T, 8], s=[T, 8])
        B, ps = tile_buffers(ctx, nc, sb, 0, shapes)
        share(B, H)
        for b in B:
            b["passed"] = passed
        X = [b["x"][:, :] for b in B]
        HC = [b["hcur"][:, :] for b in B]
        xT = [b["xT"] for b in B]
        oT = [b["oT"] for b in B]
        flat = [b["q"][:, :, :].rearrange("p h d -> p (h d)") for b in B]
        with nc.Block() as block:
            @block.sync
            def _(sp):
                for c in range(len(done)):
                    sp.dma_start(B[c]["patch"][:, :, :].rearrange("p k t -> p (k t)"),
                                 d["patches"][c, :, :]).then_inc(patch_loaded[c], 16)
                def fetch(i, done):
                    for c in range(len(done)):
                        sp.wait_ge(done[c], i * N - (N - S["embed"] - 2))
                        sp.dma_start(B[c]["patch"][:, :, :].rearrange("p k t -> p (k t)"),
                                     d["patches"][bass.ds(WAYS * i + c, 1), :, :].rearrange("a p x -> (a p) x")
                                     ).then_inc(patch_loaded[c], 16)
                with sp.Fori(1, NT // WAYS) as i:
                    fetch(i, done)
                fetch(NT // WAYS, done[:NT % WAYS])

            @block.vector
            def _(dve):
                for c in range(len(done)):
                    dve.memset(B[c]["qx"][:, :, :], 0.0)
                    dve.memset(B[c]["gs"][:, 4:12], PAD)
                    dve.memset(B[c]["sv"][:, 8:16], PAD)
                    dve.memset(B[c]["keys2"][:, :], PAD)
                    dve.memset(B[c]["keys8"][:, :], PAD)
                    ins = dve.memset(B[c]["comb"][:, 8:16], 1.0)
                ins.then_inc(zeroed, 1)
                dve.wait_ge(zeroed, 1)
                for c in range(len(done)):
                    dve.sem_inc(done[c], 1)
                def turn(i, done):
                    def go(c, step, passed=None):
                        dve.wait_ge(done[c], i * N + (S[step] + 1))
                        if passed is not None:
                            dve.sem_inc(passed, 1)

                    for c in range(len(done)):
                        go(c, "hcur")
                        dve.tensor_tensor(HC[c], ps[c][0:T, 0, 0:C], K["tok_add"][:, :], ALU.add).then_inc(done[c], 1)
                    norm_vector(dve, go, done, B, "n0", HC, X)
                    for c in range(len(done)):
                        go(c, "q_sq")
                        dve.tensor_tensor(B[c]["kv"][:, :, 0:D], B[c]["q"][:, :, :], B[c]["q"][:, :, :],
                                          ALU.mult).then_inc(done[c], 1)
                    for c in range(len(done)):
                        go(c, "q_ss")
                        dve.tensor_reduce(B[c]["small"][:, 0, :], B[c]["kv"][:, :, 0:D], AX.X, ALU.add).then_inc(done[c], 1)
                    for c in range(len(done)):
                        go(c, "q_floor")
                        dve.tensor_scalar(B[c]["small"][:, 1, :], B[c]["small"][:, 0, :], 1e-19, None, ALU.max
                                          ).then_inc(done[c], 1)
                    for c in range(len(done)):
                        go(c, "q_add")
                        dve.tensor_scalar(B[c]["small"][:, 3, :], B[c]["small"][:, 2, :], 1e-8, None, ALU.add
                                          ).then_inc(done[c], 1)
                    for c in range(len(done)):
                        go(c, "q_rc")
                        dve.reciprocal(B[c]["small"][:, 4, :], B[c]["small"][:, 3, :]).then_inc(done[c], 1)
                    for c in range(len(done)):
                        go(c, "q_n")
                        dve.tensor_tensor(B[c]["q"][:, :, :], B[c]["q"][:, :, :],
                                          over(B[c]["small"][:, 4, :].unsqueeze(2), [T, H, D]), ALU.mult
                                          ).then_inc(done[c], 1)
                    for c in range(len(done)):
                        go(c, "k_cp")
                        dve.tensor_copy(B[c]["kT"][:, :, :].rearrange("p o t -> p (o t)"), ps[c][0:CK, 1, 0:2 * T]
                                        ).then_inc(done[c], 1)
                    heads_expand(dve, go, done, B, "kx0", 0, HG, K["hmask16"])
                    for c in range(len(done)):
                        go(c, "v_one")
                        dve.memset(B[c]["vb"][:, :, :], 1.0).then_inc(done[c], 1)
                    for c in range(len(done)):
                        go(c, "K_off")
                        dve.tensor_tensor(B[c]["P"][:, :, :], B[c]["P"][:, :, :],
                                          over(K["off_diag"][:, :].unsqueeze(1), [T, H, NTOK]), ALU.mult
                                          ).then_inc(done[c], 1)
                    with dve.Fori(0, ITERS) as r:
                        def at(c, k):
                            dve.wait_ge(done[c], i * N + r * SINK + (S["it"] + 1 + k))
                        for c in range(len(done)):
                            at(c, 0)
                            dve.tensor_tensor(B[c]["kv"][:, :, :], B[c]["P"][:, :, :], B[c]["vb"][:, :, :], ALU.mult
                                              ).then_inc(done[c], 1)
                        for c in range(len(done)):
                            at(c, 1)
                            dve.tensor_reduce(B[c]["small"][:, 5, :], B[c]["kv"][:, :, :], AX.X, ALU.add
                                              ).then_inc(done[c], 1)
                        for c in range(len(done)):
                            at(c, 2)
                            dve.reciprocal(B[c]["small"][:, 6, :], B[c]["small"][:, 5, :]).then_inc(done[c], 1)
                    for c in range(len(done)):
                        go(c, "T1")
                        dve.tensor_tensor(B[c]["kv"][:, :, :], B[c]["P"][:, :, :], B[c]["vb"][:, :, :], ALU.mult
                                          ).then_inc(done[c], 1)
                    for c in range(len(done)):
                        go(c, "T2")
                        dve.tensor_tensor(B[c]["kv"][:, :, :], B[c]["kv"][:, :, :],
                                          over(B[c]["small"][:, 6, :].unsqueeze(2), [T, H, NTOK]), ALU.mult
                                          ).then_inc(done[c], 1)
                    for c in range(len(done)):
                        go(c, "rm")
                        dve.tensor_reduce(B[c]["small"][:, 0, :], B[c]["kv"][:, :, :], AX.X, ALU.max).then_inc(done[c], 1)
                    for c in range(len(done)):
                        go(c, "im")
                        dve.tensor_reduce(B[c]["MI"][:, 0:IMGS],
                                          ps[c][0:H, 0, 0:T].rearrange("p (j n) -> p j n", n=NTOK), AX.X, ALU.max
                                          ).then_inc(done[c], 1)
                    for c in range(len(done)):
                        go(c, "ix")
                        dve.tensor_copy(B[c]["MX"][:, :, :], over(B[c]["MI"][:, 0:IMGS].unsqueeze(2),
                                                                  [H, IMGS, NTOK])).then_inc(done[c], 1)
                    for c in range(len(done)):
                        go(c, "ir")
                        dve.reciprocal(B[c]["small"][:, 1, :], ps[c][0:T, 1, 0:H]).then_inc(done[c], 1)
                    for c in range(len(done)):
                        go(c, "T3")
                        dve.tensor_tensor(B[c]["kv"][:, :, :], B[c]["kv"][:, :, :],
                                          over(B[c]["small"][:, 1, :].unsqueeze(2), [T, H, NTOK]), ALU.mult
                                          ).then_inc(done[c], 1)
                    for c in range(len(done)):
                        go(c, "T4")
                        dve.tensor_tensor(B[c]["P"][:, :, :], B[c]["kv"][:, :, :],
                                          over(K["on_diag"][:, :].unsqueeze(1), [T, H, NTOK]), ALU.add
                                          ).then_inc(done[c], 1)
                    sums_vector(dve, go, done, B, H)
                    blocks_expand(dve, go, done, B, "px0", 0, 8, K["bmask"])
                    probs_copy(dve.tensor_copy, go, done, B, ps, "pc1", 1, 4)
                    for c in range(len(done)):
                        go(c, "o")
                        dve.tensor_tensor(B[c]["o"][:, :].rearrange("p (h d) -> p h d", d=D),
                                          ps[c][0:T, 0, 0:C].rearrange("p (h d) -> p h d", d=D),
                                          over(B[c]["hinv"][:, 0:H].unsqueeze(2), [T, H, D]), ALU.mult
                                          ).then_inc(done[c], 1)
                    for c in range(len(done)):
                        go(c, "h1")
                        dve.tensor_tensor(HC[c], HC[c], ps[c][0:T, 0, 0:C], ALU.add).then_inc(done[c], 1)
                    for c in range(len(done)):
                        go(c, "h2")
                        dve.tensor_tensor(HC[c], HC[c], K["l0_bproj"][:, :], ALU.add).then_inc(done[c], 1)
                    norm_vector(dve, go, done, B, "n1", HC, X)
                    for c in range(len(done)):
                        go(c, "g_cp")
                        dve.tensor_copy(B[c]["lg"][:, :], ps[c][0:T, 1, 0:E]).then_inc(done[c], 1)
                    for c in range(len(done)):
                        go(c, "g_mx")
                        dve.tensor_reduce(B[c]["mv"][:, 0:1], B[c]["lg"][:, :], AX.X, ALU.max).then_inc(done[c], 1)
                    for c in range(len(done)):
                        go(c, "g_sub")
                        dve.tensor_scalar(B[c]["lg"][:, :], B[c]["lg"][:, :], B[c]["mv"][:, 0:1], None, ALU.subtract
                                          ).then_inc(done[c], 1)
                    for c in range(len(done)):
                        go(c, "g_sum")
                        dve.tensor_reduce(B[c]["mv"][:, 0:1], B[c]["lg"][:, :], AX.X, ALU.add).then_inc(done[c], 1)
                    for c in range(len(done)):
                        go(c, "g_rc")
                        dve.reciprocal(B[c]["mv"][:, 1:2], B[c]["mv"][:, 0:1]).then_inc(done[c], 1)
                    for c in range(len(done)):
                        go(c, "g_p")
                        dve.tensor_scalar(B[c]["p"][:, :], B[c]["lg"][:, :], B[c]["mv"][:, 1:2], None, ALU.mult
                                          ).then_inc(done[c], 1)
                    for c in range(len(done)):
                        go(c, "g_s")
                        dve.tensor_tensor(B[c]["s"][:, :], B[c]["p"][:, :], K["l0_gate_b"][:, :], ALU.add
                                          ).then_inc(done[c], 1)
                    for c in range(len(done)):
                        go(c, "g_gs")
                        pair = B[c]["s"][:, :].rearrange("p (g e) -> p g e", e=2)
                        dve.tensor_tensor(B[c]["gs"][:, 0:4], pair[:, :, 0], pair[:, :, 1], ALU.add).then_inc(done[c], 1)
                    topk_vector(dve, go, done, B, "gg", "gs", "keys2", 2, 4, [b["gm"][:, :] for b in B])
                    for c in range(len(done)):
                        go(c, "g_pen")
                        dve.tensor_scalar(B[c]["gm"][:, :], B[c]["gm"][:, :], BIG, -BIG, ALU.mult, ALU.add
                                          ).then_inc(done[c], 1)
                    for c in range(len(done)):
                        go(c, "g_sm")
                        dve.tensor_tensor(B[c]["sv"][:, 0:8].rearrange("p (g e) -> p g e", e=2),
                                          B[c]["s"][:, :].rearrange("p (g e) -> p g e", e=2),
                                          over(B[c]["gm"][:, :].unsqueeze(2), [T, 4, 2]), ALU.add).then_inc(done[c], 1)
                    topk_vector(dve, go, done, B, "ge", "sv", "keys8", 2, 8, [b["mask"][:, :] for b in B])
                    for c in range(len(done)):
                        go(c, "g_w")
                        dve.tensor_tensor(B[c]["comb"][:, 0:8], B[c]["p"][:, :], B[c]["mask"][:, :], ALU.mult
                                          ).then_inc(done[c], 1)

                with dve.Fori(0, NT // WAYS) as i:
                    turn(i, done)
                turn(NT // WAYS, done[:NT % WAYS])

            @block.scalar
            def _(act):
                act.preload_act_table_set(EXP_LN)
                def turn(i, done):
                    def go(c, step):
                        act.wait_ge(done[c], i * N + (S[step] + 1))

                    def tile_of(c):
                        return WAYS * i + c
                    norm_scalar(act, go, done, B, "n0", eps5[0:T, :])
                    turn_scalar(act, go, done, "f0", ps, 1, xT)
                    for c in range(len(done)):
                        go(c, "q_cp")
                        act.copy(flat[c], ps[c][0:T, 0, 0:C]).then_inc(done[c], 1)
                        go(c, "v_cp")
                        act.copy(B[c]["V"][:, :], ps[c][0:T, 0, C:2 * C]).then_inc(done[c], 1)
                    for c in range(len(done)):
                        go(c, "q_log")
                        act.activation(B[c]["small"][:, 2, :], B[c]["small"][:, 1, :], ACT.Ln).then_inc(done[c], 1)
                    for c in range(len(done)):
                        go(c, "q_nrm")
                        act.activation(B[c]["small"][:, 2, :], B[c]["small"][:, 2, :], ACT.Exp, scale=0.5
                                       ).then_inc(done[c], 1)
                    query_blocks(act, go, done, B, ps, "q_dg", 1)
                    for c in range(len(done)):
                        go(c, "K_exp")
                        act.activation(B[c]["P"][:, :, :].rearrange("p h m -> p (h m)"),
                                       ps[c][0:T, 0, 0:H * NTOK], ACT.Exp, bias=m10[0:T, :], scale=10.0
                                       ).then_inc(done[c], 1)
                    with act.Fori(0, ITERS) as r:
                        def at(c, k):
                            act.wait_ge(done[c], i * N + r * SINK + (S["it"] + 1 + k))
                        for c in range(len(done)):
                            at(c, 5)
                            act.activation(B[c]["vb"][:, :, :].rearrange("p h m -> p (h m)"),
                                           ps[c][0:T, 1, 0:H * NTOK], ACT.Ln).then_inc(done[c], 1)
                        for c in range(len(done)):
                            at(c, 6)
                            act.activation(B[c]["vb"][:, :, :], B[c]["vb"][:, :, :], ACT.Exp, scale=-1.0
                                           ).then_inc(done[c], 1)
                    for c in range(len(done)):
                        go(c, "sm_exp")
                        act.activation(B[c]["P"][:, :, :], B[c]["P"][:, :, :], ACT.Exp,
                                       bias=K["quarter"][0:T, :], scale=D ** -0.5).then_inc(done[c], 1)
                    probs_copy(act.copy, go, done, B, ps, "pc0", 0, 0)
                    probs_copy(act.copy, go, done, B, ps, "pc2", 0, 8)
                    turn_scalar(act, go, done, "fo", ps, 1, oT)
                    norm_scalar(act, go, done, B, "n1", eps5[0:T, :])
                    turn_scalar(act, go, done, "f1", ps, 0, xT)
                    for c in range(len(done)):
                        go(c, "g_exp")
                        act.activation(B[c]["lg"][:, :], B[c]["lg"][:, :], ACT.Exp).then_inc(done[c], 1)
                    weights_out(act, "scalar", go, done, B, ps, combT, ident, tile_of, E + 1)

                with act.Fori(0, NT // WAYS) as i:
                    turn(i, done)
                turn(NT // WAYS, done[:NT % WAYS])

            @block.gpsimd
            def _(pool):
                def turn(i, done):
                    def go(c, step):
                        pool.wait_ge(done[c], i * N + (S[step] + 1))

                    def tile_of(c):
                        return WAYS * i + c
                    heads_expand(pool, go, done, B, "kx1", 1, HG, K["hmask16"])
                    with pool.Fori(0, ITERS) as r:
                        for c in range(len(done)):
                            pool.wait_ge(done[c], i * N + r * SINK + (S["it"] + 1 + 3))
                            pool.tensor_tensor(B[c]["kv"][:, :, :], B[c]["P"][:, :, :],
                                               over(B[c]["small"][:, 6, :].unsqueeze(2), [T, H, NTOK]), ALU.mult
                                               ).then_inc(done[c], 1)
                    blocks_expand(pool, go, done, B, "px1", 8, H, K["bmask"])
                    store_tile(pool, go, done, B, h_all, xT_all, tile_of, "hcur")
                    store_xT(pool, go, done, B, xT_all, tile_of)

                with pool.Fori(0, NT // WAYS) as i:
                    turn(i, done)
                turn(NT // WAYS, done[:NT % WAYS])

            @block.tensor
            def _(pe):
                def turn(i, done):
                    def go(c, step):
                        pe.wait_ge(done[c], i * N + (S[step] + 1))

                    def tile_of(c):
                        return WAYS * i + c
                    for c in range(len(done)):
                        pe.wait_ge(patch_loaded[c], 16 * i + 16)
                        go(c, "embed")
                        for k in range(6):
                            mm = pe.matmul(ps[c][0:T, 0, 0:C], B[c]["patch"][:, k, :], K["tok_w"][:, k, :],
                                           start=(k == 0), stop=(k == 5))
                        mm.then_inc(done[c], 1)
                    turn_tensor(pe, go, done, "f0", X, ps, 1, ident)
                    width_product(pe, go, done, "qv", ps, 0, xT, K["l0_wqv"], 2 * C)
                    turn_tensor_named(pe, go, done, "q_tr", flat, ps, 1, ident)
                    scores_tensor(pe, go, done, B, ps, HG)
                    with pe.Fori(0, ITERS) as r:
                        for c in range(len(done)):
                            pe.wait_ge(done[c], i * N + r * SINK + (S["it"] + 1 + 4))
                            pe.matmul(ps[c][0:T, 1, 0:H * NTOK], K["bmask"][:, :],
                                      B[c]["kv"][:, :, :].rearrange("p h m -> p (h m)"), start=True, stop=True
                                      ).then_inc(done[c], 1)
                    for c in range(len(done)):
                        go(c, "rm_tr")
                        pe.transpose(ps[c][0:H, 0, 0:T], B[c]["small"][:, 0, :], ident[0:T, 0:T]).then_inc(done[c], 1)
                    for c in range(len(done)):
                        go(c, "ix_mm")
                        pe.matmul(ps[c][0:T, 1, 0:H], B[c]["MX"][:, :, :].rearrange("p j n -> p (j n)"),
                                  ident[0:H, 0:H], start=True, stop=True).then_inc(done[c], 1)
                    values_stage(pe, go, done, B, ps, H, D, [b["V"] for b in B], H, ident)
                    turn_tensor(pe, go, done, "fo", [b["o"][:, :] for b in B], ps, 1, ident)
                    width_product(pe, go, done, "proj", ps, 0, oT, K["l0_wproj"], C)
                    turn_tensor(pe, go, done, "f1", X, ps, 0, ident)
                    width_product(pe, go, done, "gt", ps, 1, xT, K["l0_gate_w"], E)
                    weights_out(pe, "tensor", go, done, B, ps, combT, ident, tile_of, E + 1)

                with pe.Fori(0, NT // WAYS) as i:
                    turn(i, done)
                turn(NT // WAYS, done[:NT % WAYS])


def turn_tensor_named(pe, go, done, step, src, ps, bank, ident):
    for c in range(len(done)):
        go(c, step)
        for o in range(2):
            mm = pe.transpose(ps[c][0:CK, bank, o * T:(o + 1) * T], src[c][:, o * CK:(o + 1) * CK],
                              ident[0:T, 0:T])
        mm.then_inc(done[c], 1)


def rounded(ap):
    return ap.bitcast(F32R)


def split_product(pe, out_, w, x, start, stop):
    (wh, wl), (xh, xl) = w, x
    pe.matmul(out_, rounded(wh), rounded(xh), start=start, stop=False)
    pe.matmul(out_, rounded(wh), rounded(xl), start=False, stop=False)
    return pe.matmul(out_, rounded(wl), rounded(xh), start=False, stop=stop)


class ExpertPhase:

    def __init__(self, ctx, layer, E, w1_cols, w2_rows, w2_tiles, ahead, nc, d, xT_all, yT_all, combT, sem, sb, ident):
        nm = f"l{layer}e_"
        self.E, self.ahead, self.ident, self.yT_all = E, ahead, ident, yT_all
        self.w1_d, self.w2_d = d[f"l{layer}_w1"], d[f"l{layer}_w2"]
        self.raw_loaded = sem(nm + "raw_loaded")
        self.high_ready = sem(nm + "high_ready")
        self.weights_ready = sem(nm + "weights_ready")
        self.ahead_loaded = sem(nm + "ahead_loaded")
        self.cleared = sem(nm + "cleared")
        self.x_high = sem(nm + "x_high")
        self.x_split = sem(nm + "x_split")
        self.out_done = sem(nm + "out_done")
        self.passed = sem(nm + "passed")
        self.raw1 = sb(ctx, nm + "raw1", [CK, 2, w1_cols])
        self.raw2 = sb(ctx, nm + "raw2", [w2_rows, w2_tiles, C])
        self.w1 = [[sb(ctx, nm + f"w1_{s}{part}", [CK, 2, w1_cols]) for part in ("high", "low")] for s in (0, 1)]
        self.w2 = [[sb(ctx, nm + f"w2_{s}{part}", [w2_rows, w2_tiles, C]) for part in ("high", "low")] for s in (0, 1)]
        self.select = [sb(ctx, nm + f"select{s}", [E, CK]) for s in (0, 1)]
        self.xT_all, self.combT = xT_all, combT
        self.x = [sb(ctx, nm + f"x_{part}_part", [CK, 2, NP]) for part in ("high", "low")]

    def fetch(self, sp, e):
        sp.dma_start(self.raw1[:, :, :].rearrange("p k m -> p (k m)"),
                     self.w1_d[e, :, :].rearrange("a p x -> (a p) x")).then_inc(self.raw_loaded, 16)
        sp.dma_start(self.raw2[:, :, :].rearrange("p k m -> p (k m)"),
                     self.w2_d[e, :, :].rearrange("a p x -> (a p) x")).then_inc(self.raw_loaded, 16)

    def sync_program(self, sp):
        self.fetch(sp, slice(0, 1))
        start_loads(sp, self.ahead, self.ahead_loaded)
        with sp.Fori(1, self.E) as e:
            sp.wait_ge(self.weights_ready, e)
            self.fetch(sp, bass.ds(e, 1))
        if self.ahead:
            sp.wait_ge(self.ahead_loaded, 16 * len(self.ahead))

    def split_weights(self, pool, s, e, n):
        pool.wait_ge(self.raw_loaded, 32 * n + 32)
        pool.sem_inc(self.passed, 1)
        pool.tensor_copy(rounded(self.w1[s][0][:, :, :]), self.raw1[:, :, :])
        pool.tensor_copy(rounded(self.w2[s][0][:, :, :]), self.raw2[:, :, :]).then_inc(self.high_ready, 1)
        pool.tensor_copy(self.select[s][:, :], over(self.ident[0:self.E, e], [self.E, CK]))
        pool.wait_ge(self.high_ready, n + 1)
        pool.tensor_tensor(rounded(self.w1[s][1][:, :, :]), self.raw1[:, :, :], self.w1[s][0][:, :, :], ALU.subtract)
        pool.tensor_tensor(rounded(self.w2[s][1][:, :, :]), self.raw2[:, :, :], self.w2[s][0][:, :, :], ALU.subtract
                           ).then_inc(self.weights_ready, 1)

    def pool_program(self, pool):
        for s in (0, 1):
            self.split_weights(pool, s, slice(s, s + 1), s)
            if s == 0:
                pool.memset(self.yT_all[:, :, :], 0.0).then_inc(self.cleared, 1)
        with pool.Fori(1, self.E // 2) as q:
            for s in (0, 1):
                pool.wait_ge(self.out_done, 2 * NB * q + (NB * s - NB + 1))
                self.split_weights(pool, s, bass.ds(2 * q + s, 1), 2 * q + s)
        if self.E % 2:
            pool.wait_ge(self.out_done, NB * (self.E - 2) + 1)
            self.split_weights(pool, 0, slice(self.E - 1, self.E), self.E - 1)

    def high_tokens(self, act):
        for b in range(NB):
            cols = slice(b * UB, (b + 1) * UB)
            act.copy(rounded(self.x[0][:, :, cols]), self.xT_all[:, :, cols]).then_inc(self.x_high, 1)

    def low_tokens(self, dve):
        for b in range(NB):
            cols = slice(b * UB, (b + 1) * UB)
            dve.wait_ge(self.x_high, b + 1)
            dve.tensor_tensor(rounded(self.x[1][:, :, cols]), self.xT_all[:, :, cols], self.x[0][:, :, cols],
                              ALU.subtract).then_inc(self.x_split, 1)

    def spread_products(self, pe, s, out_, cols):
        return pe.matmul(out_, self.select[s][:, :], self.combT[0:self.E, cols], start=True, stop=True)

    def w1_parts(self, s, k, lo, hi):
        return [w[:, k, lo:hi] for w in self.w1[s]]

    def w2_parts(self, s, m, o):
        return [w[:, m, o * CK:(o + 1) * CK] for w in self.w2[s]]

    def x_parts(self, k, cols):
        return [x[:, k, cols] for x in self.x]


def experts_gelu(layer, func, ahead, nc, d, K, xT_all, yT_all, combT, sem, sb, ident, **_):
    E, M = 8, 6
    nm = f"l{layer}e_"
    spread_done = sem(nm + "spread_done")
    spread_copied = sem(nm + "spread_copied")
    hidden_done = sem(nm + "hidden_done")
    hidden_read = sem(nm + "hidden_read")
    hidden_high = sem(nm + "hidden_high")
    hidden_split = sem(nm + "hidden_split")
    out_read = sem(nm + "out_read")
    summed = sem(nm + "summed")
    with ExitStack() as ctx:
        phase = ExpertPhase(ctx, layer, E, 128 * M, 128, M, ahead, nc, d, xT_all, yT_all, combT, sem, sb, ident)
        out_done = phase.out_done
        hidden = sb(ctx, nm + "hidden", [128, 2, UB])
        act_out = [sb(ctx, nm + f"act_out_{part}", [128, M, UB]) for part in ("high", "low")]
        spread = sb(ctx, nm + "spread", [CK, UB])
        part = sb(ctx, nm + "part", [CK, 2, UB])
        psH = ctx.enter_context(nc.psum_tensor(nm + "psH", [128, 3, 512], F32))
        psY = ctx.enter_context(nc.psum_tensor(nm + "psY", [128, 2, 512], F32))
        psS = ctx.enter_context(nc.psum_tensor(nm + "psS", [128, 512], F32))
        with nc.Block() as block:
            @block.sync
            def _(sp):
                phase.sync_program(sp)

            @block.gpsimd
            def _(pool):
                phase.pool_program(pool)

            @block.tensor
            def _(pe):
                pe.sem_inc(out_done, 1)
                pe.wait_ge(phase.x_split, NB)
                with pe.Fori(0, E // 2) as q:
                    for s in (0, 1):
                        pe.wait_ge(phase.weights_ready, 2 * q + (s + 1))
                        pe.sem_inc(phase.passed, 1)
                        with pe.Fori(0, NB) as b:
                            n = 2 * NB * q + b + s * NB
                            cols = bass.ds(b * UB, UB)
                            pe.wait_ge(spread_copied, n + 1)
                            phase.spread_products(pe, s, psS[0:CK, 0:UB], cols).then_inc(spread_done, 1)
                            for m in range(M):
                                pe.wait_ge(hidden_read, M * n + (m + 1))
                                for k in range(2):
                                    mm = split_product(pe, psH[:, m % 3, 0:UB],
                                                       phase.w1_parts(s, k, m * 128, (m + 1) * 128),
                                                       phase.x_parts(k, cols), start=(k == 0), stop=(k == 1))
                                mm.then_inc(hidden_done, 1)
                            pe.wait_ge(out_read, n + 1)
                            for m in range(M):
                                pe.wait_ge(hidden_split, M * n + (m + 3))
                                for o in range(2):
                                    mm = split_product(pe, psY[0:CK, o, 0:UB], phase.w2_parts(s, m, o),
                                                       [a[:, m, :] for a in act_out],
                                                       start=(m == 0), stop=(m == M - 1))
                            mm.then_inc(out_done, 1)

            @block.scalar
            def _(act):
                phase.high_tokens(act)
                act.sem_inc(hidden_read, 3)
                act.sem_inc(spread_copied, 1)
                with act.Fori(0, E) as e:
                    with act.Fori(0, NB) as b:
                        n = NB * e + b
                        act.wait_ge(spread_done, n + 1)
                        act.wait_ge(out_read, n + 1)
                        act.copy(spread[:, :], psS[0:CK, 0:UB]).then_inc(spread_copied, 1)
                        for m in range(M):
                            act.wait_ge(hidden_done, M * n + (m + 1))
                            act.wait_ge(hidden_split, M * n + (m + 1))
                            act.activation(hidden[:, m % 2, :], psH[:, m % 3, 0:UB], func).then_inc(hidden_read, 1)

            @block.vector
            def _(dve):
                phase.low_tokens(dve)
                dve.sem_inc(hidden_split, 2)
                dve.sem_inc(out_read, 1)
                dve.sem_inc(summed, 1)
                dve.wait_ge(phase.cleared, 1)
                with dve.Fori(0, E) as e:
                    with dve.Fori(0, NB) as b:
                        n = NB * e + b
                        y = yT_all[:, :, bass.ds(b * UB, UB)]
                        dve.wait_ge(out_done, n + 1)
                        for m in range(M):
                            dve.wait_ge(hidden_read, M * n + (m + 4))
                            dve.tensor_copy(rounded(act_out[0][:, m, :]), hidden[:, m % 2, :]).then_inc(hidden_high, 1)
                            dve.wait_ge(hidden_high, M * n + (m + 1))
                            dve.tensor_tensor(rounded(act_out[1][:, m, :]), hidden[:, m % 2, :], act_out[0][:, m, :],
                                              ALU.subtract).then_inc(hidden_split, 1)
                        dve.wait_ge(out_done, n + 2)
                        dve.wait_ge(spread_copied, n + 2)
                        dve.wait_ge(summed, n + 1)
                        dve.tensor_tensor(part[:, :, :], psY[0:CK, :, 0:UB],
                                          over(spread[:, :].unsqueeze(1), [CK, 2, UB]), ALU.mult).then_inc(out_read, 1)
                        dve.wait_ge(out_read, n + 2)
                        dve.tensor_tensor(y, y, part[:, :, :], ALU.add).then_inc(summed, 1)
                dve.wait_ge(summed, E * NB + 1)


def experts_swiglu(layer, E, ahead, nc, d, K, xT_all, yT_all, combT, sem, sb, ident, **_):
    gated = layer == 0
    A = 1 if gated else 2
    HB = 4
    b_d = d[f"l{layer}_b"]
    nm = f"l{layer}e_"
    spread_done = sem(nm + "spread_done")
    spread_copied = sem(nm + "spread_copied")
    hidden_done = sem(nm + "hidden_done")
    third_done = sem(nm + "third_done")
    third_ready = sem(nm + "third_ready")
    hidden_read = sem(nm + "hidden_read")
    gate_ready = sem(nm + "gate_ready")
    silu_ready = sem(nm + "silu_ready")
    lin_ready = sem(nm + "lin_ready")
    glu_ready = sem(nm + "glu_ready")
    glu_high = sem(nm + "glu_high")
    glu_split = sem(nm + "glu_split")
    out_read = sem(nm + "out_read")
    summed = sem(nm + "summed")
    W1N = 384
    NBIAS = 6
    with ExitStack() as ctx:
        phase = ExpertPhase(ctx, layer, E, W1N, CK, A, ahead, nc, d, xT_all, yT_all, combT, sem, sb, ident)
        out_done = phase.out_done
        bias = sb(ctx, nm + "bias", [CK, E, NBIAS])
        bcur = [sb(ctx, nm + f"bcur{k}", [CK, NBIAS]) for k in range(4)]
        gate = sb(ctx, nm + "gate", [CK, A, UB])
        lin = sb(ctx, nm + "lin", [CK, A, UB])
        third = sb(ctx, nm + "third", [CK, 2, UB])
        prod = sb(ctx, nm + "prod", [CK, 2, UB])
        silu = sb(ctx, nm + "silu", [CK, A, UB])
        glu = sb(ctx, nm + "glu", [CK, A, UB])
        glu_parts = [sb(ctx, nm + f"glu_{part}", [CK, A, UB]) for part in ("high", "low")]
        spread = sb(ctx, nm + "spread", [CK, UB])
        part = sb(ctx, nm + "part", [CK, 2, UB])
        psH = ctx.enter_context(nc.psum_tensor(nm + "psH", [128, HB, 512], F32))
        psY = ctx.enter_context(nc.psum_tensor(nm + "psY", [128, 2, 512], F32))
        psS = ctx.enter_context(nc.psum_tensor(nm + "psS", [128, 512], F32))
        bias_loaded = sem(nm + "bias_loaded")
        bias_cur = [sem(nm + f"bias_cur{k}") for k in range(2)]
        pairs, tail = E // 2, E % 2
        full_pairs = pairs if tail else pairs - 1
        slots = [0] if tail else [0, 1]
        first = 2 * full_pairs
        with nc.Block() as block:
            @block.sync
            def _(sp):
                sp.dma_start(bias[:, :, :], b_d[:, :, :]).then_inc(bias_loaded, 16)
                phase.sync_program(sp)

            @block.gpsimd
            def _(pool):
                phase.pool_program(pool)

            def first_products(pe, n, s, cols):
                if gated:
                    pe.wait_ge(third_ready, n + 1)
                    for col in (2, 3):
                        for k in range(2):
                            mm = split_product(pe, psH[0:CK, col, 0:UB], phase.w1_parts(s, k, col * CK, (col + 1) * CK),
                                               phase.x_parts(k, cols), start=(k == 0), stop=(k == 1))
                    mm.then_inc(third_done, 1)
                for a in range(A):
                    pe.wait_ge(hidden_read, A * n + (a + 1))
                    for col in (a, A + a):
                        for k in range(2):
                            mm = split_product(pe, psH[0:CK, col, 0:UB], phase.w1_parts(s, k, col * CK, (col + 1) * CK),
                                               phase.x_parts(k, cols), start=(k == 0), stop=(k == 1))
                    mm.then_inc(hidden_done, 1)

            def second_products(pe, n, s, cols):
                pe.wait_ge(spread_copied, n + 1)
                phase.spread_products(pe, s, psS[0:CK, 0:UB], cols).then_inc(spread_done, 1)
                pe.wait_ge(out_read, n + 1)
                for a in range(A):
                    pe.wait_ge(glu_split, A * n + (a + 1 + A))
                    for o in range(2):
                        mm = split_product(pe, psY[0:CK, o, 0:UB], phase.w2_parts(s, a, o),
                                           [g[:, a, :] for g in glu_parts], start=(a == 0), stop=(a == A - 1))
                mm.then_inc(out_done, 1)

            def expert_products(pe, e, s, last):
                with pe.Fori(0, NB - 1) as b:
                    first_products(pe, NB * e + b + 1, s, bass.ds(b * UB + UB, UB))
                    second_products(pe, NB * e + b, s, bass.ds(b * UB, UB))
                if not last:
                    pe.wait_ge(phase.weights_ready, e + 2)
                    pe.sem_inc(phase.passed, 1)
                    first_products(pe, NB * e + NB, 1 - s, slice(0, UB))
                second_products(pe, NB * e + (NB - 1), s, slice((NB - 1) * UB, NB * UB))

            @block.tensor
            def _(pe):
                pe.sem_inc(out_done, 1)
                pe.wait_ge(phase.x_split, NB)
                pe.wait_ge(phase.weights_ready, 1)
                first_products(pe, 0, 0, slice(0, UB))
                with pe.Fori(0, full_pairs) as q:
                    for s in (0, 1):
                        expert_products(pe, 2 * q + s, s, last=False)
                for s in slots:
                    expert_products(pe, first + s, s, last=(s == slots[-1]))

            def scalar_first(act, n, s):
                if gated:
                    act.wait_ge(third_done, n + 1)
                    act.wait_ge(hidden_read, n + 1)
                    for col in range(2):
                        ins = act.activation(third[:, col, :], psH[0:CK, 2 + col, 0:UB], ACT.Identity,
                                             bias=bcur[2 + s][:, 2 + col:3 + col])
                    ins.then_inc(third_ready, 1)

            def scalar_second(act, n):
                for a in range(A):
                    act.wait_ge(gate_ready, A * n + (a + 1))
                    act.wait_ge(glu_ready, A * n + (a + 1))
                    act.activation(silu[:, a, :], gate[:, a, :], ACT.Silu, scale=ALPHA).then_inc(silu_ready, 1)
                for a in range(A):
                    act.wait_ge(glu_ready, A * n + (a + 1 + A))
                    act.wait_ge(out_done, n + 1)
                    act.copy(rounded(glu_parts[0][:, a, :]), glu[:, a, :]).then_inc(glu_high, 1)

            def scalar_spread(act, n):
                act.wait_ge(spread_done, n + 1)
                act.wait_ge(out_read, n + 1)
                act.copy(spread[:, :], psS[0:CK, 0:UB]).then_inc(spread_copied, 1)

            def scalar_bias(act, e, s):
                if gated:
                    act.wait_ge(third_ready, NB * e + 1)
                    act.copy(bcur[2 + s][:, :], bias[:, bass.ds(e, 1), :].rearrange("p a x -> p (a x)")
                             ).then_inc(bias_cur[1], 1)
                    act.wait_ge(bias_cur[1], e + 1)

            @block.scalar
            def _(act):
                phase.high_tokens(act)
                act.sem_inc(spread_copied, 1)
                if gated:
                    act.sem_inc(third_ready, 1)
                act.wait_ge(bias_loaded, 16)
                scalar_bias(act, 0, 0)
                scalar_first(act, 0, 0)
                scalar_second(act, 0)

                def expert(e, s, last):
                    with act.Fori(0, NB - 1) as b:
                        scalar_first(act, NB * e + b + 1, s)
                        scalar_spread(act, NB * e + b)
                        scalar_second(act, NB * e + b + 1)
                    if not last:
                        scalar_bias(act, e + 1, 1 - s)
                        scalar_first(act, NB * e + NB, 1 - s)
                    scalar_spread(act, NB * e + (NB - 1))
                    if not last:
                        scalar_second(act, NB * e + NB)

                with act.Fori(0, full_pairs) as q:
                    for s in (0, 1):
                        expert(2 * q + s, s, last=False)
                for s in slots:
                    expert(first + s, s, last=(s == slots[-1]))

            def vector_first(dve, n, s, first_block=False):
                if gated:
                    dve.wait_ge(hidden_done, n + 1)
                    dve.wait_ge(third_ready, n + 2)
                    if not first_block:
                        dve.wait_ge(gate_ready, n)
                    for col in range(2):
                        ins = dve.scalar_tensor_tensor(prod[:, col, :], psH[0:CK, col, 0:UB], bcur[s][:, col:col + 1],
                                                       third[:, col, :], ALU.add, ALU.mult)
                    ins.then_inc(hidden_read, 1)
                    dve.wait_ge(hidden_read, n + 2)
                    dve.wait_ge(glu_ready, n + 1)
                    dve.tensor_scalar(lin[:, 0, :], prod[:, 1, :], LIMIT, None, ALU.min)
                    dve.tensor_scalar(gate[:, 0, :], prod[:, 0, :], LIMIT, None, ALU.min).then_inc(gate_ready, 1)
                    return
                for a in range(A):
                    dve.wait_ge(hidden_done, A * n + (a + 1))
                    dve.wait_ge(glu_ready, A * n + (a + 1))
                    dve.tensor_scalar(lin[:, a, :], psH[0:CK, A + a, 0:UB], bcur[s][:, A + a:A + a + 1],
                                      LIMIT, ALU.add, ALU.min)
                    dve.tensor_scalar(gate[:, a, :], psH[0:CK, a, 0:UB], bcur[s][:, a:a + 1], LIMIT, ALU.add, ALU.min
                                      ).then_inc(hidden_read, 1)
                    dve.wait_ge(hidden_read, A * n + (a + 1 + A))
                    dve.sem_inc(gate_ready, 1)

            def vector_second(dve, n):
                for a in range(A):
                    dve.wait_ge(gate_ready, A * n + (a + 1))
                    dve.tensor_scalar(lin[:, a, :], lin[:, a, :], -LIMIT, 1.0, ALU.max, ALU.add).then_inc(lin_ready, 1)
                for a in range(A):
                    dve.wait_ge(lin_ready, A * n + (a + 1))
                    dve.wait_ge(silu_ready, A * n + (a + 1))
                    dve.wait_ge(glu_split, A * n + (a + 1))
                    dve.scalar_tensor_tensor(glu[:, a, :], silu[:, a, :], 1.0 / ALPHA, lin[:, a, :], ALU.mult, ALU.mult
                                             ).then_inc(glu_ready, 1)
                for a in range(A):
                    dve.wait_ge(glu_high, A * n + (a + 1))
                    dve.tensor_tensor(rounded(glu_parts[1][:, a, :]), glu[:, a, :], glu_parts[0][:, a, :],
                                      ALU.subtract).then_inc(glu_split, 1)

            def vector_sum(dve, n, s, cols):
                y = yT_all[:, :, cols]
                dve.wait_ge(out_done, n + 2)
                dve.wait_ge(spread_copied, n + 2)
                dve.wait_ge(summed, n + 1)
                for o in range(2):
                    ins = dve.scalar_tensor_tensor(part[:, o, :], psY[0:CK, o, 0:UB], bcur[s][:, 4 + o:5 + o],
                                                   spread[:, :], ALU.add, ALU.mult)
                ins.then_inc(out_read, 1)
                dve.wait_ge(out_read, n + 2)
                dve.tensor_tensor(y, y, part[:, :, :], ALU.add).then_inc(summed, 1)

            def vector_bias(dve, e, s, first_expert=False):
                if not first_expert:
                    dve.wait_ge(summed, NB * e - (NB - 1))
                dve.tensor_copy(bcur[s][:, :], bias[:, bass.ds(e, 1), :].rearrange("p a x -> p (a x)")
                                ).then_inc(bias_cur[0], 1)
                dve.wait_ge(bias_cur[0], e + 1)
                dve.sem_inc(phase.passed, 1)

            @block.vector
            def _(dve):
                phase.low_tokens(dve)
                dve.sem_inc(hidden_read, A)
                dve.sem_inc(glu_ready, A)
                dve.sem_inc(glu_split, A)
                for started in (out_read, summed):
                    dve.sem_inc(started, 1)
                dve.wait_ge(phase.cleared, 1)
                dve.wait_ge(bias_loaded, 16)
                vector_bias(dve, 0, 0, first_expert=True)
                vector_first(dve, 0, 0, first_block=True)
                vector_second(dve, 0)

                def expert(e, s, last):
                    with dve.Fori(0, NB - 1) as b:
                        vector_first(dve, NB * e + b + 1, s)
                        vector_second(dve, NB * e + b + 1)
                        vector_sum(dve, NB * e + b, s, bass.ds(b * UB, UB))
                    if not last:
                        vector_bias(dve, e + 1, 1 - s)
                        vector_first(dve, NB * e + NB, 1 - s)
                        vector_second(dve, NB * e + NB)
                    vector_sum(dve, NB * e + (NB - 1), s, slice((NB - 1) * UB, NB * UB))

                with dve.Fori(0, full_pairs) as q:
                    for s in (0, 1):
                        expert(2 * q + s, s, last=False)
                for s in slots:
                    expert(first + s, s, last=(s == slots[-1]))
                dve.wait_ge(summed, E * NB + 1)


def capacity_limit(nc, xT_all, yT_all, combT, maskT, sem, sb, **_):
    scanned, kept, cleared = sem("cap_scanned"), sem("cap_kept"), sem("cap_cleared")
    with ExitStack() as ctx:
        count = sb(ctx, "cap_count", [8, NP])
        ones = sb(ctx, "cap_ones", [8, NP])
        with nc.Block() as block:
            @block.vector
            def _(dve):
                dve.memset(ones[:, :], 1.0).then_inc(scanned, 1)
                dve.wait_ge(scanned, 1)
                dve.tensor_tensor_scan(count[:, :], ones[:, :], maskT[:, :], 0.0, ALU.mult, ALU.add
                                       ).then_inc(scanned, 1)
                dve.wait_ge(scanned, 2)
                dve.scalar_tensor_tensor(combT[0:8, :], count[:, :], CAP + 0.5, combT[0:8, :], ALU.is_lt, ALU.mult
                                         ).then_inc(kept, 1)
                dve.wait_ge(kept, 1)


def per_head(ap, D):
    return ap.rearrange("p (h d) -> p h d", d=D)


def normed_output(dve, go, done, B, ps, H, D):
    for c in range(len(done)):
        go(c, "o")
        dve.tensor_tensor(per_head(B[c]["o"][:, :], D), per_head(ps[c][0:T, 0, 0:C], D),
                          over(B[c]["hinv"][:, 0:H].unsqueeze(2), [T, H, D]), ALU.mult).then_inc(done[c], 1)


def add2(dve, go, done, step, out_, a, b):
    for c in range(len(done)):
        go(c, step)
        dve.tensor_tensor(out_[c], a[c], b[c], ALU.add).then_inc(done[c], 1)


def router_vector(dve, go, done, B, ps, E, k, gate_b):
    for c in range(len(done)):
        go(c, "g_cp")
        if gate_b is None:
            dve.tensor_copy(B[c]["sv"][:, 0:E], ps[c][0:T, 1, 0:E]).then_inc(done[c], 1)
        else:
            dve.tensor_tensor(B[c]["sv"][:, 0:E], ps[c][0:T, 1, 0:E], gate_b[:, :], ALU.add).then_inc(done[c], 1)
    topk_vector(dve, go, done, B, "ge", "sv", "keys", k, E, [b["mask"][:, 0:E] for b in B])
    for c in range(len(done)):
        go(c, "g_sub")
        dve.tensor_scalar(B[c]["lg"][:, 0:E], B[c]["sv"][:, 0:E], B[c]["max8"][:, 0:1], None, ALU.subtract
                          ).then_inc(done[c], 1)
    for c in range(len(done)):
        go(c, "g_w")
        dve.tensor_tensor(B[c]["lg"][:, 0:E], B[c]["lg"][:, 0:E], B[c]["mask"][:, 0:E], ALU.mult).then_inc(done[c], 1)
    for c in range(len(done)):
        go(c, "g_sum")
        dve.tensor_reduce(B[c]["mv"][:, 0:1], B[c]["lg"][:, 0:E], AX.X, ALU.add).then_inc(done[c], 1)
    for c in range(len(done)):
        go(c, "g_rc")
        dve.reciprocal(B[c]["mv"][:, 1:2], B[c]["mv"][:, 0:1]).then_inc(done[c], 1)
    for c in range(len(done)):
        go(c, "g_n")
        dve.tensor_scalar(B[c]["comb"][:, 0:E], B[c]["lg"][:, 0:E], B[c]["mv"][:, 1:2], None, ALU.mult
                          ).then_inc(done[c], 1)


def router_scalar(act, go, done, B, E):
    for c in range(len(done)):
        go(c, "g_exp")
        act.activation(B[c]["lg"][:, 0:E], B[c]["lg"][:, 0:E], ACT.Exp).then_inc(done[c], 1)


ROUTER = "g_cp " + topk_steps("ge") + "g_sub g_exp g_w g_sum g_rc g_n c_tr "
ROUTER_SHAPES = dict(sv=[T, 24], keys=[T, 8], mask=[T, 16], lg=[T, 16], comb=[T, 16])


def layer1_tokens(nc, d, K, h_all, xT_all, yT_all, combT, maskT, eps5, ident, sem, sb, **_):
    H, E, HP, DA = 12, 8, 6, 64
    D, HG = 16, 6
    MAIN = "sm_scale sm_max sm_sub sm_exp sm_sum sm_inv " + SPREAD
    first = MAIN.replace("sm_", "a.sm_").replace("px", "a.px").replace("pt", "a.pt").replace("pc", "a.pc").replace(
        "av", "a.av")
    S = steps("y_cp w_zero|y_tr y_add " + ln_steps("n0") + ln_steps("n1") + turn_steps("f0") +
              "wide_q wq_cp wide_k wk_cp wide_v wv_cp a.S " + first + "a.o a.o_tr a.o_cp wide_out h1 h2 " +
              ln_steps("n2") + ln_steps("n3") + turn_steps("f3") + "qkT v q_dg|k_cp v_cp kx0|kx1 S " + MAIN + "o " +
              turn_steps("fo") + "proj x2 h3 h_st " + ln_steps("n4") + turn_steps("f4") + "x_st gt " + ROUTER +
              "c_st m_tr m_st")
    N = S["end"]
    done = [sem(f"l1_tile{c}_steps") for c in range(WAYS)]
    zeroed, passed = sem("l1_zeroed"), sem("l1_passed")
    with ExitStack() as ctx:
        shapes = attention_shapes(H, D)
        shapes.update(ROUTER_SHAPES)
        shapes.update(blocks=[128, 2 * H * T], wkT=[128, HP, T], V=[T, H * DA])
        del shapes["px"], shapes["pT"]
        B, ps = tile_buffers(ctx, nc, sb, 1, shapes)
        for b in B:
            b["px"] = b["blocks"][0:T, 0:H * T].rearrange("p (h n) -> p h n", n=T)
            b["pT"] = b["blocks"][:, H * T:2 * H * T].rearrange("p (h n) -> p h n", n=T)
            b["wqx"] = b["blocks"][:, :].rearrange("p (f x) -> p f x", f=HP)
            b["wV"] = b["wo"] = b["V"]
            b["woT"] = b["wkT"]
            b["passed"] = passed
        share(B, H)
        X = [b["x"][:, :] for b in B]
        HC = [b["hcur"][:, :] for b in B]
        xT = [b["xT"] for b in B]
        oT = [b["oT"] for b in B]
        O = [b["wo"][:, 0:C] for b in B]
        order = [2 * f + r for r in (0, 1) for f in range(HP)]
        wide_scores = [[p[0:T, o, 0:HP * NTOK].rearrange("p (h m) -> p h m", m=NTOK) for o in range(2)] for p in ps]
        scores = [[score_place(p, o, HG).rearrange("p (h m) -> p h m", m=NTOK) for o in range(2)] for p in ps]
        with nc.Block() as block:
            @block.vector
            def _(dve):
                for c in range(len(done)):
                    dve.memset(B[c]["qx"][:, :, :], 0.0)
                    dve.memset(B[c]["sv"][:, :], PAD)
                    ins = dve.memset(B[c]["keys"][:, :], PAD)
                ins.then_inc(zeroed, 1)
                dve.wait_ge(zeroed, 1)
                for c in range(len(done)):
                    dve.sem_inc(done[c], 1)
                def turn(i, done):
                    def go(c, step, passed=None):
                        dve.wait_ge(done[c], i * N + (S[step] + 1))
                        if passed is not None:
                            dve.sem_inc(passed, 1)

                    def ga(c, step, passed=None):
                        go(c, "a." + step, passed)

                    def tile_of(c):
                        return WAYS * i + c
                    take_experts_back(dve, "vector", go, done, B, ps, h_all, yT_all, ident, tile_of)
                    norm_vector(dve, go, done, B, "n0", HC, X)
                    norm_vector(dve, go, done, B, "n1", X, X)
                    for c in range(len(done)):
                        go(c, "wk_cp")
                        for f in range(HP):
                            ins = dve.tensor_scalar(B[c]["wkT"][:, f, :], ps[c][:, f // 4, (f % 4) * T:(f % 4 + 1) * T],
                                                    K["l1_bk"][:, f:f + 1], None, ALU.add)
                        ins.then_inc(done[c], 1)
                    for c in range(len(done)):
                        go(c, "wv_cp")
                        for b in range(2):
                            ins = dve.tensor_tensor(B[c]["wV"][:, b * 384:(b + 1) * 384], ps[c][0:T, b, 0:384],
                                                    K["l1_bv"][:, b * 384:(b + 1) * 384], ALU.add)
                        ins.then_inc(done[c], 1)
                    softmax_vector(dve, ga, done, B, wide_scores, DA ** -0.5, K["anti_causal"], H)
                    blocks_expand(dve, ga, done, B, "px0", 0, 8, K["bmask"])
                    probs_copy(dve.tensor_copy, ga, done, B, ps, "pc1", 1, 4)
                    for c in range(len(done)):
                        ga(c, "o")
                        for b, h0, h1 in ((0, 0, 8), (1, 8, 12)):
                            ins = dve.tensor_tensor(per_head(B[c]["wo"][:, h0 * DA:h1 * DA], DA),
                                                    per_head(ps[c][0:T, b, 0:(h1 - h0) * DA], DA),
                                                    over(B[c]["hinv"][:, h0:h1].unsqueeze(2), [T, h1 - h0, DA]),
                                                    ALU.mult)
                        ins.then_inc(done[c], 1)
                    add2(dve, go, done, "h1", HC, HC, [p[0:T, 0, 0:C] for p in ps])
                    add2(dve, go, done, "h2", HC, HC, [K["l1_bo"][:, :]] * WAYS)
                    norm_vector(dve, go, done, B, "n2", HC, X)
                    norm_vector(dve, go, done, B, "n3", X, O)
                    for c in range(len(done)):
                        go(c, "k_cp")
                        dve.tensor_copy(B[c]["kT"][:, :, :].rearrange("p o t -> p (o t)"), ps[c][0:CK, 1, 0:2 * T]
                                        ).then_inc(done[c], 1)
                    heads_expand(dve, go, done, B, "kx0", 0, HG, K["hmask16"])
                    softmax_vector(dve, go, done, B, scores, D ** -0.5, K["causal"], H)
                    blocks_expand(dve, go, done, B, "px0", 0, 8, K["bmask"])
                    probs_copy(dve.tensor_copy, go, done, B, ps, "pc1", 1, 4)
                    for c in range(len(done)):
                        go(c, "o")
                        dve.tensor_tensor(per_head(O[c], D), per_head(ps[c][0:T, 0, 0:C], D),
                                          over(B[c]["hinv"][:, 0:H].unsqueeze(2), [T, H, D]), ALU.mult
                                          ).then_inc(done[c], 1)
                    add2(dve, go, done, "x2", X, X, [p[0:T, 0, 0:C] for p in ps])
                    add2(dve, go, done, "h3", HC, HC, X)
                    norm_vector(dve, go, done, B, "n4", X, X)
                    router_vector(dve, go, done, B, ps, E, 2, None)

                with dve.Fori(0, NT // WAYS) as i:
                    turn(i, done)
                turn(NT // WAYS, done[:NT % WAYS])

            @block.scalar
            def _(act):
                act.preload_act_table_set(EXP_LN)
                act.wait_ge(zeroed, 1)
                def turn(i, done):
                    def go(c, step):
                        act.wait_ge(done[c], i * N + (S[step] + 1))

                    def ga(c, step):
                        go(c, "a." + step)

                    def tile_of(c):
                        return WAYS * i + c
                    norm_scalar(act, go, done, B, "n0", eps5[0:T, :])
                    norm_scalar(act, go, done, B, "n1", eps5[0:T, :])
                    turn_scalar(act, go, done, "f0", ps, 0, xT, K["l1_ln_w"], K["l1_ln_b"])
                    for c in range(len(done)):
                        go(c, "wq_cp")
                        for f in range(HP):
                            ins = act.activation(
                                B[c]["wqx"][:, f, :].rearrange("p (j x) -> p j x", x=DIAG)[:, :, 0:NTOK],
                                ps[c][:, f // 4, (f % 4) * T:(f % 4 + 1) * T].rearrange("p (j m) -> p j m", m=NTOK),
                                ACT.Identity, bias=K["l1_bq"][:, f:f + 1])
                        ins.then_inc(done[c], 1)
                    softmax_scalar(act, ga, done, B, H)
                    probs_copy(act.copy, ga, done, B, ps, "pc0", 0, 0)
                    probs_copy(act.copy, ga, done, B, ps, "pc2", 0, 8)
                    for c in range(len(done)):
                        ga(c, "o_cp")
                        act.copy(B[c]["woT"][:, 0:4, :].rearrange("p f t -> p (f t)"), ps[c][:, 0, 0:4 * T])
                        act.copy(B[c]["woT"][:, 4:6, :].rearrange("p f t -> p (f t)"), ps[c][:, 1, 0:2 * T]
                                 ).then_inc(done[c], 1)
                    norm_scalar(act, go, done, B, "n2", eps5[0:T, :])
                    norm_scalar(act, go, done, B, "n3", eps5[0:T, :])
                    turn_scalar(act, go, done, "f3", ps, 0, xT, K["l1_ln1_w"])
                    query_blocks(act, go, done, B, ps, "q_dg", 0)
                    for c in range(len(done)):
                        go(c, "v_cp")
                        act.copy(B[c]["wV"][:, 0:C], ps[c][0:T, 0, 256:256 + C]).then_inc(done[c], 1)
                    softmax_scalar(act, go, done, B, H)
                    probs_copy(act.copy, go, done, B, ps, "pc0", 0, 0)
                    probs_copy(act.copy, go, done, B, ps, "pc2", 0, 8)
                    turn_scalar(act, go, done, "fo", ps, 1, oT)
                    norm_scalar(act, go, done, B, "n4", eps5[0:T, :])
                    turn_scalar(act, go, done, "f4", ps, 0, xT, K["l1_ln2_w"])
                    router_scalar(act, go, done, B, E)
                    weights_out(act, "scalar", go, done, B, ps, combT, ident, tile_of, E)
                    for c in range(len(done)):
                        go(c, "m_st")
                        act.copy(maskT[:, bass.ds(tile_of(c) * T, T)], ps[c][0:E, 1, 0:T]).then_inc(done[c], 1)

                with act.Fori(0, NT // WAYS) as i:
                    turn(i, done)
                turn(NT // WAYS, done[:NT % WAYS])

            @block.gpsimd
            def _(pool):
                def turn(i, done):
                    def go(c, step):
                        pool.wait_ge(done[c], i * N + (S[step] + 1))

                    def ga(c, step):
                        go(c, "a." + step)

                    def tile_of(c):
                        return WAYS * i + c
                    take_experts_back(pool, "pool", go, done, B, ps, h_all, yT_all, ident, tile_of)
                    for c in range(len(done)):
                        go(c, "w_zero")
                        pool.sem_inc(passed, 1)
                        pool.memset(B[c]["blocks"][:, :], 0.0).then_inc(done[c], 1)
                    blocks_expand(pool, ga, done, B, "px1", 8, H, K["bmask"])
                    heads_expand(pool, go, done, B, "kx1", 1, HG, K["hmask16"])
                    blocks_expand(pool, go, done, B, "px1", 8, H, K["bmask"])
                    store_tile(pool, go, done, B, h_all, xT_all, tile_of, "hcur")
                    store_xT(pool, go, done, B, xT_all, tile_of)

                with pool.Fori(0, NT // WAYS) as i:
                    turn(i, done)
                turn(NT // WAYS, done[:NT % WAYS])

            @block.tensor
            def _(pe):
                def turn(i, done):
                    def go(c, step):
                        pe.wait_ge(done[c], i * N + (S[step] + 1))

                    def ga(c, step):
                        go(c, "a." + step)

                    def tile_of(c):
                        return WAYS * i + c
                    take_experts_back(pe, "tensor", go, done, B, ps, h_all, yT_all, ident, tile_of)
                    turn_tensor(pe, go, done, "f0", X, ps, 0, ident)
                    for step, w in (("wide_q", K["l1_wq"]), ("wide_k", K["l1_wk"])):
                        for c in range(len(done)):
                            go(c, step)
                            for f in range(HP):
                                for k in range(2):
                                    mm = pe.matmul(ps[c][:, f // 4, (f % 4) * T:(f % 4 + 1) * T],
                                                   w[:, k, f * 128:(f + 1) * 128], xT[c][:, k, :],
                                                   start=(k == 0), stop=(k == 1))
                            mm.then_inc(done[c], 1)
                    for c in range(len(done)):
                        go(c, "wide_v")
                        for b in range(2):
                            for k in range(2):
                                mm = pe.matmul(ps[c][0:T, b, 0:384], xT[c][:, k, :],
                                               K["l1_wv"][:, k, b * 384:(b + 1) * 384], start=(k == 0), stop=(k == 1))
                        mm.then_inc(done[c], 1)
                    for c in range(len(done)):
                        ga(c, "S")
                        for h in range(H):
                            r = slice((h % 2) * DA, (h % 2 + 1) * DA)
                            for j in range(IMGS):
                                mm = pe.matmul(ps[c][0:T, h % 2, (h // 2) * NTOK:(h // 2 + 1) * NTOK],
                                               B[c]["wqx"][r, h // 2, j * T:(j + 1) * T],
                                               B[c]["wkT"][r, h // 2, j * NTOK:(j + 1) * NTOK],
                                               start=(j == 0), stop=(j == IMGS - 1))
                        mm.then_inc(done[c], 1)
                    values_stage(pe, ga, done, B, ps, H, DA, [b["wV"] for b in B], 8, ident, order)
                    for c in range(len(done)):
                        ga(c, "o_tr")
                        for f in range(HP):
                            mm = pe.transpose(ps[c][:, f // 4, (f % 4) * T:(f % 4 + 1) * T],
                                              B[c]["wo"][:, f * 128:(f + 1) * 128], ident[0:T, 0:T])
                        mm.then_inc(done[c], 1)
                    for c in range(len(done)):
                        go(c, "wide_out")
                        for f in range(HP):
                            mm = pe.matmul(ps[c][0:T, 0, 0:C], B[c]["woT"][:, f, :], K["l1_wo"][:, f, :],
                                           start=(f == 0), stop=(f == HP - 1))
                        mm.then_inc(done[c], 1)
                    turn_tensor(pe, go, done, "f3", O, ps, 0, ident)
                    qk_tensor(pe, go, done, ps, xT, K["l1_wqk"])
                    width_product(pe, go, done, "v", ps, 0, xT, K["l1_wv2"], C, 256)
                    scores_tensor(pe, go, done, B, ps, HG)
                    values_stage(pe, go, done, B, ps, H, D, [b["wV"] for b in B], H, ident)
                    turn_tensor(pe, go, done, "fo", O, ps, 1, ident)
                    width_product(pe, go, done, "proj", ps, 0, oT, K["l1_wproj"], C)
                    turn_tensor(pe, go, done, "f4", X, ps, 0, ident)
                    width_product(pe, go, done, "gt", ps, 1, xT, K["l1_gate_w"], E)
                    weights_out(pe, "tensor", go, done, B, ps, combT, ident, tile_of, E)
                    for c in range(len(done)):
                        go(c, "m_tr")
                        pe.transpose(ps[c][0:E, 1, 0:T], B[c]["mask"][:, 0:E], ident[0:T, 0:T]).then_inc(done[c], 1)

                with pe.Fori(0, NT // WAYS) as i:
                    turn(i, done)
                turn(NT // WAYS, done[:NT % WAYS])


def qk_tensor(pe, go, done, ps, xT, w):
    for c in range(len(done)):
        go(c, "qkT")
        for o in range(4):
            for k in range(2):
                mm = pe.matmul(ps[c][0:CK, o // 2, (o % 2) * T:(o % 2 + 1) * T], w[:, k, o * CK:(o + 1) * CK],
                               xT[c][:, k, :], start=(k == 0), stop=(k == 1))
        mm.then_inc(done[c], 1)


def layer2_tokens(nc, d, K, h_all, xT_all, yT_all, combT, eps5, ident, sem, sb, **_):
    H, D, HG, E = 16, 12, 8, 16
    S = steps("y_cp y_tr y_add " + ln_steps("n0") + turn_steps("f0") + "qkT v q_dg|k_cp v_cp kx0|kx1 S " + SOFTMAX +
              "mix_f mix_a mix_b m_sum m_inv " + SPREAD16 + "o " + turn_steps("fo") + "proj h1 h2 " + ln_steps("n1") +
              "h3 h_st " + rms_steps("r1") + turn_steps("f1") + "x_st gt " + ROUTER + "c_st")
    N = S["end"]
    done = [sem(f"l2_tile{c}_steps") for c in range(WAYS)]
    zeroed, setup, passed = sem("l2_zeroed"), sem("l2_setup"), sem("l2_passed")
    with ExitStack() as ctx:
        shapes = attention_shapes(H, D)
        shapes.update(ROUTER_SHAPES)
        
        B, ps = tile_buffers(ctx, nc, sb, 2, shapes)
        share(B, H)
        for b in B:
            b["junk"] = b["o"][:, :]
        for b in B:
            b["passed"] = passed
        pos = sb(ctx, "l2_pos", [T, H, NTOK])
        tmp = sb(ctx, "l2_tmp", [T, H, NTOK])
        hs = sb(ctx, "l2_hs", [T, 4, H])
        X = [b["x"][:, :] for b in B]
        HC = [b["hcur"][:, :] for b in B]
        xT = [b["xT"] for b in B]
        oT = [b["oT"] for b in B]
        scores = [[score_place(p, o, HG).rearrange("p (h m) -> p h m", m=NTOK) for o in range(2)] for p in ps]
        shape = [T, H, NTOK]
        with nc.Block() as block:
            @block.vector
            def _(dve):
                for c in range(len(done)):
                    dve.memset(B[c]["qx"][:, :, :], 0.0)
                    dve.memset(B[c]["sv"][:, :], PAD)
                    ins = dve.memset(B[c]["keys"][:, :], PAD)
                ins.then_inc(zeroed, 1)
                dve.wait_ge(zeroed, 1)
                dve.tensor_tensor(pos[:, :, :], over(K["rel"][:, 0, :].unsqueeze(1), shape),
                                  over(K["l2_wpos"][:, 0, :].unsqueeze(2), shape), ALU.mult).then_inc(setup, 1)
                n = 1
                for q in (1, 2):
                    dve.wait_ge(setup, n)
                    dve.tensor_tensor(tmp[:, :, :], over(K["rel"][:, q, :].unsqueeze(1), shape),
                                      over(K["l2_wpos"][:, q, :].unsqueeze(2), shape), ALU.mult).then_inc(setup, 1)
                    dve.wait_ge(setup, n + 1)
                    dve.tensor_tensor(pos[:, :, :], pos[:, :, :], tmp[:, :, :], ALU.add).then_inc(setup, 1)
                    n += 2
                dve.wait_ge(setup, 5)
                dve.tensor_tensor(pos[:, :, :], pos[:, :, :], over(K["l2_bpos"][:, :].unsqueeze(2), shape), ALU.add
                                  ).then_inc(setup, 1)
                dve.wait_ge(setup, 6)
                dve.tensor_reduce(hs[:, 0, :], pos[:, :, :], AX.X, ALU.max).then_inc(setup, 1)
                dve.wait_ge(setup, 7)
                dve.tensor_tensor(pos[:, :, :], pos[:, :, :], over(hs[:, 0, :].unsqueeze(2), shape), ALU.subtract
                                  ).then_inc(setup, 1)
                dve.wait_ge(setup, 10)
                dve.tensor_reduce(hs[:, 1, :], pos[:, :, :], AX.X, ALU.add).then_inc(setup, 1)
                dve.wait_ge(setup, 11)
                dve.tensor_scalar(hs[:, 2, :], hs[:, 2, :], 1.0, None, ALU.add).then_inc(setup, 1)
                dve.wait_ge(setup, 12)
                dve.tensor_tensor(hs[:, 1, :], hs[:, 1, :], hs[:, 2, :], ALU.mult).then_inc(setup, 1)
                dve.wait_ge(setup, 13)
                dve.reciprocal(hs[:, 1, :], hs[:, 1, :]).then_inc(setup, 1)
                dve.wait_ge(setup, 14)
                dve.reciprocal(hs[:, 2, :], hs[:, 2, :]).then_inc(setup, 1)
                dve.wait_ge(setup, 15)
                dve.tensor_scalar(hs[:, 3, :], hs[:, 2, :], -1.0, 1.0, ALU.mult, ALU.add).then_inc(setup, 1)
                dve.wait_ge(setup, 16)
                dve.tensor_tensor(pos[:, :, :], pos[:, :, :], over(hs[:, 1, :].unsqueeze(2), shape), ALU.mult
                                  ).then_inc(setup, 1)
                dve.wait_ge(setup, 17)
                for c in range(len(done)):
                    dve.sem_inc(done[c], 1)
                def turn(i, done):
                    def go(c, step, passed=None):
                        dve.wait_ge(done[c], i * N + (S[step] + 1))
                        if passed is not None:
                            dve.sem_inc(passed, 1)

                    def tile_of(c):
                        return WAYS * i + c
                    take_experts_back(dve, "vector", go, done, B, ps, h_all, yT_all, ident, tile_of)
                    norm_vector(dve, go, done, B, "n0", HC, X)
                    for c in range(len(done)):
                        go(c, "k_cp")
                        dve.tensor_copy(B[c]["kT"][:, :, :].rearrange("p o t -> p (o t)"), ps[c][0:CK, 1, 0:2 * T]
                                        ).then_inc(done[c], 1)
                    heads_expand(dve, go, done, B, "kx0", 0, HG, K["hmask12"])
                    softmax_vector(dve, go, done, B, scores, D ** -0.5, None, H)
                    for c in range(len(done)):
                        go(c, "mix_f")
                        dve.tensor_tensor(B[c]["hmax"][:, 0:H], B[c]["hinv"][:, 0:H], hs[:, 3, :], ALU.mult
                                          ).then_inc(done[c], 1)
                    for c in range(len(done)):
                        go(c, "mix_a")
                        dve.tensor_tensor(B[c]["P"][:, :, :], B[c]["P"][:, :, :],
                                          over(B[c]["hmax"][:, 0:H].unsqueeze(2), shape), ALU.mult).then_inc(done[c], 1)
                    for c in range(len(done)):
                        go(c, "mix_b")
                        dve.tensor_tensor(B[c]["P"][:, :, :], B[c]["P"][:, :, :], pos[:, :, :], ALU.add
                                          ).then_inc(done[c], 1)
                    for c in range(len(done)):
                        go(c, "m_sum")
                        dve.tensor_reduce(B[c]["hsum"][:, 0:H], B[c]["P"][:, 0:H, :], AX.X, ALU.add
                                          ).then_inc(done[c], 1)
                    for c in range(len(done)):
                        go(c, "m_inv")
                        dve.reciprocal(B[c]["hinv"][:, 0:H], B[c]["hsum"][:, 0:H]).then_inc(done[c], 1)
                    blocks_expand(dve, go, done, B, "px0", 0, 11, K["bmask"])
                    probs_copy(dve.tensor_copy, go, done, B, ps, "pc1", 1, 4)
                    probs_copy(dve.tensor_copy, go, done, B, ps, "pc3", 1, 12)
                    normed_output(dve, go, done, B, ps, H, D)
                    add2(dve, go, done, "h1", HC, HC, [p[0:T, 0, 0:C] for p in ps])
                    add2(dve, go, done, "h2", HC, HC, [K["l2_bproj"][:, :]] * WAYS)
                    norm_vector(dve, go, done, B, "n1", HC, X)
                    add2(dve, go, done, "h3", HC, HC, X)
                    rms_vector(dve, go, done, B, "r1", X, X)
                    router_vector(dve, go, done, B, ps, E, 4, K["l2_gate_b"])

                with dve.Fori(0, NT // WAYS) as i:
                    turn(i, done)
                turn(NT // WAYS, done[:NT % WAYS])

            @block.scalar
            def _(act):
                act.preload_act_table_set(EXP_LN)
                act.wait_ge(setup, 8)
                act.activation(pos[:, :, :], pos[:, :, :], ACT.Exp).then_inc(setup, 1)
                act.activation(hs[:, 2, :], K["l2_gating"][:, :], ACT.Exp, scale=-1.0).then_inc(setup, 1)
                def turn(i, done):
                    def go(c, step):
                        act.wait_ge(done[c], i * N + (S[step] + 1))

                    def tile_of(c):
                        return WAYS * i + c
                    norm_scalar(act, go, done, B, "n0", eps5[0:T, :])
                    turn_scalar(act, go, done, "f0", ps, 0, xT)
                    query_blocks(act, go, done, B, ps, "q_dg", 0)
                    for c in range(len(done)):
                        go(c, "v_cp")
                        act.copy(B[c]["V"][:, :], ps[c][0:T, 0, 256:256 + C]).then_inc(done[c], 1)
                    softmax_scalar(act, go, done, B, H)
                    probs_copy(act.copy, go, done, B, ps, "pc0", 0, 0)
                    probs_copy(act.copy, go, done, B, ps, "pc2", 0, 8)
                    turn_scalar(act, go, done, "fo", ps, 1, oT)
                    norm_scalar(act, go, done, B, "n1", eps5[0:T, :])
                    rms_scalar(act, go, done, B, "r1", X, eps5[0:T, :])
                    turn_scalar(act, go, done, "f1", ps, 0, xT, K["l2_scale"])
                    router_scalar(act, go, done, B, E)
                    weights_out(act, "scalar", go, done, B, ps, combT, ident, tile_of, E)

                with act.Fori(0, NT // WAYS) as i:
                    turn(i, done)
                turn(NT // WAYS, done[:NT % WAYS])

            @block.gpsimd
            def _(pool):
                def turn(i, done):
                    def go(c, step):
                        pool.wait_ge(done[c], i * N + (S[step] + 1))

                    def tile_of(c):
                        return WAYS * i + c
                    take_experts_back(pool, "pool", go, done, B, ps, h_all, yT_all, ident, tile_of)
                    heads_expand(pool, go, done, B, "kx1", 1, HG, K["hmask12"])
                    blocks_expand(pool, go, done, B, "px1", 11, H, K["bmask"])
                    store_tile(pool, go, done, B, h_all, xT_all, tile_of, "hcur")
                    store_xT(pool, go, done, B, xT_all, tile_of)

                with pool.Fori(0, NT // WAYS) as i:
                    turn(i, done)
                turn(NT // WAYS, done[:NT % WAYS])

            @block.tensor
            def _(pe):
                def turn(i, done):
                    def go(c, step):
                        pe.wait_ge(done[c], i * N + (S[step] + 1))

                    def tile_of(c):
                        return WAYS * i + c
                    take_experts_back(pe, "tensor", go, done, B, ps, h_all, yT_all, ident, tile_of)
                    turn_tensor(pe, go, done, "f0", X, ps, 0, ident)
                    qk_tensor(pe, go, done, ps, xT, K["l2_wqk"])
                    width_product(pe, go, done, "v", ps, 0, xT, K["l2_wv"], C, 256)
                    scores_tensor(pe, go, done, B, ps, HG)
                    values_stage(pe, go, done, B, ps, H, D, [b["V"] for b in B], H, ident)
                    turn_tensor(pe, go, done, "fo", [b["o"][:, :] for b in B], ps, 1, ident)
                    width_product(pe, go, done, "proj", ps, 0, oT, K["l2_wproj"], C)
                    turn_tensor(pe, go, done, "f1", X, ps, 0, ident)
                    width_product(pe, go, done, "gt", ps, 1, xT, K["l2_gate_w"], E)
                    weights_out(pe, "tensor", go, done, B, ps, combT, ident, tile_of, E)

                with pe.Fori(0, NT // WAYS) as i:
                    turn(i, done)
                turn(NT // WAYS, done[:NT % WAYS])


def layer3_tokens(nc, d, K, h_all, xT_all, yT_all, combT, eps5, eps6, ident, sem, sb, **_):
    H, D, HG, E, DV = 12, 16, 6, 8, 17
    HID = 4
    S = steps("y_cp y_tr y_add " + ln_steps("n0") + rms_steps("r1") + turn_steps("f1") +
              "lat lat_act big big_cp qk_sq qk_ss qk_log qk_rs qk_n qk_w r_cos|r_sin r_add e_min e_exp e_max "
              "q_tr q_dg|k_cp p_sig p_amp p_ph p_abs p_cos p_mul p_tmp p_sig2 p_lin p_clip p_dec v_x "
              "kx0|kx1 S P_m " + SPREAD + "d_s d_m d_r d_f o " + rms_steps("r2") + turn_steps("fo") +
              "proj og ao x2 h3 " + rms_steps("r3") + turn_steps("f3") + "ff1 ff_s ff_m ff2 h4 h_st " +
              ln_steps("n4") + turn_steps("f4") + "x_st gt " + ROUTER + "c_st")
    N = S["end"]
    done = [sem(f"l3_tile{c}_steps") for c in range(WAYS)]
    zeroed, setup, passed = sem("l3_zeroed"), sem("l3_setup"), sem("l3_passed")
    with ExitStack() as ctx:
        shapes = attention_shapes(H, D)
        shapes.update(ROUTER_SHAPES)
        shapes.update(latT=[128, T], big=[T, 816], rA=[T, 2 * H, D], rB=[T, 2 * H, D], sg=[T, H, 4],
                      pm=[T, 4, H], Vx=[T, H, DV], qs=[T, 3, 2 * H])
        B, ps = tile_buffers(ctx, nc, sb, 3, shapes)
        share(B, H)
        for b in B:
            b["ff"] = b["pT"][:, 0:HID, :]
            b["og"] = b["rA"][:, 0:H, :].rearrange("p h d -> p (h d)")
            b["junk"] = b["rB"][:, 0:H, :].rearrange("p h d -> p (h d)")
        for b in B:
            b["passed"] = passed
        hs = sb(ctx, "l3_hs", [T, 6, H])
        X = [b["x"][:, :] for b in B]
        O = [b["o"][:, :] for b in B]
        HC = [b["hcur"][:, :] for b in B]
        xT = [b["xT"] for b in B]
        oT = [b["oT"] for b in B]
        qk = [b["big"][:, 0:2 * C].rearrange("p (h d) -> p h d", d=D) for b in B]
        shape24 = [T, 2 * H, D]
        half_pi = K["half_pi"]
        with nc.Block() as block:
            @block.vector
            def _(dve):
                for c in range(len(done)):
                    dve.memset(B[c]["qx"][:, :, :], 0.0)
                    dve.memset(B[c]["sv"][:, :], PAD)
                    ins = dve.memset(B[c]["keys"][:, :], PAD)
                ins.then_inc(zeroed, 1)
                dve.wait_ge(zeroed, 1)
                dve.wait_ge(setup, 1)
                dve.tensor_scalar(hs[:, 1, :], hs[:, 0, :], 1.0, None, ALU.add).then_inc(setup, 1)
                dve.wait_ge(setup, 2)
                dve.reciprocal(hs[:, 0, :], hs[:, 1, :]).then_inc(setup, 1)
                dve.wait_ge(setup, 3)
                dve.tensor_scalar(hs[:, 1, :], hs[:, 0, :], 0.65, 0.3, ALU.mult, ALU.add).then_inc(setup, 1)
                dve.wait_ge(setup, 4)
                dve.tensor_scalar(hs[:, 0, :], hs[:, 1, :], 1e-5, 0.999, ALU.max, ALU.min).then_inc(setup, 1)
                dve.wait_ge(setup, 7)
                dve.tensor_scalar(hs[:, 3, :], hs[:, 0, :], -1.0, 1.0, ALU.mult, ALU.add).then_inc(setup, 1)
                dve.tensor_scalar(hs[:, 4, :], hs[:, 2, :], 1e-8, None, ALU.add).then_inc(setup, 1)
                dve.wait_ge(setup, 9)
                dve.reciprocal(hs[:, 5, :], hs[:, 4, :]).then_inc(setup, 1)
                dve.wait_ge(setup, 10)
                dve.tensor_tensor(hs[:, 4, :], hs[:, 5, :], hs[:, 3, :], ALU.mult).then_inc(setup, 1)
                dve.wait_ge(setup, 11)
                for c in range(len(done)):
                    ins = dve.tensor_copy(B[c]["Vx"][:, :, D:D + 1], hs[:, 4, :].unsqueeze(2))
                ins.then_inc(setup, 1)
                dve.wait_ge(setup, 12)
                for c in range(len(done)):
                    dve.sem_inc(done[c], 1)
                def turn(i, done):
                    def go(c, step, passed=None):
                        dve.wait_ge(done[c], i * N + (S[step] + 1))
                        if passed is not None:
                            dve.sem_inc(passed, 1)

                    def tile_of(c):
                        return WAYS * i + c
                    take_experts_back(dve, "vector", go, done, B, ps, h_all, yT_all, ident, tile_of)
                    norm_vector(dve, go, done, B, "n0", HC, X)
                    rms_vector(dve, go, done, B, "r1", X, O)
                    for c in range(len(done)):
                        go(c, "qk_sq")
                        dve.tensor_tensor(B[c]["rA"][:, :, :], qk[c], qk[c], ALU.mult).then_inc(done[c], 1)
                    for c in range(len(done)):
                        go(c, "qk_ss")
                        dve.tensor_reduce(B[c]["qs"][:, 0, :], B[c]["rA"][:, :, :], AX.X, ALU.add).then_inc(done[c], 1)
                    for c in range(len(done)):
                        go(c, "qk_n")
                        dve.tensor_tensor(qk[c], qk[c], over(B[c]["qs"][:, 2, :].unsqueeze(2), shape24), ALU.mult
                                          ).then_inc(done[c], 1)
                    for c in range(len(done)):
                        go(c, "qk_w")
                        for w in range(2):
                            v = qk[c][:, w * H:(w + 1) * H, :]
                            ins = dve.tensor_tensor(v, v, over(K["l3_qkn"][:, w, :].unsqueeze(1), [T, H, D]), ALU.mult)
                        ins.then_inc(done[c], 1)
                    for c in range(len(done)):
                        go(c, "r_cos")
                        dve.tensor_tensor(B[c]["rA"][:, :, :], qk[c], over(K["rope_cos"][:, :].unsqueeze(1), shape24),
                                          ALU.mult).then_inc(done[c], 1)
                    for c in range(len(done)):
                        go(c, "r_add")
                        dve.tensor_tensor(qk[c], B[c]["rA"][:, :, :], B[c]["rB"][:, :, :], ALU.add
                                          ).then_inc(done[c], 1)
                    for c in range(len(done)):
                        go(c, "e_min")
                        dve.tensor_scalar(B[c]["rA"][:, :, :], qk[c], 0.0, None, ALU.min).then_inc(done[c], 1)
                    for c in range(len(done)):
                        go(c, "e_max")
                        dve.scalar_tensor_tensor(qk[c], qk[c], 0.0, B[c]["rA"][:, :, :], ALU.max, ALU.add
                                                 ).then_inc(done[c], 1)
                    for c in range(len(done)):
                        go(c, "k_cp")
                        dve.tensor_copy(B[c]["kT"][:, :, :].rearrange("p o t -> p (o t)"), ps[c][0:CK, 1, 0:2 * T]
                                        ).then_inc(done[c], 1)
                    for c in range(len(done)):
                        go(c, "p_amp")
                        dve.tensor_tensor(B[c]["pm"][:, 0, :], B[c]["sg"][:, :, 0], B[c]["sg"][:, :, 2], ALU.mult
                                          ).then_inc(done[c], 1)
                    for c in range(len(done)):
                        go(c, "p_ph")
                        dve.tensor_tensor(B[c]["pm"][:, 1, :], B[c]["sg"][:, :, 1], B[c]["sg"][:, :, 3], ALU.subtract
                                          ).then_inc(done[c], 1)
                    for c in range(len(done)):
                        go(c, "p_abs")
                        dve.scalar_tensor_tensor(B[c]["pm"][:, 2, :], B[c]["pm"][:, 1, :], -1.0, B[c]["pm"][:, 1, :],
                                                 ALU.mult, ALU.max).then_inc(done[c], 1)
                    for c in range(len(done)):
                        go(c, "p_mul")
                        dve.tensor_tensor(B[c]["pm"][:, 0, :], B[c]["pm"][:, 0, :], B[c]["pm"][:, 1, :], ALU.mult
                                          ).then_inc(done[c], 1)
                    for c in range(len(done)):
                        go(c, "p_tmp")
                        dve.tensor_scalar(B[c]["pm"][:, 1, :], B[c]["pm"][:, 0, :], K["l3_temp"][:, 0:1], None,
                                          ALU.mult).then_inc(done[c], 1)
                    for c in range(len(done)):
                        go(c, "p_lin")
                        dve.tensor_scalar(B[c]["pm"][:, 1, :], B[c]["pm"][:, 2, :], 1.2, -0.1, ALU.mult, ALU.add
                                          ).then_inc(done[c], 1)
                    for c in range(len(done)):
                        go(c, "p_clip")
                        dve.tensor_scalar(B[c]["pm"][:, 2, :], B[c]["pm"][:, 1, :], 0.05, 0.95, ALU.max, ALU.min
                                          ).then_inc(done[c], 1)
                    for c in range(len(done)):
                        go(c, "p_dec")
                        dve.tensor_tensor(B[c]["pm"][:, 3, :], B[c]["pm"][:, 2, :], hs[:, 4, :], ALU.mult
                                          ).then_inc(done[c], 1)
                    for c in range(len(done)):
                        go(c, "v_x")
                        dve.tensor_tensor(B[c]["Vx"][:, :, 0:D], per_head(B[c]["big"][:, 2 * C:3 * C], D),
                                          over(B[c]["pm"][:, 3, :].unsqueeze(2), [T, H, D]), ALU.mult
                                          ).then_inc(done[c], 1)
                    heads_expand(dve, go, done, B, "kx0", 0, HG, K["hmask16"])
                    for c in range(len(done)):
                        go(c, "P_m")
                        dve.tensor_tensor(B[c]["P"][:, :, :],
                                          ps[c][0:T, 0, 0:H * NTOK].rearrange("p (h m) -> p h m", m=NTOK),
                                          over(K["causal01"][:, :].unsqueeze(1), [T, H, NTOK]), ALU.mult
                                          ).then_inc(done[c], 1)
                    blocks_expand(dve, go, done, B, "px0", 0, 8, K["bmask"])
                    probs_copy(dve.tensor_copy, go, done, B, ps, "pc1", 1, 4)
                    AV = [p[0:T, 0, 0:H * DV].rearrange("p (h d) -> p h d", d=DV) for p in ps]
                    for c in range(len(done)):
                        go(c, "d_s")
                        dve.tensor_tensor(B[c]["hsum"][:, 0:H], AV[c][:, :, D], hs[:, 2, :], ALU.mult
                                          ).then_inc(done[c], 1)
                    for c in range(len(done)):
                        go(c, "d_m")
                        dve.tensor_scalar(B[c]["hmax"][:, 0:H], B[c]["hsum"][:, 0:H], 1e-5, None, ALU.max
                                          ).then_inc(done[c], 1)
                    for c in range(len(done)):
                        go(c, "d_r")
                        dve.reciprocal(B[c]["hinv"][:, 0:H], B[c]["hmax"][:, 0:H]).then_inc(done[c], 1)
                    for c in range(len(done)):
                        go(c, "d_f")
                        dve.tensor_tensor(B[c]["hsum"][:, 0:H], B[c]["hinv"][:, 0:H], hs[:, 2, :], ALU.mult
                                          ).then_inc(done[c], 1)
                    for c in range(len(done)):
                        go(c, "o")
                        dve.tensor_tensor(per_head(O[c], D), AV[c][:, :, 0:D],
                                          over(B[c]["hsum"][:, 0:H].unsqueeze(2), [T, H, D]), ALU.mult
                                          ).then_inc(done[c], 1)
                    rms_vector(dve, go, done, B, "r2", O, O)
                    for c in range(len(done)):
                        go(c, "ao")
                        dve.tensor_tensor(O[c], ps[c][0:T, 0, 0:C], B[c]["og"], ALU.mult).then_inc(done[c], 1)
                    add2(dve, go, done, "x2", X, X, O)
                    add2(dve, go, done, "h3", HC, HC, X)
                    rms_vector(dve, go, done, B, "r3", X, O)
                    for c in range(len(done)):
                        go(c, "ff_m")
                        ff = B[c]["ff"][:, :, :].rearrange("p f t -> p (f t)")
                        dve.tensor_tensor(ff, ff, ps[c][:, 1, 0:HID * T], ALU.mult).then_inc(done[c], 1)
                    add2(dve, go, done, "h4", HC, HC, [p[0:T, 0, 0:C] for p in ps])
                    norm_vector(dve, go, done, B, "n4", HC, X)
                    router_vector(dve, go, done, B, ps, E, 2, None)

                with dve.Fori(0, NT // WAYS) as i:
                    turn(i, done)
                turn(NT // WAYS, done[:NT % WAYS])

            @block.scalar
            def _(act):
                act.preload_act_table_set(EXP_LN)
                act.activation(hs[:, 0, :], K["l3_hd"][:, :], ACT.Exp, scale=-1.0).then_inc(setup, 1)
                act.wait_ge(setup, 5)
                act.activation(hs[:, 1, :], hs[:, 0, :], ACT.Ln).then_inc(setup, 1)
                act.wait_ge(setup, 6)
                act.activation(hs[:, 2, :], hs[:, 1, :], ACT.Exp, scale=K["pos1"][:, 0:1]).then_inc(setup, 1)
                def turn(i, done):
                    def go(c, step):
                        act.wait_ge(done[c], i * N + (S[step] + 1))

                    def tile_of(c):
                        return WAYS * i + c
                    norm_scalar(act, go, done, B, "n0", eps5[0:T, :])
                    rms_scalar(act, go, done, B, "r1", X, eps6[0:T, :])
                    turn_scalar(act, go, done, "f1", ps, 0, xT, K["l3_ln_w"])
                    for c in range(len(done)):
                        go(c, "lat_act")
                        act.activation(B[c]["latT"][:, :], ps[c][:, 1, 0:T], ACT.Silu).then_inc(done[c], 1)
                    for c in range(len(done)):
                        go(c, "big_cp")
                        for b in range(2):
                            ins = act.copy(B[c]["big"][:, b * 408:(b + 1) * 408], ps[c][0:T, b, 0:408])
                        ins.then_inc(done[c], 1)
                    for c in range(len(done)):
                        go(c, "qk_log")
                        act.activation(B[c]["qs"][:, 1, :], B[c]["qs"][:, 0, :], ACT.Ln, bias=eps6[0:T, :],
                                       scale=1.0 / D).then_inc(done[c], 1)
                    for c in range(len(done)):
                        go(c, "qk_rs")
                        act.activation(B[c]["qs"][:, 2, :], B[c]["qs"][:, 1, :], ACT.Exp, scale=-0.5
                                       ).then_inc(done[c], 1)
                    for c in range(len(done)):
                        go(c, "e_exp")
                        act.activation(B[c]["rA"][:, :, :], B[c]["rA"][:, :, :], ACT.Exp).then_inc(done[c], 1)
                    query_blocks(act, go, done, B, ps, "q_dg", 0)
                    for c in range(len(done)):
                        go(c, "p_sig")
                        act.activation(B[c]["sg"][:, :, :].rearrange("p h f -> p (h f)"), B[c]["big"][:, 576:624],
                                       ACT.Sigmoid).then_inc(done[c], 1)
                    for c in range(len(done)):
                        go(c, "p_cos")
                        act.activation(B[c]["pm"][:, 1, :], B[c]["pm"][:, 2, :], ACT.Sin, bias=half_pi[0:T, :],
                                       scale=-float(np.pi)).then_inc(done[c], 1)
                    for c in range(len(done)):
                        go(c, "p_sig2")
                        act.activation(B[c]["pm"][:, 2, :], B[c]["pm"][:, 1, :], ACT.Sigmoid).then_inc(done[c], 1)
                    probs_copy(act.copy, go, done, B, ps, "pc0", 0, 0)
                    probs_copy(act.copy, go, done, B, ps, "pc2", 0, 8)
                    rms_scalar(act, go, done, B, "r2", O, eps6[0:T, :])
                    turn_scalar(act, go, done, "fo", ps, 1, oT, K["l3_memn_w"])
                    for c in range(len(done)):
                        go(c, "og")
                        act.activation(B[c]["og"], B[c]["big"][:, 624:816], ACT.Silu).then_inc(done[c], 1)
                    rms_scalar(act, go, done, B, "r3", X, eps6[0:T, :])
                    turn_scalar(act, go, done, "f3", ps, 0, xT, K["l3_ffn_ln_w"])
                    for c in range(len(done)):
                        go(c, "ff_s")
                        act.activation(B[c]["ff"][:, :, :].rearrange("p f t -> p (f t)"), ps[c][:, 0, 0:HID * T],
                                       ACT.Silu).then_inc(done[c], 1)
                    norm_scalar(act, go, done, B, "n4", eps5[0:T, :])
                    turn_scalar(act, go, done, "f4", ps, 0, xT)
                    router_scalar(act, go, done, B, E)
                    weights_out(act, "scalar", go, done, B, ps, combT, ident, tile_of, E)

                with act.Fori(0, NT // WAYS) as i:
                    turn(i, done)
                turn(NT // WAYS, done[:NT % WAYS])

            @block.gpsimd
            def _(pool):
                def turn(i, done):
                    def go(c, step):
                        pool.wait_ge(done[c], i * N + (S[step] + 1))

                    def tile_of(c):
                        return WAYS * i + c
                    take_experts_back(pool, "pool", go, done, B, ps, h_all, yT_all, ident, tile_of)
                    for c in range(len(done)):
                        go(c, "r_sin")
                        hd = D // 2
                        for a, z in ((0, hd), (hd, 0)):
                            ins = pool.tensor_tensor(B[c]["rB"][:, :, a:a + hd], qk[c][:, :, z:z + hd],
                                                     over(K["rope_sin"][:, a:a + hd].unsqueeze(1), [T, 2 * H, hd]),
                                                     ALU.mult)
                        ins.then_inc(done[c], 1)
                    heads_expand(pool, go, done, B, "kx1", 1, HG, K["hmask16"])
                    blocks_expand(pool, go, done, B, "px1", 8, H, K["bmask"])
                    store_tile(pool, go, done, B, h_all, xT_all, tile_of, "hcur")
                    store_xT(pool, go, done, B, xT_all, tile_of)

                with pool.Fori(0, NT // WAYS) as i:
                    turn(i, done)
                turn(NT // WAYS, done[:NT % WAYS])

            @block.tensor
            def _(pe):
                pe.wait_ge(setup, 12)
                def turn(i, done):
                    def go(c, step):
                        pe.wait_ge(done[c], i * N + (S[step] + 1))

                    def tile_of(c):
                        return WAYS * i + c
                    take_experts_back(pe, "tensor", go, done, B, ps, h_all, yT_all, ident, tile_of)
                    turn_tensor(pe, go, done, "f1", O, ps, 0, ident)
                    for c in range(len(done)):
                        go(c, "lat")
                        for k in range(2):
                            mm = pe.matmul(ps[c][:, 1, 0:T], K["l3_wcomp"][:, k, :], xT[c][:, k, :],
                                           start=(k == 0), stop=(k == 1))
                        mm.then_inc(done[c], 1)
                    for c in range(len(done)):
                        go(c, "big")
                        for b in range(2):
                            mm = pe.matmul(ps[c][0:T, b, 0:408], B[c]["latT"][:, :],
                                           K["l3_wcat"][:, b * 408:(b + 1) * 408], start=True, stop=True)
                        mm.then_inc(done[c], 1)
                    for c in range(len(done)):
                        go(c, "q_tr")
                        for w in range(2):
                            for o in range(2):
                                mm = pe.transpose(ps[c][0:CK, w, o * T:(o + 1) * T],
                                                  B[c]["big"][:, w * C + o * CK:w * C + (o + 1) * CK], ident[0:T, 0:T])
                        mm.then_inc(done[c], 1)
                    scores_tensor(pe, go, done, B, ps, HG)
                    values_stage(pe, go, done, B, ps, H, DV, [b["Vx"][:, :, :].rearrange("p h d -> p (h d)") for b in B], H, ident)
                    turn_tensor(pe, go, done, "fo", O, ps, 1, ident)
                    width_product(pe, go, done, "proj", ps, 0, oT, K["l3_wproj"], C)
                    turn_tensor(pe, go, done, "f3", O, ps, 0, ident)
                    for c in range(len(done)):
                        go(c, "ff1")
                        for b in range(2):
                            for f in range(HID):
                                for k in range(2):
                                    mm = pe.matmul(ps[c][:, b, f * T:(f + 1) * T],
                                                   K["l3_w12"][:, k, (b * HID + f) * 128:(b * HID + f + 1) * 128],
                                                   xT[c][:, k, :], start=(k == 0), stop=(k == 1))
                        mm.then_inc(done[c], 1)
                    for c in range(len(done)):
                        go(c, "ff2")
                        for f in range(HID):
                            mm = pe.matmul(ps[c][0:T, 0, 0:C], B[c]["ff"][:, f, :], K["l3_w3"][:, f, :],
                                           start=(f == 0), stop=(f == HID - 1))
                        mm.then_inc(done[c], 1)
                    turn_tensor(pe, go, done, "f4", X, ps, 0, ident)
                    width_product(pe, go, done, "gt", ps, 1, xT, K["l3_gate_w"], E)
                    weights_out(pe, "tensor", go, done, B, ps, combT, ident, tile_of, E)

                with pe.Fori(0, NT // WAYS) as i:
                    turn(i, done)
                turn(NT // WAYS, done[:NT % WAYS])


def last_tokens(nc, out, h_all, yT_all, ident, sem, sb, **_):
    S = steps("y_cp y_tr y_add")
    N = S["end"]
    done = [sem(f"out_tile{c}_steps") for c in range(WAYS)]
    stored = [sem(f"out_stored{c}") for c in range(WAYS)]
    with ExitStack() as ctx:
        B, ps = tile_buffers(ctx, nc, sb, 4, {})
        with nc.Block() as block:
            @block.gpsimd
            def _(pool):
                def turn(i, done):
                    take_experts_back(pool, "pool", lambda c, s: pool.wait_ge(done[c], i * N + (S[s] + 1)), done, B, ps,
                                      h_all, yT_all, ident, lambda c: WAYS * i + c)

                with pool.Fori(0, NT // WAYS) as i:
                    turn(i, done)
                turn(NT // WAYS, done[:NT % WAYS])

            @block.tensor
            def _(pe):
                def turn(i, done):
                    take_experts_back(pe, "tensor", lambda c, s: pe.wait_ge(done[c], i * N + (S[s] + 1)), done, B, ps,
                                      h_all, yT_all, ident, lambda c: WAYS * i + c)

                with pe.Fori(0, NT // WAYS) as i:
                    turn(i, done)
                turn(NT // WAYS, done[:NT % WAYS])

            @block.vector
            def _(dve):
                for c in range(len(done)):
                    dve.sem_inc(done[c], 1)
                def turn(i, done):
                    for c in range(len(done)):
                        dve.wait_ge(stored[c], 16 * i + 1)
                    take_experts_back(dve, "vector", lambda c, s: dve.wait_ge(done[c], i * N + (S[s] + 1)), done, B, ps,
                                      h_all, yT_all, ident, lambda c: WAYS * i + c)

                with dve.Fori(0, NT // WAYS) as i:
                    turn(i, done)
                turn(NT // WAYS, done[:NT % WAYS])

            @block.sync
            def _(sp):
                for c in range(len(done)):
                    sp.sem_inc(stored[c], 1)
                def turn(i, done):
                    for c in range(len(done)):
                        sp.wait_ge(done[c], i * N + (N + 1))
                        sp.dma_start(out[bass.ds(WAYS * i + c, 1), :, :].rearrange("a t c -> (a t) c"),
                                     B[c]["hcur"][:, :]).then_inc(stored[c], 16)

                with sp.Fori(0, NT // WAYS) as i:
                    turn(i, done)
                turn(NT // WAYS, done[:NT % WAYS])
                for c in range(len(done)):
                    sp.wait_ge(stored[c], 16 * ((NT - c + WAYS - 1) // WAYS) + 1)



COMMON = ["ident", "bmask", "hmask16", "hmask12", "off_diag", "on_diag", "causal", "anti_causal", "causal01",
          "quarter", "half_pi", "pos1"]
LAYER_WEIGHTS = [
    ["tok_w", "tok_base", "tok_pos", "l0_wqv", "l0_wproj", "l0_bproj", "l0_gate_w", "l0_gate_b"],
    ["l1_wq", "l1_wk", "l1_wv", "l1_bq", "l1_bk", "l1_bv", "l1_wo", "l1_bo", "l1_ln_w", "l1_ln_b", "l1_ln1_w",
     "l1_ln2_w", "l1_wqk", "l1_wv2", "l1_wproj", "l1_gate_w"],
    ["rel", "l2_wqk", "l2_wv", "l2_wproj", "l2_bproj", "l2_wpos", "l2_bpos", "l2_gating", "l2_scale", "l2_gate_w",
     "l2_gate_b"],
    ["rope_cos", "rope_sin", "l3_ln_w", "l3_wcomp", "l3_wcat", "l3_qkn", "l3_hd", "l3_temp", "l3_wproj",
     "l3_memn_w", "l3_ffn_ln_w", "l3_w12", "l3_w3", "l3_gate_w"]]


def shape_constants():
    f = np.float32
    n = np.arange(T) % NTOK
    img = np.arange(T) // NTOK
    m = np.arange(NTOK)
    side = int(round(NTOK ** 0.5))
    dx = (m % side)[None, :] - (n % side)[:, None]
    dy = (m // side)[None, :] - (n // side)[:, None]
    half = np.arange(0, 16, 2, dtype=f) / f(16)
    freq = np.outer(np.arange(NTOK, dtype=f), f(1.0) / (f(10000.0) ** half)).astype(f)
    cos = np.concatenate([np.cos(freq), np.cos(freq)], 1)[n]
    sin = np.concatenate([-np.sin(freq), np.sin(freq)], 1)[n]
    row = np.arange(CK)
    return {
        "ident": np.eye(128, dtype=f),
        "bmask": (img[:, None] == img[None, :]).astype(f),
        "hmask16": (row[:, None] // 16 == np.arange(6)[None, :]).astype(f),
        "hmask12": (row[:, None] // 12 == np.arange(8)[None, :]).astype(f),
        "on_diag": (n[:, None] == m[None, :]).astype(f),
        "off_diag": (n[:, None] != m[None, :]).astype(f),
        "causal": np.where(m[None, :] <= n[:, None], 0.0, -BIG).astype(f),
        "anti_causal": np.where(m[None, :] >= n[:, None], 0.0, -BIG).astype(f),
        "causal01": (m[None, :] <= n[:, None]).astype(f),
        "quarter": np.full((128, 1), -0.25, f),
        "half_pi": np.full((128, 1), np.pi / 2, f),
        "pos1": (n + 1).astype(f)[:, None],
        "rel": np.stack([dx, dy, dx * dx + dy * dy], 1).astype(f),
        "rope_cos": cos.astype(f),
        "rope_sin": sin.astype(f),
    }


def lay_out(a):
    def kxm(w, rows):
        return w.reshape(w.shape[0] // rows, rows, w.shape[1]).transpose(1, 0, 2)

    def rows(v):
        return np.broadcast_to(v[None, :], (T, v.shape[0]))

    def col(v, r):
        return v.reshape(-1, r).T

    def tiles(v, r):
        e, k, m = v.shape
        return v.reshape(e, k // r, r, m).transpose(0, 2, 1, 3).reshape(e, r, k // r * m)

    o = shape_constants()
    x = a["x"].reshape(BATCH, 3, 6, 16, 6, 16).transpose(0, 1, 2, 4, 3, 5).reshape(BATCH, 36, 768)
    full = np.zeros((NT * IMGS, NTOK, 768), x.dtype)
    full[:BATCH, 1:] = x
    o["patches"] = full.reshape(NT, T, 6, 128).transpose(0, 3, 2, 1).reshape(NT, 128, 6 * T)
    o["tok_w"] = kxm(a["L0_tok_W"].T, 128)
    o["tok_base"] = np.tile(np.concatenate([a["L0_tok_class_token"], np.broadcast_to(a["L0_tok_b"], (36, C))]),
                            (IMGS, 1))
    o["tok_pos"] = np.tile(a["L0_tok_pos_embedding"], (IMGS, 1))
    q = a["L0_attn_w_qkv"]
    o["l0_wqv"] = kxm(np.concatenate([q[0:C], q[2 * C:3 * C]]).T, CK)
    o["l0_wproj"] = kxm(a["L0_attn_w_proj"].T, CK)
    o["l0_bproj"] = rows(a["L0_attn_b_proj"])
    o["l0_gate_w"] = kxm(a["L0_ffn_gate_w"].T, CK)
    o["l0_gate_b"] = rows(a["L0_ffn_gate_b"])
    apart = np.concatenate([np.arange(0, C, 2), np.arange(1, C, 2)])
    w1 = np.concatenate([a["L0_ffn_W1"], a["L0_ffn_Ws1"][None]])[:, :, apart]
    w3 = np.concatenate([a["L0_ffn_W3"], a["L0_ffn_Ws3"][None]])[:, :, apart]
    o["l0_w1"] = tiles(np.concatenate([w1, w3], 2), CK)
    o["l0_w2"] = tiles(np.concatenate([a["L0_ffn_W2"], a["L0_ffn_Ws2"][None]]), CK)
    b = np.concatenate([np.concatenate([a["L0_ffn_B1"], a["L0_ffn_Bs1"][None]])[:, apart],
                        np.concatenate([a["L0_ffn_B3"], a["L0_ffn_Bs3"][None]])[:, apart],
                        np.concatenate([a["L0_ffn_B2"], a["L0_ffn_Bs2"][None]])], 1)
    o["l0_b"] = b.reshape(9, 6, CK).transpose(2, 0, 1)
    for n in "qkv":
        o["l1_w" + n] = kxm(a["L1_attn_w" + n], CK)
    o["l1_bq"] = col(a["L1_attn_bq"], 128)
    o["l1_bk"] = col(a["L1_attn_bk"], 128)
    o["l1_bv"] = rows(a["L1_attn_bv"])
    order = np.concatenate([np.arange(0, 12, 2), np.arange(1, 12, 2)])
    o["l1_wo"] = kxm(a["L1_attn_wo"].reshape(12, 64, C)[order].reshape(768, C), 128)
    o["l1_bo"] = rows(a["L1_attn_bo"])
    o["l1_ln_w"] = col(a["L1_attn_ln_w"], CK)
    o["l1_ln_b"] = col(a["L1_attn_ln_b"], CK)
    o["l1_ln1_w"] = col(a["L1_ffn_ln1_w"], CK)
    o["l1_ln2_w"] = col(a["L1_ffn_ln2_w"], CK)
    w = a["L1_ffn_c_attn_w"].T
    o["l1_wqk"] = kxm(w[:, 0:2 * C], CK)
    o["l1_wv2"] = kxm(w[:, 2 * C:3 * C], CK)
    o["l1_wproj"] = kxm(a["L1_ffn_c_proj_w"].T, CK)
    o["l1_gate_w"] = kxm(a["L1_ffn_w_g"].T, CK)
    o["l1_w1"] = tiles(a["L1_ffn_c_fc"], CK)
    o["l1_w2"] = tiles(a["L1_ffn_c_proj_e"], 128)
    o["l2_wqk"] = kxm(a["L2_attn_w_qk"].T, CK)
    o["l2_wv"] = kxm(a["L2_attn_w_v"].T, CK)
    o["l2_wproj"] = kxm(a["L2_attn_w_proj"].T, CK)
    o["l2_bproj"] = rows(a["L2_attn_b_proj"])
    o["l2_wpos"] = np.broadcast_to(a["L2_attn_w_pos"].T[None], (T, 3, 16))
    o["l2_bpos"] = rows(a["L2_attn_b_pos"])
    o["l2_gating"] = rows(a["L2_attn_gating"])
    o["l2_scale"] = col(a["L2_ffn_scale"], CK)
    o["l2_gate_w"] = kxm(a["L2_ffn_gate_w"].T, CK)
    o["l2_gate_b"] = rows(a["L2_ffn_gate_b"])
    o["l2_w1"] = tiles(a["L2_ffn_w1"], CK)
    o["l2_w2"] = tiles(a["L2_ffn_w2"], CK)
    o["l2_b"] = np.concatenate([a["L2_ffn_b1"], a["L2_ffn_b2"]], 1).reshape(16, 6, CK).transpose(2, 0, 1)
    o["l3_ln_w"] = col(a["L3_attn_ln_w"], CK)
    o["l3_wcomp"] = kxm(a["L3_attn_w_comp"], CK)
    o["l3_wcat"] = np.concatenate([a["L3_attn_w_qkv"], a["L3_attn_w_reso"], a["L3_attn_w_outgate"]], 1)
    o["l3_qkn"] = np.broadcast_to(np.stack([a["L3_attn_qn_w"], a["L3_attn_kn_w"]])[None], (T, 2, 16))
    o["l3_hd"] = rows(a["L3_attn_head_decay"])
    o["l3_temp"] = rows(a["L3_attn_temperature"])
    o["l3_wproj"] = kxm(a["L3_attn_w_proj"], CK)
    o["l3_memn_w"] = col(a["L3_attn_memn_w"], CK)
    o["l3_ffn_ln_w"] = col(a["L3_attn_ffn_ln_w"], CK)
    o["l3_w12"] = kxm(np.concatenate([a["L3_attn_w1"], a["L3_attn_w2"]], 1), CK)
    o["l3_w3"] = kxm(a["L3_attn_w3"], 128)
    o["l3_gate_w"] = kxm(a["L3_ffn_w_gate"], CK)
    o["l3_w1"] = tiles(a["L3_ffn_w_fc"].reshape(C, 768, 8).transpose(2, 0, 1), CK)
    o["l3_w2"] = tiles(a["L3_ffn_w_proj"].reshape(768, C, 8).transpose(2, 0, 1), 128)
    return {n: np.ascontiguousarray(v) for n, v in o.items()}


def kernel(**inputs):
    import concourse.bacc as _bacc
    from concourse.bass_utils import run_bass_kernel_spmd as _run

    arrays = {f"in_{n}": v for n, v in lay_out({n: np.asarray(v) for n, v in inputs.items()}).items()}
    nc = _bacc.Bacc("TRN2", target_bir_lowering=False, num_devices=1)
    d = {n[3:]: nc.dram_tensor(n, v.shape, mybir.dt.from_np(v.dtype), kind="ExternalInput").ap()
         for n, v in arrays.items()}
    out = nc.dram_tensor("out", (NT, T, C), F32, kind="ExternalOutput").ap()
    vit_tower(nc, d, out)
    r = _run(nc, [arrays], core_ids=[0])
    got = r.results[0]["out"].reshape(NT * IMGS, NTOK, C)
    return np.ascontiguousarray(got[:BATCH])
```

```python
from contextlib import ExitStack

import numpy as np
import concourse.bass as bass
from concourse import mybir

F32 = mybir.dt.float32
F32R = mybir.dt.float32r
ALU = mybir.AluOpType
ACT = mybir.ActivationFunctionType
AX = mybir.AxisListType

C = 192
CK = 96
NTOK = 37
IMGS = 3
T = IMGS * NTOK
BATCH = 64
NT = 22
NP = NT * T
WAYS = 4
UB = 474
NB = 5
DIAG = NTOK + T
BIG = 1.0e30
PAD = -3.0e38
MARK = 3.0e38
ALPHA, LIMIT = 1.702, 7.0
CAP = 592


def steps(text):
    out, n = {}, 0
    for group in text.split():
        names = group.split("|")
        size = 0
        for name in names:
            name, _, many = name.partition(":")
            assert name not in out, name
            out[name] = n
            size += int(many) if many else 1
        n += size
    out["end"] = n
    return out


def ln_steps(g):
    return f"{g}_stats {g}_aggr {g}_log {g}_rstd {g}_norm "


def rms_steps(g):
    return f"{g}_sq {g}_log {g}_rstd {g}_norm "


def turn_steps(g):
    return f"{g}_tr {g}_cp "


SOFTMAX = "sm_scale sm_max sm_sub sm_exp sm_sum sm_inv "
SPREAD = "px0|px1 pt pc0|pc1 pt2 pc2 av "
SPREAD16 = "px0|px1 pt pc0|pc1 pt2 pc2|pc3 av "


def topk_steps(g):
    return f"{g}_top {g}_keys {g}_repl {g}_mask "



def over(ap, shape):
    return ap.broadcast_to(shape)



def run(stages):
    for _ in stages:
        pass


def wide(stages):
    for step in stages:
        yield "a." + step


def two_by_two(done):
    tiles = list(done)
    return [tiles[n:n + 2] for n in range(0, len(tiles), 2)]


def first_tiles(done):
    return {c: done[c] for c in range(NT % WAYS)}


LENGTH = {"wide_q": 10, "wq_cp": 5, "wide_k": 10, "wk_cp": 6, "wide_v": 10, "wv_cp": 4, "S": 13, "sm_scale": 2,
          "sm_max": 2, "sm_sub": 2, "sm_exp": 2, "sm_sum": 2, "px0": 6, "pt": 5, "pc0": 2, "pt2": 3, "pc2": 2,
          "av": 13, "o_tr": 4, "o_cp": 4, "wide_out": 8, "qkT": 11, "v": 3, "kx0": 6, "proj": 3, "lat": 2, "big": 8,
          "big_cp": 4, "ff1": 24, "ff_m": 2, "ff2": 7, "mix_a": 3, "mix_b": 3, "m_sum": 3, "r_cos": 4, "P_m": 2}


def side_by_side(S, cut, second, first):
    length = [1] * (S["end"] + 1)
    for step, n in S.items():
        length[n] = max(length[n], LENGTH.get(step.rpartition(".")[2], 1))

    def place(stages, start, end):
        step = next(stages, None)
        return None if step is None else sum(length[start:S[step]]) / sum(length[start:end])

    spans = [(second, S[cut], S["end"]), (first, 0, S[cut])]
    places = [place(*span) for span in spans]
    while places[0] is not None or places[1] is not None:
        n = 0 if places[1] is None or (places[0] is not None and places[0] <= places[1]) else 1
        places[n] = place(*spans[n])


def two_at_once(eng, turn, S, cut, done):
    ahead = {c: done[c] for c in range(WAYS // 2)}
    behind = {c: done[c] for c in range(WAYS // 2, WAYS)}
    run(turn(0, ahead, 0))
    with eng.Fori(0, NT // WAYS) as i:
        side_by_side(S, cut, turn(i, ahead, 1), turn(i, behind, 0))
        side_by_side(S, cut, turn(i, behind, 1), turn(i + 1, ahead, 0))
    run(turn(NT // WAYS, ahead, 1))



def norm_vector(dve, go, done, B, g, src, dst):
    yield f"{g}_stats"
    for c in done:
        go(c, f"{g}_stats")
        dve.bn_stats(B[c]["stats"][:, :], src[c]).then_inc(done[c], 1)
    yield f"{g}_aggr"
    for c in done:
        go(c, f"{g}_aggr", B[c]["passed"])
        dve.bn_aggr(B[c]["mv"][:, :], B[c]["stats"][:, :]).then_inc(done[c], 1)
    yield f"{g}_norm"
    for c in done:
        go(c, f"{g}_norm")
        dve.tensor_scalar(dst[c], src[c], B[c]["mv"][:, 0:1], B[c]["rstd"][:, 1:2],
                          ALU.subtract, ALU.mult).then_inc(done[c], 1)


def norm_scalar(act, go, done, B, g, eps):
    yield f"{g}_log"
    for c in done:
        go(c, f"{g}_log")
        act.activation(B[c]["rstd"][:, 0:1], B[c]["mv"][:, 1:2], ACT.Ln, bias=eps).then_inc(done[c], 1)
    yield f"{g}_rstd"
    for c in done:
        go(c, f"{g}_rstd")
        act.activation(B[c]["rstd"][:, 1:2], B[c]["rstd"][:, 0:1], ACT.Exp, scale=-0.5).then_inc(done[c], 1)


def rms_scalar(act, go, done, B, g, src, eps):
    yield f"{g}_sq"
    for c in done:
        go(c, f"{g}_sq")
        act.activation(B[c]["junk"], src[c], ACT.Square, accum_out=B[c]["mv"][:, 0:1]).then_inc(done[c], 1)
    yield f"{g}_log"
    for c in done:
        go(c, f"{g}_log")
        act.activation(B[c]["rstd"][:, 0:1], B[c]["mv"][:, 0:1], ACT.Ln, bias=eps, scale=1.0 / C).then_inc(done[c], 1)
    yield f"{g}_rstd"
    for c in done:
        go(c, f"{g}_rstd")
        act.activation(B[c]["rstd"][:, 1:2], B[c]["rstd"][:, 0:1], ACT.Exp, scale=-0.5).then_inc(done[c], 1)


def rms_vector(dve, go, done, B, g, src, dst):
    yield f"{g}_norm"
    for c in done:
        go(c, f"{g}_norm")
        dve.tensor_scalar(dst[c], src[c], B[c]["rstd"][:, 1:2], None, ALU.mult).then_inc(done[c], 1)


def turn_tensor(pe, go, done, g, src, ps, bank, ident):
    yield f"{g}_tr"
    for c in done:
        go(c, f"{g}_tr")
        for o in range(2):
            mm = pe.transpose(ps[c][0:CK, bank, o * T:(o + 1) * T], src[c][:, o * CK:(o + 1) * CK],
                              ident[0:T, 0:T])
        mm.then_inc(done[c], 1)


def turn_scalar(act, go, done, g, ps, bank, dst, scale=None, bias=None):
    yield f"{g}_cp"
    for c in done:
        go(c, f"{g}_cp")
        if scale is None:
            act.copy(dst[c][:, :, :].rearrange("p o t -> p (o t)"), ps[c][0:CK, bank, 0:2 * T]).then_inc(done[c], 1)
            continue
        for o in range(2):
            kw = {} if bias is None else {"bias": bias[:, o:o + 1]}
            ins = act.activation(dst[c][:, o, :], ps[c][0:CK, bank, o * T:(o + 1) * T], ACT.Identity,
                                 scale=scale[:, o:o + 1], **kw)
        ins.then_inc(done[c], 1)


def heads_expand(eng, go, done, B, step, o, HG, hmask):
    yield step
    for c in done:
        go(c, step)
        for j in range(IMGS):
            k = B[c]["kT"][:, o, j * NTOK:(j + 1) * NTOK].unsqueeze(1)
            ins = eng.tensor_tensor(B[c]["kx"][:, o, j, 0:HG, :], over(k, [CK, HG, NTOK]),
                                    over(hmask[:, 0:HG].unsqueeze(2), [CK, HG, NTOK]), ALU.mult)
        ins.then_inc(done[c], 1)


def score_place(ps, o, HG):
    if 2 * HG * NTOK <= 512:
        return ps[0:T, 0, o * HG * NTOK:(o + 1) * HG * NTOK]
    return ps[0:T, o, 0:HG * NTOK]


def scores_tensor(pe, go, done, B, ps, HG):
    yield "S"
    for c in done:
        go(c, "S")
        for o in range(2):
            for j in range(IMGS):
                mm = pe.matmul(score_place(ps[c], o, HG), B[c]["qx"][:, o, j * T:(j + 1) * T],
                               B[c]["kx"][:, o, j, 0:HG, :].rearrange("p h m -> p (h m)"),
                               start=(j == 0), stop=(j == IMGS - 1))
        mm.then_inc(done[c], 1)


def query_blocks(act, go, done, B, ps, step, bank):
    yield step
    for c in done:
        go(c, step)
        for o in range(2):
            ins = act.copy(B[c]["qx"][:, o, :].rearrange("p (j x) -> p j x", x=DIAG)[:, :, 0:NTOK],
                           ps[c][0:CK, bank, o * T:(o + 1) * T].rearrange("p (j m) -> p j m", m=NTOK))
        ins.then_inc(done[c], 1)


def softmax_vector(dve, go, done, B, S, scale, bias, H):
    yield "sm_scale"
    for c in done:
        go(c, "sm_scale")
        h = 0
        for src in S[c]:
            dst = B[c]["P"][:, h:h + src.shape[1], :]
            if bias is None:
                ins = dve.tensor_scalar(dst, src, scale, None, ALU.mult)
            else:
                ins = dve.scalar_tensor_tensor(dst, src, scale, over(bias[:, :].unsqueeze(1), list(src.shape)),
                                               ALU.mult, ALU.add)
            h += src.shape[1]
        ins.then_inc(done[c], 1)
    yield "sm_max"
    for c in done:
        go(c, "sm_max")
        dve.tensor_reduce(B[c]["hmax"][:, 0:H], B[c]["P"][:, 0:H, :], AX.X, ALU.max).then_inc(done[c], 1)
    yield "sm_sub"
    for c in done:
        go(c, "sm_sub")
        dve.tensor_tensor(B[c]["P"][:, 0:H, :], B[c]["P"][:, 0:H, :],
                          over(B[c]["hmax"][:, 0:H].unsqueeze(2), [T, H, NTOK]), ALU.subtract).then_inc(done[c], 1)


def sums_vector(dve, go, done, B, H):
    yield "sm_sum"
    for c in done:
        go(c, "sm_sum")
        dve.tensor_reduce(B[c]["hsum"][:, 0:H], B[c]["P"][:, 0:H, :], AX.X, ALU.add).then_inc(done[c], 1)
    yield "sm_inv"
    for c in done:
        go(c, "sm_inv")
        dve.reciprocal(B[c]["hinv"][:, 0:H], B[c]["hsum"][:, 0:H]).then_inc(done[c], 1)


def softmax_scalar(act, go, done, B, H):
    yield "sm_exp"
    for c in done:
        go(c, "sm_exp")
        act.activation(B[c]["P"][:, 0:H, :], B[c]["P"][:, 0:H, :], ACT.Exp).then_inc(done[c], 1)


def blocks_expand(eng, go, done, B, step, h0, h1, bmask):
    yield step
    for c in done:
        go(c, step)
        for h in range(h0, h1):
            ins = eng.tensor_tensor(B[c]["px"][:, h, :].rearrange("p (j m) -> p j m", m=NTOK),
                                    over(B[c]["P"][:, h, :].unsqueeze(1), [T, IMGS, NTOK]),
                                    bmask[:, :].rearrange("p (j m) -> p j m", m=NTOK), ALU.mult)
        ins.then_inc(done[c], 1)


def probs_turn_tensor(pe, go, done, B, ps, step, h0, h1, ident):
    yield step
    for c in done:
        go(c, step)
        for h in range(h0, h1):
            r = h - h0
            mm = pe.transpose(ps[c][0:T, r // 4, (r % 4) * T:(r % 4 + 1) * T], B[c]["px"][:, h, :],
                              ident[0:T, 0:T])
        mm.then_inc(done[c], 1)


def probs_copy(copy, go, done, B, ps, step, b, h0):
    yield step
    for c in done:
        go(c, step)
        copy(B[c]["pT"][0:T, h0:h0 + 4, :].rearrange("p h n -> p (h n)"), ps[c][0:T, b, 0:4 * T]).then_inc(done[c], 1)


def values_stage(pe, go, done, B, ps, H, D, V, per_bank, ident):
    yield from probs_turn_tensor(pe, go, done, B, ps, "pt", 0, 8, ident)
    yield from probs_turn_tensor(pe, go, done, B, ps, "pt2", 8, H, ident)
    yield from values_tensor(pe, go, done, B, ps, H, D, V, per_bank)


def values_tensor(pe, go, done, B, ps, H, D, V, per_bank):
    yield "av"
    for c in done:
        go(c, "av")
        for h in range(H):
            b, r = h // per_bank, h % per_bank
            mm = pe.matmul(ps[c][0:T, b, r * D:(r + 1) * D], B[c]["pT"][0:T, h, :], V[c][:, h * D:(h + 1) * D],
                           start=True, stop=True)
        mm.then_inc(done[c], 1)


def topk_vector(dve, go, done, B, g, vals, keys, k, E, mask):
    yield f"{g}_top"
    for c in done:
        go(c, f"{g}_top", B[c]["passed"])
        dve.max(B[c]["max8"][:, :], B[c][vals][:, 0:E + 8]).then_inc(done[c], 1)
    yield f"{g}_keys"
    for c in done:
        go(c, f"{g}_keys")
        dve.tensor_copy(B[c][keys][:, 0:k], B[c]["max8"][:, 0:k]).then_inc(done[c], 1)
    yield f"{g}_repl"
    for c in done:
        go(c, f"{g}_repl", B[c]["passed"])
        dve.match_replace(B[c]["repl"][:, 0:E + 8], B[c][keys][:, :], B[c][vals][:, 0:E + 8], MARK).then_inc(done[c], 1)
    yield f"{g}_mask"
    for c in done:
        go(c, f"{g}_mask")
        dve.tensor_scalar(mask[c], B[c]["repl"][:, 0:E], 0.5 * MARK, None, ALU.is_ge).then_inc(done[c], 1)



def vit_tower(nc, d, out):
    root = ExitStack()

    def sb(ctx, name, shape):
        return ctx.enter_context(nc.sbuf_tensor(name, shape, F32))

    def sem(name):
        return root.enter_context(nc.semaphore(name))

    with root:
        K = {}
        resident = load_list(root, sb, d, K, COMMON)
        K["tok_add"] = sb(root, "tok_add", [T, C])
        h_all = sb(root, "h_all", [T, NT, C])
        xT_all = sb(root, "xT_all", [CK, 2, NP])
        yT_all = sb(root, "yT_all", [CK, 2, NP])
        combT = sb(root, "combT", [40, NP])
        maskT = combT[32:40, :]
        eps5 = sb(root, "eps5", [128, 1])
        eps6 = sb(root, "eps6", [128, 1])
        m10 = sb(root, "m10", [128, 1])
        ident = K["ident"]

        layer_weights = ExitStack()
        resident += load_list(layer_weights, sb, d, K, LAYER_WEIGHTS[0])
        resident_loaded = sem("resident_loaded")
        with nc.Block() as block:
            @block.sync
            def _(sp):
                start_loads(sp, resident, resident_loaded)
                sp.wait_ge(resident_loaded, 16 * len(resident))

            @block.vector
            def _(dve):
                dve.memset(eps5[:, :], 1e-5)
                dve.memset(eps6[:, :], 1e-6)
                dve.memset(m10[:, :], -10.0)
                dve.wait_ge(resident_loaded, 16 * len(resident))
                dve.tensor_tensor(K["tok_add"][:, :], K["tok_base"][:, :], K["tok_pos"][:, :], ALU.add)

        env = dict(nc=nc, d=d, out=out, K=K, h_all=h_all, xT_all=xT_all, yT_all=yT_all, combT=combT, maskT=maskT,
                   eps5=eps5, eps6=eps6, m10=m10, ident=ident, sem=sem, sb=sb)
        with layer_weights:
            layer0_tokens(**env)
        with ExitStack() as layer_weights:
            ahead = load_list(layer_weights, sb, d, K, LAYER_WEIGHTS[1])
            experts_swiglu(layer=0, E=9, ahead=ahead, **env)
            layer1_tokens(**env)
        capacity_limit(**env)
        with ExitStack() as layer_weights:
            ahead = load_list(layer_weights, sb, d, K, LAYER_WEIGHTS[2])
            experts_gelu(layer=1, func=ACT.Gelu, ahead=ahead, **env)
            layer2_tokens(**env)
        with ExitStack() as layer_weights:
            ahead = load_list(layer_weights, sb, d, K, LAYER_WEIGHTS[3])
            experts_swiglu(layer=2, E=16, ahead=ahead, **env)
            layer3_tokens(**env)
        experts_gelu(layer=3, func=ACT.Gelu_apprx_tanh, ahead=[], **env)
        last_tokens(**env)


def load_list(ctx, sb, d, K, names):
    for n in names:
        K[n] = sb(ctx, "c_" + n, list(d[n].shape))
    return [(K[n], d[n]) for n in names]


def start_loads(sp, loads, loaded):
    for tile, src in loads:
        idx = tuple(slice(None) for _ in src.shape)
        sp.dma_start(tile[idx], src[idx]).then_inc(loaded, 16)


def tile_buffers(ctx, nc, sb, layer, shapes):
    small = dict(stats=[T, 6], mv=[T, 2], rstd=[T, 2], hmax=[T, 16], hsum=[T, 16], hinv=[T, 16],
                 max8=[T, 8], repl=[T, 24], x=[T, C], hcur=[T, C], xT=[CK, 2, T])
    B = []
    for c in range(WAYS):
        one = {n: sb(ctx, f"L{layer}t{c}_{n}", s) for n, s in {**small, **shapes}.items()}
        B.append(one)
    ps = [ctx.enter_context(nc.psum_tensor(f"L{layer}ps{c}", [128, 2, 512], F32)) for c in range(WAYS)]
    return B, ps


def attention_shapes(H, D):
    HG = H // 2
    return dict(P=[T, H, NTOK], px=[T, H, T], pT=[128, H, T], kT=[CK, 2, T],
                qx=[CK, 2, IMGS * DIAG], V=[T, C])


def share(B, H):
    for b in B:
        b["kx"] = b["px"][0:CK, :, :].rearrange("p h n -> p (h n)").rearrange(
            "p (o j h m) -> p o j h m", o=2, j=IMGS, h=H // 2)
        b["oT"] = b["kT"]
        b["o"] = b["V"]


def take_experts_back(eng, kind, go, done, B, ps, h_all, yT_all, ident, tile_of):
    if kind == "pool":
        yield "y_cp"
        for c in done:
            go(c, "y_cp")
            eng.tensor_copy(B[c]["xT"][:, :, :], yT_all[:, :, bass.ds(tile_of(c) * T, T)]).then_inc(done[c], 1)
    if kind == "tensor":
        yield "y_tr"
        for c in done:
            go(c, "y_tr")
            for o in range(2):
                mm = eng.transpose(ps[c][0:T, 0, o * CK:(o + 1) * CK], B[c]["xT"][:, o, :], ident[0:CK, 0:CK])
            mm.then_inc(done[c], 1)
    if kind == "vector":
        yield "y_add"
        for c in done:
            go(c, "y_add")
            eng.tensor_tensor(B[c]["hcur"][:, :], ps[c][0:T, 0, 0:C],
                              h_all[:, bass.ds(tile_of(c), 1), :].rearrange("p a c -> p (a c)"),
                              ALU.add).then_inc(done[c], 1)


def width_product(pe, go, done, step, ps, bank, lhsT, rhs, N, at=0):
    yield step
    for c in done:
        go(c, step)
        for k in range(2):
            mm = pe.matmul(ps[c][0:T, bank, at:at + N], lhsT[c][:, k, :], rhs[:, k, 0:N], start=(k == 0), stop=(k == 1))
        mm.then_inc(done[c], 1)


def store_tile(pool, go, done, B, h_all, xT_all, tile_of, src):
    yield "h_st"
    for c in done:
        go(c, "h_st")
        pool.tensor_copy(h_all[:, bass.ds(tile_of(c), 1), :].rearrange("p a c -> p (a c)"),
                         B[c][src][:, :]).then_inc(done[c], 1)


def store_xT(pool, go, done, B, xT_all, tile_of):
    yield "x_st"
    for c in done:
        go(c, "x_st")
        pool.tensor_copy(xT_all[:, :, bass.ds(tile_of(c) * T, T)], B[c]["xT"][:, :, :]).then_inc(done[c], 1)


def weights_out(eng, kind, go, done, B, ps, combT, ident, tile_of, E):
    yield "c_tr"
    for c in done:
        if kind == "tensor":
            go(c, "c_tr")
            eng.transpose(ps[c][0:E, 0, 0:T], B[c]["comb"][:, 0:E], ident[0:T, 0:T]).then_inc(done[c], 1)
        else:
            go(c, "c_st")
            eng.copy(combT[0:E, bass.ds(tile_of(c) * T, T)], ps[c][0:E, 0, 0:T]).then_inc(done[c], 1)


EXP_LN = "natural_log_exp_and_others"
SILU_SIN = "silu_and_others"
GELU = {ACT.Gelu: "gelu_and_others", ACT.Gelu_apprx_tanh: "gelu_apprx_tanh_and_others"}
SINK = 7
ITERS = 10


def layer0_tokens(nc, d, K, h_all, xT_all, yT_all, combT, eps5, m10, ident, sem, sb, **_):
    H, D, HG, E = 12, 16, 6, 8
    S = steps("embed hcur " + ln_steps("n0") + turn_steps("f0") + "qv q_cp v_cp|q_sq q_ss q_floor q_log q_nrm q_add "
              "q_rc q_n q_tr q_dg k_cp kx0|kx1 S K_exp|v_one K_off it:%d " % (SINK * ITERS) +
              "T1 T2 rm rm_tr im ix ix_mm ir T3 T4 sm_exp sm_sum sm_inv " + SPREAD + "o " + turn_steps("fo") +
              "proj h1 h2 h_st|" + ln_steps("n1") + turn_steps("f1") + "x_st|gt g_cp g_mx g_sub g_exp g_sum g_rc "
              "g_p g_s g_gs " + topk_steps("gg") + "g_pen g_sm " + topk_steps("ge") + "g_w c_tr c_st")
    N = S["end"]
    done = {c: sem(f"l0_tile{c}_steps") for c in range(WAYS)}
    patch_loaded = [sem(f"l0_patch_loaded{c}") for c in range(WAYS)]
    zeroed, passed = sem("l0_zeroed"), sem("l0_passed")
    with ExitStack() as ctx:
        shapes = attention_shapes(H, D)
        shapes.update(patch=[128, 6, T], q=[T, H, D], vb=[T, H, NTOK], kv=[T, H, NTOK], small=[T, 8, 12],
                      MX=[12, IMGS, NTOK], MI=[12, 4], rmT=[12, T], lg=[T, 8], gs=[T, 12], gm=[T, 4], sv=[T, 16],
                      keys2=[T, 8], keys8=[T, 8], mask=[T, 8], comb=[T, 16], p=[T, 8], s=[T, 8])
        B, ps = tile_buffers(ctx, nc, sb, 0, shapes)
        share(B, H)
        for b in B:
            b["passed"] = passed
        X = [b["x"][:, :] for b in B]
        HC = [b["hcur"][:, :] for b in B]
        xT = [b["xT"] for b in B]
        oT = [b["oT"] for b in B]
        flat = [b["q"][:, :, :].rearrange("p h d -> p (h d)") for b in B]
        with nc.Block() as block:
            @block.sync
            def _(sp):
                for c in done:
                    sp.dma_start(B[c]["patch"][:, :, :].rearrange("p k t -> p (k t)"),
                                 d["patches"][c, :, :]).then_inc(patch_loaded[c], 16)
                def fetch(i, done):
                    for c in done:
                        sp.wait_ge(done[c], i * N - (N - S["embed"] - 2))
                        sp.dma_start(B[c]["patch"][:, :, :].rearrange("p k t -> p (k t)"),
                                     d["patches"][bass.ds(WAYS * i + c, 1), :, :].rearrange("a p x -> (a p) x")
                                     ).then_inc(patch_loaded[c], 16)
                with sp.Fori(1, NT // WAYS) as i:
                    fetch(i, done)
                fetch(NT // WAYS, first_tiles(done))

            @block.vector
            def _(dve):
                for c in done:
                    dve.memset(B[c]["qx"][:, :, :], 0.0)
                    dve.memset(B[c]["gs"][:, 4:12], PAD)
                    dve.memset(B[c]["sv"][:, 8:16], PAD)
                    dve.memset(B[c]["keys2"][:, :], PAD)
                    dve.memset(B[c]["keys8"][:, :], PAD)
                    ins = dve.memset(B[c]["comb"][:, 8:16], 1.0)
                ins.then_inc(zeroed, 1)
                dve.wait_ge(zeroed, 1)
                for c in done:
                    dve.sem_inc(done[c], 1)
                def turn(i, done):
                    def go(c, step, passed=None):
                        dve.wait_ge(done[c], i * N + (S[step] + 1))
                        if passed is not None:
                            dve.sem_inc(passed, 1)

                    yield "hcur"
                    for c in done:
                        go(c, "hcur")
                        dve.tensor_tensor(HC[c], ps[c][0:T, 0, 0:C], K["tok_add"][:, :], ALU.add).then_inc(done[c], 1)
                    yield from norm_vector(dve, go, done, B, "n0", HC, X)
                    yield "q_sq"
                    for c in done:
                        go(c, "q_sq")
                        dve.tensor_tensor(B[c]["kv"][:, :, 0:D], B[c]["q"][:, :, :], B[c]["q"][:, :, :],
                                          ALU.mult).then_inc(done[c], 1)
                    yield "q_ss"
                    for c in done:
                        go(c, "q_ss")
                        dve.tensor_reduce(B[c]["small"][:, 0, :], B[c]["kv"][:, :, 0:D], AX.X, ALU.add).then_inc(done[c], 1)
                    yield "q_floor"
                    for c in done:
                        go(c, "q_floor")
                        dve.tensor_scalar(B[c]["small"][:, 1, :], B[c]["small"][:, 0, :], 1e-19, None, ALU.max
                                          ).then_inc(done[c], 1)
                    yield "q_add"
                    for c in done:
                        go(c, "q_add")
                        dve.tensor_scalar(B[c]["small"][:, 3, :], B[c]["small"][:, 2, :], 1e-8, None, ALU.add
                                          ).then_inc(done[c], 1)
                    yield "q_rc"
                    for c in done:
                        go(c, "q_rc")
                        dve.reciprocal(B[c]["small"][:, 4, :], B[c]["small"][:, 3, :]).then_inc(done[c], 1)
                    yield "q_n"
                    for c in done:
                        go(c, "q_n")
                        dve.tensor_tensor(B[c]["q"][:, :, :], B[c]["q"][:, :, :],
                                          over(B[c]["small"][:, 4, :].unsqueeze(2), [T, H, D]), ALU.mult
                                          ).then_inc(done[c], 1)
                    yield "k_cp"
                    for c in done:
                        go(c, "k_cp")
                        dve.tensor_copy(B[c]["kT"][:, :, :].rearrange("p o t -> p (o t)"), ps[c][0:CK, 1, 0:2 * T]
                                        ).then_inc(done[c], 1)
                    yield from heads_expand(dve, go, done, B, "kx0", 0, HG, K["hmask16"])
                    yield "v_one"
                    for c in done:
                        go(c, "v_one")
                        dve.memset(B[c]["vb"][:, :, :], 1.0).then_inc(done[c], 1)
                    yield "K_off"
                    for c in done:
                        go(c, "K_off")
                        dve.tensor_tensor(B[c]["P"][:, :, :], B[c]["P"][:, :, :],
                                          over(K["off_diag"][:, :].unsqueeze(1), [T, H, NTOK]), ALU.mult
                                          ).then_inc(done[c], 1)
                    with dve.Fori(0, ITERS) as r:
                        def at(c, k):
                            dve.wait_ge(done[c], i * N + r * SINK + (S["it"] + 1 + k))
                        for pair in two_by_two(done):
                            for c in pair:
                                at(c, 0)
                                dve.tensor_tensor(B[c]["kv"][:, :, :], B[c]["P"][:, :, :], B[c]["vb"][:, :, :],
                                                  ALU.mult).then_inc(done[c], 1)
                            for c in pair:
                                at(c, 1)
                                dve.tensor_reduce(B[c]["small"][:, 5, :], B[c]["kv"][:, :, :], AX.X, ALU.add
                                                  ).then_inc(done[c], 1)
                            for c in pair:
                                at(c, 2)
                                dve.reciprocal(B[c]["small"][:, 6, :], B[c]["small"][:, 5, :]).then_inc(done[c], 1)
                    yield "T1"
                    for c in done:
                        go(c, "T1")
                        dve.tensor_tensor(B[c]["kv"][:, :, :], B[c]["P"][:, :, :], B[c]["vb"][:, :, :], ALU.mult
                                          ).then_inc(done[c], 1)
                    yield "T2"
                    for c in done:
                        go(c, "T2")
                        dve.tensor_tensor(B[c]["kv"][:, :, :], B[c]["kv"][:, :, :],
                                          over(B[c]["small"][:, 6, :].unsqueeze(2), [T, H, NTOK]), ALU.mult
                                          ).then_inc(done[c], 1)
                    yield "rm"
                    for c in done:
                        go(c, "rm")
                        dve.tensor_reduce(B[c]["small"][:, 0, :], B[c]["kv"][:, :, :], AX.X, ALU.max).then_inc(done[c], 1)
                    yield "im"
                    for c in done:
                        go(c, "im")
                        dve.tensor_reduce(B[c]["MI"][:, 0:IMGS],
                                          ps[c][0:H, 0, 0:T].rearrange("p (j n) -> p j n", n=NTOK), AX.X, ALU.max
                                          ).then_inc(done[c], 1)
                    yield "ix"
                    for c in done:
                        go(c, "ix")
                        dve.tensor_copy(B[c]["MX"][:, :, :], over(B[c]["MI"][:, 0:IMGS].unsqueeze(2),
                                                                  [H, IMGS, NTOK])).then_inc(done[c], 1)
                    yield "ir"
                    for c in done:
                        go(c, "ir")
                        dve.reciprocal(B[c]["small"][:, 1, :], ps[c][0:T, 1, 0:H]).then_inc(done[c], 1)
                    yield "T3"
                    for c in done:
                        go(c, "T3")
                        dve.tensor_tensor(B[c]["kv"][:, :, :], B[c]["kv"][:, :, :],
                                          over(B[c]["small"][:, 1, :].unsqueeze(2), [T, H, NTOK]), ALU.mult
                                          ).then_inc(done[c], 1)
                    yield "T4"
                    for c in done:
                        go(c, "T4")
                        dve.tensor_tensor(B[c]["P"][:, :, :], B[c]["kv"][:, :, :],
                                          over(K["on_diag"][:, :].unsqueeze(1), [T, H, NTOK]), ALU.add
                                          ).then_inc(done[c], 1)
                    yield from sums_vector(dve, go, done, B, H)
                    yield from blocks_expand(dve, go, done, B, "px0", 0, 8, K["bmask"])
                    yield from probs_copy(dve.tensor_copy, go, done, B, ps, "pc1", 1, 4)
                    yield "o"
                    for c in done:
                        go(c, "o")
                        dve.tensor_tensor(B[c]["o"][:, :].rearrange("p (h d) -> p h d", d=D),
                                          ps[c][0:T, 0, 0:C].rearrange("p (h d) -> p h d", d=D),
                                          over(B[c]["hinv"][:, 0:H].unsqueeze(2), [T, H, D]), ALU.mult
                                          ).then_inc(done[c], 1)
                    yield "h1"
                    for c in done:
                        go(c, "h1")
                        dve.tensor_tensor(HC[c], HC[c], ps[c][0:T, 0, 0:C], ALU.add).then_inc(done[c], 1)
                    yield "h2"
                    for c in done:
                        go(c, "h2")
                        dve.tensor_tensor(HC[c], HC[c], K["l0_bproj"][:, :], ALU.add).then_inc(done[c], 1)
                    yield from norm_vector(dve, go, done, B, "n1", HC, X)
                    yield "g_cp"
                    for c in done:
                        go(c, "g_cp")
                        dve.tensor_copy(B[c]["lg"][:, :], ps[c][0:T, 1, 0:E]).then_inc(done[c], 1)
                    yield "g_mx"
                    for c in done:
                        go(c, "g_mx")
                        dve.tensor_reduce(B[c]["mv"][:, 0:1], B[c]["lg"][:, :], AX.X, ALU.max).then_inc(done[c], 1)
                    yield "g_sub"
                    for c in done:
                        go(c, "g_sub")
                        dve.tensor_scalar(B[c]["lg"][:, :], B[c]["lg"][:, :], B[c]["mv"][:, 0:1], None, ALU.subtract
                                          ).then_inc(done[c], 1)
                    yield "g_sum"
                    for c in done:
                        go(c, "g_sum")
                        dve.tensor_reduce(B[c]["mv"][:, 0:1], B[c]["lg"][:, :], AX.X, ALU.add).then_inc(done[c], 1)
                    yield "g_rc"
                    for c in done:
                        go(c, "g_rc")
                        dve.reciprocal(B[c]["mv"][:, 1:2], B[c]["mv"][:, 0:1]).then_inc(done[c], 1)
                    yield "g_p"
                    for c in done:
                        go(c, "g_p")
                        dve.tensor_scalar(B[c]["p"][:, :], B[c]["lg"][:, :], B[c]["mv"][:, 1:2], None, ALU.mult
                                          ).then_inc(done[c], 1)
                    yield "g_s"
                    for c in done:
                        go(c, "g_s")
                        dve.tensor_tensor(B[c]["s"][:, :], B[c]["p"][:, :], K["l0_gate_b"][:, :], ALU.add
                                          ).then_inc(done[c], 1)
                    yield "g_gs"
                    for c in done:
                        go(c, "g_gs")
                        pair = B[c]["s"][:, :].rearrange("p (g e) -> p g e", e=2)
                        dve.tensor_tensor(B[c]["gs"][:, 0:4], pair[:, :, 0], pair[:, :, 1], ALU.add).then_inc(done[c], 1)
                    yield from topk_vector(dve, go, done, B, "gg", "gs", "keys2", 2, 4, [b["gm"][:, :] for b in B])
                    yield "g_pen"
                    for c in done:
                        go(c, "g_pen")
                        dve.tensor_scalar(B[c]["gm"][:, :], B[c]["gm"][:, :], BIG, -BIG, ALU.mult, ALU.add
                                          ).then_inc(done[c], 1)
                    yield "g_sm"
                    for c in done:
                        go(c, "g_sm")
                        dve.tensor_tensor(B[c]["sv"][:, 0:8].rearrange("p (g e) -> p g e", e=2),
                                          B[c]["s"][:, :].rearrange("p (g e) -> p g e", e=2),
                                          over(B[c]["gm"][:, :].unsqueeze(2), [T, 4, 2]), ALU.add).then_inc(done[c], 1)
                    yield from topk_vector(dve, go, done, B, "ge", "sv", "keys8", 2, 8, [b["mask"][:, :] for b in B])
                    yield "g_w"
                    for c in done:
                        go(c, "g_w")
                        dve.tensor_tensor(B[c]["comb"][:, 0:8], B[c]["p"][:, :], B[c]["mask"][:, :], ALU.mult
                                          ).then_inc(done[c], 1)

                with dve.Fori(0, NT // WAYS) as i:
                    run(turn(i, done))
                run(turn(NT // WAYS, first_tiles(done)))

            @block.scalar
            def _(act):
                act.preload_act_table_set(EXP_LN)
                def turn(i, done):
                    def go(c, step):
                        act.wait_ge(done[c], i * N + (S[step] + 1))

                    def tile_of(c):
                        return WAYS * i + c
                    yield from norm_scalar(act, go, done, B, "n0", eps5[0:T, :])
                    yield from turn_scalar(act, go, done, "f0", ps, 1, xT)
                    yield "q_cp"
                    for c in done:
                        go(c, "q_cp")
                        act.copy(flat[c], ps[c][0:T, 0, 0:C]).then_inc(done[c], 1)
                        go(c, "v_cp")
                        act.copy(B[c]["V"][:, :], ps[c][0:T, 0, C:2 * C]).then_inc(done[c], 1)
                    yield "q_log"
                    for c in done:
                        go(c, "q_log")
                        act.activation(B[c]["small"][:, 2, :], B[c]["small"][:, 1, :], ACT.Ln).then_inc(done[c], 1)
                    yield "q_nrm"
                    for c in done:
                        go(c, "q_nrm")
                        act.activation(B[c]["small"][:, 2, :], B[c]["small"][:, 2, :], ACT.Exp, scale=0.5
                                       ).then_inc(done[c], 1)
                    yield from query_blocks(act, go, done, B, ps, "q_dg", 1)
                    yield "K_exp"
                    for c in done:
                        go(c, "K_exp")
                        act.activation(B[c]["P"][:, :, :].rearrange("p h m -> p (h m)"),
                                       ps[c][0:T, 0, 0:H * NTOK], ACT.Exp, bias=m10[0:T, :], scale=10.0
                                       ).then_inc(done[c], 1)
                    with act.Fori(0, ITERS) as r:
                        def at(c, k):
                            act.wait_ge(done[c], i * N + r * SINK + (S["it"] + 1 + k))
                        for c in done:
                            at(c, 5)
                            act.activation(B[c]["vb"][:, :, :].rearrange("p h m -> p (h m)"),
                                           ps[c][0:T, 1, 0:H * NTOK], ACT.Ln).then_inc(done[c], 1)
                            at(c, 6)
                            act.activation(B[c]["vb"][:, :, :], B[c]["vb"][:, :, :], ACT.Exp, scale=-1.0
                                           ).then_inc(done[c], 1)
                    yield "sm_exp"
                    for c in done:
                        go(c, "sm_exp")
                        act.activation(B[c]["P"][:, :, :], B[c]["P"][:, :, :], ACT.Exp,
                                       bias=K["quarter"][0:T, :], scale=D ** -0.5).then_inc(done[c], 1)
                    yield from probs_copy(act.copy, go, done, B, ps, "pc0", 0, 0)
                    yield from probs_copy(act.copy, go, done, B, ps, "pc2", 0, 8)
                    yield from turn_scalar(act, go, done, "fo", ps, 1, oT)
                    yield from norm_scalar(act, go, done, B, "n1", eps5[0:T, :])
                    yield from turn_scalar(act, go, done, "f1", ps, 0, xT)
                    yield "g_exp"
                    for c in done:
                        go(c, "g_exp")
                        act.activation(B[c]["lg"][:, :], B[c]["lg"][:, :], ACT.Exp).then_inc(done[c], 1)
                    yield from weights_out(act, "scalar", go, done, B, ps, combT, ident, tile_of, E + 1)

                with act.Fori(0, NT // WAYS) as i:
                    run(turn(i, done))
                run(turn(NT // WAYS, first_tiles(done)))

            @block.gpsimd
            def _(pool):
                def turn(i, done):
                    def go(c, step):
                        pool.wait_ge(done[c], i * N + (S[step] + 1))

                    def tile_of(c):
                        return WAYS * i + c
                    yield from heads_expand(pool, go, done, B, "kx1", 1, HG, K["hmask16"])
                    with pool.Fori(0, ITERS) as r:
                        for c in done:
                            pool.wait_ge(done[c], i * N + r * SINK + (S["it"] + 1 + 3))
                            pool.tensor_tensor(B[c]["kv"][:, :, :], B[c]["P"][:, :, :],
                                               over(B[c]["small"][:, 6, :].unsqueeze(2), [T, H, NTOK]), ALU.mult
                                               ).then_inc(done[c], 1)
                    yield from blocks_expand(pool, go, done, B, "px1", 8, H, K["bmask"])
                    yield from store_tile(pool, go, done, B, h_all, xT_all, tile_of, "hcur")
                    yield from store_xT(pool, go, done, B, xT_all, tile_of)

                with pool.Fori(0, NT // WAYS) as i:
                    run(turn(i, done))
                run(turn(NT // WAYS, first_tiles(done)))

            @block.tensor
            def _(pe):
                def turn(i, done):
                    def go(c, step):
                        pe.wait_ge(done[c], i * N + (S[step] + 1))

                    def tile_of(c):
                        return WAYS * i + c
                    yield "embed"
                    for c in done:
                        pe.wait_ge(patch_loaded[c], 16 * i + 16)
                        go(c, "embed")
                        for k in range(6):
                            mm = pe.matmul(ps[c][0:T, 0, 0:C], B[c]["patch"][:, k, :], K["tok_w"][:, k, :],
                                           start=(k == 0), stop=(k == 5))
                        mm.then_inc(done[c], 1)
                    yield from turn_tensor(pe, go, done, "f0", X, ps, 1, ident)
                    yield from width_product(pe, go, done, "qv", ps, 0, xT, K["l0_wqv"], 2 * C)
                    yield from turn_tensor_named(pe, go, done, "q_tr", flat, ps, 1, ident)
                    yield from scores_tensor(pe, go, done, B, ps, HG)
                    with pe.Fori(0, ITERS) as r:
                        for c in done:
                            pe.wait_ge(done[c], i * N + r * SINK + (S["it"] + 1 + 4))
                            pe.matmul(ps[c][0:T, 1, 0:H * NTOK], K["bmask"][:, :],
                                      B[c]["kv"][:, :, :].rearrange("p h m -> p (h m)"), start=True, stop=True
                                      ).then_inc(done[c], 1)
                    yield "rm_tr"
                    for c in done:
                        go(c, "rm_tr")
                        pe.transpose(ps[c][0:H, 0, 0:T], B[c]["small"][:, 0, :], ident[0:T, 0:T]).then_inc(done[c], 1)
                    yield "ix_mm"
                    for c in done:
                        go(c, "ix_mm")
                        pe.matmul(ps[c][0:T, 1, 0:H], B[c]["MX"][:, :, :].rearrange("p j n -> p (j n)"),
                                  ident[0:H, 0:H], start=True, stop=True).then_inc(done[c], 1)
                    yield from values_stage(pe, go, done, B, ps, H, D, [b["V"] for b in B], H, ident)
                    yield from turn_tensor(pe, go, done, "fo", [b["o"][:, :] for b in B], ps, 1, ident)
                    yield from width_product(pe, go, done, "proj", ps, 0, oT, K["l0_wproj"], C)
                    yield from turn_tensor(pe, go, done, "f1", X, ps, 0, ident)
                    yield from width_product(pe, go, done, "gt", ps, 1, xT, K["l0_gate_w"], E)
                    yield from weights_out(pe, "tensor", go, done, B, ps, combT, ident, tile_of, E + 1)

                with pe.Fori(0, NT // WAYS) as i:
                    run(turn(i, done))
                run(turn(NT // WAYS, first_tiles(done)))


def turn_tensor_named(pe, go, done, step, src, ps, bank, ident):
    yield step
    for c in done:
        go(c, step)
        for o in range(2):
            mm = pe.transpose(ps[c][0:CK, bank, o * T:(o + 1) * T], src[c][:, o * CK:(o + 1) * CK],
                              ident[0:T, 0:T])
        mm.then_inc(done[c], 1)


def rounded(ap):
    return ap.bitcast(F32R)


def split_product(pe, out_, w, x, start, stop):
    (wh, wl), (xh, xl) = w, x
    pe.matmul(out_, rounded(wh), rounded(xh), start=start, stop=False)
    pe.matmul(out_, rounded(wh), rounded(xl), start=False, stop=False)
    return pe.matmul(out_, rounded(wl), rounded(xh), start=False, stop=stop)


class ExpertPhase:

    def __init__(self, ctx, layer, E, w1_cols, w2_rows, w2_tiles, ahead, nc, d, xT_all, yT_all, combT, sem, sb, ident):
        nm = f"l{layer}e_"
        self.E, self.ahead, self.ident, self.yT_all = E, ahead, ident, yT_all
        self.w1_d, self.w2_d = d[f"l{layer}_w1"], d[f"l{layer}_w2"]
        self.raw_loaded = sem(nm + "raw_loaded")
        self.high_ready = sem(nm + "high_ready")
        self.weights_ready = sem(nm + "weights_ready")
        self.ahead_loaded = sem(nm + "ahead_loaded")
        self.cleared = sem(nm + "cleared")
        self.x_high = sem(nm + "x_high")
        self.x_split = sem(nm + "x_split")
        self.out_done = sem(nm + "out_done")
        self.passed = sem(nm + "passed")
        self.raw1 = sb(ctx, nm + "raw1", [CK, 2, w1_cols])
        self.raw2 = sb(ctx, nm + "raw2", [w2_rows, w2_tiles, C])
        self.w1 = [[sb(ctx, nm + f"w1_{s}{part}", [CK, 2, w1_cols]) for part in ("high", "low")] for s in (0, 1)]
        self.w2 = [[sb(ctx, nm + f"w2_{s}{part}", [w2_rows, w2_tiles, C]) for part in ("high", "low")] for s in (0, 1)]
        self.select = [sb(ctx, nm + f"select{s}", [E, CK]) for s in (0, 1)]
        self.xT_all, self.combT = xT_all, combT
        self.x = [sb(ctx, nm + f"x_{part}_part", [CK, 2, NP]) for part in ("high", "low")]

    def fetch(self, sp, e):
        sp.dma_start(self.raw1[:, :, :].rearrange("p k m -> p (k m)"),
                     self.w1_d[e, :, :].rearrange("a p x -> (a p) x")).then_inc(self.raw_loaded, 16)
        sp.dma_start(self.raw2[:, :, :].rearrange("p k m -> p (k m)"),
                     self.w2_d[e, :, :].rearrange("a p x -> (a p) x")).then_inc(self.raw_loaded, 16)

    def sync_program(self, sp):
        self.fetch(sp, slice(0, 1))
        start_loads(sp, self.ahead, self.ahead_loaded)
        with sp.Fori(1, self.E) as e:
            sp.wait_ge(self.weights_ready, e)
            self.fetch(sp, bass.ds(e, 1))
        if self.ahead:
            sp.wait_ge(self.ahead_loaded, 16 * len(self.ahead))

    def split_weights(self, pool, s, e, n):
        pool.wait_ge(self.raw_loaded, 32 * n + 32)
        pool.sem_inc(self.passed, 1)
        pool.tensor_copy(rounded(self.w1[s][0][:, :, :]), self.raw1[:, :, :])
        pool.tensor_copy(rounded(self.w2[s][0][:, :, :]), self.raw2[:, :, :]).then_inc(self.high_ready, 1)
        pool.tensor_copy(self.select[s][:, :], over(self.ident[0:self.E, e], [self.E, CK]))
        pool.wait_ge(self.high_ready, n + 1)
        pool.tensor_tensor(rounded(self.w1[s][1][:, :, :]), self.raw1[:, :, :], self.w1[s][0][:, :, :], ALU.subtract)
        pool.tensor_tensor(rounded(self.w2[s][1][:, :, :]), self.raw2[:, :, :], self.w2[s][0][:, :, :], ALU.subtract
                           ).then_inc(self.weights_ready, 1)

    def pool_program(self, pool):
        for s in (0, 1):
            self.split_weights(pool, s, slice(s, s + 1), s)
            if s == 0:
                pool.memset(self.yT_all[:, :, :], 0.0).then_inc(self.cleared, 1)
        with pool.Fori(1, self.E // 2) as q:
            for s in (0, 1):
                pool.wait_ge(self.out_done, 2 * NB * q + (NB * s - NB + 1))
                self.split_weights(pool, s, bass.ds(2 * q + s, 1), 2 * q + s)
        if self.E % 2:
            pool.wait_ge(self.out_done, NB * (self.E - 2) + 1)
            self.split_weights(pool, 0, slice(self.E - 1, self.E), self.E - 1)

    def high_tokens(self, act):
        for b in range(NB):
            cols = slice(b * UB, (b + 1) * UB)
            act.copy(rounded(self.x[0][:, :, cols]), self.xT_all[:, :, cols]).then_inc(self.x_high, 1)

    def low_tokens(self, dve):
        for b in range(NB):
            cols = slice(b * UB, (b + 1) * UB)
            dve.wait_ge(self.x_high, b + 1)
            dve.tensor_tensor(rounded(self.x[1][:, :, cols]), self.xT_all[:, :, cols], self.x[0][:, :, cols],
                              ALU.subtract).then_inc(self.x_split, 1)

    def spread_products(self, pe, s, out_, cols):
        return pe.matmul(out_, self.select[s][:, :], self.combT[0:self.E, cols], start=True, stop=True)

    def w1_parts(self, s, k, lo, hi):
        return [w[:, k, lo:hi] for w in self.w1[s]]

    def w2_parts(self, s, m, o):
        return [w[:, m, o * CK:(o + 1) * CK] for w in self.w2[s]]

    def x_parts(self, k, cols):
        return [x[:, k, cols] for x in self.x]


def experts_gelu(layer, func, ahead, nc, d, K, xT_all, yT_all, combT, sem, sb, ident, **_):
    E, M = 8, 6
    nm = f"l{layer}e_"
    spread_done = sem(nm + "spread_done")
    spread_copied = sem(nm + "spread_copied")
    hidden_done = sem(nm + "hidden_done")
    hidden_read = sem(nm + "hidden_read")
    hidden_high = sem(nm + "hidden_high")
    hidden_split = sem(nm + "hidden_split")
    out_read = sem(nm + "out_read")
    summed = sem(nm + "summed")
    with ExitStack() as ctx:
        phase = ExpertPhase(ctx, layer, E, 128 * M, 128, M, ahead, nc, d, xT_all, yT_all, combT, sem, sb, ident)
        out_done = phase.out_done
        hidden = sb(ctx, nm + "hidden", [128, 2, UB])
        act_out = [sb(ctx, nm + f"act_out_{part}", [128, M, UB]) for part in ("high", "low")]
        spread = sb(ctx, nm + "spread", [CK, UB])
        part = sb(ctx, nm + "part", [CK, 2, UB])
        psH = ctx.enter_context(nc.psum_tensor(nm + "psH", [128, 3, 512], F32))
        psY = ctx.enter_context(nc.psum_tensor(nm + "psY", [128, 2, 512], F32))
        psS = ctx.enter_context(nc.psum_tensor(nm + "psS", [128, 512], F32))
        with nc.Block() as block:
            @block.sync
            def _(sp):
                phase.sync_program(sp)

            @block.gpsimd
            def _(pool):
                phase.pool_program(pool)

            @block.tensor
            def _(pe):
                pe.sem_inc(out_done, 1)
                pe.wait_ge(phase.x_split, NB)
                with pe.Fori(0, E // 2) as q:
                    for s in (0, 1):
                        pe.wait_ge(phase.weights_ready, 2 * q + (s + 1))
                        pe.sem_inc(phase.passed, 1)
                        with pe.Fori(0, NB) as b:
                            n = 2 * NB * q + b + s * NB
                            cols = bass.ds(b * UB, UB)
                            pe.wait_ge(spread_copied, n + 1)
                            phase.spread_products(pe, s, psS[0:CK, 0:UB], cols).then_inc(spread_done, 1)
                            for m in range(M):
                                pe.wait_ge(hidden_read, M * n + (m + 1))
                                for k in range(2):
                                    mm = split_product(pe, psH[:, m % 3, 0:UB],
                                                       phase.w1_parts(s, k, m * 128, (m + 1) * 128),
                                                       phase.x_parts(k, cols), start=(k == 0), stop=(k == 1))
                                mm.then_inc(hidden_done, 1)
                            pe.wait_ge(out_read, n + 1)
                            for m in range(M):
                                pe.wait_ge(hidden_split, M * n + (m + 3))
                                for o in range(2):
                                    mm = split_product(pe, psY[0:CK, o, 0:UB], phase.w2_parts(s, m, o),
                                                       [a[:, m, :] for a in act_out],
                                                       start=(m == 0), stop=(m == M - 1))
                            mm.then_inc(out_done, 1)

            @block.scalar
            def _(act):
                act.preload_act_table_set(GELU[func])
                phase.high_tokens(act)
                act.sem_inc(hidden_read, 3)
                act.sem_inc(spread_copied, 1)
                with act.Fori(0, E) as e:
                    with act.Fori(0, NB) as b:
                        n = NB * e + b
                        act.wait_ge(spread_done, n + 1)
                        act.wait_ge(out_read, n + 1)
                        act.copy(spread[:, :], psS[0:CK, 0:UB]).then_inc(spread_copied, 1)
                        for m in range(M):
                            act.wait_ge(hidden_done, M * n + (m + 1))
                            act.wait_ge(hidden_split, M * n + (m + 1))
                            act.activation(hidden[:, m % 2, :], psH[:, m % 3, 0:UB], func).then_inc(hidden_read, 1)

            @block.vector
            def _(dve):
                phase.low_tokens(dve)
                dve.sem_inc(hidden_split, 2)
                dve.sem_inc(out_read, 1)
                dve.sem_inc(summed, 1)
                dve.wait_ge(phase.cleared, 1)
                with dve.Fori(0, E) as e:
                    with dve.Fori(0, NB) as b:
                        n = NB * e + b
                        y = yT_all[:, :, bass.ds(b * UB, UB)]
                        dve.wait_ge(out_done, n + 1)
                        for m in range(M):
                            dve.wait_ge(hidden_read, M * n + (m + 4))
                            dve.tensor_copy(rounded(act_out[0][:, m, :]), hidden[:, m % 2, :]).then_inc(hidden_high, 1)
                            dve.wait_ge(hidden_high, M * n + (m + 1))
                            dve.tensor_tensor(rounded(act_out[1][:, m, :]), hidden[:, m % 2, :], act_out[0][:, m, :],
                                              ALU.subtract).then_inc(hidden_split, 1)
                        dve.wait_ge(out_done, n + 2)
                        dve.wait_ge(spread_copied, n + 2)
                        dve.wait_ge(summed, n + 1)
                        dve.tensor_tensor(part[:, :, :], psY[0:CK, :, 0:UB],
                                          over(spread[:, :].unsqueeze(1), [CK, 2, UB]), ALU.mult).then_inc(out_read, 1)
                        dve.wait_ge(out_read, n + 2)
                        dve.tensor_tensor(y, y, part[:, :, :], ALU.add).then_inc(summed, 1)
                dve.wait_ge(summed, E * NB + 1)


def experts_swiglu(layer, E, ahead, nc, d, K, xT_all, yT_all, combT, sem, sb, ident, **_):
    gated = layer == 0
    A = 1 if gated else 2
    HB = 4
    b_d = d[f"l{layer}_b"]
    nm = f"l{layer}e_"
    spread_done = sem(nm + "spread_done")
    spread_copied = sem(nm + "spread_copied")
    hidden_done = sem(nm + "hidden_done")
    third_done = sem(nm + "third_done")
    third_ready = sem(nm + "third_ready")
    hidden_read = sem(nm + "hidden_read")
    gate_ready = sem(nm + "gate_ready")
    silu_ready = sem(nm + "silu_ready")
    lin_ready = sem(nm + "lin_ready")
    glu_ready = sem(nm + "glu_ready")
    glu_high = sem(nm + "glu_high")
    glu_split = sem(nm + "glu_split")
    out_read = sem(nm + "out_read")
    summed = sem(nm + "summed")
    W1N = 384
    NBIAS = 6
    with ExitStack() as ctx:
        phase = ExpertPhase(ctx, layer, E, W1N, CK, A, ahead, nc, d, xT_all, yT_all, combT, sem, sb, ident)
        out_done = phase.out_done
        bias = sb(ctx, nm + "bias", [CK, E, NBIAS])
        bcur = [sb(ctx, nm + f"bcur{k}", [CK, NBIAS]) for k in range(4)]
        gate = sb(ctx, nm + "gate", [CK, A, UB])
        lin = sb(ctx, nm + "lin", [CK, A, UB])
        third = sb(ctx, nm + "third", [CK, 2, UB])
        prod = sb(ctx, nm + "prod", [CK, 2, UB])
        silu = sb(ctx, nm + "silu", [CK, A, UB])
        glu = sb(ctx, nm + "glu", [CK, A, UB])
        glu_parts = [sb(ctx, nm + f"glu_{part}", [CK, A, UB]) for part in ("high", "low")]
        spread = sb(ctx, nm + "spread", [CK, UB])
        part = sb(ctx, nm + "part", [CK, 2, UB])
        psH = ctx.enter_context(nc.psum_tensor(nm + "psH", [128, HB, 512], F32))
        psY = ctx.enter_context(nc.psum_tensor(nm + "psY", [128, 2, 512], F32))
        psS = ctx.enter_context(nc.psum_tensor(nm + "psS", [128, 512], F32))
        bias_loaded = sem(nm + "bias_loaded")
        bias_cur = [sem(nm + f"bias_cur{k}") for k in range(2)]
        pairs, tail = E // 2, E % 2
        full_pairs = pairs if tail else pairs - 1
        slots = [0] if tail else [0, 1]
        first = 2 * full_pairs
        with nc.Block() as block:
            @block.sync
            def _(sp):
                sp.dma_start(bias[:, :, :], b_d[:, :, :]).then_inc(bias_loaded, 16)
                phase.sync_program(sp)

            @block.gpsimd
            def _(pool):
                phase.pool_program(pool)

            def first_products(pe, n, s, cols):
                if gated:
                    pe.wait_ge(third_ready, n + 1)
                    for col in (2, 3):
                        for k in range(2):
                            mm = split_product(pe, psH[0:CK, col, 0:UB], phase.w1_parts(s, k, col * CK, (col + 1) * CK),
                                               phase.x_parts(k, cols), start=(k == 0), stop=(k == 1))
                    mm.then_inc(third_done, 1)
                for a in range(A):
                    pe.wait_ge(hidden_read, A * n + (a + 1))
                    for col in (a, A + a):
                        for k in range(2):
                            mm = split_product(pe, psH[0:CK, col, 0:UB], phase.w1_parts(s, k, col * CK, (col + 1) * CK),
                                               phase.x_parts(k, cols), start=(k == 0), stop=(k == 1))
                    mm.then_inc(hidden_done, 1)

            def second_products(pe, n, s, cols):
                pe.wait_ge(spread_copied, n + 1)
                phase.spread_products(pe, s, psS[0:CK, 0:UB], cols).then_inc(spread_done, 1)
                pe.wait_ge(out_read, n + 1)
                for a in range(A):
                    pe.wait_ge(glu_split, A * n + (a + 1 + A))
                    for o in range(2):
                        mm = split_product(pe, psY[0:CK, o, 0:UB], phase.w2_parts(s, a, o),
                                           [g[:, a, :] for g in glu_parts], start=(a == 0), stop=(a == A - 1))
                mm.then_inc(out_done, 1)

            def expert_products(pe, e, s, last):
                with pe.Fori(0, NB - 1) as b:
                    first_products(pe, NB * e + b + 1, s, bass.ds(b * UB + UB, UB))
                    second_products(pe, NB * e + b, s, bass.ds(b * UB, UB))
                if not last:
                    pe.wait_ge(phase.weights_ready, e + 2)
                    pe.sem_inc(phase.passed, 1)
                    first_products(pe, NB * e + NB, 1 - s, slice(0, UB))
                second_products(pe, NB * e + (NB - 1), s, slice((NB - 1) * UB, NB * UB))

            @block.tensor
            def _(pe):
                pe.sem_inc(out_done, 1)
                pe.wait_ge(phase.x_split, NB)
                pe.wait_ge(phase.weights_ready, 1)
                first_products(pe, 0, 0, slice(0, UB))
                with pe.Fori(0, full_pairs) as q:
                    for s in (0, 1):
                        expert_products(pe, 2 * q + s, s, last=False)
                for s in slots:
                    expert_products(pe, first + s, s, last=(s == slots[-1]))

            def scalar_first(act, n, s):
                if gated:
                    act.wait_ge(third_done, n + 1)
                    act.wait_ge(hidden_read, n + 1)
                    for col in range(2):
                        ins = act.activation(third[:, col, :], psH[0:CK, 2 + col, 0:UB], ACT.Identity,
                                             bias=bcur[2 + s][:, 2 + col:3 + col])
                    ins.then_inc(third_ready, 1)

            def scalar_second(act, n):
                for a in range(A):
                    act.wait_ge(gate_ready, A * n + (a + 1))
                    act.wait_ge(glu_ready, A * n + (a + 1))
                    act.activation(silu[:, a, :], gate[:, a, :], ACT.Silu, scale=ALPHA).then_inc(silu_ready, 1)
                for a in range(A):
                    act.wait_ge(glu_ready, A * n + (a + 1 + A))
                    act.wait_ge(out_done, n + 1)
                    act.copy(rounded(glu_parts[0][:, a, :]), glu[:, a, :]).then_inc(glu_high, 1)

            def scalar_spread(act, n):
                act.wait_ge(spread_done, n + 1)
                act.wait_ge(out_read, n + 1)
                act.copy(spread[:, :], psS[0:CK, 0:UB]).then_inc(spread_copied, 1)

            def scalar_bias(act, e, s):
                if gated:
                    act.wait_ge(third_ready, NB * e + 1)
                    act.copy(bcur[2 + s][:, :], bias[:, bass.ds(e, 1), :].rearrange("p a x -> p (a x)")
                             ).then_inc(bias_cur[1], 1)
                    act.wait_ge(bias_cur[1], e + 1)

            @block.scalar
            def _(act):
                phase.high_tokens(act)
                act.sem_inc(spread_copied, 1)
                if gated:
                    act.sem_inc(third_ready, 1)
                act.wait_ge(bias_loaded, 16)
                scalar_bias(act, 0, 0)
                scalar_first(act, 0, 0)
                scalar_second(act, 0)

                def expert(e, s, last):
                    with act.Fori(0, NB - 1) as b:
                        scalar_first(act, NB * e + b + 1, s)
                        scalar_spread(act, NB * e + b)
                        scalar_second(act, NB * e + b + 1)
                    if not last:
                        scalar_bias(act, e + 1, 1 - s)
                        scalar_first(act, NB * e + NB, 1 - s)
                    scalar_spread(act, NB * e + (NB - 1))
                    if not last:
                        scalar_second(act, NB * e + NB)

                with act.Fori(0, full_pairs) as q:
                    for s in (0, 1):
                        expert(2 * q + s, s, last=False)
                for s in slots:
                    expert(first + s, s, last=(s == slots[-1]))

            def vector_first(dve, n, s, first_block=False):
                if gated:
                    dve.wait_ge(hidden_done, n + 1)
                    dve.wait_ge(third_ready, n + 2)
                    if not first_block:
                        dve.wait_ge(gate_ready, n)
                    for col in range(2):
                        ins = dve.scalar_tensor_tensor(prod[:, col, :], psH[0:CK, col, 0:UB], bcur[s][:, col:col + 1],
                                                       third[:, col, :], ALU.add, ALU.mult)
                    ins.then_inc(hidden_read, 1)
                    dve.wait_ge(hidden_read, n + 2)
                    dve.wait_ge(glu_ready, n + 1)
                    dve.tensor_scalar(lin[:, 0, :], prod[:, 1, :], LIMIT, None, ALU.min)
                    dve.tensor_scalar(gate[:, 0, :], prod[:, 0, :], LIMIT, None, ALU.min).then_inc(gate_ready, 1)
                    return
                for a in range(A):
                    dve.wait_ge(hidden_done, A * n + (a + 1))
                    dve.wait_ge(glu_ready, A * n + (a + 1))
                    dve.tensor_scalar(lin[:, a, :], psH[0:CK, A + a, 0:UB], bcur[s][:, A + a:A + a + 1],
                                      LIMIT, ALU.add, ALU.min)
                    dve.tensor_scalar(gate[:, a, :], psH[0:CK, a, 0:UB], bcur[s][:, a:a + 1], LIMIT, ALU.add, ALU.min
                                      ).then_inc(hidden_read, 1)
                    dve.wait_ge(hidden_read, A * n + (a + 1 + A))
                    dve.sem_inc(gate_ready, 1)

            def vector_second(dve, n):
                for a in range(A):
                    dve.wait_ge(gate_ready, A * n + (a + 1))
                    dve.tensor_scalar(lin[:, a, :], lin[:, a, :], -LIMIT, 1.0, ALU.max, ALU.add).then_inc(lin_ready, 1)
                for a in range(A):
                    dve.wait_ge(lin_ready, A * n + (a + 1))
                    dve.wait_ge(silu_ready, A * n + (a + 1))
                    dve.wait_ge(glu_split, A * n + (a + 1))
                    dve.scalar_tensor_tensor(glu[:, a, :], silu[:, a, :], 1.0 / ALPHA, lin[:, a, :], ALU.mult, ALU.mult
                                             ).then_inc(glu_ready, 1)
                for a in range(A):
                    dve.wait_ge(glu_high, A * n + (a + 1))
                    dve.tensor_tensor(rounded(glu_parts[1][:, a, :]), glu[:, a, :], glu_parts[0][:, a, :],
                                      ALU.subtract).then_inc(glu_split, 1)

            def vector_sum(dve, n, s, cols):
                y = yT_all[:, :, cols]
                dve.wait_ge(out_done, n + 2)
                dve.wait_ge(spread_copied, n + 2)
                dve.wait_ge(summed, n + 1)
                for o in range(2):
                    ins = dve.scalar_tensor_tensor(part[:, o, :], psY[0:CK, o, 0:UB], bcur[s][:, 4 + o:5 + o],
                                                   spread[:, :], ALU.add, ALU.mult)
                ins.then_inc(out_read, 1)
                dve.wait_ge(out_read, n + 2)
                dve.tensor_tensor(y, y, part[:, :, :], ALU.add).then_inc(summed, 1)

            def vector_bias(dve, e, s, first_expert=False):
                if not first_expert:
                    dve.wait_ge(summed, NB * e - (NB - 1))
                dve.tensor_copy(bcur[s][:, :], bias[:, bass.ds(e, 1), :].rearrange("p a x -> p (a x)")
                                ).then_inc(bias_cur[0], 1)
                dve.wait_ge(bias_cur[0], e + 1)
                dve.sem_inc(phase.passed, 1)

            @block.vector
            def _(dve):
                phase.low_tokens(dve)
                dve.sem_inc(hidden_read, A)
                dve.sem_inc(glu_ready, A)
                dve.sem_inc(glu_split, A)
                for started in (out_read, summed):
                    dve.sem_inc(started, 1)
                dve.wait_ge(phase.cleared, 1)
                dve.wait_ge(bias_loaded, 16)
                vector_bias(dve, 0, 0, first_expert=True)
                vector_first(dve, 0, 0, first_block=True)
                vector_second(dve, 0)

                def expert(e, s, last):
                    with dve.Fori(0, NB - 1) as b:
                        vector_first(dve, NB * e + b + 1, s)
                        vector_second(dve, NB * e + b + 1)
                        vector_sum(dve, NB * e + b, s, bass.ds(b * UB, UB))
                    if not last:
                        vector_bias(dve, e + 1, 1 - s)
                        vector_first(dve, NB * e + NB, 1 - s)
                        vector_second(dve, NB * e + NB)
                    vector_sum(dve, NB * e + (NB - 1), s, slice((NB - 1) * UB, NB * UB))

                with dve.Fori(0, full_pairs) as q:
                    for s in (0, 1):
                        expert(2 * q + s, s, last=False)
                for s in slots:
                    expert(first + s, s, last=(s == slots[-1]))
                dve.wait_ge(summed, E * NB + 1)


def capacity_limit(nc, xT_all, yT_all, combT, maskT, sem, sb, **_):
    scanned, kept = sem("cap_scanned"), sem("cap_kept")
    with ExitStack() as ctx:
        count = sb(ctx, "cap_count", [8, NP])
        ones = sb(ctx, "cap_ones", [8, NP])
        with nc.Block() as block:
            @block.vector
            def _(dve):
                dve.memset(ones[:, :], 1.0).then_inc(scanned, 1)
                dve.wait_ge(scanned, 1)
                dve.tensor_tensor_scan(count[:, :], ones[:, :], maskT[:, :], 0.0, ALU.mult, ALU.add
                                       ).then_inc(scanned, 1)
                dve.wait_ge(scanned, 2)
                dve.scalar_tensor_tensor(combT[0:8, :], count[:, :], CAP + 0.5, combT[0:8, :], ALU.is_lt, ALU.mult
                                         ).then_inc(kept, 1)
                dve.wait_ge(kept, 1)


def per_head(ap, D):
    return ap.rearrange("p (h d) -> p h d", d=D)


def normed_output(dve, go, done, B, ps, H, D):
    yield "o"
    for c in done:
        go(c, "o")
        dve.tensor_tensor(per_head(B[c]["o"][:, :], D), per_head(ps[c][0:T, 0, 0:C], D),
                          over(B[c]["hinv"][:, 0:H].unsqueeze(2), [T, H, D]), ALU.mult).then_inc(done[c], 1)


def add2(dve, go, done, step, out_, a, b):
    yield step
    for c in done:
        go(c, step)
        dve.tensor_tensor(out_[c], a[c], b[c], ALU.add).then_inc(done[c], 1)


def router_vector(dve, go, done, B, ps, E, k, gate_b):
    yield "g_cp"
    for c in done:
        go(c, "g_cp")
        if gate_b is None:
            dve.tensor_copy(B[c]["sv"][:, 0:E], ps[c][0:T, 1, 0:E]).then_inc(done[c], 1)
        else:
            dve.tensor_tensor(B[c]["sv"][:, 0:E], ps[c][0:T, 1, 0:E], gate_b[:, :], ALU.add).then_inc(done[c], 1)
    yield from topk_vector(dve, go, done, B, "ge", "sv", "keys", k, E, [b["mask"][:, 0:E] for b in B])
    yield "g_sub"
    for c in done:
        go(c, "g_sub")
        dve.tensor_scalar(B[c]["lg"][:, 0:E], B[c]["sv"][:, 0:E], B[c]["max8"][:, 0:1], None, ALU.subtract
                          ).then_inc(done[c], 1)
    yield "g_w"
    for c in done:
        go(c, "g_w")
        dve.tensor_tensor(B[c]["lg"][:, 0:E], B[c]["lg"][:, 0:E], B[c]["mask"][:, 0:E], ALU.mult).then_inc(done[c], 1)
    yield "g_sum"
    for c in done:
        go(c, "g_sum")
        dve.tensor_reduce(B[c]["mv"][:, 0:1], B[c]["lg"][:, 0:E], AX.X, ALU.add).then_inc(done[c], 1)
    yield "g_rc"
    for c in done:
        go(c, "g_rc")
        dve.reciprocal(B[c]["mv"][:, 1:2], B[c]["mv"][:, 0:1]).then_inc(done[c], 1)
    yield "g_n"
    for c in done:
        go(c, "g_n")
        dve.tensor_scalar(B[c]["comb"][:, 0:E], B[c]["lg"][:, 0:E], B[c]["mv"][:, 1:2], None, ALU.mult
                          ).then_inc(done[c], 1)


def router_scalar(act, go, done, B, E):
    yield "g_exp"
    for c in done:
        go(c, "g_exp")
        act.activation(B[c]["lg"][:, 0:E], B[c]["lg"][:, 0:E], ACT.Exp).then_inc(done[c], 1)


ROUTER = "g_cp " + topk_steps("ge") + "g_sub g_exp g_w g_sum g_rc g_n c_tr "
ROUTER_SHAPES = dict(sv=[T, 24], keys=[T, 8], mask=[T, 16], lg=[T, 16], comb=[T, 16])


def layer1_tokens(nc, d, K, h_all, xT_all, yT_all, combT, maskT, eps5, ident, sem, sb, **_):
    H, E, HP, DA = 12, 8, 6, 64
    D, HG = 16, 6
    MAIN = "sm_scale sm_max sm_sub sm_exp sm_sum sm_inv " + SPREAD
    first = MAIN.replace("sm_max", "wide_v|sm_max").replace("sm_exp", "wv_cp|sm_exp")
    for name in ("sm_", "px", "pt", "pc", "av"):
        first = first.replace(name, "a." + name)
    S = steps("y_cp y_tr y_add " + ln_steps("n0") + ln_steps("n1") + turn_steps("f0") +
              "w_zero|wide_q wq_cp wide_k wk_cp a.S " + first + "a.o a.o_tr a.o_cp wide_out h1 h2 " +
              ln_steps("n2") + ln_steps("n3") + turn_steps("f3") + "qkT v q_dg|k_cp v_cp|kx0|kx1 S " + MAIN + "o " +
              turn_steps("fo") + "proj x2 h3 h_st|" + ln_steps("n4") + turn_steps("f4") + "x_st|gt " + ROUTER +
              "c_st m_tr m_st")
    N = S["end"]
    done = {c: sem(f"l1_tile{c}_steps") for c in range(WAYS)}
    zeroed, passed = sem("l1_zeroed"), sem("l1_passed")
    with ExitStack() as ctx:
        shapes = attention_shapes(H, D)
        shapes.update(ROUTER_SHAPES)
        shapes.update(blocks=[128, 2 * H * T], wide=[128, H * DA + HP * T])
        del shapes["px"], shapes["pT"], shapes["V"]
        B, ps = tile_buffers(ctx, nc, sb, 1, shapes)
        for b in B:
            b["px"] = b["blocks"][0:T, 0:H * T].rearrange("p (h n) -> p h n", n=T)
            b["pT"] = b["blocks"][:, H * T:2 * H * T].rearrange("p (h n) -> p h n", n=T)
            b["wqx"] = b["blocks"][:, :].rearrange("p (f x) -> p f x", f=HP)
            b["wkx"] = b["wide"][:, 0:IMGS * H * NTOK].rearrange("p (f j r m) -> p f j r m", f=HP, j=IMGS, r=2)
            b["wV"] = b["wo"] = b["V"] = b["wide"][0:T, 0:H * DA]
            b["woT"] = b["wide"][:, H * DA:].rearrange("p (f t) -> p f t", f=HP)
            b["passed"] = passed
        share(B, H)
        X = [b["x"][:, :] for b in B]
        HC = [b["hcur"][:, :] for b in B]
        xT = [b["xT"] for b in B]
        oT = [b["oT"] for b in B]
        O = [b["wo"][:, 0:C] for b in B]
        wide_scores = [[p[0:T, 0, 0:H * NTOK].rearrange("p (h m) -> p h m", m=NTOK)] for p in ps]
        scores = [[score_place(p, o, HG).rearrange("p (h m) -> p h m", m=NTOK) for o in range(2)] for p in ps]
        with nc.Block() as block:
            @block.vector
            def _(dve):
                for c in done:
                    dve.memset(B[c]["qx"][:, :, :], 0.0)
                    dve.memset(B[c]["sv"][:, :], PAD)
                    ins = dve.memset(B[c]["keys"][:, :], PAD)
                ins.then_inc(zeroed, 1)
                dve.wait_ge(zeroed, 1)
                for c in done:
                    dve.sem_inc(done[c], 1)
                def turn(i, done, half):
                    def go(c, step, passed=None):
                        dve.wait_ge(done[c], i * N + (S[step] + 1))
                        if passed is not None:
                            dve.sem_inc(passed, 1)

                    def ga(c, step, passed=None):
                        go(c, "a." + step, passed)

                    def tile_of(c):
                        return WAYS * i + c
                    if half == 0:
                        yield from take_experts_back(dve, "vector", go, done, B, ps, h_all, yT_all, ident, tile_of)
                        yield from norm_vector(dve, go, done, B, "n0", HC, X)
                        yield from norm_vector(dve, go, done, B, "n1", X, X)
                        yield "wk_cp"
                        for c in done:
                            go(c, "wk_cp")
                            for r in (0, 1):
                                rows = slice(r * DA, (r + 1) * DA)
                                for b, f0, f1 in ((0, 0, 4), (1, 4, 6)):
                                    for f in range(f0, f1):
                                        ins = dve.tensor_scalar(
                                            B[c]["wkx"][rows, f, :, r, :],
                                            ps[c][rows, b, (f - f0) * T:(f - f0 + 1) * T].rearrange(
                                                "p (j m) -> p j m", m=NTOK),
                                            K["l1_bk"][rows, f:f + 1], None, ALU.add)
                            ins.then_inc(done[c], 1)
                        yield from wide(softmax_vector(dve, ga, done, B, wide_scores, DA ** -0.5, K["anti_causal"], H))
                        yield "wv_cp"
                        for c in done:
                            go(c, "wv_cp")
                            for b in range(2):
                                ins = dve.tensor_tensor(B[c]["wV"][:, b * 384:(b + 1) * 384], ps[c][0:T, b, 0:384],
                                                        K["l1_bv"][:, b * 384:(b + 1) * 384], ALU.add)
                            ins.then_inc(done[c], 1)
                        yield from wide(sums_vector(dve, ga, done, B, H))
                        yield from wide(blocks_expand(dve, ga, done, B, "px0", 0, 8, K["bmask"]))
                        yield from wide(probs_copy(dve.tensor_copy, ga, done, B, ps, "pc1", 1, 4))
                    else:
                        yield "a.o"
                        for c in done:
                            ga(c, "o")
                            for b, h0, h1 in ((0, 0, 8), (1, 8, 12)):
                                ins = dve.tensor_tensor(per_head(B[c]["wo"][:, h0 * DA:h1 * DA], DA),
                                                        per_head(ps[c][0:T, b, 0:(h1 - h0) * DA], DA),
                                                        over(B[c]["hinv"][:, h0:h1].unsqueeze(2), [T, h1 - h0, DA]),
                                                        ALU.mult)
                            ins.then_inc(done[c], 1)
                        yield from add2(dve, go, done, "h1", HC, HC, [p[0:T, 0, 0:C] for p in ps])
                        yield from add2(dve, go, done, "h2", HC, HC, [K["l1_bo"][:, :]] * WAYS)
                        yield from norm_vector(dve, go, done, B, "n2", HC, X)
                        yield from norm_vector(dve, go, done, B, "n3", X, O)
                        yield "k_cp"
                        for c in done:
                            go(c, "k_cp")
                            dve.tensor_copy(B[c]["kT"][:, :, :].rearrange("p o t -> p (o t)"), ps[c][0:CK, 1, 0:2 * T]
                                            ).then_inc(done[c], 1)
                        yield from heads_expand(dve, go, done, B, "kx0", 0, HG, K["hmask16"])
                        yield from softmax_vector(dve, go, done, B, scores, D ** -0.5, K["causal"], H)
                        yield from sums_vector(dve, go, done, B, H)
                        yield from blocks_expand(dve, go, done, B, "px0", 0, 8, K["bmask"])
                        yield from probs_copy(dve.tensor_copy, go, done, B, ps, "pc1", 1, 4)
                        yield "o"
                        for c in done:
                            go(c, "o")
                            dve.tensor_tensor(per_head(O[c], D), per_head(ps[c][0:T, 0, 0:C], D),
                                              over(B[c]["hinv"][:, 0:H].unsqueeze(2), [T, H, D]), ALU.mult
                                              ).then_inc(done[c], 1)
                        yield from add2(dve, go, done, "x2", X, X, [p[0:T, 0, 0:C] for p in ps])
                        yield from add2(dve, go, done, "h3", HC, HC, X)
                        yield from norm_vector(dve, go, done, B, "n4", X, X)
                        yield from router_vector(dve, go, done, B, ps, E, 2, None)

                two_at_once(dve, turn, S, "a.o", done)

            @block.scalar
            def _(act):
                act.preload_act_table_set(EXP_LN)
                act.wait_ge(zeroed, 1)
                def turn(i, done, half):
                    def go(c, step):
                        act.wait_ge(done[c], i * N + (S[step] + 1))

                    def ga(c, step):
                        go(c, "a." + step)

                    def tile_of(c):
                        return WAYS * i + c
                    if half == 0:
                        yield from norm_scalar(act, go, done, B, "n0", eps5[0:T, :])
                        yield from norm_scalar(act, go, done, B, "n1", eps5[0:T, :])
                        yield from turn_scalar(act, go, done, "f0", ps, 0, xT, K["l1_ln_w"], K["l1_ln_b"])
                        yield "wq_cp"
                        for c in done:
                            go(c, "wq_cp")
                            for f in range(HP):
                                ins = act.activation(
                                    B[c]["wqx"][:, f, :].rearrange("p (j x) -> p j x", x=DIAG)[:, :, 0:NTOK],
                                    ps[c][:, f // 4, (f % 4) * T:(f % 4 + 1) * T].rearrange("p (j m) -> p j m", m=NTOK),
                                    ACT.Identity, bias=K["l1_bq"][:, f:f + 1])
                            ins.then_inc(done[c], 1)
                        yield from wide(softmax_scalar(act, ga, done, B, H))
                        yield from wide(probs_copy(act.copy, ga, done, B, ps, "pc0", 0, 0))
                        yield from wide(probs_copy(act.copy, ga, done, B, ps, "pc2", 0, 8))
                    else:
                        yield "a.o_cp"
                        for c in done:
                            ga(c, "o_cp")
                            act.copy(B[c]["woT"][:, 0:4, :].rearrange("p f t -> p (f t)"), ps[c][:, 0, 0:4 * T])
                            act.copy(B[c]["woT"][:, 4:6, :].rearrange("p f t -> p (f t)"), ps[c][:, 1, 0:2 * T]
                                     ).then_inc(done[c], 1)
                        yield from norm_scalar(act, go, done, B, "n2", eps5[0:T, :])
                        yield from norm_scalar(act, go, done, B, "n3", eps5[0:T, :])
                        yield from turn_scalar(act, go, done, "f3", ps, 0, xT, K["l1_ln1_w"])
                        yield from query_blocks(act, go, done, B, ps, "q_dg", 0)
                        yield "v_cp"
                        for c in done:
                            go(c, "v_cp")
                            act.copy(B[c]["wV"][:, 0:C], ps[c][0:T, 0, 256:256 + C]).then_inc(done[c], 1)
                        yield from softmax_scalar(act, go, done, B, H)
                        yield from probs_copy(act.copy, go, done, B, ps, "pc0", 0, 0)
                        yield from probs_copy(act.copy, go, done, B, ps, "pc2", 0, 8)
                        yield from turn_scalar(act, go, done, "fo", ps, 1, oT)
                        yield from norm_scalar(act, go, done, B, "n4", eps5[0:T, :])
                        yield from turn_scalar(act, go, done, "f4", ps, 0, xT, K["l1_ln2_w"])
                        yield from router_scalar(act, go, done, B, E)
                        yield from weights_out(act, "scalar", go, done, B, ps, combT, ident, tile_of, E)
                        yield "m_st"
                        for c in done:
                            go(c, "m_st")
                            act.copy(maskT[:, bass.ds(tile_of(c) * T, T)], ps[c][0:E, 1, 0:T]).then_inc(done[c], 1)

                two_at_once(act, turn, S, "a.o", done)

            @block.gpsimd
            def _(pool):
                def turn(i, done, half):
                    def go(c, step):
                        pool.wait_ge(done[c], i * N + (S[step] + 1))

                    def ga(c, step):
                        go(c, "a." + step)

                    def tile_of(c):
                        return WAYS * i + c
                    if half == 0:
                        yield from take_experts_back(pool, "pool", go, done, B, ps, h_all, yT_all, ident, tile_of)
                        yield "w_zero"
                        for c in done:
                            go(c, "w_zero")
                            pool.sem_inc(passed, 1)
                            pool.memset(B[c]["wide"][:, 0:IMGS * H * NTOK], 0.0)
                            pool.memset(B[c]["blocks"][:, :], 0.0).then_inc(done[c], 1)
                        yield from wide(blocks_expand(pool, ga, done, B, "px1", 8, H, K["bmask"]))
                    else:
                        yield from heads_expand(pool, go, done, B, "kx1", 1, HG, K["hmask16"])
                        yield from blocks_expand(pool, go, done, B, "px1", 8, H, K["bmask"])
                        yield from store_tile(pool, go, done, B, h_all, xT_all, tile_of, "hcur")
                        yield from store_xT(pool, go, done, B, xT_all, tile_of)

                two_at_once(pool, turn, S, "a.o", done)

            @block.tensor
            def _(pe):
                def turn(i, done, half):
                    def go(c, step):
                        pe.wait_ge(done[c], i * N + (S[step] + 1))

                    def ga(c, step):
                        go(c, "a." + step)

                    def tile_of(c):
                        return WAYS * i + c
                    if half == 0:
                        yield from take_experts_back(pe, "tensor", go, done, B, ps, h_all, yT_all, ident, tile_of)
                        yield from turn_tensor(pe, go, done, "f0", X, ps, 0, ident)
                        for step, w in (("wide_q", K["l1_wq"]), ("wide_k", K["l1_wk"])):
                            yield step
                            for c in done:
                                go(c, step)
                                for f in range(HP):
                                    for k in range(2):
                                        mm = pe.matmul(ps[c][:, f // 4, (f % 4) * T:(f % 4 + 1) * T],
                                                       w[:, k, f * 128:(f + 1) * 128], xT[c][:, k, :],
                                                       start=(k == 0), stop=(k == 1))
                                mm.then_inc(done[c], 1)
                        yield "a.S"
                        for c in done:
                            ga(c, "S")
                            for f in range(HP):
                                for j in range(IMGS):
                                    mm = pe.matmul(ps[c][0:T, 0, 2 * f * NTOK:2 * (f + 1) * NTOK],
                                                   B[c]["wqx"][:, f, j * T:(j + 1) * T],
                                                   B[c]["wkx"][:, f, j, :, :].rearrange("p r m -> p (r m)"),
                                                   start=(j == 0), stop=(j == IMGS - 1))
                            mm.then_inc(done[c], 1)
                        yield "wide_v"
                        for c in done:
                            go(c, "wide_v")
                            for b in range(2):
                                for k in range(2):
                                    mm = pe.matmul(ps[c][0:T, b, 0:384], xT[c][:, k, :],
                                                   K["l1_wv"][:, k, b * 384:(b + 1) * 384], start=(k == 0), stop=(k == 1))
                            mm.then_inc(done[c], 1)
                        yield from wide(values_stage(pe, ga, done, B, ps, H, DA, [b["wV"] for b in B], 8, ident))
                    else:
                        yield "a.o_tr"
                        for c in done:
                            ga(c, "o_tr")
                            for f in range(HP):
                                mm = pe.transpose(ps[c][:, f // 4, (f % 4) * T:(f % 4 + 1) * T],
                                                  B[c]["wo"][:, f * 128:(f + 1) * 128], ident[0:T, 0:T])
                            mm.then_inc(done[c], 1)
                        yield "wide_out"
                        for c in done:
                            go(c, "wide_out")
                            for f in range(HP):
                                mm = pe.matmul(ps[c][0:T, 0, 0:C], B[c]["woT"][:, f, :], K["l1_wo"][:, f, :],
                                               start=(f == 0), stop=(f == HP - 1))
                            mm.then_inc(done[c], 1)
                        yield from turn_tensor(pe, go, done, "f3", O, ps, 0, ident)
                        yield from qk_tensor(pe, go, done, ps, xT, K["l1_wqk"])
                        yield from width_product(pe, go, done, "v", ps, 0, xT, K["l1_wv2"], C, 256)
                        yield from scores_tensor(pe, go, done, B, ps, HG)
                        yield from values_stage(pe, go, done, B, ps, H, D, [b["wV"] for b in B], H, ident)
                        yield from turn_tensor(pe, go, done, "fo", O, ps, 1, ident)
                        yield from width_product(pe, go, done, "proj", ps, 0, oT, K["l1_wproj"], C)
                        yield from turn_tensor(pe, go, done, "f4", X, ps, 0, ident)
                        yield from width_product(pe, go, done, "gt", ps, 1, xT, K["l1_gate_w"], E)
                        yield from weights_out(pe, "tensor", go, done, B, ps, combT, ident, tile_of, E)
                        yield "m_tr"
                        for c in done:
                            go(c, "m_tr")
                            pe.transpose(ps[c][0:E, 1, 0:T], B[c]["mask"][:, 0:E], ident[0:T, 0:T]).then_inc(done[c], 1)

                two_at_once(pe, turn, S, "a.o", done)


def qk_tensor(pe, go, done, ps, xT, w):
    yield "qkT"
    for c in done:
        go(c, "qkT")
        for o in range(4):
            for k in range(2):
                mm = pe.matmul(ps[c][0:CK, o // 2, (o % 2) * T:(o % 2 + 1) * T], w[:, k, o * CK:(o + 1) * CK],
                               xT[c][:, k, :], start=(k == 0), stop=(k == 1))
        mm.then_inc(done[c], 1)


def layer2_tokens(nc, d, K, h_all, xT_all, yT_all, combT, eps5, ident, sem, sb, **_):
    H, D, HG, E = 16, 12, 8, 16
    S = steps("y_cp y_tr y_add " + ln_steps("n0") + turn_steps("f0") + "qkT v q_dg|k_cp v_cp|kx0|kx1 S " + SOFTMAX +
              "mix_f mix_a mix_b m_sum m_inv " + SPREAD16 + "o " + turn_steps("fo") + "proj h1 h2 " + ln_steps("n1") +
              "h3 h_st|" + rms_steps("r1") + turn_steps("f1") + "x_st|gt " + ROUTER + "c_st")
    N = S["end"]
    done = {c: sem(f"l2_tile{c}_steps") for c in range(WAYS)}
    zeroed, setup, passed = sem("l2_zeroed"), sem("l2_setup"), sem("l2_passed")
    with ExitStack() as ctx:
        shapes = attention_shapes(H, D)
        shapes.update(ROUTER_SHAPES)
        
        B, ps = tile_buffers(ctx, nc, sb, 2, shapes)
        share(B, H)
        for b in B:
            b["junk"] = b["o"][:, :]
        for b in B:
            b["passed"] = passed
        pos = sb(ctx, "l2_pos", [T, H, NTOK])
        tmp = sb(ctx, "l2_tmp", [T, H, NTOK])
        hs = sb(ctx, "l2_hs", [T, 4, H])
        X = [b["x"][:, :] for b in B]
        HC = [b["hcur"][:, :] for b in B]
        xT = [b["xT"] for b in B]
        oT = [b["oT"] for b in B]
        scores = [[score_place(p, o, HG).rearrange("p (h m) -> p h m", m=NTOK) for o in range(2)] for p in ps]
        shape = [T, H, NTOK]
        with nc.Block() as block:
            @block.vector
            def _(dve):
                for c in done:
                    dve.memset(B[c]["qx"][:, :, :], 0.0)
                    dve.memset(B[c]["sv"][:, :], PAD)
                    ins = dve.memset(B[c]["keys"][:, :], PAD)
                ins.then_inc(zeroed, 1)
                dve.wait_ge(zeroed, 1)
                dve.tensor_tensor(pos[:, :, :], over(K["rel"][:, 0, :].unsqueeze(1), shape),
                                  over(K["l2_wpos"][:, 0, :].unsqueeze(2), shape), ALU.mult).then_inc(setup, 1)
                n = 1
                for q in (1, 2):
                    dve.wait_ge(setup, n)
                    dve.tensor_tensor(tmp[:, :, :], over(K["rel"][:, q, :].unsqueeze(1), shape),
                                      over(K["l2_wpos"][:, q, :].unsqueeze(2), shape), ALU.mult).then_inc(setup, 1)
                    dve.wait_ge(setup, n + 1)
                    dve.tensor_tensor(pos[:, :, :], pos[:, :, :], tmp[:, :, :], ALU.add).then_inc(setup, 1)
                    n += 2
                dve.wait_ge(setup, 5)
                dve.tensor_tensor(pos[:, :, :], pos[:, :, :], over(K["l2_bpos"][:, :].unsqueeze(2), shape), ALU.add
                                  ).then_inc(setup, 1)
                dve.wait_ge(setup, 6)
                dve.tensor_reduce(hs[:, 0, :], pos[:, :, :], AX.X, ALU.max).then_inc(setup, 1)
                dve.wait_ge(setup, 7)
                dve.tensor_tensor(pos[:, :, :], pos[:, :, :], over(hs[:, 0, :].unsqueeze(2), shape), ALU.subtract
                                  ).then_inc(setup, 1)
                dve.wait_ge(setup, 10)
                dve.tensor_reduce(hs[:, 1, :], pos[:, :, :], AX.X, ALU.add).then_inc(setup, 1)
                dve.wait_ge(setup, 11)
                dve.tensor_scalar(hs[:, 2, :], hs[:, 2, :], 1.0, None, ALU.add).then_inc(setup, 1)
                dve.wait_ge(setup, 12)
                dve.tensor_tensor(hs[:, 1, :], hs[:, 1, :], hs[:, 2, :], ALU.mult).then_inc(setup, 1)
                dve.wait_ge(setup, 13)
                dve.reciprocal(hs[:, 1, :], hs[:, 1, :]).then_inc(setup, 1)
                dve.wait_ge(setup, 14)
                dve.reciprocal(hs[:, 2, :], hs[:, 2, :]).then_inc(setup, 1)
                dve.wait_ge(setup, 15)
                dve.tensor_scalar(hs[:, 3, :], hs[:, 2, :], -1.0, 1.0, ALU.mult, ALU.add).then_inc(setup, 1)
                dve.wait_ge(setup, 16)
                dve.tensor_tensor(pos[:, :, :], pos[:, :, :], over(hs[:, 1, :].unsqueeze(2), shape), ALU.mult
                                  ).then_inc(setup, 1)
                dve.wait_ge(setup, 17)
                for c in done:
                    dve.sem_inc(done[c], 1)
                def turn(i, done, half):
                    def go(c, step, passed=None):
                        dve.wait_ge(done[c], i * N + (S[step] + 1))
                        if passed is not None:
                            dve.sem_inc(passed, 1)

                    def tile_of(c):
                        return WAYS * i + c
                    if half == 0:
                        yield from take_experts_back(dve, "vector", go, done, B, ps, h_all, yT_all, ident, tile_of)
                        yield from norm_vector(dve, go, done, B, "n0", HC, X)
                        yield "k_cp"
                        for c in done:
                            go(c, "k_cp")
                            dve.tensor_copy(B[c]["kT"][:, :, :].rearrange("p o t -> p (o t)"), ps[c][0:CK, 1, 0:2 * T]
                                            ).then_inc(done[c], 1)
                        yield from heads_expand(dve, go, done, B, "kx0", 0, HG, K["hmask12"])
                    else:
                        yield from softmax_vector(dve, go, done, B, scores, D ** -0.5, None, H)
                        yield from sums_vector(dve, go, done, B, H)
                        yield "mix_f"
                        for c in done:
                            go(c, "mix_f")
                            dve.tensor_tensor(B[c]["hmax"][:, 0:H], B[c]["hinv"][:, 0:H], hs[:, 3, :], ALU.mult
                                              ).then_inc(done[c], 1)
                        yield "mix_a"
                        for c in done:
                            go(c, "mix_a")
                            dve.tensor_tensor(B[c]["P"][:, :, :], B[c]["P"][:, :, :],
                                              over(B[c]["hmax"][:, 0:H].unsqueeze(2), shape), ALU.mult).then_inc(done[c], 1)
                        yield "mix_b"
                        for c in done:
                            go(c, "mix_b")
                            dve.tensor_tensor(B[c]["P"][:, :, :], B[c]["P"][:, :, :], pos[:, :, :], ALU.add
                                              ).then_inc(done[c], 1)
                        yield "m_sum"
                        for c in done:
                            go(c, "m_sum")
                            dve.tensor_reduce(B[c]["hsum"][:, 0:H], B[c]["P"][:, 0:H, :], AX.X, ALU.add
                                              ).then_inc(done[c], 1)
                        yield "m_inv"
                        for c in done:
                            go(c, "m_inv")
                            dve.reciprocal(B[c]["hinv"][:, 0:H], B[c]["hsum"][:, 0:H]).then_inc(done[c], 1)
                        yield from blocks_expand(dve, go, done, B, "px0", 0, 11, K["bmask"])
                        yield from probs_copy(dve.tensor_copy, go, done, B, ps, "pc1", 1, 4)
                        yield from probs_copy(dve.tensor_copy, go, done, B, ps, "pc3", 1, 12)
                        yield from normed_output(dve, go, done, B, ps, H, D)
                        yield from add2(dve, go, done, "h1", HC, HC, [p[0:T, 0, 0:C] for p in ps])
                        yield from add2(dve, go, done, "h2", HC, HC, [K["l2_bproj"][:, :]] * WAYS)
                        yield from norm_vector(dve, go, done, B, "n1", HC, X)
                        yield from add2(dve, go, done, "h3", HC, HC, X)
                        yield from rms_vector(dve, go, done, B, "r1", X, X)
                        yield from router_vector(dve, go, done, B, ps, E, 4, K["l2_gate_b"])

                two_at_once(dve, turn, S, "sm_scale", done)

            @block.scalar
            def _(act):
                act.preload_act_table_set(EXP_LN)
                act.wait_ge(setup, 8)
                act.activation(pos[:, :, :], pos[:, :, :], ACT.Exp).then_inc(setup, 1)
                act.activation(hs[:, 2, :], K["l2_gating"][:, :], ACT.Exp, scale=-1.0).then_inc(setup, 1)
                def turn(i, done, half):
                    def go(c, step):
                        act.wait_ge(done[c], i * N + (S[step] + 1))

                    def tile_of(c):
                        return WAYS * i + c
                    if half == 0:
                        yield from norm_scalar(act, go, done, B, "n0", eps5[0:T, :])
                        yield from turn_scalar(act, go, done, "f0", ps, 0, xT)
                        yield from query_blocks(act, go, done, B, ps, "q_dg", 0)
                        yield "v_cp"
                        for c in done:
                            go(c, "v_cp")
                            act.copy(B[c]["V"][:, :], ps[c][0:T, 0, 256:256 + C]).then_inc(done[c], 1)
                    else:
                        yield from softmax_scalar(act, go, done, B, H)
                        yield from probs_copy(act.copy, go, done, B, ps, "pc0", 0, 0)
                        yield from probs_copy(act.copy, go, done, B, ps, "pc2", 0, 8)
                        yield from turn_scalar(act, go, done, "fo", ps, 1, oT)
                        yield from norm_scalar(act, go, done, B, "n1", eps5[0:T, :])
                        yield from rms_scalar(act, go, done, B, "r1", X, eps5[0:T, :])
                        yield from turn_scalar(act, go, done, "f1", ps, 0, xT, K["l2_scale"])
                        yield from router_scalar(act, go, done, B, E)
                        yield from weights_out(act, "scalar", go, done, B, ps, combT, ident, tile_of, E)

                two_at_once(act, turn, S, "sm_scale", done)

            @block.gpsimd
            def _(pool):
                def turn(i, done, half):
                    def go(c, step):
                        pool.wait_ge(done[c], i * N + (S[step] + 1))

                    def tile_of(c):
                        return WAYS * i + c
                    if half == 0:
                        yield from take_experts_back(pool, "pool", go, done, B, ps, h_all, yT_all, ident, tile_of)
                        yield from heads_expand(pool, go, done, B, "kx1", 1, HG, K["hmask12"])
                    else:
                        yield from blocks_expand(pool, go, done, B, "px1", 11, H, K["bmask"])
                        yield from store_tile(pool, go, done, B, h_all, xT_all, tile_of, "hcur")
                        yield from store_xT(pool, go, done, B, xT_all, tile_of)

                two_at_once(pool, turn, S, "sm_scale", done)

            @block.tensor
            def _(pe):
                def turn(i, done, half):
                    def go(c, step):
                        pe.wait_ge(done[c], i * N + (S[step] + 1))

                    def tile_of(c):
                        return WAYS * i + c
                    if half == 0:
                        yield from take_experts_back(pe, "tensor", go, done, B, ps, h_all, yT_all, ident, tile_of)
                        yield from turn_tensor(pe, go, done, "f0", X, ps, 0, ident)
                        yield from qk_tensor(pe, go, done, ps, xT, K["l2_wqk"])
                        yield from width_product(pe, go, done, "v", ps, 0, xT, K["l2_wv"], C, 256)
                        yield from scores_tensor(pe, go, done, B, ps, HG)
                    else:
                        yield from values_stage(pe, go, done, B, ps, H, D, [b["V"] for b in B], H, ident)
                        yield from turn_tensor(pe, go, done, "fo", [b["o"][:, :] for b in B], ps, 1, ident)
                        yield from width_product(pe, go, done, "proj", ps, 0, oT, K["l2_wproj"], C)
                        yield from turn_tensor(pe, go, done, "f1", X, ps, 0, ident)
                        yield from width_product(pe, go, done, "gt", ps, 1, xT, K["l2_gate_w"], E)
                        yield from weights_out(pe, "tensor", go, done, B, ps, combT, ident, tile_of, E)

                two_at_once(pe, turn, S, "sm_scale", done)


def layer3_tokens(nc, d, K, h_all, xT_all, yT_all, combT, eps5, eps6, ident, sem, sb, **_):
    H, D, HG, E, DV = 12, 16, 6, 8, 17
    HID = 4
    S = steps("y_cp y_tr y_add " + ln_steps("n0") + rms_steps("r1") + turn_steps("f1") +
              "lat lat_act big big_cp qk_sq qk_ss qk_log qk_rs qk_n qk_w r_cos|r_sin r_add e_min e_exp e_max "
              "q_tr q_dg|k_cp p_sig p_one p_inv p_amp p_ph p_abs p_cos p_mul p_tmp p_sig2 p_one2 p_inv2 p_lin p_clip p_dec v_x "
              "kx0|kx1 S P_m " + SPREAD + "d_s d_m d_r d_f o " + rms_steps("r2") + turn_steps("fo") +
              "proj og ao x2 h3 " + rms_steps("r3") + turn_steps("f3") + "ff1 ff_s ff_m ff2 h4 h_st " +
              ln_steps("n4") + turn_steps("f4") + "x_st|gt " + ROUTER + "c_st")
    N = S["end"]
    done = {c: sem(f"l3_tile{c}_steps") for c in range(WAYS)}
    zeroed, setup, passed = sem("l3_zeroed"), sem("l3_setup"), sem("l3_passed")
    with ExitStack() as ctx:
        shapes = attention_shapes(H, D)
        shapes.update(ROUTER_SHAPES)
        shapes.update(latT=[128, T], big=[T, 816], rA=[T, 2 * H, D], rB=[T, 2 * H, D], sg=[T, H, 4],
                      pm=[T, 4, H], Vx=[T, H, DV], qs=[T, 3, 2 * H])
        B, ps = tile_buffers(ctx, nc, sb, 3, shapes)
        share(B, H)
        for b in B:
            b["ff"] = b["pT"][:, 0:HID, :]
            b["og"] = b["rA"][:, 0:H, :].rearrange("p h d -> p (h d)")
            b["junk"] = b["rB"][:, 0:H, :].rearrange("p h d -> p (h d)")
        for b in B:
            b["passed"] = passed
        hs = sb(ctx, "l3_hs", [T, 6, H])
        X = [b["x"][:, :] for b in B]
        O = [b["o"][:, :] for b in B]
        HC = [b["hcur"][:, :] for b in B]
        xT = [b["xT"] for b in B]
        oT = [b["oT"] for b in B]
        qk = [b["big"][:, 0:2 * C].rearrange("p (h d) -> p h d", d=D) for b in B]
        shape24 = [T, 2 * H, D]
        half_pi = K["half_pi"]
        with nc.Block() as block:
            @block.vector
            def _(dve):
                for c in done:
                    dve.memset(B[c]["qx"][:, :, :], 0.0)
                    dve.memset(B[c]["sv"][:, :], PAD)
                    ins = dve.memset(B[c]["keys"][:, :], PAD)
                ins.then_inc(zeroed, 1)
                dve.wait_ge(zeroed, 1)
                dve.wait_ge(setup, 1)
                dve.tensor_scalar(hs[:, 1, :], hs[:, 0, :], 1.0, None, ALU.add).then_inc(setup, 1)
                dve.wait_ge(setup, 2)
                dve.reciprocal(hs[:, 0, :], hs[:, 1, :]).then_inc(setup, 1)
                dve.wait_ge(setup, 3)
                dve.tensor_scalar(hs[:, 1, :], hs[:, 0, :], 0.65, 0.3, ALU.mult, ALU.add).then_inc(setup, 1)
                dve.wait_ge(setup, 4)
                dve.tensor_scalar(hs[:, 0, :], hs[:, 1, :], 1e-5, 0.999, ALU.max, ALU.min).then_inc(setup, 1)
                dve.wait_ge(setup, 7)
                dve.tensor_scalar(hs[:, 3, :], hs[:, 0, :], -1.0, 1.0, ALU.mult, ALU.add).then_inc(setup, 1)
                dve.tensor_scalar(hs[:, 4, :], hs[:, 2, :], 1e-8, None, ALU.add).then_inc(setup, 1)
                dve.wait_ge(setup, 9)
                dve.reciprocal(hs[:, 5, :], hs[:, 4, :]).then_inc(setup, 1)
                dve.wait_ge(setup, 10)
                dve.tensor_tensor(hs[:, 4, :], hs[:, 5, :], hs[:, 3, :], ALU.mult).then_inc(setup, 1)
                dve.wait_ge(setup, 11)
                for c in done:
                    ins = dve.tensor_copy(B[c]["Vx"][:, :, D:D + 1], hs[:, 4, :].unsqueeze(2))
                ins.then_inc(setup, 1)
                dve.wait_ge(setup, 12)
                for c in done:
                    dve.sem_inc(done[c], 1)
                def turn(i, done, half):
                    def go(c, step, passed=None):
                        dve.wait_ge(done[c], i * N + (S[step] + 1))
                        if passed is not None:
                            dve.sem_inc(passed, 1)

                    def tile_of(c):
                        return WAYS * i + c
                    if half == 0:
                        yield from take_experts_back(dve, "vector", go, done, B, ps, h_all, yT_all, ident, tile_of)
                        yield from norm_vector(dve, go, done, B, "n0", HC, X)
                        yield from rms_vector(dve, go, done, B, "r1", X, O)
                        yield "qk_sq"
                        for c in done:
                            go(c, "qk_sq")
                            dve.tensor_tensor(B[c]["rA"][:, :, :], qk[c], qk[c], ALU.mult).then_inc(done[c], 1)
                        yield "qk_ss"
                        for c in done:
                            go(c, "qk_ss")
                            dve.tensor_reduce(B[c]["qs"][:, 0, :], B[c]["rA"][:, :, :], AX.X, ALU.add).then_inc(done[c], 1)
                        yield "qk_n"
                        for c in done:
                            go(c, "qk_n")
                            dve.tensor_tensor(qk[c], qk[c], over(B[c]["qs"][:, 2, :].unsqueeze(2), shape24), ALU.mult
                                              ).then_inc(done[c], 1)
                        yield "qk_w"
                        for c in done:
                            go(c, "qk_w")
                            for w in range(2):
                                v = qk[c][:, w * H:(w + 1) * H, :]
                                ins = dve.tensor_tensor(v, v, over(K["l3_qkn"][:, w, :].unsqueeze(1), [T, H, D]), ALU.mult)
                            ins.then_inc(done[c], 1)
                        yield "r_cos"
                        for c in done:
                            go(c, "r_cos")
                            dve.tensor_tensor(B[c]["rA"][:, :, :], qk[c], over(K["rope_cos"][:, :].unsqueeze(1), shape24),
                                              ALU.mult).then_inc(done[c], 1)
                        yield "r_add"
                        for c in done:
                            go(c, "r_add")
                            dve.tensor_tensor(qk[c], B[c]["rA"][:, :, :], B[c]["rB"][:, :, :], ALU.add
                                              ).then_inc(done[c], 1)
                        yield "e_min"
                        for c in done:
                            go(c, "e_min")
                            dve.tensor_scalar(B[c]["rA"][:, :, :], qk[c], 0.0, None, ALU.min).then_inc(done[c], 1)
                        yield "e_max"
                        for c in done:
                            go(c, "e_max")
                            dve.scalar_tensor_tensor(qk[c], qk[c], 0.0, B[c]["rA"][:, :, :], ALU.max, ALU.add
                                                     ).then_inc(done[c], 1)
                        yield "k_cp"
                        for c in done:
                            go(c, "k_cp")
                            dve.tensor_copy(B[c]["kT"][:, :, :].rearrange("p o t -> p (o t)"), ps[c][0:CK, 1, 0:2 * T]
                                            ).then_inc(done[c], 1)
                        yield "p_one"
                        for c in done:
                            go(c, "p_one")
                            dve.tensor_scalar(B[c]["sg"][:, :, :], B[c]["sg"][:, :, :], 1.0, None, ALU.add
                                              ).then_inc(done[c], 1)
                        yield "p_inv"
                        for c in done:
                            go(c, "p_inv")
                            dve.reciprocal(B[c]["sg"][:, :, :], B[c]["sg"][:, :, :]).then_inc(done[c], 1)
                        yield "p_amp"
                        for c in done:
                            go(c, "p_amp")
                            dve.tensor_tensor(B[c]["pm"][:, 0, :], B[c]["sg"][:, :, 0], B[c]["sg"][:, :, 2], ALU.mult
                                              ).then_inc(done[c], 1)
                        yield "p_ph"
                        for c in done:
                            go(c, "p_ph")
                            dve.tensor_tensor(B[c]["pm"][:, 1, :], B[c]["sg"][:, :, 1], B[c]["sg"][:, :, 3], ALU.subtract
                                              ).then_inc(done[c], 1)
                        yield "p_abs"
                        for c in done:
                            go(c, "p_abs")
                            dve.scalar_tensor_tensor(B[c]["pm"][:, 2, :], B[c]["pm"][:, 1, :], -1.0, B[c]["pm"][:, 1, :],
                                                     ALU.mult, ALU.max).then_inc(done[c], 1)
                        yield "p_mul"
                        for c in done:
                            go(c, "p_mul")
                            dve.tensor_tensor(B[c]["pm"][:, 0, :], B[c]["pm"][:, 0, :], B[c]["pm"][:, 1, :], ALU.mult
                                              ).then_inc(done[c], 1)
                        yield "p_tmp"
                        for c in done:
                            go(c, "p_tmp")
                            dve.tensor_scalar(B[c]["pm"][:, 1, :], B[c]["pm"][:, 0, :], K["l3_temp"][:, 0:1], None,
                                              ALU.mult).then_inc(done[c], 1)
                        yield "p_one2"
                        for c in done:
                            go(c, "p_one2")
                            dve.tensor_scalar(B[c]["pm"][:, 1, :], B[c]["pm"][:, 0, :], 1.0, None, ALU.add
                                              ).then_inc(done[c], 1)
                        yield "p_inv2"
                        for c in done:
                            go(c, "p_inv2")
                            dve.reciprocal(B[c]["pm"][:, 2, :], B[c]["pm"][:, 1, :]).then_inc(done[c], 1)
                        yield "p_lin"
                        for c in done:
                            go(c, "p_lin")
                            dve.tensor_scalar(B[c]["pm"][:, 1, :], B[c]["pm"][:, 2, :], 1.2, -0.1, ALU.mult, ALU.add
                                              ).then_inc(done[c], 1)
                        yield "p_clip"
                        for c in done:
                            go(c, "p_clip")
                            dve.tensor_scalar(B[c]["pm"][:, 2, :], B[c]["pm"][:, 1, :], 0.05, 0.95, ALU.max, ALU.min
                                              ).then_inc(done[c], 1)
                        yield "p_dec"
                        for c in done:
                            go(c, "p_dec")
                            dve.tensor_tensor(B[c]["pm"][:, 3, :], B[c]["pm"][:, 2, :], hs[:, 4, :], ALU.mult
                                              ).then_inc(done[c], 1)
                        yield "v_x"
                        for c in done:
                            go(c, "v_x")
                            dve.tensor_tensor(B[c]["Vx"][:, :, 0:D], per_head(B[c]["big"][:, 2 * C:3 * C], D),
                                              over(B[c]["pm"][:, 3, :].unsqueeze(2), [T, H, D]), ALU.mult
                                              ).then_inc(done[c], 1)
                        yield from heads_expand(dve, go, done, B, "kx0", 0, HG, K["hmask16"])
                        yield "P_m"
                        for c in done:
                            go(c, "P_m")
                            dve.tensor_tensor(B[c]["P"][:, :, :],
                                              ps[c][0:T, 0, 0:H * NTOK].rearrange("p (h m) -> p h m", m=NTOK),
                                              over(K["causal01"][:, :].unsqueeze(1), [T, H, NTOK]), ALU.mult
                                              ).then_inc(done[c], 1)
                        yield from blocks_expand(dve, go, done, B, "px0", 0, 8, K["bmask"])
                        yield from probs_copy(dve.tensor_copy, go, done, B, ps, "pc1", 1, 4)
                    else:
                        AV = [p[0:T, 0, 0:H * DV].rearrange("p (h d) -> p h d", d=DV) for p in ps]
                        yield "d_s"
                        for c in done:
                            go(c, "d_s")
                            dve.tensor_tensor(B[c]["hsum"][:, 0:H], AV[c][:, :, D], hs[:, 2, :], ALU.mult
                                              ).then_inc(done[c], 1)
                        yield "d_m"
                        for c in done:
                            go(c, "d_m")
                            dve.tensor_scalar(B[c]["hmax"][:, 0:H], B[c]["hsum"][:, 0:H], 1e-5, None, ALU.max
                                              ).then_inc(done[c], 1)
                        yield "d_r"
                        for c in done:
                            go(c, "d_r")
                            dve.reciprocal(B[c]["hinv"][:, 0:H], B[c]["hmax"][:, 0:H]).then_inc(done[c], 1)
                        yield "d_f"
                        for c in done:
                            go(c, "d_f")
                            dve.tensor_tensor(B[c]["hsum"][:, 0:H], B[c]["hinv"][:, 0:H], hs[:, 2, :], ALU.mult
                                              ).then_inc(done[c], 1)
                        yield "o"
                        for c in done:
                            go(c, "o")
                            dve.tensor_tensor(per_head(O[c], D), AV[c][:, :, 0:D],
                                              over(B[c]["hsum"][:, 0:H].unsqueeze(2), [T, H, D]), ALU.mult
                                              ).then_inc(done[c], 1)
                        yield from rms_vector(dve, go, done, B, "r2", O, O)
                        yield "ao"
                        for c in done:
                            go(c, "ao")
                            dve.tensor_tensor(O[c], ps[c][0:T, 0, 0:C], B[c]["og"], ALU.mult).then_inc(done[c], 1)
                        yield from add2(dve, go, done, "x2", X, X, O)
                        yield from add2(dve, go, done, "h3", HC, HC, X)
                        yield from rms_vector(dve, go, done, B, "r3", X, O)
                        yield "ff_m"
                        for c in done:
                            go(c, "ff_m")
                            ff = B[c]["ff"][:, :, :].rearrange("p f t -> p (f t)")
                            dve.tensor_tensor(ff, ff, ps[c][:, 1, 0:HID * T], ALU.mult).then_inc(done[c], 1)
                        yield from add2(dve, go, done, "h4", HC, HC, [p[0:T, 0, 0:C] for p in ps])
                        yield from norm_vector(dve, go, done, B, "n4", HC, X)
                        yield from router_vector(dve, go, done, B, ps, E, 2, None)

                two_at_once(dve, turn, S, "d_s", done)

            @block.scalar
            def _(act):
                act.preload_act_table_set(EXP_LN)
                act.activation(hs[:, 0, :], K["l3_hd"][:, :], ACT.Exp, scale=-1.0).then_inc(setup, 1)
                act.wait_ge(setup, 5)
                act.activation(hs[:, 1, :], hs[:, 0, :], ACT.Ln).then_inc(setup, 1)
                act.wait_ge(setup, 6)
                act.activation(hs[:, 2, :], hs[:, 1, :], ACT.Exp, scale=K["pos1"][:, 0:1]).then_inc(setup, 1)
                here = [None]

                def table(step):
                    if step in ("lat_act", "p_cos", "og", "ff_s"):
                        want = SILU_SIN
                    elif step.endswith(("_log", "_rstd")) or step in ("qk_rs", "e_exp", "p_sig", "p_sig2", "g_exp"):
                        want = EXP_LN
                    else:
                        return
                    if here[0] != want:
                        act.preload_act_table_set(want)
                        here[0] = want

                def turn(i, done, half):
                    def go(c, step):
                        table(step)
                        act.wait_ge(done[c], i * N + (S[step] + 1))

                    def tile_of(c):
                        return WAYS * i + c
                    if half == 0:
                        yield from norm_scalar(act, go, done, B, "n0", eps5[0:T, :])
                        yield from rms_scalar(act, go, done, B, "r1", X, eps6[0:T, :])
                        yield from turn_scalar(act, go, done, "f1", ps, 0, xT, K["l3_ln_w"])
                        yield "lat_act"
                        for c in done:
                            go(c, "lat_act")
                            act.activation(B[c]["latT"][:, :], ps[c][:, 1, 0:T], ACT.Silu).then_inc(done[c], 1)
                        yield "big_cp"
                        for c in done:
                            go(c, "big_cp")
                            for b in range(2):
                                ins = act.copy(B[c]["big"][:, b * 408:(b + 1) * 408], ps[c][0:T, b, 0:408])
                            ins.then_inc(done[c], 1)
                        yield "qk_log"
                        for c in done:
                            go(c, "qk_log")
                            act.activation(B[c]["qs"][:, 1, :], B[c]["qs"][:, 0, :], ACT.Ln, bias=eps6[0:T, :],
                                           scale=1.0 / D).then_inc(done[c], 1)
                        yield "qk_rs"
                        for c in done:
                            go(c, "qk_rs")
                            act.activation(B[c]["qs"][:, 2, :], B[c]["qs"][:, 1, :], ACT.Exp, scale=-0.5
                                           ).then_inc(done[c], 1)
                        yield "e_exp"
                        for c in done:
                            go(c, "e_exp")
                            act.activation(B[c]["rA"][:, :, :], B[c]["rA"][:, :, :], ACT.Exp).then_inc(done[c], 1)
                        yield from query_blocks(act, go, done, B, ps, "q_dg", 0)
                        yield "p_sig"
                        for c in done:
                            go(c, "p_sig")
                            act.activation(B[c]["sg"][:, :, :].rearrange("p h f -> p (h f)"), B[c]["big"][:, 576:624],
                                           ACT.Exp, scale=-1.0).then_inc(done[c], 1)
                        yield "p_cos"
                        for c in done:
                            go(c, "p_cos")
                            act.activation(B[c]["pm"][:, 1, :], B[c]["pm"][:, 2, :], ACT.Sin, bias=half_pi[0:T, :],
                                           scale=-float(np.pi)).then_inc(done[c], 1)
                        yield "p_sig2"
                        for c in done:
                            go(c, "p_sig2")
                            act.activation(B[c]["pm"][:, 0, :], B[c]["pm"][:, 1, :], ACT.Exp, scale=-1.0
                                           ).then_inc(done[c], 1)
                        yield from probs_copy(act.copy, go, done, B, ps, "pc0", 0, 0)
                        yield from probs_copy(act.copy, go, done, B, ps, "pc2", 0, 8)
                    else:
                        yield from rms_scalar(act, go, done, B, "r2", O, eps6[0:T, :])
                        yield from turn_scalar(act, go, done, "fo", ps, 1, oT, K["l3_memn_w"])
                        yield "og"
                        for c in done:
                            go(c, "og")
                            act.activation(B[c]["og"], B[c]["big"][:, 624:816], ACT.Silu).then_inc(done[c], 1)
                        yield from rms_scalar(act, go, done, B, "r3", X, eps6[0:T, :])
                        yield from turn_scalar(act, go, done, "f3", ps, 0, xT, K["l3_ffn_ln_w"])
                        yield "ff_s"
                        for c in done:
                            go(c, "ff_s")
                            act.activation(B[c]["ff"][:, :, :].rearrange("p f t -> p (f t)"), ps[c][:, 0, 0:HID * T],
                                           ACT.Silu).then_inc(done[c], 1)
                        yield from norm_scalar(act, go, done, B, "n4", eps5[0:T, :])
                        yield from turn_scalar(act, go, done, "f4", ps, 0, xT)
                        yield from router_scalar(act, go, done, B, E)
                        yield from weights_out(act, "scalar", go, done, B, ps, combT, ident, tile_of, E)

                two_at_once(act, turn, S, "d_s", done)

            @block.gpsimd
            def _(pool):
                def turn(i, done, half):
                    def go(c, step):
                        pool.wait_ge(done[c], i * N + (S[step] + 1))

                    def tile_of(c):
                        return WAYS * i + c
                    if half == 0:
                        yield from take_experts_back(pool, "pool", go, done, B, ps, h_all, yT_all, ident, tile_of)
                        yield "r_sin"
                        for c in done:
                            go(c, "r_sin")
                            hd = D // 2
                            for a, z in ((0, hd), (hd, 0)):
                                ins = pool.tensor_tensor(B[c]["rB"][:, :, a:a + hd], qk[c][:, :, z:z + hd],
                                                         over(K["rope_sin"][:, a:a + hd].unsqueeze(1), [T, 2 * H, hd]),
                                                         ALU.mult)
                            ins.then_inc(done[c], 1)
                        yield from heads_expand(pool, go, done, B, "kx1", 1, HG, K["hmask16"])
                        yield from blocks_expand(pool, go, done, B, "px1", 8, H, K["bmask"])
                    else:
                        yield from store_tile(pool, go, done, B, h_all, xT_all, tile_of, "hcur")
                        yield from store_xT(pool, go, done, B, xT_all, tile_of)

                two_at_once(pool, turn, S, "d_s", done)

            @block.tensor
            def _(pe):
                pe.wait_ge(setup, 12)
                def turn(i, done, half):
                    def go(c, step):
                        pe.wait_ge(done[c], i * N + (S[step] + 1))

                    def tile_of(c):
                        return WAYS * i + c
                    if half == 0:
                        yield from take_experts_back(pe, "tensor", go, done, B, ps, h_all, yT_all, ident, tile_of)
                        yield from turn_tensor(pe, go, done, "f1", O, ps, 0, ident)
                        yield "lat"
                        for c in done:
                            go(c, "lat")
                            for k in range(2):
                                mm = pe.matmul(ps[c][:, 1, 0:T], K["l3_wcomp"][:, k, :], xT[c][:, k, :],
                                               start=(k == 0), stop=(k == 1))
                            mm.then_inc(done[c], 1)
                        yield "big"
                        for c in done:
                            go(c, "big")
                            for b in range(2):
                                mm = pe.matmul(ps[c][0:T, b, 0:408], B[c]["latT"][:, :],
                                               K["l3_wcat"][:, b * 408:(b + 1) * 408], start=True, stop=True)
                            mm.then_inc(done[c], 1)
                        yield "q_tr"
                        for c in done:
                            go(c, "q_tr")
                            for w in range(2):
                                for o in range(2):
                                    mm = pe.transpose(ps[c][0:CK, w, o * T:(o + 1) * T],
                                                      B[c]["big"][:, w * C + o * CK:w * C + (o + 1) * CK], ident[0:T, 0:T])
                            mm.then_inc(done[c], 1)
                        yield from scores_tensor(pe, go, done, B, ps, HG)
                        yield from values_stage(pe, go, done, B, ps, H, DV,
                                                [b["Vx"][:, :, :].rearrange("p h d -> p (h d)") for b in B], H, ident)
                    else:
                        yield from turn_tensor(pe, go, done, "fo", O, ps, 1, ident)
                        yield from width_product(pe, go, done, "proj", ps, 0, oT, K["l3_wproj"], C)
                        yield from turn_tensor(pe, go, done, "f3", O, ps, 0, ident)
                        yield "ff1"
                        for c in done:
                            go(c, "ff1")
                            for b in range(2):
                                for f in range(HID):
                                    for k in range(2):
                                        mm = pe.matmul(ps[c][:, b, f * T:(f + 1) * T],
                                                       K["l3_w12"][:, k, (b * HID + f) * 128:(b * HID + f + 1) * 128],
                                                       xT[c][:, k, :], start=(k == 0), stop=(k == 1))
                            mm.then_inc(done[c], 1)
                        yield "ff2"
                        for c in done:
                            go(c, "ff2")
                            for f in range(HID):
                                mm = pe.matmul(ps[c][0:T, 0, 0:C], B[c]["ff"][:, f, :], K["l3_w3"][:, f, :],
                                               start=(f == 0), stop=(f == HID - 1))
                            mm.then_inc(done[c], 1)
                        yield from turn_tensor(pe, go, done, "f4", X, ps, 0, ident)
                        yield from width_product(pe, go, done, "gt", ps, 1, xT, K["l3_gate_w"], E)
                        yield from weights_out(pe, "tensor", go, done, B, ps, combT, ident, tile_of, E)

                two_at_once(pe, turn, S, "d_s", done)


def last_tokens(nc, out, h_all, yT_all, ident, sem, sb, **_):
    S = steps("y_cp y_tr y_add")
    N = S["end"]
    done = {c: sem(f"out_tile{c}_steps") for c in range(WAYS)}
    stored = [sem(f"out_stored{c}") for c in range(WAYS)]
    with ExitStack() as ctx:
        B, ps = tile_buffers(ctx, nc, sb, 4, {})
        with nc.Block() as block:
            @block.gpsimd
            def _(pool):
                def turn(i, done):
                    yield from take_experts_back(pool, "pool", lambda c, s: pool.wait_ge(done[c], i * N + (S[s] + 1)), done, B, ps,
                                      h_all, yT_all, ident, lambda c: WAYS * i + c)

                with pool.Fori(0, NT // WAYS) as i:
                    run(turn(i, done))
                run(turn(NT // WAYS, first_tiles(done)))

            @block.tensor
            def _(pe):
                def turn(i, done):
                    yield from take_experts_back(pe, "tensor", lambda c, s: pe.wait_ge(done[c], i * N + (S[s] + 1)), done, B, ps,
                                      h_all, yT_all, ident, lambda c: WAYS * i + c)

                with pe.Fori(0, NT // WAYS) as i:
                    run(turn(i, done))
                run(turn(NT // WAYS, first_tiles(done)))

            @block.vector
            def _(dve):
                for c in done:
                    dve.sem_inc(done[c], 1)
                def turn(i, done):
                    for c in done:
                        dve.wait_ge(stored[c], 16 * i + 1)
                    yield from take_experts_back(dve, "vector", lambda c, s: dve.wait_ge(done[c], i * N + (S[s] + 1)), done, B, ps,
                                      h_all, yT_all, ident, lambda c: WAYS * i + c)

                with dve.Fori(0, NT // WAYS) as i:
                    run(turn(i, done))
                run(turn(NT // WAYS, first_tiles(done)))

            @block.sync
            def _(sp):
                for c in done:
                    sp.sem_inc(stored[c], 1)
                def turn(i, done):
                    for c in done:
                        sp.wait_ge(done[c], i * N + (N + 1))
                        sp.dma_start(out[bass.ds(WAYS * i + c, 1), :, :].rearrange("a t c -> (a t) c"),
                                     B[c]["hcur"][:, :]).then_inc(stored[c], 16)

                with sp.Fori(0, NT // WAYS) as i:
                    turn(i, done)
                turn(NT // WAYS, first_tiles(done))
                for c in done:
                    sp.wait_ge(stored[c], 16 * ((NT - c + WAYS - 1) // WAYS) + 1)



COMMON = ["ident", "bmask", "hmask16", "hmask12", "off_diag", "on_diag", "causal", "anti_causal", "causal01",
          "quarter", "half_pi", "pos1"]
LAYER_WEIGHTS = [
    ["tok_w", "tok_base", "tok_pos", "l0_wqv", "l0_wproj", "l0_bproj", "l0_gate_w", "l0_gate_b"],
    ["l1_wq", "l1_wk", "l1_wv", "l1_bq", "l1_bk", "l1_bv", "l1_wo", "l1_bo", "l1_ln_w", "l1_ln_b", "l1_ln1_w",
     "l1_ln2_w", "l1_wqk", "l1_wv2", "l1_wproj", "l1_gate_w"],
    ["rel", "l2_wqk", "l2_wv", "l2_wproj", "l2_bproj", "l2_wpos", "l2_bpos", "l2_gating", "l2_scale", "l2_gate_w",
     "l2_gate_b"],
    ["rope_cos", "rope_sin", "l3_ln_w", "l3_wcomp", "l3_wcat", "l3_qkn", "l3_hd", "l3_temp", "l3_wproj",
     "l3_memn_w", "l3_ffn_ln_w", "l3_w12", "l3_w3", "l3_gate_w"]]


def shape_constants():
    f = np.float32
    n = np.arange(T) % NTOK
    img = np.arange(T) // NTOK
    m = np.arange(NTOK)
    side = int(round(NTOK ** 0.5))
    dx = (m % side)[None, :] - (n % side)[:, None]
    dy = (m // side)[None, :] - (n // side)[:, None]
    half = np.arange(0, 16, 2, dtype=f) / f(16)
    freq = np.outer(np.arange(NTOK, dtype=f), f(1.0) / (f(10000.0) ** half)).astype(f)
    cos = np.concatenate([np.cos(freq), np.cos(freq)], 1)[n]
    sin = np.concatenate([-np.sin(freq), np.sin(freq)], 1)[n]
    row = np.arange(CK)
    return {
        "ident": np.eye(128, dtype=f),
        "bmask": (img[:, None] == img[None, :]).astype(f),
        "hmask16": (row[:, None] // 16 == np.arange(6)[None, :]).astype(f),
        "hmask12": (row[:, None] // 12 == np.arange(8)[None, :]).astype(f),
        "on_diag": (n[:, None] == m[None, :]).astype(f),
        "off_diag": (n[:, None] != m[None, :]).astype(f),
        "causal": np.where(m[None, :] <= n[:, None], 0.0, -BIG).astype(f),
        "anti_causal": np.where(m[None, :] >= n[:, None], 0.0, -BIG).astype(f),
        "causal01": (m[None, :] <= n[:, None]).astype(f),
        "quarter": np.full((128, 1), -0.25, f),
        "half_pi": np.full((128, 1), np.pi / 2, f),
        "pos1": (n + 1).astype(f)[:, None],
        "rel": np.stack([dx, dy, dx * dx + dy * dy], 1).astype(f),
        "rope_cos": cos.astype(f),
        "rope_sin": sin.astype(f),
    }


def lay_out(a):
    def kxm(w, rows):
        return w.reshape(w.shape[0] // rows, rows, w.shape[1]).transpose(1, 0, 2)

    def rows(v):
        return np.broadcast_to(v[None, :], (T, v.shape[0]))

    def col(v, r):
        return v.reshape(-1, r).T

    def tiles(v, r):
        e, k, m = v.shape
        return v.reshape(e, k // r, r, m).transpose(0, 2, 1, 3).reshape(e, r, k // r * m)

    o = shape_constants()
    x = a["x"].reshape(BATCH, 3, 6, 16, 6, 16).transpose(0, 1, 2, 4, 3, 5).reshape(BATCH, 36, 768)
    full = np.zeros((NT * IMGS, NTOK, 768), x.dtype)
    full[:BATCH, 1:] = x
    o["patches"] = full.reshape(NT, T, 6, 128).transpose(0, 3, 2, 1).reshape(NT, 128, 6 * T)
    o["tok_w"] = kxm(a["L0_tok_W"].T, 128)
    o["tok_base"] = np.tile(np.concatenate([a["L0_tok_class_token"], np.broadcast_to(a["L0_tok_b"], (36, C))]),
                            (IMGS, 1))
    o["tok_pos"] = np.tile(a["L0_tok_pos_embedding"], (IMGS, 1))
    q = a["L0_attn_w_qkv"]
    o["l0_wqv"] = kxm(np.concatenate([q[0:C], q[2 * C:3 * C]]).T, CK)
    o["l0_wproj"] = kxm(a["L0_attn_w_proj"].T, CK)
    o["l0_bproj"] = rows(a["L0_attn_b_proj"])
    o["l0_gate_w"] = kxm(a["L0_ffn_gate_w"].T, CK)
    o["l0_gate_b"] = rows(a["L0_ffn_gate_b"])
    apart = np.concatenate([np.arange(0, C, 2), np.arange(1, C, 2)])
    w1 = np.concatenate([a["L0_ffn_W1"], a["L0_ffn_Ws1"][None]])[:, :, apart]
    w3 = np.concatenate([a["L0_ffn_W3"], a["L0_ffn_Ws3"][None]])[:, :, apart]
    o["l0_w1"] = tiles(np.concatenate([w1, w3], 2), CK)
    o["l0_w2"] = tiles(np.concatenate([a["L0_ffn_W2"], a["L0_ffn_Ws2"][None]]), CK)
    b = np.concatenate([np.concatenate([a["L0_ffn_B1"], a["L0_ffn_Bs1"][None]])[:, apart],
                        np.concatenate([a["L0_ffn_B3"], a["L0_ffn_Bs3"][None]])[:, apart],
                        np.concatenate([a["L0_ffn_B2"], a["L0_ffn_Bs2"][None]])], 1)
    o["l0_b"] = b.reshape(9, 6, CK).transpose(2, 0, 1)
    for n in "qkv":
        o["l1_w" + n] = kxm(a["L1_attn_w" + n], CK)
    o["l1_bq"] = col(a["L1_attn_bq"], 128)
    o["l1_bk"] = col(a["L1_attn_bk"], 128)
    o["l1_bv"] = rows(a["L1_attn_bv"])
    o["l1_wo"] = kxm(a["L1_attn_wo"], 128)
    o["l1_bo"] = rows(a["L1_attn_bo"])
    o["l1_ln_w"] = col(a["L1_attn_ln_w"], CK)
    o["l1_ln_b"] = col(a["L1_attn_ln_b"], CK)
    o["l1_ln1_w"] = col(a["L1_ffn_ln1_w"], CK)
    o["l1_ln2_w"] = col(a["L1_ffn_ln2_w"], CK)
    w = a["L1_ffn_c_attn_w"].T
    o["l1_wqk"] = kxm(w[:, 0:2 * C], CK)
    o["l1_wv2"] = kxm(w[:, 2 * C:3 * C], CK)
    o["l1_wproj"] = kxm(a["L1_ffn_c_proj_w"].T, CK)
    o["l1_gate_w"] = kxm(a["L1_ffn_w_g"].T, CK)
    o["l1_w1"] = tiles(a["L1_ffn_c_fc"], CK)
    o["l1_w2"] = tiles(a["L1_ffn_c_proj_e"], 128)
    o["l2_wqk"] = kxm(a["L2_attn_w_qk"].T, CK)
    o["l2_wv"] = kxm(a["L2_attn_w_v"].T, CK)
    o["l2_wproj"] = kxm(a["L2_attn_w_proj"].T, CK)
    o["l2_bproj"] = rows(a["L2_attn_b_proj"])
    o["l2_wpos"] = np.broadcast_to(a["L2_attn_w_pos"].T[None], (T, 3, 16))
    o["l2_bpos"] = rows(a["L2_attn_b_pos"])
    o["l2_gating"] = rows(a["L2_attn_gating"])
    o["l2_scale"] = col(a["L2_ffn_scale"], CK)
    o["l2_gate_w"] = kxm(a["L2_ffn_gate_w"].T, CK)
    o["l2_gate_b"] = rows(a["L2_ffn_gate_b"])
    o["l2_w1"] = tiles(a["L2_ffn_w1"], CK)
    o["l2_w2"] = tiles(a["L2_ffn_w2"], CK)
    o["l2_b"] = np.concatenate([a["L2_ffn_b1"], a["L2_ffn_b2"]], 1).reshape(16, 6, CK).transpose(2, 0, 1)
    o["l3_ln_w"] = col(a["L3_attn_ln_w"], CK)
    o["l3_wcomp"] = kxm(a["L3_attn_w_comp"], CK)
    o["l3_wcat"] = np.concatenate([a["L3_attn_w_qkv"], a["L3_attn_w_reso"], a["L3_attn_w_outgate"]], 1)
    o["l3_qkn"] = np.broadcast_to(np.stack([a["L3_attn_qn_w"], a["L3_attn_kn_w"]])[None], (T, 2, 16))
    o["l3_hd"] = rows(a["L3_attn_head_decay"])
    o["l3_temp"] = rows(a["L3_attn_temperature"])
    o["l3_wproj"] = kxm(a["L3_attn_w_proj"], CK)
    o["l3_memn_w"] = col(a["L3_attn_memn_w"], CK)
    o["l3_ffn_ln_w"] = col(a["L3_attn_ffn_ln_w"], CK)
    o["l3_w12"] = kxm(np.concatenate([a["L3_attn_w1"], a["L3_attn_w2"]], 1), CK)
    o["l3_w3"] = kxm(a["L3_attn_w3"], 128)
    o["l3_gate_w"] = kxm(a["L3_ffn_w_gate"], CK)
    o["l3_w1"] = tiles(a["L3_ffn_w_fc"].reshape(C, 768, 8).transpose(2, 0, 1), CK)
    o["l3_w2"] = tiles(a["L3_ffn_w_proj"].reshape(768, C, 8).transpose(2, 0, 1), 128)
    return {n: np.ascontiguousarray(v) for n, v in o.items()}


def kernel(**inputs):
    import concourse.bacc as _bacc
    from concourse.bass_utils import run_bass_kernel_spmd as _run

    arrays = {f"in_{n}": v for n, v in lay_out({n: np.asarray(v) for n, v in inputs.items()}).items()}
    nc = _bacc.Bacc("TRN2", target_bir_lowering=False, num_devices=1)
    d = {n[3:]: nc.dram_tensor(n, v.shape, mybir.dt.from_np(v.dtype), kind="ExternalInput").ap()
         for n, v in arrays.items()}
    out = nc.dram_tensor("out", (NT, T, C), F32, kind="ExternalOutput").ap()
    vit_tower(nc, d, out)
    r = _run(nc, [arrays], core_ids=[0])
    got = r.results[0]["out"].reshape(NT * IMGS, NTOK, C)
    return np.ascontiguousarray(got[:BATCH])
```
